# Optimizing a Trainium2 kernel written in Bass

```python
import numpy as np
import jax
import jax.numpy as jnp

def _softmax(x, axis=-1):
    return jax.nn.softmax(x, axis=axis)

def _gelu(x):
    return jax.nn.gelu(x, approximate=True)

def _silu(x):
    return jax.nn.silu(x)

def _sigmoid(x):
    return jax.nn.sigmoid(x)

def _layernorm(x, axis=-1, eps=1e-05):
    m = jnp.mean(x, axis=axis, keepdims=True)
    v = jnp.var(x, axis=axis, keepdims=True)
    return (x - m) / jnp.sqrt(v + eps)

def _scatter_add(tgt, idx, src, axis=0):
    return tgt.at[idx].add(src)

def _segment_sum(src, seg, n):
    return jax.ops.segment_sum(src, seg, n)
kernel_name = 'mk_hybrid_d2_jaxref_r8_e9b8e3'

def setup_inputs(seed: int=0):
    np.random.seed(seed)
    _w = jnp.asarray

    def _L0_attn_a_setup():
        import jax, jax.numpy as jnp
        import numpy as np
        B_, L_, D_RES, D_INNER, N_STATE, K_CONV = (2, 128, 128, 64, 32, 3)

        def _causal_dwconv(x, w, b):
            xt = jnp.transpose(x, (0, 2, 1))
            k = w.shape[-1]
            out = jax.lax.conv_general_dilated(xt, w, (1,), [(k - 1, 0)], feature_group_count=w.shape[0])
            return jnp.transpose(out, (0, 2, 1)) + b

        def _s6(u, W_delta, b_delta, W_B, W_C, A_log, D):
            A = -jnp.exp(A_log)
            delta = jax.nn.softplus(u @ W_delta + b_delta)
            Bm = u @ W_B
            Cm = u @ W_C

            def step(h, inputs):
                u_t, d_t, b_t, c_t = inputs
                dA = jnp.exp(d_t[..., None] * A)
                h = dA * h + (d_t * u_t)[..., None] * b_t[:, None, :]
                y = jnp.einsum('bdn,bn->bd', h, c_t)
                return (h, y)
            h0 = jnp.zeros((u.shape[0], A.shape[0], A.shape[1]), u.dtype)
            xs = (jnp.swapaxes(u, 0, 1), jnp.swapaxes(delta, 0, 1), jnp.swapaxes(Bm, 0, 1), jnp.swapaxes(Cm, 0, 1))
            _, ys = jax.lax.scan(step, h0, xs)
            return jnp.swapaxes(ys, 0, 1) + u * D
        key = jax.random.key(seed)
        ks = jax.random.split(key, 8)
        s = lambda k, shp, sc: jax.random.normal(k, shp, dtype=jnp.float32) * sc
        return {'x': s(ks[0], (B_, L_, D_RES), 1.0), 'ln_gamma': jnp.ones((D_RES,), jnp.float32), 'ln_beta': jnp.zeros((D_RES,), jnp.float32), 'W_up': s(ks[1], (D_RES, 2 * D_INNER), 0.02), 'b_up': jnp.zeros((2 * D_INNER,), jnp.float32), 'conv_w': s(ks[2], (D_INNER, 1, K_CONV), 0.2), 'conv_b': jnp.zeros((D_INNER,), jnp.float32), 'W_delta': s(ks[3], (D_INNER, D_INNER), 0.02), 'b_delta': jnp.full((D_INNER,), -4.0, jnp.float32), 'W_B': s(ks[4], (D_INNER, N_STATE), 0.02), 'W_C': s(ks[5], (D_INNER, N_STATE), 0.02), 'A_log': jnp.log(jnp.broadcast_to(jnp.arange(1, N_STATE + 1, dtype=jnp.float32), (D_INNER, N_STATE))).copy(), 'D': jnp.ones((D_INNER,), jnp.float32), 'W_down': s(ks[6], (D_INNER, D_RES), 0.02), 'b_down': jnp.zeros((D_RES,), jnp.float32)}
    _L0_attn_a_in = _L0_attn_a_setup()

    def _L0_attn_b_setup():
        import jax, jax.numpy as jnp
        import numpy as np
        BATCH, SEQ, HIDDEN = (8, 256, 128)
        WSIZE = 64
        NEG_INF = -1000000000.0
        key = jax.random.key(seed)
        k1, k2 = jax.random.split(key)
        repr_ = jax.random.normal(k1, (BATCH, SEQ, HIDDEN), dtype=jnp.float32)
        W = jax.random.normal(k2, (HIDDEN, HIDDEN), dtype=jnp.float32) * 0.02
        return {'repr': repr_, 'W': W}
    _L0_attn_b_in = _L0_attn_b_setup()

    def _L0_ffn_setup():
        import math
        import jax, jax.numpy as jnp
        import numpy as np
        B, T, D = (4, 512, 128)
        H = 16
        HD = D // H
        CAP = int(512 * 0.125)
        DFF = int(D * 4 * 2 / 3)
        EPS = 1e-06

        def rmsnorm(x, g):
            return x * jax.lax.rsqrt(jnp.mean(x * x, axis=-1, keepdims=True) + EPS) * g
        key = jax.random.key(seed)
        ks = jax.random.split(key, 9)
        s = lambda k, shape: jax.random.normal(k, shape, jnp.float32) * 0.02
        return {'x': jax.random.normal(ks[0], (B, T, D), jnp.float32), 'w_router': s(ks[1], (D,)), 'W_qkv': s(ks[2], (3 * D, D)), 'W_out': s(ks[3], (D, D)), 'g1': jnp.ones((D,), jnp.float32), 'g2': jnp.ones((D,), jnp.float32), 'W1': s(ks[4], (DFF, D)), 'W2': s(ks[5], (DFF, D)), 'W3': s(ks[6], (D, DFF))}
    _L0_ffn_in = _L0_ffn_setup()

    def _L1_attn_a_setup():
        import jax, jax.numpy as jnp
        import numpy as np
        D_MODEL = 128
        NUM_HEADS = 16
        D_K = D_MODEL // NUM_HEADS
        BATCH, SEQ = (2, 256)
        key = jax.random.key(seed)
        k = jax.random.split(key, 5)
        std = np.sqrt(2.0 / (D_MODEL + D_MODEL)).astype(np.float32)
        return {'x': jax.random.normal(k[0], (BATCH, SEQ, D_MODEL), dtype=jnp.float32), 'WQ': jax.random.normal(k[1], (D_MODEL, D_MODEL), dtype=jnp.float32) * std, 'WK': jax.random.normal(k[2], (D_MODEL, D_MODEL), dtype=jnp.float32) * std, 'WV': jax.random.normal(k[3], (D_MODEL, D_MODEL), dtype=jnp.float32) * std, 'WO': jax.random.normal(k[4], (D_MODEL, D_MODEL), dtype=jnp.float32) * std}
    _L1_attn_a_in = _L1_attn_a_setup()

    def _L1_attn_b_setup():
        import jax, jax.numpy as jnp
        import numpy as np
        from jax import lax
        D_MODEL = 128
        D_INNER = 256
        D_STATE = 16
        D_CONV = 4
        DT_RANK = 64
        B, L = (2, 256)
        LN_EPS = 1e-05

        def _layernorm(x, g, b):
            mu = jnp.mean(x, axis=-1, keepdims=True)
            var = jnp.mean(jnp.square(x - mu), axis=-1, keepdims=True)
            return (x - mu) * lax.rsqrt(var + LN_EPS) * g + b

        def _selective_scan(x_h, dt, Bm, Cm, A):
            b = x_h.shape[0]
            xs = (jnp.swapaxes(x_h, 0, 1), jnp.swapaxes(dt, 0, 1), jnp.swapaxes(Bm, 0, 1), jnp.swapaxes(Cm, 0, 1))
            h0 = jnp.zeros((b, D_INNER, D_STATE), x_h.dtype)

            def step(ht, inp):
                x_t, dt_t, B_t, C_t = inp
                dA = jnp.exp(dt_t[..., None] * A)
                dB = dt_t[..., None] * B_t[:, None, :]
                ht = dA * ht + dB * x_t[..., None]
                y_t = jnp.sum(ht * C_t[:, None, :], axis=-1)
                return (ht, y_t)
            _, ys = lax.scan(step, h0, xs)
            return jnp.swapaxes(ys, 0, 1)
        key = jax.random.key(seed)
        ks = jax.random.split(key, 10)
        s = 0.02
        x = jax.random.normal(ks[0], (B, L, D_MODEL), dtype=jnp.float32)
        ln_g = jnp.ones((D_MODEL,), jnp.float32)
        ln_b = jnp.zeros((D_MODEL,), jnp.float32)
        W_in = jax.random.normal(ks[1], (2 * D_INNER, D_MODEL)) * s
        W_x = jax.random.normal(ks[2], (DT_RANK + 2 * D_STATE, D_INNER)) * s
        W_dt = jax.random.normal(ks[3], (D_INNER, DT_RANK)) * s
        b_dt = jax.random.normal(ks[4], (D_INNER,)) * s
        W_out = jax.random.normal(ks[5], (D_MODEL, D_INNER)) * s
        conv_w = jax.random.normal(ks[6], (D_INNER, 1, D_CONV)) * s
        conv_b = jnp.zeros((D_INNER,), jnp.float32)
        A_log = jnp.log(jnp.tile(jnp.arange(1, D_STATE + 1, dtype=jnp.float32), (D_INNER, 1)))
        D_param = jnp.ones((D_INNER,), jnp.float32)
        alpha = jnp.full((1,), 0.5, jnp.float32)
        return dict(x=x, ln_g=ln_g, ln_b=ln_b, W_in=W_in, W_x=W_x, W_dt=W_dt, b_dt=b_dt, W_out=W_out, conv_w=conv_w, conv_b=conv_b, A_log=A_log, D_param=D_param, alpha=alpha)
    _L1_attn_b_in = _L1_attn_b_setup()

    def _L1_ffn_setup():
        import jax, jax.numpy as jnp
        import numpy as np
        DIM = 128
        DEPTH = 2
        HEADS = 8
        DIM_HEAD = 64
        WINDOW = 64
        INNER = HEADS * DIM_HEAD
        HID = int(DIM * 4 * 2 / 3)
        B, N = (2, 1024)
        QK_SCALE = 8.0

        def shift_token(t):
            t1, t2 = jnp.split(t, 2, axis=-1)
            t2 = jnp.pad(t2, ((0, 0), (1, 0), (0, 0)))[:, :-1]
            return jnp.concatenate([t1, t2], axis=-1)

        def l2norm(t):
            return t / jnp.clip(jnp.linalg.norm(t, axis=-1, keepdims=True), 1e-12)

        def rotate_half(x):
            x1, x2 = jnp.split(x, 2, axis=-1)
            return jnp.concatenate([-x2, x1], axis=-1)

        def rotary_xpos(q, k):
            n = q.shape[-2]
            half_idx = jnp.arange(0, DIM_HEAD, 2, dtype=jnp.float32)
            inv_freq = 1.0 / 10000.0 ** (half_idx / DIM_HEAD)
            t = jnp.arange(n, dtype=jnp.float32)
            freqs = t[:, None] * inv_freq[None, :]
            freqs = jnp.concatenate([freqs, freqs], axis=-1)
            base = (half_idx + 0.4 * DIM_HEAD) / (1.4 * DIM_HEAD)
            power = (t - n // 2) / float(WINDOW // 2)
            scale = base[None, :] ** power[:, None]
            scale = jnp.concatenate([scale, scale], axis=-1)
            cos, sin = (jnp.cos(freqs), jnp.sin(freqs))
            q = q * cos * scale + rotate_half(q) * sin * scale
            k = k * cos / scale + rotate_half(k) * sin / scale
            return (q, k)

        def local_attention(q, k, v):
            b, h, n, d = q.shape
            w = n // WINDOW
            bq = q.reshape(b, h, w, WINDOW, d) * QK_SCALE
            bk = k.reshape(b, h, w, WINDOW, d)
            bv = v.reshape(b, h, w, WINDOW, d)

            def look_around(t):
                p = jnp.pad(t, ((0, 0), (0, 0), (1, 0), (0, 0), (0, 0)))
                return jnp.concatenate([p[:, :, :w], p[:, :, 1:]], axis=3)
            bk, bv = (look_around(bk), look_around(bv))
            bt = jnp.arange(n).reshape(w, WINDOW)
            btp = jnp.pad(bt, ((1, 0), (0, 0)), constant_values=-1)
            btk = jnp.concatenate([btp[:w], btp[1:]], axis=1)
            sim = jnp.einsum('bhwid,bhwjd->bhwij', bq, bk)
            i = bt[:, :, None]
            j = btk[:, None, :]
            mask = (i < j) | (i > j + WINDOW) | (j == -1)
            sim = jnp.where(mask, -jnp.finfo(sim.dtype).max, sim)
            attn = jax.nn.softmax(sim, axis=-1)
            out = jnp.einsum('bhwij,bhwjd->bhwid', attn, bv)
            return out.reshape(b, h, n, d)

        def _layer(x, wqkv, qs, ksc, wo, lg, lb, w1, b1, w2, b2):
            b, n, _ = x.shape
            h = shift_token(x)
            qkv = h @ wqkv
            q, k, v = jnp.split(qkv, 3, axis=-1)
            to_heads = lambda t: t.reshape(b, n, HEADS, DIM_HEAD).transpose(0, 2, 1, 3)
            q, k, v = (to_heads(q), to_heads(k), to_heads(v))
            q = l2norm(q) * qs
            k = l2norm(k) * ksc
            q, k = rotary_xpos(q, k)
            o = local_attention(q, k, v)
            o = o.transpose(0, 2, 1, 3).reshape(b, n, INNER)
            x = x + o @ wo
            h = shift_token(x)
            mu = h.mean(-1, keepdims=True)
            var = h.var(-1, keepdims=True)
            h = (h - mu) / jnp.sqrt(var + 1e-05) * lg + lb
            h = h @ w1 + b1
            a, g = jnp.split(h, 2, axis=-1)
            h = a * jax.nn.gelu(g, approximate=False)
            x = x + h @ w2 + b2
            return x
        key = jax.random.key(seed)
        ks = jax.random.split(key, 6)
        return {'x': jax.random.normal(ks[0], (B, N, DIM), jnp.float32), 'wqkv': jax.random.normal(ks[1], (DEPTH, DIM, 3 * INNER), jnp.float32) * 0.02, 'q_scale': jnp.ones((DEPTH, DIM_HEAD), jnp.float32), 'k_scale': jnp.ones((DEPTH, DIM_HEAD), jnp.float32), 'wo': jax.random.normal(ks[2], (DEPTH, INNER, DIM), jnp.float32) * 0.02, 'ln_g': jnp.ones((DEPTH, DIM), jnp.float32), 'ln_b': jnp.zeros((DEPTH, DIM), jnp.float32), 'w1': jax.random.normal(ks[3], (DEPTH, DIM, 2 * HID), jnp.float32) * 0.02, 'b1': jnp.zeros((DEPTH, 2 * HID), jnp.float32), 'w2': jax.random.normal(ks[4], (DEPTH, HID, DIM), jnp.float32) * 0.02, 'b2': jnp.zeros((DEPTH, DIM), jnp.float32)}
    _L1_ffn_in = _L1_ffn_setup()
    _d = {'L0_attn_a_x': _L0_attn_a_in['x'], 'L0_attn_a_ln_gamma': _L0_attn_a_in['ln_gamma'], 'L0_attn_a_ln_beta': _L0_attn_a_in['ln_beta'], 'L0_attn_a_W_up': _L0_attn_a_in['W_up'], 'L0_attn_a_b_up': _L0_attn_a_in['b_up'], 'L0_attn_a_conv_w': _L0_attn_a_in['conv_w'], 'L0_attn_a_conv_b': _L0_attn_a_in['conv_b'], 'L0_attn_a_W_delta': _L0_attn_a_in['W_delta'], 'L0_attn_a_b_delta': _L0_attn_a_in['b_delta'], 'L0_attn_a_W_B': _L0_attn_a_in['W_B'], 'L0_attn_a_W_C': _L0_attn_a_in['W_C'], 'L0_attn_a_A_log': _L0_attn_a_in['A_log'], 'L0_attn_a_D': _L0_attn_a_in['D'], 'L0_attn_a_W_down': _L0_attn_a_in['W_down'], 'L0_attn_a_b_down': _L0_attn_a_in['b_down'], 'L0_attn_b_W': _L0_attn_b_in['W'], 'L0_ffn_w_router': _L0_ffn_in['w_router'], 'L0_ffn_W_qkv': _L0_ffn_in['W_qkv'], 'L0_ffn_W_out': _L0_ffn_in['W_out'], 'L0_ffn_g1': _L0_ffn_in['g1'], 'L0_ffn_g2': _L0_ffn_in['g2'], 'L0_ffn_W1': _L0_ffn_in['W1'], 'L0_ffn_W2': _L0_ffn_in['W2'], 'L0_ffn_W3': _L0_ffn_in['W3'], 'L1_attn_a_WQ': _L1_attn_a_in['WQ'], 'L1_attn_a_WK': _L1_attn_a_in['WK'], 'L1_attn_a_WV': _L1_attn_a_in['WV'], 'L1_attn_a_WO': _L1_attn_a_in['WO'], 'L1_attn_b_ln_g': _L1_attn_b_in['ln_g'], 'L1_attn_b_ln_b': _L1_attn_b_in['ln_b'], 'L1_attn_b_W_in': _L1_attn_b_in['W_in'], 'L1_attn_b_W_x': _L1_attn_b_in['W_x'], 'L1_attn_b_W_dt': _L1_attn_b_in['W_dt'], 'L1_attn_b_b_dt': _L1_attn_b_in['b_dt'], 'L1_attn_b_W_out': _L1_attn_b_in['W_out'], 'L1_attn_b_conv_w': _L1_attn_b_in['conv_w'], 'L1_attn_b_conv_b': _L1_attn_b_in['conv_b'], 'L1_attn_b_A_log': _L1_attn_b_in['A_log'], 'L1_attn_b_D_param': _L1_attn_b_in['D_param'], 'L1_attn_b_alpha': _L1_attn_b_in['alpha'], 'L1_ffn_wqkv': _L1_ffn_in['wqkv'], 'L1_ffn_q_scale': _L1_ffn_in['q_scale'], 'L1_ffn_k_scale': _L1_ffn_in['k_scale'], 'L1_ffn_wo': _L1_ffn_in['wo'], 'L1_ffn_ln_g': _L1_ffn_in['ln_g'], 'L1_ffn_ln_b': _L1_ffn_in['ln_b'], 'L1_ffn_w1': _L1_ffn_in['w1'], 'L1_ffn_b1': _L1_ffn_in['b1'], 'L1_ffn_w2': _L1_ffn_in['w2'], 'L1_ffn_b2': _L1_ffn_in['b2']}
    _x0 = _d['L0_attn_a_x']
    _d['L0_attn_a_x'] = jax.random.normal(jax.random.fold_in(jax.random.key(seed), 1), (4, 1024, 128), dtype=_x0.dtype)
    del _x0
    return _d

def reference(L0_attn_a_x, L0_attn_a_ln_gamma, L0_attn_a_ln_beta, L0_attn_a_W_up, L0_attn_a_b_up, L0_attn_a_conv_w, L0_attn_a_conv_b, L0_attn_a_W_delta, L0_attn_a_b_delta, L0_attn_a_W_B, L0_attn_a_W_C, L0_attn_a_A_log, L0_attn_a_D, L0_attn_a_W_down, L0_attn_a_b_down, L0_attn_b_W, L0_ffn_w_router, L0_ffn_W_qkv, L0_ffn_W_out, L0_ffn_g1, L0_ffn_g2, L0_ffn_W1, L0_ffn_W2, L0_ffn_W3, L1_attn_a_WQ, L1_attn_a_WK, L1_attn_a_WV, L1_attn_a_WO, L1_attn_b_ln_g, L1_attn_b_ln_b, L1_attn_b_W_in, L1_attn_b_W_x, L1_attn_b_W_dt, L1_attn_b_b_dt, L1_attn_b_W_out, L1_attn_b_conv_w, L1_attn_b_conv_b, L1_attn_b_A_log, L1_attn_b_D_param, L1_attn_b_alpha, L1_ffn_wqkv, L1_ffn_q_scale, L1_ffn_k_scale, L1_ffn_wo, L1_ffn_ln_g, L1_ffn_ln_b, L1_ffn_w1, L1_ffn_b1, L1_ffn_w2, L1_ffn_b2):

    def _L0_attn_a_ref(x, ln_gamma, ln_beta, W_up, b_up, conv_w, conv_b, W_delta, b_delta, W_B, W_C, A_log, D, W_down, b_down):
        import jax, jax.numpy as jnp
        import numpy as np
        B_, L_, D_RES, D_INNER, N_STATE, K_CONV = (2, 128, 128, 64, 32, 3)

        def _causal_dwconv(x, w, b):
            xt = jnp.transpose(x, (0, 2, 1))
            k = w.shape[-1]
            out = jax.lax.conv_general_dilated(xt, w, (1,), [(k - 1, 0)], feature_group_count=w.shape[0])
            return jnp.transpose(out, (0, 2, 1)) + b

        def _s6(u, W_delta, b_delta, W_B, W_C, A_log, D):
            A = -jnp.exp(A_log)
            delta = jax.nn.softplus(u @ W_delta + b_delta)
            Bm = u @ W_B
            Cm = u @ W_C

            def step(h, inputs):
                u_t, d_t, b_t, c_t = inputs
                dA = jnp.exp(d_t[..., None] * A)
                h = dA * h + (d_t * u_t)[..., None] * b_t[:, None, :]
                y = jnp.einsum('bdn,bn->bd', h, c_t)
                return (h, y)
            h0 = jnp.zeros((u.shape[0], A.shape[0], A.shape[1]), u.dtype)
            xs = (jnp.swapaxes(u, 0, 1), jnp.swapaxes(delta, 0, 1), jnp.swapaxes(Bm, 0, 1), jnp.swapaxes(Cm, 0, 1))
            _, ys = jax.lax.scan(step, h0, xs)
            return jnp.swapaxes(ys, 0, 1) + u * D
        mu = jnp.mean(x, -1, keepdims=True)
        var = jnp.mean((x - mu) ** 2, -1, keepdims=True)
        y = (x - mu) * jax.lax.rsqrt(var + 1e-05) * ln_gamma + ln_beta
        up = y @ W_up + b_up
        left, right = jnp.split(up, 2, axis=-1)
        left = jax.nn.silu(_causal_dwconv(left, conv_w, conv_b))
        left = _s6(left, W_delta, b_delta, W_B, W_C, A_log, D)
        gated = left * jax.nn.silu(right)
        return x + gated @ W_down + b_down

    def _L0_attn_b_ref(repr, W):
        import jax, jax.numpy as jnp
        import numpy as np
        BATCH, SEQ, HIDDEN = (8, 256, 128)
        WSIZE = 64
        NEG_INF = -1000000000.0
        b, s, d = repr.shape
        idx = jnp.arange(s)
        mask = jnp.abs(idx[:, None] - idx[None, :]) > WSIZE
        scores = jnp.einsum('bqd,de,bke->bqk', repr, W, repr)
        scores = jnp.where(mask[None, :, :], NEG_INF, scores)
        probs = jax.nn.softmax(scores, axis=-1)
        ra = jnp.einsum('bqk,bkd->bqd', probs, repr)
        return repr + jax.nn.relu(ra)

    def _L0_ffn_ref(x, w_router, W_qkv, W_out, g1, g2, W1, W2, W3):
        import math
        import jax, jax.numpy as jnp
        import numpy as np
        B, T, D = (4, 512, 128)
        H = 16
        HD = D // H
        CAP = int(512 * 0.125)
        DFF = int(D * 4 * 2 / 3)
        EPS = 1e-06

        def rmsnorm(x, g):
            return x * jax.lax.rsqrt(jnp.mean(x * x, axis=-1, keepdims=True) + EPS) * g
        Bq, Tq, Dq = x.shape
        scores = x @ w_router
        _, idx = jax.lax.top_k(scores, CAP)
        x_sel = jnp.take_along_axis(x, idx[:, :, None], axis=1)
        h = rmsnorm(x_sel, g1)
        qkv = (h @ W_qkv.T).reshape(Bq, CAP, 3, H, HD)
        q, k, v = jnp.moveaxis(qkv, 2, 0)
        att = jnp.einsum('bqhd,bkhd->bhqk', q, k) / math.sqrt(HD)
        mask = jnp.triu(jnp.ones((CAP, CAP), bool), 1)
        att = jnp.where(mask, -jnp.inf, att)
        att = jax.nn.softmax(att, axis=-1)
        o = jnp.einsum('bhqk,bkhd->bqhd', att, v).reshape(Bq, CAP, Dq)
        x_attn = o @ W_out.T
        h2 = rmsnorm(x_sel + x_attn, g2)
        x_ff = jax.nn.silu(h2 @ W1.T) * (h2 @ W2.T) @ W3.T
        x_proc = x_sel + x_attn + x_ff
        out = x.at[jnp.arange(Bq)[:, None], idx].set(x_proc)
        return out

    def _L1_attn_a_ref(x, WQ, WK, WV, WO):
        import jax, jax.numpy as jnp
        import numpy as np
        D_MODEL = 128
        NUM_HEADS = 16
        D_K = D_MODEL // NUM_HEADS
        BATCH, SEQ = (2, 256)
        B, S, E = x.shape
        mask = jnp.where(jnp.triu(jnp.ones((S, S), dtype=bool), k=1), -jnp.inf, 0.0).astype(x.dtype)

        def heads(W):
            return (x @ W).reshape(B, S, NUM_HEADS, D_K).transpose(0, 2, 1, 3)
        Q, K, V = (heads(WQ), heads(WK), heads(WV))
        score = jnp.einsum('bhqd,bhkd->bhqk', Q, K) / jnp.sqrt(jnp.asarray(D_K, x.dtype))
        score = score + mask
        score = score - jnp.max(score, axis=-1, keepdims=True)
        score = jnp.exp(score)
        score = score / jnp.sum(score, axis=-1, keepdims=True)
        out = jnp.einsum('bhqk,bhkd->bhqd', score, V)
        out = out.transpose(0, 2, 1, 3).reshape(B, S, E)
        return out @ WO

    def _L1_attn_b_ref(x, ln_g, ln_b, W_in, W_x, W_dt, b_dt, W_out, conv_w, conv_b, A_log, D_param, alpha):
        import jax, jax.numpy as jnp
        import numpy as np
        from jax import lax
        D_MODEL = 128
        D_INNER = 256
        D_STATE = 16
        D_CONV = 4
        DT_RANK = 64
        B, L = (2, 256)
        LN_EPS = 1e-05

        def _layernorm(x, g, b):
            mu = jnp.mean(x, axis=-1, keepdims=True)
            var = jnp.mean(jnp.square(x - mu), axis=-1, keepdims=True)
            return (x - mu) * lax.rsqrt(var + LN_EPS) * g + b

        def _selective_scan(x_h, dt, Bm, Cm, A):
            b = x_h.shape[0]
            xs = (jnp.swapaxes(x_h, 0, 1), jnp.swapaxes(dt, 0, 1), jnp.swapaxes(Bm, 0, 1), jnp.swapaxes(Cm, 0, 1))
            h0 = jnp.zeros((b, D_INNER, D_STATE), x_h.dtype)

            def step(ht, inp):
                x_t, dt_t, B_t, C_t = inp
                dA = jnp.exp(dt_t[..., None] * A)
                dB = dt_t[..., None] * B_t[:, None, :]
                ht = dA * ht + dB * x_t[..., None]
                y_t = jnp.sum(ht * C_t[:, None, :], axis=-1)
                return (ht, y_t)
            _, ys = lax.scan(step, h0, xs)
            return jnp.swapaxes(ys, 0, 1)
        residual = x
        h = _layernorm(x, ln_g, ln_b)
        x_and_res = h @ W_in.T
        x_h, res = jnp.split(x_and_res, [D_INNER], axis=-1)
        xc = jnp.swapaxes(x_h, 1, 2)
        xc = lax.conv_general_dilated(xc, conv_w, window_strides=(1,), padding=[(D_CONV - 1, 0)], dimension_numbers=('NCH', 'OIH', 'NCH'), feature_group_count=D_INNER)
        xc = xc + conv_b[None, :, None]
        x_h = jax.nn.silu(jnp.swapaxes(xc, 1, 2))
        x_dbl = x_h @ W_x.T
        dt, Bm, Cm = jnp.split(x_dbl, [DT_RANK, DT_RANK + D_STATE], axis=-1)
        dt = jax.nn.softplus(dt @ W_dt.T + b_dt)
        A = -jnp.exp(A_log)
        y = _selective_scan(x_h, dt, Bm, Cm, A) + x_h * D_param
        y = y * jax.nn.silu(res)
        out = y @ W_out.T
        return residual + alpha * out

    def _L1_ffn_ref(x, wqkv, q_scale, k_scale, wo, ln_g, ln_b, w1, b1, w2, b2):
        import jax, jax.numpy as jnp
        import numpy as np
        DIM = 128
        DEPTH = 2
        HEADS = 8
        DIM_HEAD = 64
        WINDOW = 64
        INNER = HEADS * DIM_HEAD
        HID = int(DIM * 4 * 2 / 3)
        B, N = (2, 1024)
        QK_SCALE = 8.0

        def shift_token(t):
            t1, t2 = jnp.split(t, 2, axis=-1)
            t2 = jnp.pad(t2, ((0, 0), (1, 0), (0, 0)))[:, :-1]
            return jnp.concatenate([t1, t2], axis=-1)

        def l2norm(t):
            return t / jnp.clip(jnp.linalg.norm(t, axis=-1, keepdims=True), 1e-12)

        def rotate_half(x):
            x1, x2 = jnp.split(x, 2, axis=-1)
            return jnp.concatenate([-x2, x1], axis=-1)

        def rotary_xpos(q, k):
            n = q.shape[-2]
            half_idx = jnp.arange(0, DIM_HEAD, 2, dtype=jnp.float32)
            inv_freq = 1.0 / 10000.0 ** (half_idx / DIM_HEAD)
            t = jnp.arange(n, dtype=jnp.float32)
            freqs = t[:, None] * inv_freq[None, :]
            freqs = jnp.concatenate([freqs, freqs], axis=-1)
            base = (half_idx + 0.4 * DIM_HEAD) / (1.4 * DIM_HEAD)
            power = (t - n // 2) / float(WINDOW // 2)
            scale = base[None, :] ** power[:, None]
            scale = jnp.concatenate([scale, scale], axis=-1)
            cos, sin = (jnp.cos(freqs), jnp.sin(freqs))
            q = q * cos * scale + rotate_half(q) * sin * scale
            k = k * cos / scale + rotate_half(k) * sin / scale
            return (q, k)

        def local_attention(q, k, v):
            b, h, n, d = q.shape
            w = n // WINDOW
            bq = q.reshape(b, h, w, WINDOW, d) * QK_SCALE
            bk = k.reshape(b, h, w, WINDOW, d)
            bv = v.reshape(b, h, w, WINDOW, d)

            def look_around(t):
                p = jnp.pad(t, ((0, 0), (0, 0), (1, 0), (0, 0), (0, 0)))
                return jnp.concatenate([p[:, :, :w], p[:, :, 1:]], axis=3)
            bk, bv = (look_around(bk), look_around(bv))
            bt = jnp.arange(n).reshape(w, WINDOW)
            btp = jnp.pad(bt, ((1, 0), (0, 0)), constant_values=-1)
            btk = jnp.concatenate([btp[:w], btp[1:]], axis=1)
            sim = jnp.einsum('bhwid,bhwjd->bhwij', bq, bk)
            i = bt[:, :, None]
            j = btk[:, None, :]
            mask = (i < j) | (i > j + WINDOW) | (j == -1)
            sim = jnp.where(mask, -jnp.finfo(sim.dtype).max, sim)
            attn = jax.nn.softmax(sim, axis=-1)
            out = jnp.einsum('bhwij,bhwjd->bhwid', attn, bv)
            return out.reshape(b, h, n, d)

        def _layer(x, wqkv, qs, ksc, wo, lg, lb, w1, b1, w2, b2):
            b, n, _ = x.shape
            h = shift_token(x)
            qkv = h @ wqkv
            q, k, v = jnp.split(qkv, 3, axis=-1)
            to_heads = lambda t: t.reshape(b, n, HEADS, DIM_HEAD).transpose(0, 2, 1, 3)
            q, k, v = (to_heads(q), to_heads(k), to_heads(v))
            q = l2norm(q) * qs
            k = l2norm(k) * ksc
            q, k = rotary_xpos(q, k)
            o = local_attention(q, k, v)
            o = o.transpose(0, 2, 1, 3).reshape(b, n, INNER)
            x = x + o @ wo
            h = shift_token(x)
            mu = h.mean(-1, keepdims=True)
            var = h.var(-1, keepdims=True)
            h = (h - mu) / jnp.sqrt(var + 1e-05) * lg + lb
            h = h @ w1 + b1
            a, g = jnp.split(h, 2, axis=-1)
            h = a * jax.nn.gelu(g, approximate=False)
            x = x + h @ w2 + b2
            return x
        for l in range(DEPTH):
            x = _layer(x, wqkv[l], q_scale[l], k_scale[l], wo[l], ln_g[l], ln_b[l], w1[l], b1[l], w2[l], b2[l])
        return x
    x = L0_attn_a_x
    x = x + _L0_attn_a_ref(_layernorm(x, axis=-1), L0_attn_a_ln_gamma, L0_attn_a_ln_beta, L0_attn_a_W_up, L0_attn_a_b_up, L0_attn_a_conv_w, L0_attn_a_conv_b, L0_attn_a_W_delta, L0_attn_a_b_delta, L0_attn_a_W_B, L0_attn_a_W_C, L0_attn_a_A_log, L0_attn_a_D, L0_attn_a_W_down, L0_attn_a_b_down)
    x = x + _L0_ffn_ref(_layernorm(x, axis=-1), L0_ffn_w_router, L0_ffn_W_qkv, L0_ffn_W_out, L0_ffn_g1, L0_ffn_g2, L0_ffn_W1, L0_ffn_W2, L0_ffn_W3)
    x = x + _L0_attn_b_ref(_layernorm(x, axis=-1), L0_attn_b_W)
    x = x + _L0_ffn_ref(_layernorm(x, axis=-1), L0_ffn_w_router, L0_ffn_W_qkv, L0_ffn_W_out, L0_ffn_g1, L0_ffn_g2, L0_ffn_W1, L0_ffn_W2, L0_ffn_W3)
    x = x + _L1_attn_a_ref(_layernorm(x, axis=-1), L1_attn_a_WQ, L1_attn_a_WK, L1_attn_a_WV, L1_attn_a_WO)
    x = x + _L1_ffn_ref(_layernorm(x, axis=-1), L1_ffn_wqkv, L1_ffn_q_scale, L1_ffn_k_scale, L1_ffn_wo, L1_ffn_ln_g, L1_ffn_ln_b, L1_ffn_w1, L1_ffn_b1, L1_ffn_w2, L1_ffn_b2)
    x = x + _L1_attn_b_ref(_layernorm(x, axis=-1), L1_attn_b_ln_g, L1_attn_b_ln_b, L1_attn_b_W_in, L1_attn_b_W_x, L1_attn_b_W_dt, L1_attn_b_b_dt, L1_attn_b_W_out, L1_attn_b_conv_w, L1_attn_b_conv_b, L1_attn_b_A_log, L1_attn_b_D_param, L1_attn_b_alpha)
    x = x + _L1_ffn_ref(_layernorm(x, axis=-1), L1_ffn_wqkv, L1_ffn_q_scale, L1_ffn_k_scale, L1_ffn_wo, L1_ffn_ln_g, L1_ffn_ln_b, L1_ffn_w1, L1_ffn_b1, L1_ffn_w2, L1_ffn_b2)
    return x

_drawn_inputs = setup_inputs


def setup_inputs(seed=0):
    import zlib

    import numpy as np

    out = dict(_drawn_inputs(seed))
    spreads = {'L0_attn_a_ln_gamma': (1.0, 0.2),
     'L0_attn_a_ln_beta': (0.0, 0.1),
     'L0_attn_a_b_up': (0.0, 0.1),
     'L0_attn_a_conv_b': (0.0, 0.1),
     'L0_attn_a_b_delta': (-4.0, 0.2),
     'L0_attn_a_D': (1.0, 0.2),
     'L0_attn_a_b_down': (0.0, 0.1),
     'L0_ffn_g1': (1.0, 0.2),
     'L0_ffn_g2': (1.0, 0.2),
     'L1_attn_b_ln_g': (1.0, 0.2),
     'L1_attn_b_ln_b': (0.0, 0.1),
     'L1_attn_b_conv_b': (0.0, 0.1),
     'L1_attn_b_D_param': (1.0, 0.2),
     'L1_ffn_q_scale': (1.0, 0.2),
     'L1_ffn_k_scale': (1.0, 0.2),
     'L1_ffn_ln_g': (1.0, 0.2),
     'L1_ffn_ln_b': (0.0, 0.1),
     'L1_ffn_b1': (0.0, 0.1),
     'L1_ffn_b2': (0.0, 0.1)}
    factors = {}
    for name, (base, spread) in spreads.items():
        noise = np.random.default_rng([zlib.crc32(name.encode()), seed]).standard_normal(out[name].shape)
        drawn = base * np.exp(spread * noise) if base else spread * noise
        out[name] = jnp.asarray(drawn.astype(out[name].dtype))
    for name, factor in factors.items():
        out[name] = (out[name] * factor).astype(out[name].dtype)
    return out
```

```python
from contextlib import ExitStack

import numpy as np

import concourse.bass as bass
from concourse import mybir

F32 = mybir.dt.float32
BF16 = mybir.dt.bfloat16
U32 = mybir.dt.uint32
ALU = mybir.AluOpType
ACT = mybir.ActivationFunctionType
AX_X = mybir.AxisListType.X

P = 128
D = 128
BATCH, SEQ = 4, 1024
TOK = BATCH * SEQ
TILES = TOK // P
TPB = SEQ // P
BANK = 512
MASKED = -1.0e30

STAGES = (1, 2, 3, 4, 5, 6, 7, 8)


class Count:

    def __init__(self, sem):
        self.sem, self.base = sem, 0

    def at(self, n):
        return self.base + n

    def passed(self, n):
        self.base += n


class Core:
    pass





def layernorm(k, second_eps=None):
    nc = k.nc
    EPS = 1e-5
    X = k.X
    total, centred, squared, var, factor, scaled = (
        k.count(n) for n in ("ln_total", "ln_centred", "ln_squared", "ln_var", "ln_factor", "ln_scaled"))
    STEPS = 2 if second_eps is None else 8
    with ExitStack() as mem:
        SQ = k.arena[4].rearrange("p (t d) -> p t d", d=D)
        st = mem.enter_context(nc.sbuf_tensor(k.name("ln_st"), [P, 8, TILES], F32))
        block = mem.enter_context(nc.Block())
        SUM, MEAN, VARSUM, VAR, RSTD, VAR2, T, RSTD2 = range(8)

        def row(r, q):
            return st[:, r, TPB * q:TPB * (q + 1)]

        def wide(r, q):
            return row(r, q).unsqueeze(2).broadcast_to([P, TPB, D])

        def part(m, q):
            return m[:, TPB * q:TPB * (q + 1), :]

        @block.vector
        def _(dve):
            for q in range(BATCH):
                dve.tensor_reduce(row(SUM, q), part(X, q), AX_X, ALU.add).then_inc(total.sem, 1)
                dve.wait_ge(total.sem, total.at(2 * q + 1))
                dve.tensor_scalar(row(MEAN, q), row(SUM, q), 1.0 / D, None, ALU.mult).then_inc(total.sem, 1)
                dve.wait_ge(total.sem, total.at(2 * q + 2))
                dve.tensor_tensor(k.zpart(q), part(X, q), wide(MEAN, q), ALU.subtract).then_inc(centred.sem, 1)
            for q in range(BATCH):
                dve.wait_ge(squared.sem, squared.at(q + 1))
                dve.tensor_reduce(row(VARSUM, q), part(SQ, q), AX_X, ALU.add).then_inc(var.sem, 1)
            for q in range(BATCH):
                dve.wait_ge(factor.sem, factor.at(STEPS * (q + 1)))
                if second_eps is not None:
                    dve.tensor_tensor(part(k.ZZ, q), k.zpart(q), wide(RSTD2, q), ALU.mult).then_inc(scaled.sem, 1)
                    dve.wait_ge(scaled.sem, scaled.at(q + 1))
                dve.tensor_tensor(k.zpart(q), k.zpart(q), wide(RSTD, q), ALU.mult)

        @block.scalar
        def _(act):
            for q in range(BATCH):
                act.wait_ge(centred.sem, centred.at(q + 1))
                act.activation(part(SQ, q), k.zpart(q), ACT.Square).then_inc(squared.sem, 1)

        @block.gpsimd
        def _(pool):
            half = k.minus_half[:, 0:TPB]
            for q in range(BATCH):
                s = STEPS * q
                pool.wait_ge(var.sem, var.at(q + 1))
                pool.tensor_scalar(row(VAR, q), row(VARSUM, q), 1.0 / D, EPS, ALU.mult, ALU.add).then_inc(factor.sem, 1)
                pool.wait_ge(factor.sem, factor.at(s + 1))
                pool.tensor_tensor(row(RSTD, q), row(VAR, q), half, ALU.pow).then_inc(factor.sem, 1)
                if second_eps is not None:
                    pool.tensor_scalar(row(VAR2, q), row(VARSUM, q), 1.0 / D, 0.0, ALU.mult, ALU.add).then_inc(factor.sem, 1)
                    pool.wait_ge(factor.sem, factor.at(s + 3))
                    pool.tensor_tensor(row(T, q), row(VAR2, q), row(RSTD, q), ALU.mult).then_inc(factor.sem, 1)
                    pool.wait_ge(factor.sem, factor.at(s + 4))
                    pool.tensor_tensor(row(VAR2, q), row(T, q), row(RSTD, q), ALU.mult).then_inc(factor.sem, 1)
                    pool.wait_ge(factor.sem, factor.at(s + 5))
                    pool.tensor_scalar(row(T, q), row(VAR2, q), 1.0, second_eps, ALU.mult, ALU.add).then_inc(factor.sem, 1)
                    pool.wait_ge(factor.sem, factor.at(s + 6))
                    pool.tensor_tensor(row(VAR2, q), row(T, q), half, ALU.pow).then_inc(factor.sem, 1)
                    pool.wait_ge(factor.sem, factor.at(s + 7))
                    pool.tensor_tensor(row(RSTD2, q), row(VAR2, q), row(RSTD, q), ALU.mult).then_inc(factor.sem, 1)

    total.passed(2 * BATCH)
    factor.passed(STEPS * BATCH)
    for s in (centred, squared, var):
        s.passed(BATCH)
    if second_eps is not None:
        scaled.passed(BATCH)



def scan(k, batches, halves_n, delta, du, parts, sel, a_col, fold, diag, u, out, gate):
    nc = k.nc
    J, U = 16, 2
    M = fold.shape[1]
    b_up, c_up, b_copied, decay_up, input_up, scanned, weighted, summed, y_taken = [
        k.count("scan_" + n) for n in ("b_up", "c_up", "b_copied", "decay_up", "input_up", "scanned", "weighted",
                                       "summed", "y_taken")]
    begun = k.count("scan_input_begun")
    credited = (b_copied, input_up, scanned, weighted, summed, y_taken)
    for s in credited:
        s.passed(U)
    with ExitStack() as mem:
        ring = k.arena[4].rearrange("p (r s t) -> p r s t", r=2, t=SEQ)
        ring2 = k.arena6.rearrange("p (r s t) -> p r s t", r=3, t=SEQ)
        decay, b_lane = ring[:, 0], ring[:, 1]
        inputs, state, weight = ring2[:, 0], ring2[:, 1], ring2[:, 2]
        bank = k.bank
        block = mem.enter_context(nc.Block())

        def two(first):
            return k.psum[:, first * BANK:(first + 2) * BANK]

        def steps(eng, body, begin=None, end=None):
            with eng.Fori(0, batches) as b:
                for hf in range(halves_n):
                    o = b * halves_n + hf
                    if begin:
                        begin(b, hf, o)
                    with eng.Fori(0, J // U) as jj:
                        for s in range(U):
                            body(b, hf, o, jj * U + s, s)
                    if end:
                        end(b, hf, o)

        @block.sync
        def _(sp):
            for s in credited:
                sp.sem_inc(s.sem, U)

        @block.tensor
        def _(pe):
            def spread(b, j, i, s):
                pe.wait_ge(b_copied.sem, b_copied.at(i))
                for c in range(2):
                    mm = pe.matmul(bank[c], sel(j), parts(0, b, c), start=True, stop=True)
                mm.then_inc(b_up.sem, 1)
                pe.wait_ge(weighted.sem, weighted.at(i - 1))
                for c in range(2):
                    mm = pe.matmul(bank[2 + 2 * s + c], sel(j), parts(1, b, c), start=True, stop=True)
                mm.then_inc(c_up.sem, 1)

            def gather(i, s, last):
                pe.wait_ge(weighted.sem, weighted.at(i + 1))
                for c in range(2):
                    mm = pe.matmul(bank[6 + c][0:M, :], fold, weight[:, s, c * BANK:(c + 1) * BANK], start=False,
                                   stop=last, skip_group_check=True)
                mm.then_inc(summed.sem, 1)

            with pe.Fori(0, batches) as b:
                for hf in range(halves_n):
                    o = b * halves_n + hf
                    pe.wait_ge(y_taken.sem, y_taken.at(o))
                    for c in range(2):
                        pe.matmul(bank[6 + c][0:M, :], diag(hf), u(b, hf, c), start=True, stop=False,
                                  skip_group_check=True)
                    spread(b, 0, o * J, 0)
                    with pe.Fori(0, J // U - 1) as jj:
                        for s in range(U):
                            j = jj * U + s
                            spread(b, j + 1, o * J + j + 1, 1 - s)
                            gather(o * J + j, s, False)
                    spread(b, J - 1, o * J + J - 1, 1)
                    gather(o * J + J - 2, 0, False)
                    gather(o * J + J - 1, 1, True)

        @block.scalar
        def _(act):
            def body(b, hf, o, j, s):
                i = o * J + j
                act.wait_ge(b_up.sem, b_up.at(i + 1))
                act.wait_ge(input_up.sem, input_up.at(i - 1))
                act.activation(b_lane[:, s], two(0), ACT.Copy).then_inc(b_copied.sem, 1)
                act.wait_ge(scanned.sem, scanned.at(i - 1))
                act.activation(decay[:, s], delta(b, hf), ACT.Exp, scale=a_col(hf, j)).then_inc(decay_up.sem, 1)
            steps(act, body)

        @block.gpsimd
        def _(pool):
            def body(b, hf, o, j, s):
                i = o * J + j
                pool.wait_ge(b_copied.sem, b_copied.at(i + 1))
                pool.wait_ge(scanned.sem, scanned.at(i - 1))
                pool.sem_inc(begun.sem, 1)
                pool.tensor_tensor(inputs[:, s], b_lane[:, s], du(b, hf), ALU.mult).then_inc(input_up.sem, 1)
            steps(pool, body)

        @block.vector
        def _(dve):
            def body(b, hf, o, j, s):
                i = o * J + j
                dve.wait_ge(decay_up.sem, decay_up.at(i + 1))
                dve.wait_ge(input_up.sem, input_up.at(i + 1))
                dve.tensor_tensor_scan(state[:, s], decay[:, s], inputs[:, s], 0.0, ALU.mult, ALU.add).then_inc(
                    scanned.sem, 1)
                dve.wait_ge(scanned.sem, scanned.at(i + 1))
                dve.wait_ge(c_up.sem, c_up.at(i + 1))
                dve.wait_ge(summed.sem, summed.at(i - 1))
                dve.tensor_tensor(weight[:, s], state[:, s], two(2 + 2 * s), ALU.mult).then_inc(weighted.sem, 1)

            def end(b, hf, o):
                dve.wait_ge(summed.sem, summed.at((o + 1) * J))
                dve.tensor_tensor(out(b, hf), two(6)[0:M, :], gate(b, hf), ALU.mult).then_inc(y_taken.sem, 1)
            steps(dve, body, end=end)

    n = batches * halves_n
    for s in (b_up, c_up, b_copied, decay_up, input_up, scanned, weighted, summed):
        s.passed(n * J)
    y_taken.passed(n)



def mamba_small(k):
    nc, w = k.nc, k.w
    DI, NS, KC = 64, 32, 3
    layernorm(k, second_eps=1e-5)
    A = k.arena
    FT = A[1]
    LEFT = k.arena_wide[:, 0:BATCH * (SEQ + KC - 1)].rearrange("p (b t) -> p b t", b=BATCH)
    R = A[3][0:DI].rearrange("p (b t) -> p b t", b=BATCH)
    DELTA = A[1].rearrange("p (b t) -> p b t", b=BATCH)
    U = A[0].rearrange("p (b t) -> p b t", b=BATCH)
    DU = A[2].rearrange("p (b t) -> p b t", b=BATCH)
    TMP = A[4].rearrange("p (s t) -> p s t", t=SEQ)
    PARTS = A[5].bitcast(BF16).rearrange("p (m b t) -> p m b t", m=2, b=BATCH)
    NPART = 3 * NS
    bank, psum = k.bank, k.psum

    def two(first):
        return psum[:, first * BANK:(first + 2) * BANK]

    names = ("turned", "normed", "left_up", "right_up", "left", "right", "conv", "u", "residual")
    turned, normed, left_up, right_up, left, right, conv, u_up, resid = cs = [k.count("m1_" + n) for n in names]
    with nc.Block() as block:
        @block.tensor
        def _(pe):
            for b in range(BATCH):
                if b:
                    pe.wait_ge(normed.sem, normed.at(b))
                for j in range(TPB):
                    mm = pe.transpose(bank[j // 4][:, P * (j % 4):P * (j % 4 + 1)], k.ZZ[:, b * TPB + j, :], k.ident)
                mm.then_inc(turned.sem, 1)
                pe.wait_ge(normed.sem, normed.at(b + 1))
                if b:
                    pe.wait_ge(left.sem, left.at(b + 1))
                for c in range(2):
                    mm = pe.matmul(bank[2 + c], w["up_left2"], FT[:, b * SEQ + c * BANK:][:, 0:BANK], start=True, stop=True)
                mm.then_inc(left_up.sem, 1)
                if b:
                    pe.wait_ge(right.sem, right.at(b))
                for c in range(2):
                    mm = pe.matmul(bank[4 + c][0:DI, :], w["W_up"][:, DI:2 * DI], FT[:, b * SEQ + c * BANK:][:, 0:BANK],
                                   start=True, stop=True)
                mm.then_inc(right_up.sem, 1)

        @block.vector
        def _(dve):
            dve.memset(LEFT[:, :, 0:KC - 1], 0.0).then_inc(left.sem, 1)
            for b in range(BATCH):
                dve.wait_ge(turned.sem, turned.at(b + 1))
                dve.tensor_scalar(FT[:, b * SEQ:(b + 1) * SEQ], two(0), w["ln_gamma"], w["ln_beta"], ALU.mult,
                                  ALU.add).then_inc(normed.sem, 1)
                dve.wait_ge(left_up.sem, left_up.at(b + 1))
                dve.tensor_scalar(LEFT[:, b, KC - 1:], two(2), w["b_left2"], None, ALU.add).then_inc(left.sem, 1)
                dve.wait_ge(left.sem, left.at(b + 2))
                if b >= 2:
                    dve.wait_ge(u_up.sem, u_up.at(b - 1))
                acc = TMP[:, b % 2]
                dve.tensor_scalar(acc, LEFT[:, b, 0:SEQ], w["conv_w2"][:, 0:1], None, ALU.mult).then_inc(conv.sem, 1)
                for tap in range(1, KC):
                    dve.wait_ge(conv.sem, conv.at(KC * b + tap))
                    dve.scalar_tensor_tensor(out=acc, in0=LEFT[:, b, tap:tap + SEQ], scalar=w["conv_w2"][:, tap:tap + 1],
                                             in1=acc, op0=ALU.mult, op1=ALU.add).then_inc(conv.sem, 1)

        @block.scalar
        def _(act):
            for b in range(BATCH):
                act.wait_ge(right_up.sem, right_up.at(b + 1))
                act.activation(R[:, b, :], two(4)[0:DI, :], ACT.Silu, bias=w["b_right"]).then_inc(right.sem, 1)
                act.wait_ge(conv.sem, conv.at(KC * (b + 1)))
                act.activation(U[:, b, :], TMP[:, b % 2], ACT.Silu, bias=w["conv_b2"]).then_inc(u_up.sem, 1)

        @block.gpsimd
        def _(pool):
            bias = w["b_down_row"].unsqueeze(1).broadcast_to([P, TPB, D])
            for b in range(BATCH):
                pool.tensor_tensor(k.zpart(b), k.zpart(b), bias, ALU.add).then_inc(resid.sem, 1)
            for b in range(BATCH):
                pool.wait_ge(resid.sem, resid.at(b + 1))
                pool.tensor_tensor(k.xpart(b), k.xpart(b), k.zpart(b), ALU.add)

    names = ("d_up", "b_up", "c_up", "soft", "d_taken", "first", "rest", "mid", "parts", "delta")
    d_up, b_up, c_up, soft, d_taken, first, rest, mid, done, delta_up = [k.count("m1p_" + n) for n in names]
    bc = (b_up, c_up)
    with nc.Block() as block:
        @block.tensor
        def _(pe):
            for b in range(BATCH):
                if b:
                    pe.wait_ge(d_taken.sem, d_taken.at(b))
                    pe.wait_ge(soft.sem, soft.at(3 * b))
                for c in range(2):
                    mm = pe.matmul(bank[c], w["delta2"], U[0:DI, b, c * BANK:(c + 1) * BANK], start=True, stop=True)
                mm.then_inc(d_up.sem, 1)
                for m in range(2):
                    if b:
                        pe.wait_ge(rest.sem, rest.at(2 * (b - 1) + m + 1))
                    for c in range(2):
                        mm = pe.matmul(bank[2 + 2 * m + c][0:NPART, :], w["bc3"][:, m, :], U[0:DI, b, c * BANK:(c + 1) * BANK],
                                       start=True, stop=True)
                    mm.then_inc(bc[m].sem, 1)

        @block.scalar
        def _(act):
            for b in range(BATCH):
                t = TMP[:, b % 2]
                act.wait_ge(d_up.sem, d_up.at(b + 1))
                if b >= 2:
                    act.wait_ge(delta_up.sem, delta_up.at(b - 1))
                act.activation(t, two(0), ACT.Abs, bias=w["b_delta2"]).then_inc(soft.sem, 1)
                act.wait_ge(soft.sem, soft.at(3 * b + 1))
                act.activation(t, t, ACT.Exp, scale=-1.0).then_inc(soft.sem, 1)
                act.wait_ge(soft.sem, soft.at(3 * b + 2))
                act.activation(t, t, ACT.Ln, bias=1.0).then_inc(soft.sem, 1)
                for m in range(2):
                    n = 2 * b + m
                    act.wait_ge(bc[m].sem, bc[m].at(b + 1))
                    act.activation(PARTS[0:NPART, m, b, :], two(2 + 2 * m)[0:NPART, :], ACT.Copy).then_inc(first.sem, 1)
                    act.wait_ge(rest.sem, rest.at(n + 1))
                    act.activation(PARTS[NS:2 * NS, m, b, :], TMP[NS:2 * NS, 2 + m, :], ACT.Copy)
                    act.activation(PARTS[2 * NS:NPART, m, b, :], TMP[2 * NS:NPART, 2 + m, :], ACT.Copy).then_inc(mid.sem, 1)

        @block.vector
        def _(dve):
            for b in range(BATCH):
                dve.wait_ge(soft.sem, soft.at(3 * b + 1))
                dve.tensor_scalar(DELTA[:, b, :], two(0), w["b_delta2"], 0.0, ALU.add, ALU.max).then_inc(d_taken.sem, 1)
                dve.wait_ge(d_taken.sem, d_taken.at(b + 1))
                dve.wait_ge(soft.sem, soft.at(3 * b + 3))
                dve.tensor_tensor(DELTA[:, b, :], DELTA[:, b, :], TMP[:, b % 2], ALU.add).then_inc(delta_up.sem, 1)
                for m in range(2):
                    n = 2 * b + m
                    dve.wait_ge(first.sem, first.at(n + 1))
                    if n >= 2:
                        dve.wait_ge(done.sem, done.at(n - 1))
                    dve.tensor_tensor(TMP[0:NPART, 2 + m, :], two(2 + 2 * m)[0:NPART, :], PARTS[0:NPART, m, b, :],
                                      ALU.subtract).then_inc(rest.sem, 1)
                    dve.wait_ge(mid.sem, mid.at(n + 1))
                    dve.tensor_tensor(PARTS[2 * NS:NPART, m, b, :], TMP[2 * NS:NPART, 2 + m, :],
                                      PARTS[2 * NS:NPART, m, b, :], ALU.subtract).then_inc(done.sem, 1)

        @block.gpsimd
        def _(pool):
            for b in range(BATCH):
                pool.wait_ge(delta_up.sem, delta_up.at(b + 1))
                pool.tensor_tensor(DU[:, b, :], DELTA[:, b, :], U[:, b, :], ALU.mult)

    with ExitStack() as mem:
        selt = mem.enter_context(nc.sbuf_tensor("m1_sel", [NPART, 16 * P], BF16))
        loaded = k.count("m1_sel_in")
        with nc.Block() as block:
            @block.sync
            def _(sp):
                sp.dma_start(selt[:, :], k.dram["c_sel1"]).then_inc(loaded.sem, 16)
                sp.wait_ge(loaded.sem, loaded.at(16))
        scan(k, BATCH, 1, lambda b, hf: DELTA[:, b, :], lambda b, hf: DU[:, b, :],
             lambda m, b, c: PARTS[0:NPART, m, b, c * BANK:(c + 1) * BANK],
             lambda j: selt[:, bass.ds(j * P, P)], lambda hf, j: w["A1"][:, bass.ds(j, 1)], w["fold"], lambda hf: w["D1"],
             lambda b, hf, c: U[:, b, c * BANK:(c + 1) * BANK], lambda b, hf: R[:, b, :], lambda b, hf: R[:, b, :])

    project_back(k, [R.rearrange("p b t -> p (b t)")], [w["W_down"]])


def project_back(k, sources, weights, batches=range(BATCH), scale=None):
    nc = k.nc
    up, added = k.count("back_up"), k.count("back_added")
    with nc.Block() as block:
        @block.tensor
        def _(pe):
            for b in range(len(batches)):
                if b >= 2:
                    pe.wait_ge(added.sem, added.at(b - 1))
                for j in range(TPB):
                    o = k.bank[2 * (b % 2) + j // 4][:, P * (j % 4):P * (j % 4 + 1)]
                    t = (b * TPB + j) * P
                    for n, (src, wt) in enumerate(zip(sources, weights)):
                        mm = pe.matmul(o, src[:, t:t + P], wt, start=n == 0, stop=n == len(sources) - 1)
                mm.then_inc(up.sem, 1)

        @block.vector
        def _(dve):
            for b, seq in enumerate(batches):
                x = k.X[:, seq * TPB:(seq + 1) * TPB, :]
                y = k.psum[:, 2 * (b % 2) * BANK:(2 * (b % 2) + 2) * BANK].rearrange("p (j d) -> p j d", d=D)
                dve.wait_ge(up.sem, up.at(b + 1))
                if scale is None:
                    dve.tensor_tensor(x, x, y, ALU.add).then_inc(added.sem, 1)
                else:
                    dve.scalar_tensor_tensor(out=x, in0=y, scalar=scale, in1=x, op0=ALU.mult,
                                             op1=ALU.add).then_inc(added.sem, 1)
    for s in (up, added):
        s.passed(len(batches))



def mamba_large(k):
    nc, w, bank, psum = k.nc, k.w, k.bank, k.psum
    HV, KC, NS = 2, 4, 16
    RANK, GAP = 64, 32
    NPART = 3 * GAP
    PAIR = 2
    layernorm(k, second_eps=1e-5)
    FT = k.Zpad.rearrange("p t d -> p (t d)")[:, 0:TOK]
    turned, normed, resid = k.count("m7_turned"), k.count("m7_normed"), k.count("m7_residual")
    with nc.Block() as block:
        @block.gpsimd
        def _(pool):
            for b in range(BATCH):
                pool.tensor_tensor(k.xpart(b), k.xpart(b), k.zpart(b), ALU.add).then_inc(resid.sem, 1)

        @block.tensor
        def _(pe):
            for b in range(BATCH):
                for j in range(TPB):
                    mm = pe.transpose(bank[2 * b + j // 4][:, P * (j % 4):P * (j % 4 + 1)], k.ZZ[:, b * TPB + j, :], k.ident)
                mm.then_inc(turned.sem, 1)

        @block.vector
        def _(dve):
            for b in range(BATCH):
                dve.wait_ge(turned.sem, turned.at(b + 1))
                dve.wait_ge(resid.sem, resid.at(BATCH))
                dve.tensor_scalar(FT[:, b * SEQ:(b + 1) * SEQ], psum[:, 2 * b * BANK:(2 * b + 2) * BANK], w["ln7_g"], w["ln7_b"],
                                  ALU.mult, ALU.add).then_inc(normed.sem, 1)

    def quad(a):
        return a.rearrange("p (h b t) -> p h b t", h=HV, b=PAIR)

    U, DELTA, DU, R = (quad(k.arena[n]) for n in (0, 1, 2, 3))
    LEFT = k.arena_wide[:, 0:HV * PAIR * (SEQ + KC - 1)].rearrange("p (h b t) -> p h b t", h=HV, b=PAIR)
    TMP = quad(k.arena[4])
    REST = k.arena6.rearrange("p (s t) -> p s t", t=SEQ)
    PARTS = k.arena[5].bitcast(BF16)[:, 0:2 * PAIR * SEQ].rearrange("p (m b t) -> p m b t", m=2, b=PAIR)

    def two(first):
        return psum[:, first * BANK:(first + 2) * BANK]

    with ExitStack() as mem:
        selt = mem.enter_context(nc.sbuf_tensor("m7_sel", [NPART, NS * P], BF16))
        loaded = k.count("m7_sel_in")
        with nc.Block() as block:
            @block.sync
            def _(sp):
                sp.dma_start(selt[:, :], k.dram["c_sel7"]).then_inc(loaded.sem, 16)
                sp.wait_ge(loaded.sem, loaded.at(16))
        for pair in range(BATCH // PAIR):
            channels(k, pair, two, FT, LEFT, U, R, TMP, HV, KC, PAIR)
            deltas(k, two, U, DELTA, DU, TMP, REST, PARTS, HV, PAIR, RANK, GAP, NPART)
            scan(k, PAIR, HV, lambda b, hf: DELTA[:, hf, b, :], lambda b, hf: DU[:, hf, b, :],
                 lambda m, b, c: PARTS[0:NPART, m, b, c * BANK:(c + 1) * BANK],
                 lambda j: selt[:, bass.ds(j * P, P)], lambda hf, j: w["A7"][:, hf, bass.ds(j, 1)], k.ident,
                 lambda hf: w["D7"][:, hf, :], lambda b, hf, c: U[:, hf, b, c * BANK:(c + 1) * BANK],
                 lambda b, hf: R[:, hf, b, :], lambda b, hf: R[:, hf, b, :])
            project_back(k, [R[:, hf].rearrange("p b t -> p (b t)") for hf in range(HV)],
                         [w["w7_outT"][:, hf, :] for hf in range(HV)], range(pair * PAIR, (pair + 1) * PAIR), w["alpha"])


def channels(k, pair, two, FT, LEFT, U, R, TMP, HV, KC, PAIR):
    nc, w, bank = k.nc, k.w, k.bank
    left_up, right_up, left, right, conv = cs = [k.count("m7c_" + n) for n in ("left_up", "right_up", "left", "right", "conv")]
    with nc.Block() as block:
        @block.tensor
        def _(pe):
            for b in range(PAIR):
                for q in range(2 * HV):
                    n = b * HV + q % HV
                    if b:
                        done = left if q < HV else right
                        pe.wait_ge(done.sem, done.at((1 if q < HV else 0) + n - HV + 1))
                    for c in range(2):
                        at = (pair * PAIR + b) * SEQ + c * BANK
                        mm = pe.matmul(bank[2 * q + c], w["w7_inT"][:, q * P:(q + 1) * P], FT[:, at:at + BANK], start=True, stop=True)
                    mm.then_inc((left_up if q < HV else right_up).sem, 1)

        @block.vector
        def _(dve):
            dve.memset(LEFT[:, :, :, 0:KC - 1], 0.0).then_inc(left.sem, 1)
            for b in range(PAIR):
                for hf in range(HV):
                    n = b * HV + hf
                    dve.wait_ge(left_up.sem, left_up.at(n + 1))
                    dve.tensor_copy(LEFT[:, hf, b, KC - 1:], two(2 * hf)).then_inc(left.sem, 1)
                    dve.wait_ge(left.sem, left.at(n + 2))
                    acc, taps = TMP[:, hf, b, :], w["conv7_w"][:, hf, :]
                    dve.tensor_scalar(acc, LEFT[:, hf, b, 0:SEQ], taps[:, 0:1], None, ALU.mult).then_inc(conv.sem, 1)
                    for tap in range(1, KC):
                        dve.wait_ge(conv.sem, conv.at(KC * n + tap))
                        dve.scalar_tensor_tensor(out=acc, in0=LEFT[:, hf, b, tap:tap + SEQ], scalar=taps[:, tap:tap + 1],
                                                 in1=acc, op0=ALU.mult, op1=ALU.add).then_inc(conv.sem, 1)

        @block.scalar
        def _(act):
            for b in range(PAIR):
                for hf in range(HV):
                    act.wait_ge(right_up.sem, right_up.at(b * HV + hf + 1))
                    act.activation(R[:, hf, b, :], two(4 + 2 * hf), ACT.Silu).then_inc(right.sem, 1)
                for hf in range(HV):
                    act.wait_ge(conv.sem, conv.at(KC * (b * HV + hf + 1)))
                    act.activation(U[:, hf, b, :], TMP[:, hf, b, :], ACT.Silu, bias=w["conv7_b"][:, hf:hf + 1])
    for s in (left_up, right_up, right):
        s.passed(HV * PAIR)
    left.passed(HV * PAIR + 1)
    conv.passed(KC * HV * PAIR)


def deltas(k, two, U, DELTA, DU, TMP, REST, PARTS, HV, PAIR, RANK, GAP, NPART):
    nc, w, bank = k.nc, k.w, k.bank
    names = ("t_up", "dt", "d_up", "b_up", "c_up", "soft", "d_taken", "first", "rest", "mid", "parts", "delta")
    t_up, dt_in, d_up, b_up, c_up, soft, d_taken, first, rest, mid, done, delta_up = [k.count("m7d_" + n) for n in names]
    bc = (b_up, c_up)
    DT = REST[0:RANK, 2:2 + PAIR, :]
    with nc.Block() as block:
        @block.tensor
        def _(pe):
            for b in range(PAIR):
                if b:
                    pe.wait_ge(d_taken.sem, d_taken.at(HV * (b - 1) + 1))
                    pe.wait_ge(soft.sem, soft.at(3 * HV * (b - 1) + 3))
                for c in range(2):
                    for hf in range(HV):
                        mm = pe.matmul(bank[c][0:RANK, :], w["w7_dtin"][:, hf, :], U[:, hf, b, c * BANK:(c + 1) * BANK],
                                       start=hf == 0, stop=hf == HV - 1)
                mm.then_inc(t_up.sem, 1)
                for m in range(2):
                    if b:
                        pe.wait_ge(rest.sem, rest.at(2 * (b - 1) + m + 1))
                    for c in range(2):
                        for hf in range(HV):
                            mm = pe.matmul(bank[2 + 2 * m + c][0:NPART, :], w["bc7"][:, m, hf, :],
                                           U[:, hf, b, c * BANK:(c + 1) * BANK], start=hf == 0, stop=hf == HV - 1)
                    mm.then_inc(bc[m].sem, 1)
                pe.wait_ge(dt_in.sem, dt_in.at(b + 1))
                for hf in range(HV):
                    if b and hf:
                        pe.wait_ge(d_taken.sem, d_taken.at(HV * b))
                        pe.wait_ge(soft.sem, soft.at(3 * HV * b))
                    for c in range(2):
                        mm = pe.matmul(bank[6 * hf + c], w["w7_dtT"][:, hf * P:(hf + 1) * P], DT[:, b, c * BANK:(c + 1) * BANK],
                                       start=True, stop=True)
                    mm.then_inc(d_up.sem, 1)

        @block.scalar
        def _(act):
            for b in range(PAIR):
                for m in range(2):
                    n = 2 * b + m
                    act.wait_ge(bc[m].sem, bc[m].at(b + 1))
                    act.activation(PARTS[0:NPART, m, b, :], two(2 + 2 * m)[0:NPART, :], ACT.Copy).then_inc(first.sem, 1)
                    act.wait_ge(rest.sem, rest.at(n + 1))
                    act.activation(PARTS[GAP:2 * GAP, m, b, :], REST[GAP:2 * GAP, m, :], ACT.Copy)
                    act.activation(PARTS[2 * GAP:NPART, m, b, :], REST[2 * GAP:NPART, m, :], ACT.Copy).then_inc(mid.sem, 1)
                for hf in range(HV):
                    t, n, bias = TMP[:, hf, b, :], 3 * (HV * b + hf), w["b7_dt"][:, hf:hf + 1]
                    act.wait_ge(d_up.sem, d_up.at(HV * b + hf + 1))
                    act.activation(t, two(6 * hf), ACT.Abs, bias=bias).then_inc(soft.sem, 1)
                    act.wait_ge(soft.sem, soft.at(n + 1))
                    act.activation(t, t, ACT.Exp, scale=-1.0).then_inc(soft.sem, 1)
                    act.wait_ge(soft.sem, soft.at(n + 2))
                    act.activation(t, t, ACT.Ln, bias=1.0).then_inc(soft.sem, 1)

        @block.vector
        def _(dve):
            for b in range(PAIR):
                dve.wait_ge(t_up.sem, t_up.at(b + 1))
                dve.tensor_copy(DT[:, b, :], two(0)[0:RANK, :]).then_inc(dt_in.sem, 1)
                for m in range(2):
                    n = 2 * b + m
                    dve.wait_ge(first.sem, first.at(n + 1))
                    if n >= 2:
                        dve.wait_ge(done.sem, done.at(n - 1))
                    dve.tensor_tensor(REST[0:NPART, m, :], two(2 + 2 * m)[0:NPART, :], PARTS[0:NPART, m, b, :],
                                      ALU.subtract).then_inc(rest.sem, 1)
                    dve.wait_ge(mid.sem, mid.at(n + 1))
                    dve.tensor_tensor(PARTS[2 * GAP:NPART, m, b, :], REST[2 * GAP:NPART, m, :],
                                      PARTS[2 * GAP:NPART, m, b, :], ALU.subtract).then_inc(done.sem, 1)
                for hf in range(HV):
                    n = HV * b + hf
                    dve.wait_ge(soft.sem, soft.at(3 * n + 1))
                    dve.tensor_scalar(DELTA[:, hf, b, :], two(6 * hf), w["b7_dt"][:, hf:hf + 1], 0.0, ALU.add,
                                      ALU.max).then_inc(d_taken.sem, 1)
                    dve.wait_ge(d_taken.sem, d_taken.at(n + 1))
                    dve.wait_ge(soft.sem, soft.at(3 * n + 3))
                    dve.tensor_tensor(DELTA[:, hf, b, :], DELTA[:, hf, b, :], TMP[:, hf, b, :], ALU.add).then_inc(delta_up.sem, 1)

        @block.gpsimd
        def _(pool):
            for b in range(PAIR):
                for hf in range(HV):
                    pool.wait_ge(delta_up.sem, delta_up.at(HV * b + hf + 1))
                    pool.tensor_tensor(DU[:, hf, b, :], DELTA[:, hf, b, :], U[:, hf, b, :], ALU.mult)
    for s in (t_up, dt_in, b_up, c_up):
        s.passed(PAIR)
    for s in (d_up, d_taken, delta_up):
        s.passed(HV * PAIR)
    for s in (first, rest, mid, done):
        s.passed(2 * PAIR)
    soft.passed(3 * HV * PAIR)



def in_pairs(eng, n, step, reach=2):
    loops = (n - reach) // 2
    with eng.Fori(0, loops) as p:
        for s in range(2):
            step(p * 2 + s, s, reach)
    for i in range(2 * loops, n):
        step(i, i % 2, n - 1 - i)


def turn_stream(k, into, stride, lead):
    nc, bank = k.nc, k.bank
    turned, taken = k.count("turned"), k.count("turned_taken")
    with nc.Block() as block:
        @block.tensor
        def _(pe):
            for b in range(BATCH):
                for j in range(TPB):
                    mm = pe.transpose(bank[2 * b + j // 4][:, P * (j % 4):P * (j % 4 + 1)], k.Zpad[:, k.zindex(b * TPB + j), :], k.ident)
                mm.then_inc(turned.sem, 1)

        def take(eng, copy, b):
            eng.wait_ge(turned.sem, turned.at(b + 1))
            copy(into[:, b * stride + lead:b * stride + lead + SEQ], k.psum[:, 2 * b * BANK:(2 * b + 2) * BANK])

        @block.vector
        def _(dve):
            for b in range(0, BATCH, 2):
                take(dve, dve.tensor_copy, b)

        @block.scalar
        def _(act):
            for b in range(1, BATCH, 2):
                take(act, act.copy, b)
    turned.passed(BATCH)



def band_attention(k):
    nc, w, bank = k.nc, k.w, k.bank
    WIN, KEYS = 64, 256
    layernorm(k)
    stride = SEQ + 2 * WIN
    ZT = k.big[:, TOK:TOK + BATCH * stride]
    names = ("qw", "q", "scores", "peak", "probs", "pt", "pts", "o", "inverse", "relu", "added", "cleared", "resid")
    qw, q_up, scores, peak, probs, pt, pts, o_up, inverse, relu, added, cleared, resid = [k.count("band_" + n) for n in names]
    credited = (q_up, pts, relu, added, pt, o_up)
    with ExitStack() as mem:
        def sb(name, shape, dt=F32):
            return mem.enter_context(nc.sbuf_tensor("band_" + name, shape, dt))

        mask = sb("mask", [P, TPB, KEYS], BF16)
        Q = sb("q", [P, 2, P])
        PR = sb("probs", [P, 2, KEYS + 2 * WIN])
        PT = sb("pt", [P, 2, 3 * P])
        RO = sb("relu", [P, 2, D])
        top, low, total, inv = (sb(n, [P, 2]) for n in ("top", "low", "total", "inv"))
        with nc.Block() as block:
            @block.sync
            def _(sp):
                sp.dma_start(mask[:, :, :], k.dram["c_band"].rearrange("p (j c) -> p j c", j=TPB)).then_inc(cleared.sem, 16)
                for s in credited:
                    sp.sem_inc(s.sem, 2)
                sp.wait_ge(cleared.sem, cleared.at(16))

            @block.gpsimd
            def _(pool):
                pool.memset(PR[:, :, :], 0.0)
                pool.memset(ZT, 0.0)
        for s in credited:
            s.passed(2)
        turn_stream(k, ZT, stride, WIN)

        with nc.Block() as block:
            @block.tensor
            def _(pe):
                def column(i):
                    return i * P + (i // TPB) * (2 * WIN)

                def query(i, s):
                    pe.wait_ge(q_up.sem, q_up.at(i - 1))
                    pe.matmul(bank[s][:, 0:P], w["W_band"], ZT[:, bass.ds(column(i) + WIN, P)], start=True,
                              stop=True).then_inc(qw.sem, 1)

                def score(i, s):
                    pe.wait_ge(q_up.sem, q_up.at(i + 1))
                    pe.matmul(bank[2 + s][:, 0:KEYS], Q[:, s, :], ZT[:, bass.ds(column(i), KEYS)], start=True, stop=False)
                    pe.matmul(bank[2 + s][:, 0:KEYS], k.identb, mask[:, i % TPB, :], start=False,
                              stop=True).then_inc(scores.sem, 1)

                query(0, 0)
                query(1, 1)
                score(0, 0)

                def step(i, s, ahead):
                    pe.wait_ge(probs.sem, probs.at(i + 1))
                    pe.wait_ge(pts.sem, pts.at(i - 1))
                    for n in range(3):
                        mm = pe.transpose(bank[4 + s][:, n * P:(n + 1) * P], PR[:, s, n * P:(n + 1) * P], k.ident)
                    mm.then_inc(pt.sem, 1)
                    if ahead > 1:
                        query(i + 2, s)
                    if ahead:
                        score(i + 1, 1 - s)
                    pe.wait_ge(relu.sem, relu.at(i - 1))
                    pe.wait_ge(pts.sem, pts.at(i + 1))
                    for n in range(3):
                        mm = pe.matmul(bank[6 + s][:, 0:D], PT[:, s, n * P:(n + 1) * P], k.Zpad[:, k.zindex(i) - 1 + n, :], start=n == 0, stop=n == 2)
                    mm.then_inc(o_up.sem, 1)
                in_pairs(pe, TILES, step)

            @block.scalar
            def _(act):
                def copy_q(i, s):
                    act.wait_ge(qw.sem, qw.at(i + 1))
                    act.copy(Q[:, s, :], bank[s][:, 0:P]).then_inc(q_up.sem, 1)

                copy_q(0, 0)

                def step(i, s, ahead):
                    act.wait_ge(pt.sem, pt.at(i - 1))
                    act.wait_ge(peak.sem, peak.at(2 * i + 2))
                    act.activation(PR[:, s, WIN:WIN + KEYS], bank[2 + s][:, 0:KEYS], ACT.Exp, bias=low[:, s:s + 1],
                                   accum_out=total[:, s:s + 1]).then_inc(probs.sem, 1)
                    if ahead:
                        copy_q(i + 1, 1 - s)
                    act.wait_ge(o_up.sem, o_up.at(i + 1))
                    act.wait_ge(inverse.sem, inverse.at(i + 1))
                    act.wait_ge(added.sem, added.at(i - 1))
                    act.activation(RO[:, s, :], bank[6 + s][:, 0:D], ACT.Relu, scale=inv[:, s:s + 1]).then_inc(relu.sem, 1)
                in_pairs(act, TILES, step)

            @block.vector
            def _(dve):
                def maximum(i, s):
                    dve.wait_ge(scores.sem, scores.at(i + 1))
                    dve.tensor_reduce(top[:, s:s + 1], bank[2 + s][:, 0:KEYS], AX_X, ALU.max).then_inc(peak.sem, 1)
                    dve.wait_ge(peak.sem, peak.at(2 * i + 1))
                    dve.tensor_scalar(low[:, s:s + 1], top[:, s:s + 1], -1.0, None, ALU.mult).then_inc(peak.sem, 1)

                dve.wait_ge(resid.sem, resid.at(1))
                maximum(0, 0)

                def step(i, s, ahead):
                    dve.wait_ge(pt.sem, pt.at(i + 1))
                    dve.wait_ge(o_up.sem, o_up.at(i - 1))
                    dve.tensor_copy(PT[:, s, :], bank[4 + s][:, 0:3 * P]).then_inc(pts.sem, 1)
                    dve.reciprocal(inv[:, s:s + 1], total[:, s:s + 1]).then_inc(inverse.sem, 1)
                    if ahead:
                        maximum(i + 1, 1 - s)
                    dve.wait_ge(relu.sem, relu.at(i + 1))
                    dve.tensor_tensor(k.X[:, i, :], k.X[:, i, :], RO[:, s, :], ALU.add).then_inc(added.sem, 1)
                in_pairs(dve, TILES, step)

            @block.gpsimd
            def _(pool):
                for b in range(BATCH):
                    add = pool.tensor_tensor(k.xpart(b), k.xpart(b), k.zpart(b), ALU.add)
                add.then_inc(resid.sem, 1)



def causal_attention(k):
    nc, w, bank = k.nc, k.w, k.bank
    HEADS, HD, STRIP = 16, 8, 32
    GROUPS, IN = 4, 4
    SCALE = float(1.0 / np.sqrt(HD))
    A = k.arena
    layernorm(k)
    FT = A[0]
    turn_stream(k, FT, SEQ, 0)
    units = [(qt, hh) for qt in range(TPB) for hh in range(IN)]
    chunks = []
    of_unit = []
    for u, (qt, _) in enumerate(units):
        of_unit.append(range(len(chunks), len(chunks) + len(halves(qt + 1, 4))))
        chunks += [(u, a, n) for a, n in halves(qt + 1, 4)]
    NU, NC = len(units), len(chunks)
    assert NC % 2 == 0
    names = ("ft", "ws", "qk_up", "qk", "v_up", "v", "scores", "peak", "probs", "pt", "pt_dve", "pt_act", "pv", "inverse", "o",
             "oT_up", "oT", "y_up", "added", "cleared")
    (ft_in, ws_in, qk_up, qk_in, v_up, v_in, scores, peak, probs, pt, pt_dve, pt_act, pv, inverse, o_in, oT_up, oT_in, y_up,
     added, cleared) = [k.count("causal_" + n) for n in names]
    with ExitStack() as mem:
        def sb(name, shape, dt=F32):
            return mem.enter_context(nc.sbuf_tensor("causal_" + name, shape, dt))

        mask = sb("mask", [P, P], BF16)
        WP = sb("wp", [P, 2, GROUPS, IN, STRIP])
        WS = sb("ws", [P, 2, P])
        low, top, total, inv = (sb(n, [P, NU]) for n in ("low", "top", "total", "inv"))
        FB = A[1][:, 0:SEQ]
        QK = A[1][:, SEQ:3 * SEQ].rearrange("p (m t) -> p m t", m=2)
        OT = A[1][:, 3 * SEQ:3 * SEQ + 2 * P].rearrange("p (s t) -> p s t", s=2)
        V = A[2][:, 0:SEQ].rearrange("p (j d) -> p j d", d=D)
        O = A[2][:, SEQ:2 * SEQ].rearrange("p (j d) -> p j d", d=D)
        PR = A[3][:, 0:2 * SEQ].rearrange("p (s t) -> p s t", s=2)
        PT = A[3][:, 2 * SEQ:4 * SEQ].rearrange("p (s t) -> p s t", s=2)
        with nc.Block() as block:
            @block.sync
            def _(sp):
                sp.dma_start(mask[:, :], k.dram["c_causal"]).then_inc(cleared.sem, 16)
                for s, n in ((qk_in, 2), (v_in, 1), (ft_in, 1), (ws_in, 1), (v_up, 1), (qk_up, 2), (pv, NU), (o_in, 1), (scores, NU),
                             (oT_up, 2), (added, 2), (pt_dve, 1), (pt_act, 1)):
                    sp.sem_inc(s.sem, n)
                    s.passed(n)
                sp.wait_ge(cleared.sem, cleared.at(16))

            @block.vector
            def _(dve):
                dve.memset(WP[:, :, :, :, :], 0.0).then_inc(peak.sem, 1)
                dve.wait_ge(peak.sem, peak.at(1))
                for m, n in enumerate("QK"):
                    dve.tensor_copy(WP[:, m, :, :, 0:HD], w["W" + n].rearrange("p (g h e) -> p g h e", g=GROUPS, h=IN))
        peak.passed(1)

        def rounds(eng, begin, body, end):
            with eng.Fori(0, BATCH) as b:
                begin(b)
                with eng.Fori(0, GROUPS) as g:
                    body(b, g, b * GROUPS + g)
                end(b)

        def two(first):
            return k.psum[:, first * BANK:(first + 2) * BANK]

        with nc.Block() as block:
            @block.gpsimd
            def _(pool):
                def begin(b):
                    pool.wait_ge(qk_up.sem, qk_up.at(2 * GROUPS * b))
                    pool.wait_ge(v_up.sem, v_up.at(b))
                    pool.sem_inc(cleared.sem, 1)
                    pool.tensor_copy(FB, FT[:, bass.ds(b * SEQ, SEQ)]).then_inc(ft_in.sem, 1)

                def body(b, g, r):
                    pool.wait_ge(qk_up.sem, qk_up.at(2 * r))
                    pool.sem_inc(cleared.sem, 1)
                    pool.tensor_copy(WS[:, :, :], WP[:, :, bass.ds(g, 1), :, :].rearrange("p m a h e -> p m (a h e)")).then_inc(
                        ws_in.sem, 1)
                rounds(pool, begin, body, lambda b: None)

            @block.tensor
            def _(pe):
                def begin(b):
                    pe.wait_ge(ft_in.sem, ft_in.at(b + 1))
                    pe.wait_ge(added.sem, added.at(TPB * b))
                    pe.wait_ge(pv.sem, pv.at(NU * GROUPS * b))
                    for j in range(TPB):
                        mm = pe.matmul(bank[4 + j // 4][:, P * (j % 4):P * (j % 4 + 1)], FB[:, j * P:(j + 1) * P], w["WV"],
                                       start=True, stop=True)
                    mm.then_inc(v_up.sem, 1)

                def body(b, g, r):
                    pe.wait_ge(ws_in.sem, ws_in.at(r + 1))
                    pe.wait_ge(v_in.sem, v_in.at(b + 1))
                    for m in range(2):
                        for c in range(2):
                            mm = pe.matmul(bank[2 * m + c], WS[:, m, :], FB[:, c * BANK:(c + 1) * BANK], start=True, stop=True)
                        mm.then_inc(qk_up.sem, 1)
                    pe.wait_ge(qk_in.sem, qk_in.at(2 * r + 2))

                    def score(u):
                        qt, hh = units[u]
                        rows = slice(STRIP * hh, STRIP * (hh + 1))
                        for a, n in halves((qt + 1) * P, BANK):
                            mm = pe.matmul(bank[2 * (u % 2) + a // BANK][:, 0:n], QK[rows, 0, qt * P:(qt + 1) * P],
                                           QK[rows, 1, a:a + n], start=True, stop=True)
                        mm = pe.matmul(bank[2 * (u % 2) + a // BANK][:, n - P:n], k.identb, mask[:, :], start=False, stop=True,
                                       skip_group_check=True)
                        mm.then_inc(scores.sem, 1)

                    def values(u):
                        qt, hh = units[u]
                        last = chunks[of_unit[u][-1]]
                        for c in of_unit[u]:
                            t = pt_dve if c % 2 == 0 else pt_act
                            pe.wait_ge(t.sem, t.at(r * (NC // 2) + c // 2 + 1))
                            _, a, n = chunks[c]
                            for blk in range(a, a + n):
                                mm = pe.matmul(bank[6][:, 0:TPB * IN * HD].rearrange("p (j h e) -> p j h e", j=TPB, h=IN)[:, qt, hh, :],
                                               PT[:, u % 2, blk * P:(blk + 1) * P], V[:, blk, :].rearrange(
                                                   "p (g c) -> p g c", g=GROUPS)[:, bass.ds(g, 1), hh * HD:(hh + 1) * HD].rearrange("p a c -> p (a c)"),
                                               start=blk == 0, stop=blk == qt)
                        mm.then_inc(pv.sem, 1)

                    score(0)
                    for u in range(NU):
                        if u + 1 < NU:
                            if u >= 1:
                                pe.wait_ge(probs.sem, probs.at(r * NU + u))
                            score(u + 1)
                        pe.wait_ge(probs.sem, probs.at(r * NU + u + 1))
                        for c in of_unit[u]:
                            t = pt_dve if c % 2 == 0 else pt_act
                            pe.wait_ge(t.sem, t.at(r * (NC // 2) + c // 2))
                            _, a, n = chunks[c]
                            for i in range(n):
                                mm = pe.transpose(bank[4 + c % 2][:, i * P:(i + 1) * P], PR[:, u % 2, (a + i) * P:(a + i + 1) * P], k.ident)
                            mm.then_inc(pt.sem, 1)
                        if u == 0:
                            pe.wait_ge(o_in.sem, o_in.at(r))
                        if u >= 1:
                            values(u - 1)
                    values(NU - 1)

                def end(b):
                    pe.wait_ge(o_in.sem, o_in.at((b + 1) * GROUPS))
                    for j in range(TPB):
                        s = j % 2
                        pe.transpose(bank[s][:, 0:P], O[:, j, :], k.ident).then_inc(oT_up.sem, 1)
                        pe.wait_ge(oT_in.sem, oT_in.at(b * TPB + j + 1))
                        if j >= 2:
                            pe.wait_ge(added.sem, added.at(b * TPB + j - 1))
                        pe.matmul(bank[2 + s][:, 0:D], OT[:, s, :], w["WO"], start=True, stop=True).then_inc(y_up.sem, 1)
                    pe.wait_ge(added.sem, added.at((b + 1) * TPB))
                rounds(pe, begin, body, end)

            def take(eng, copy, t, u, c, r):
                _, a, n = chunks[c]
                eng.wait_ge(pt.sem, pt.at(r * NC + c + 1))
                eng.wait_ge(pv.sem, pv.at(r * NU + u - 1))
                copy(PT[:, u % 2, a * P:(a + n) * P], bank[4 + c % 2][:, 0:n * P]).then_inc(t.sem, 1)

            @block.scalar
            def _(act):
                def begin(b):
                    act.wait_ge(v_up.sem, v_up.at(b + 1))
                    act.copy(V.rearrange("p j d -> p (j d)"), two(4)).then_inc(v_in.sem, 1)

                def body(b, g, r):
                    act.wait_ge(qk_up.sem, qk_up.at(2 * r + 1))
                    act.wait_ge(scores.sem, scores.at(r * NU))
                    act.copy(QK[:, 0, :], two(0)).then_inc(qk_in.sem, 1)

                    def exponential(u):
                        qt, hh = units[u]
                        n = (qt + 1) * P
                        act.wait_ge(peak.sem, peak.at(2 * (r * NU + u) + 2))
                        if u >= 2:
                            act.wait_ge(pt.sem, pt.at(r * NC + of_unit[u - 2][-1] + 1))
                        act.activation(PR[:, u % 2, 0:n], two(2 * (u % 2))[:, 0:n], ACT.Exp, bias=low[:, u:u + 1], scale=SCALE,
                                       accum_out=total[:, u:u + 1]).then_inc(probs.sem, 1)

                    exponential(0)
                    for u in range(NU):
                        if u + 1 < NU:
                            exponential(u + 1)
                        for c in of_unit[u]:
                            if c % 2:
                                take(act, act.copy, pt_act, u, c, r)

                def end(b):
                    for j in range(TPB):
                        act.wait_ge(oT_up.sem, oT_up.at(b * TPB + j + 1))
                        if j >= 2:
                            act.wait_ge(y_up.sem, y_up.at(b * TPB + j - 1))
                        act.copy(OT[:, j % 2, :], bank[j % 2][:, 0:P]).then_inc(oT_in.sem, 1)
                rounds(act, begin, body, end)

            @block.vector
            def _(dve):
                def body(b, g, r):
                    dve.wait_ge(qk_up.sem, qk_up.at(2 * r + 2))
                    dve.wait_ge(scores.sem, scores.at(r * NU))
                    dve.tensor_copy(QK[:, 1, :], two(2)).then_inc(qk_in.sem, 1)

                    def maximum(u):
                        qt, hh = units[u]
                        dve.wait_ge(scores.sem, scores.at(r * NU + u + 1))
                        dve.tensor_reduce(top[:, u:u + 1], two(2 * (u % 2))[:, 0:(qt + 1) * P], AX_X, ALU.max).then_inc(peak.sem, 1)
                        dve.wait_ge(peak.sem, peak.at(2 * (r * NU + u) + 1))
                        dve.tensor_scalar(low[:, u:u + 1], top[:, u:u + 1], -SCALE, None, ALU.mult).then_inc(peak.sem, 1)

                    maximum(0)
                    for u in range(NU):
                        if u + 1 < NU:
                            maximum(u + 1)
                        for c in of_unit[u]:
                            if c % 2 == 0:
                                take(dve, dve.tensor_copy, pt_dve, u, c, r)
                    dve.reciprocal(inv[:, :], total[:, :]).then_inc(inverse.sem, 1)
                    dve.wait_ge(pv.sem, pv.at((r + 1) * NU))
                    dve.wait_ge(inverse.sem, inverse.at(r + 1))
                    dve.wait_ge(oT_up.sem, oT_up.at(TPB * b))
                    og = O.rearrange("p j (g h e) -> p j g h e", g=GROUPS, h=IN)[:, :, bass.ds(g, 1), :, :].rearrange(
                        "p j a h e -> p j (a h) e")
                    dve.tensor_tensor(og, bank[6][:, 0:TPB * IN * HD].rearrange("p (j h e) -> p j h e", j=TPB, h=IN),
                                      inv[:, :].rearrange("p (j h) -> p j h", h=IN).unsqueeze(3).broadcast_to([P, TPB, IN, HD]),
                                      ALU.mult).then_inc(o_in.sem, 1)

                def end(b):
                    for j in range(TPB):
                        x = k.X[:, b * TPB + j, :]
                        dve.wait_ge(y_up.sem, y_up.at(b * TPB + j + 1))
                        dve.tensor_tensor(x, x, bank[2 + j % 2][:, 0:D], ALU.add).then_inc(added.sem, 1)
                rounds(dve, lambda b: None, body, end)



def local_transformer(k):
    nc = k.nc
    layernorm(k)
    for depth in range(2):
        local_attention(k, depth)
        gated_units(k, depth)
    with nc.Block() as block:
        @block.vector
        def _(dve):
            for b in range(0, BATCH, 2):
                dve.tensor_tensor(k.xpart(b), k.xpart(b), k.zpart(b), ALU.add)

        @block.gpsimd
        def _(pool):
            for b in range(1, BATCH, 2):
                pool.tensor_tensor(k.xpart(b), k.xpart(b), k.zpart(b), ALU.add)


def local_attention(k, depth):
    nc, bank, psum = k.nc, k.bank, k.psum
    HEADS, HD, WIN = 8, 64, 64
    PAIRS, KEYS = HEADS // 2, WIN + P
    INNER = HEADS * HD
    A = k.arena
    w = k.layer
    names = ("zs", "ht_up", "ht", "qkv_up", "raw", "v_in", "sq", "ss", "ab", "rn", "rot", "tr_up", "qkt", "s_up", "peak", "probs",
             "pt_up", "pt_a", "pt_b", "pv_up", "o_in", "ot_up", "ot", "y_up", "added", "loaded", "ready", "ready2", "held")
    (zs_in, ht_up, ht_in, qkv_up, raw_in, v_in, sq_in, ss_in, ab_in, rn_in, rot, tr_up, qkt, s_up, peak, probs, pt_up, pt_a, pt_b,
     pv_up, o_in, ot_up, ot_in, y_up, added, loaded, ready, ready2, held) = [k.count("local_" + n) for n in names]

    def cut(i, size, first, shape):
        n = int(np.prod(shape))
        flat = A[i][:, first:first + n]
        names = "abcd"[:len(shape)]
        return flat.rearrange(f"p ({' '.join(names)}) -> p {' '.join(names)}", **dict(zip(names, shape)))

    TABLE = cut(0, 0, 0, (TPB, 2, 2, HD))
    BASE = cut(0, 0, 2048, (TPB, 2, 2, HD))
    RAW = cut(1, 0, 0, (2, 2 * INNER))
    SQ = cut(1, 0, 2048, (2 * INNER,))
    HT = cut(1, 0, 3072, (2, P))
    ZS = cut(1, 0, 3328, (2, KEYS))
    COS = cut(2, 0, 0, (2, 2 * INNER))
    SIN = cut(2, 0, 2048, (2, 2 * INNER))
    QT = cut(3, 0, 0, (2, PAIRS, P))
    KT = cut(3, 0, 1024, (2, PAIRS, KEYS))
    O = cut(3, 0, 2560, (INNER,))
    OT = cut(3, 0, 3072, (PAIRS, P))
    MASK = A[3][:, 3584:4096].bitcast(BF16)[:, 0:2 * KEYS].rearrange("p (m c) -> p m c", m=2)
    PR = cut(4, 0, 0, (2, HEADS, 2 * P))
    PT = cut(5, 0, 0, (HEADS, 2, P))
    V = cut(5, 0, 2048, (4, INNER))
    small = k.arena6[:, 0:512].rearrange("p (s c) -> p s c", c=16)
    SS, RN, TOP, LOW, SUM, INV = (small[:, 2 * n:2 * n + 2, :] for n in range(6))
    SC = k.arena6[:, 512:768].rearrange("p (m a d) -> p m a d", m=2, a=2)
    SHIFT, CARRY = k.w["shift"], k.w["carry"]

    credited = (ht_in, v_in, qkt, added, ot_in, pt_a, pt_b, ht_up, tr_up, rot, ab_in, s_up, pv_up, probs, pt_up, o_in, y_up, ot_up,
                raw_in, ss_in, sq_in, zs_in, qkv_up, rn_in)
    CREDIT = 4
    with nc.Block() as block:
        @block.sync
        def _(sp):
            d = k.dram
            n = 0
            sp.dma_start(BASE, d["c_rope"].rearrange("p (j a m d) -> p j a m d", j=TPB, a=2, m=2)).then_inc(loaded.sem, 16)
            sp.dma_start(MASK, d["c_local"].rearrange("p (m c) -> p m c", m=2)).then_inc(loaded.sem, 16)
            half = HD // 2
            for m, name in enumerate(("q_scale", "k_scale")):
                row = d["L1_ffn_" + name][depth]
                sp.dma_start(SC[:, 0, m, :], row.partition_broadcast(P)).then_inc(loaded.sem, 16)
                sp.dma_start(SC[:, 1, m, 0:half], row[half:HD].partition_broadcast(P)).then_inc(loaded.sem, 16)
                sp.dma_start(SC[:, 1, m, half:HD], row[0:half].partition_broadcast(P)).then_inc(loaded.sem, 16)
            load_layer(k, sp, depth, loaded)
            for s in credited:
                sp.sem_inc(s.sem, CREDIT)
            sp.wait_ge(loaded.sem, loaded.at(16 * (8 + LAYER_LOADS)))

        @block.vector
        def _(dve):
            dve.memset(KT, 0.0)
            dve.memset(V, 0.0)
            dve.memset(k.Zpad[:, 0:TILES + BATCH + 1:TPB + 1, :], 0.0)
            dve.wait_ge(loaded.sem, loaded.at(16 * (8 + LAYER_LOADS)))
            scales = SC.rearrange("p m a d -> p (m a) d")
            for j in range(TPB):
                dve.tensor_tensor(TABLE[:, j].rearrange("p m a d -> p (m a) d"), BASE[:, j].rearrange("p m a d -> p (m a) d"),
                                  scales, ALU.mult)

        @block.gpsimd
        def _(pool):
            pool.memset(PR, 0.0)
    for s in credited:
        s.passed(CREDIT)
    loaded.passed(16 * (8 + LAYER_LOADS))

    REACH = 3

    def scores_of(i):
        return psum[:, 3 * BANK:7 * BANK].rearrange("p (r c) -> p r c", c=2 * P)[:, :, 0:KEYS]

    with nc.Block() as block:
        @block.tensor
        def _(pe):
            def turn_in(i, s):
                pe.wait_ge(zs_in.sem, zs_in.at(i + 1))
                pe.wait_ge(ht_in.sem, ht_in.at(i))
                pe.wait_ge(ot_in.sem, ot_in.at(i - REACH))
                pe.matmul(bank[7][0:64, 0:P], ZS[:, s, 64:128], k.ident, start=True, stop=True)
                pe.matmul(bank[7][64:P, 0:P], ZS[:, s, 128:192], SHIFT, start=True, stop=False)
                pe.matmul(bank[7][64:P, 0:P], ZS[:, s, 0:64], CARRY, start=False, stop=True).then_inc(ht_up.sem, 1)

            def project(i, s):
                pe.wait_ge(ht_in.sem, ht_in.at(i + 1))
                pe.wait_ge(qkt.sem, qkt.at(i - 1))
                pe.wait_ge(added.sem, added.at(i - 2))
                for m in range(3):
                    mm = pe.matmul(bank[m], HT[:, s, :], w["wqkv"][:, m * INNER:(m + 1) * INNER], start=True, stop=True)
                mm.then_inc(qkv_up.sem, 1)

            def turn_qk(i, s):
                pe.wait_ge(rot.sem, rot.at(i + 1))
                for m in range(2):
                    for c in range(PAIRS):
                        mm = pe.transpose(bank[m][:, c * P:(c + 1) * P], COS[:, s, m * INNER + c * P:m * INNER + (c + 1) * P], k.ident)
                mm.then_inc(tr_up.sem, 1)

            turn_in(0, 0)
            project(0, 0)
            turn_in(1, 1)
            pe.wait_ge(raw_in.sem, raw_in.at(1))
            pe.wait_ge(v_in.sem, v_in.at(1))
            turn_qk(0, 0)
            pe.wait_ge(qkt.sem, qkt.at(1))
            project(1, 1)
            turn_in(2, 0)

            def step(i, s, ahead):
                pe.wait_ge(qkt.sem, qkt.at(i + 1))
                pe.wait_ge(pt_a.sem, pt_a.at(i))
                pe.wait_ge(pt_b.sem, pt_b.at(i))
                for c in range(PAIRS):
                    for hh in range(2):
                        r = hh * PAIRS + c
                        o = bank[3 + r // 2][:, 2 * P * (r % 2):2 * P * (r % 2) + KEYS]
                        pe.matmul(o, QT[64 * hh:64 * hh + 64, s, c, :], KT[64 * hh:64 * hh + 64, s, c, :], start=c % 2 == 0, stop=True,
                                  skip_group_check=True)
                for n in range(4):
                    o = bank[3 + n].rearrange("p (a c) -> p a c", a=2)[:, :, 0:KEYS]
                    rows = MASK[:, bass.ds((i % TPB + TPB - 1) // TPB, 1), :].broadcast_to([P, 2, KEYS])
                    mm = pe.matmul(o, k.identb, rows, start=False, stop=True, skip_group_check=True)
                mm.then_inc(s_up.sem, 1)
                if ahead > 2:
                    turn_in(i + 3, 1 - s)
                if ahead > 1:
                    project(i + 2, s)
                pe.wait_ge(probs.sem, probs.at(i + 1))
                for r in range(HEADS):
                    for n in range(2):
                        mm = pe.transpose(bank[3 + r // 2][:, P * (2 * (r % 2) + n):P * (2 * (r % 2) + n + 1)],
                                          PR[:, s, r, n * P:(n + 1) * P], k.ident)
                mm.then_inc(pt_up.sem, 1)
                if ahead > 1:
                    pe.wait_ge(v_in.sem, v_in.at(i + 3))
                    pe.wait_ge(raw_in.sem, raw_in.at(i + 3))
                else:
                    pe.wait_ge(added.sem, added.at(i))
                pe.wait_ge(pt_a.sem, pt_a.at(i + 1))
                pe.wait_ge(pt_b.sem, pt_b.at(i + 1))
                for r in range(HEADS):
                    h = 2 * (r % PAIRS) + r // PAIRS
                    for n in range(2):
                        mm = pe.matmul(bank[2][:, h * HD:(h + 1) * HD], PT[:, r, n, :], V[:, (i + 3 + n) % 4, h * HD:(h + 1) * HD],
                                       start=n == 0, stop=n == 1)
                mm.then_inc(pv_up.sem, 1)
                if ahead:
                    turn_qk(i + 1, 1 - s)
                pe.wait_ge(o_in.sem, o_in.at(i + 1))
                if ahead > 2:
                    pe.wait_ge(ht_in.sem, ht_in.at(i + 4))
                for c in range(PAIRS):
                    mm = pe.transpose(bank[7][:, c * P:(c + 1) * P], O[:, c * P:(c + 1) * P], k.ident)
                mm.then_inc(ot_up.sem, 1)
                pe.wait_ge(ot_in.sem, ot_in.at(i + 1))
                for c in range(PAIRS):
                    mm = pe.matmul(bank[2][:, 0:D], OT[:, c, :], w["wo"][:, c, :], start=c == 0, stop=c == PAIRS - 1)
                mm.then_inc(y_up.sem, 1)
            in_pairs(pe, TILES, step, REACH)

        @block.scalar
        def _(act):
            def copy_h(i, s):
                act.wait_ge(ht_up.sem, ht_up.at(i + 1))
                act.wait_ge(qkv_up.sem, qkv_up.at(i - 1))
                act.copy(HT[:, s, :], bank[7][:, 0:P]).then_inc(ht_in.sem, 1)

            def take(i, s):
                act.wait_ge(qkv_up.sem, qkv_up.at(i + 1))
                act.wait_ge(ab_in.sem, ab_in.at(i - 1))
                act.copy(RAW[:, s, :], psum[:, 0:2 * BANK]).then_inc(raw_in.sem, 1)
                act.wait_ge(raw_in.sem, raw_in.at(i + 1))
                act.wait_ge(ss_in.sem, ss_in.at(i))
                act.activation(SQ, RAW[:, s, :], ACT.Square).then_inc(sq_in.sem, 1)

            def take_v(i):
                act.wait_ge(pv_up.sem, pv_up.at(i - 3))
                act.sem_inc(held.sem, 1)
                act.copy(V[:, i % 4, :], bank[2]).then_inc(v_in.sem, 1)

            copy_h(0, 0)
            take(0, 0)
            take_v(0)
            copy_h(1, 1)
            take(1, 1)
            take_v(1)
            copy_h(2, 0)

            def step(i, s, ahead):
                if ahead > 2:
                    copy_h(i + 3, 1 - s)
                act.wait_ge(peak.sem, peak.at(2 * i + 2))
                act.wait_ge(pt_up.sem, pt_up.at(i - 1))
                for r in range(HEADS):
                    e = act.activation(PR[:, s, r, WIN:], scores_of(i)[:, r, :], ACT.Exp, bias=LOW[:, s, r:r + 1],
                                       accum_out=SUM[:, s, r:r + 1])
                e.then_inc(probs.sem, 1)
                if ahead > 1:
                    take(i + 2, s)
                    take_v(i + 2)
                act.wait_ge(pt_up.sem, pt_up.at(i + 1))
                act.wait_ge(pv_up.sem, pv_up.at(i))
                act.copy(PT[:, 0:4].rearrange("p r n t -> p (r n t)"), psum[:, 3 * BANK:5 * BANK]).then_inc(pt_a.sem, 1)
            in_pairs(act, TILES, step, REACH)

        @block.vector
        def _(dve):
            def rotate(i, s):
                j = i % TPB
                dve.wait_ge(raw_in.sem, raw_in.at(i + 1))
                dve.wait_ge(tr_up.sem, tr_up.at(i - 1))
                raw = RAW[:, s, :].rearrange("p (m h d) -> p m h d", m=2, d=HD)
                cos = COS[:, s, :].rearrange("p (m h d) -> p m h d", m=2, d=HD)
                sin = SIN[:, s, :].rearrange("p (m h d) -> p m h d", m=2, d=HD)

                def table(a, lo, hi):
                    t = TABLE[:, bass.ds(j, 1), a, :, lo:hi].rearrange("p a m d -> p (a m) d")
                    return t.unsqueeze(2).broadcast_to([P, 2, HEADS, hi - lo])

                half = HD // 2
                dve.tensor_tensor(cos, raw, table(0, 0, HD), ALU.mult)
                dve.tensor_tensor(sin[:, :, :, 0:half], raw[:, :, :, half:HD], table(1, 0, half), ALU.mult)
                dve.tensor_tensor(sin[:, :, :, half:HD], raw[:, :, :, 0:half], table(1, half, HD), ALU.mult).then_inc(ab_in.sem, 1)
                dve.wait_ge(sq_in.sem, sq_in.at(i + 1))
                dve.wait_ge(rn_in.sem, rn_in.at(2 * (i - 1)))
                dve.tensor_reduce(SS[:, s, :], SQ.rearrange("p (h d) -> p h d", d=HD), AX_X, ALU.add).then_inc(ss_in.sem, 1)

            def copy_qk(i, s):
                dve.wait_ge(tr_up.sem, tr_up.at(i + 1))
                dve.wait_ge(s_up.sem, s_up.at(i))
                keys = bank[1].rearrange("p (c t) -> p c t", t=P)
                dve.tensor_copy(QT[:, s].rearrange("p c t -> p (c t)"), bank[0])
                dve.tensor_copy(KT[:, s, :, WIN:], keys)
                dve.tensor_copy(KT[:, 1 - s, :, 0:WIN], keys[:, :, P - WIN:P]).then_inc(qkt.sem, 1)

            rotate(0, 0)
            copy_qk(0, 0)
            rotate(1, 1)

            def step(i, s, ahead):
                dve.wait_ge(s_up.sem, s_up.at(i + 1))
                dve.tensor_reduce(TOP[:, s, 0:HEADS], scores_of(i), AX_X, ALU.max).then_inc(peak.sem, 1)
                dve.wait_ge(peak.sem, peak.at(2 * i + 1))
                dve.tensor_scalar(LOW[:, s, 0:HEADS], TOP[:, s, 0:HEADS], -1.0, None, ALU.mult).then_inc(peak.sem, 1)
                dve.wait_ge(pt_up.sem, pt_up.at(i + 1))
                dve.wait_ge(pv_up.sem, pv_up.at(i))
                dve.tensor_copy(PT[:, 4:8].rearrange("p r n t -> p (r n t)"), psum[:, 5 * BANK:7 * BANK]).then_inc(pt_b.sem, 1)
                dve.reciprocal(INV[:, s, 0:HEADS], SUM[:, s, 0:HEADS]).then_inc(ready.sem, 1)
                if ahead > 1:
                    rotate(i + 2, s)
                dve.wait_ge(pv_up.sem, pv_up.at(i + 1))
                dve.wait_ge(ready.sem, ready.at(i + 1))
                dve.wait_ge(ot_up.sem, ot_up.at(i))
                inv = INV[:, s, 0:HEADS].rearrange("p (a c) -> p c a", a=2).unsqueeze(3).broadcast_to([P, PAIRS, 2, HD])
                dve.tensor_tensor(O.rearrange("p (c a d) -> p c a d", a=2, d=HD), bank[2].rearrange("p (c a d) -> p c a d", a=2, d=HD),
                                  inv, ALU.mult).then_inc(o_in.sem, 1)
                if ahead:
                    copy_qk(i + 1, 1 - s)
                dve.wait_ge(ot_up.sem, ot_up.at(i + 1))
                dve.wait_ge(y_up.sem, y_up.at(i))
                dve.tensor_copy(OT.rearrange("p c t -> p (c t)"), bank[7]).then_inc(ot_in.sem, 1)
                dve.wait_ge(y_up.sem, y_up.at(i + 1))
                z = k.Zpad[:, bass.ds(k.zindex(i), 1), :].rearrange("p a d -> p (a d)")
                dve.tensor_tensor(z, z, bank[2][:, 0:D], ALU.add).then_inc(added.sem, 1)
            in_pairs(dve, TILES, step, REACH)

        @block.gpsimd
        def _(pool):
            def fetch(i, s):
                pool.wait_ge(ht_up.sem, ht_up.at(i - 1))
                pool.sem_inc(held.sem, 1)
                flat = k.Zpad.rearrange("p t d -> p (t d)")
                pool.tensor_copy(ZS[:, s, :], flat[:, bass.ds(k.zindex(i) * D - 64, KEYS)]).then_inc(zs_in.sem, 1)

            def norm(i, s):
                pool.wait_ge(ss_in.sem, ss_in.at(i + 1))
                pool.tensor_tensor(RN[:, s, :], SS[:, s, :], k.minus_half[:, 0:2 * HEADS], ALU.pow).then_inc(rn_in.sem, 1)
                pool.wait_ge(rn_in.sem, rn_in.at(2 * i + 1))
                pool.sem_inc(held.sem, 1)
                pool.tensor_scalar(RN[:, s, :], RN[:, s, :], 1e12, 0.0, ALU.min, ALU.max).then_inc(rn_in.sem, 1)
                pool.wait_ge(ab_in.sem, ab_in.at(i + 1))
                pool.tensor_tensor(COS[:, s, :], COS[:, s, :], SIN[:, s, :], ALU.add).then_inc(ready2.sem, 1)
                pool.wait_ge(ready2.sem, ready2.at(i + 1))
                pool.wait_ge(rn_in.sem, rn_in.at(2 * i + 2))
                heads = COS[:, s, :].rearrange("p (h d) -> p h d", d=HD)
                pool.tensor_tensor(heads, heads, RN[:, s, :].unsqueeze(2).broadcast_to([P, 2 * HEADS, HD]), ALU.mult).then_inc(
                    rot.sem, 1)

            for i in range(3):
                fetch(i, i % 2)
            norm(0, 0)
            norm(1, 1)

            def step(i, s, ahead):
                if ahead > 2:
                    fetch(i + 3, 1 - s)
                if ahead > 1:
                    norm(i + 2, s)
            in_pairs(pool, TILES, step, REACH)

    for s in (zs_in, ht_up, ht_in, qkv_up, raw_in, v_in, sq_in, ss_in, ab_in, rot, tr_up, qkt, s_up, probs, pt_up, pt_a, pt_b, pv_up,
              o_in, ot_up, ot_in, y_up, added, ready, ready2):
        s.passed(TILES)
    for s in (peak, rn_in):
        s.passed(2 * TILES)


LAYER_LOADS = 14


def load_layer(k, sp, depth, loaded):
    d, w, f = k.dram, k.layer, "L1_ffn_"
    HID = d[f + "w2"].shape[1]
    whole = HID // P
    rest = HID - whole * P
    pairs = [
        (w["wqkv"], d[f + "wqkv"][depth]),
        (w["wo"], d[f + "wo"][depth].rearrange("(c p) d -> p c d", p=P)),
        (w["w1"], d[f + "w1"][depth].rearrange("p (m h) -> p m h", m=2)),
        (w["w2"][:, 0:whole, :], d[f + "w2"][depth][0:whole * P].rearrange("(c p) d -> p c d", p=P)),
        (w["w2"][0:rest, whole, :], d[f + "w2"][depth][whole * P:HID]),
        (w["w2"][rest:rest + 1, whole, :], d[f + "b2"][depth].rearrange("(a d) -> a d", a=1)),
        (w["ln"][:, 0:1], d[f + "ln_g"][depth].rearrange("(p a) -> p a", a=1)),
        (w["ln"][:, 1:2], d[f + "ln_b"][depth].rearrange("(p a) -> p a", a=1))]
    for m in range(2):
        for c, (a, r) in enumerate(halves(HID, P)):
            pairs.append((w["b1"][0:r, m, c:c + 1], d[f + "b1"][depth][m * HID + a:m * HID + a + r].rearrange("(p a) -> p a", a=1)))
    assert len(pairs) == LAYER_LOADS
    for into, source in pairs:
        sp.dma_start(into, source).then_inc(loaded.sem, 16)


def gated_units(k, depth):
    nc, bank, w = k.nc, k.bank, k.layer
    EPS = 1e-5
    UNIT = 4
    UNITS = TILES // UNIT
    HID = w["w1"].shape[2]
    CHUNKS = halves(HID, P)
    NC = len(CHUNKS)
    A = k.arena
    HN = A[0][:, 0:2 * BANK].rearrange("p (s j d) -> p s j d", s=2, d=D)
    HNT = A[0][:, 2 * BANK:4 * BANK].rearrange("p (s t) -> p s t", s=2)
    GL = A[1][:, 0:2 * BANK].rearrange("p (s t) -> p s t", s=2)
    PROD = A[2][:, 0:2 * NC * BANK].rearrange("p (s c t) -> p s c t", s=2, c=NC)
    small = k.arena6[:, 0:128]
    STATS = small[:, 0:24].rearrange("p (j c) -> p j c", j=UNIT)
    MV = small[:, 32:48].rearrange("p (s j c) -> p s j c", s=2, j=UNIT)
    RSTD = small[:, 48:56].rearrange("p (s j) -> p s j", s=2)
    VAR = small[:, 56:64].rearrange("p (s j) -> p s j", s=2)
    names = ("h_up", "stats", "moments", "rstd", "hn", "t_up", "hnt", "ag_up", "gelu", "prod", "y_up", "added", "held")
    h_up, stats, moments, rstd, hn, t_up, hnt, ag_up, gelu, prod, y_up, added, held = [k.count("units_" + n) for n in names]
    credited = (hn, hnt, prod, gelu, y_up, added, t_up, ag_up, h_up, rstd, moments, stats)
    CREDIT = 8
    for s in credited:
        s.passed(CREDIT)
    with nc.Block() as block:
        @block.sync
        def _(sp):
            for s in credited:
                sp.sem_inc(s.sem, CREDIT)

        @block.vector
        def _(dve):
            dve.memset(PROD, 1.0)

    with nc.Block() as block:
        @block.tensor
        def _(pe):
            def shifted(u):
                pe.wait_ge(hn.sem, hn.at(u))
                for j in range(UNIT):
                    i = u * UNIT + j
                    z = k.zindex(i)
                    o = bank[0][:, j * P:(j + 1) * P]
                    pe.matmul(o[:, 0:64], k.ident, k.Zpad[:, z, 0:64], start=j == 0, stop=True, skip_group_check=True)
                    pe.matmul(o[:, 64:P], k.w["shift"], k.Zpad[:, z, 64:P], start=False, stop=False, skip_group_check=True)
                    mm = pe.matmul(o[:, 64:P], k.w["carry"], k.Zpad[:, z - 1, 64:P], start=False, stop=True, skip_group_check=True)
                mm.then_inc(h_up.sem, 1)

            def turn(u, s):
                pe.wait_ge(hn.sem, hn.at(u + 1))
                pe.wait_ge(hnt.sem, hnt.at(u))
                for j in range(UNIT):
                    mm = pe.transpose(bank[1][:, j * P:(j + 1) * P], HN[:, s, j, :], k.ident)
                mm.then_inc(t_up.sem, 1)

            shifted(0)
            turn(0, 0)
            shifted(1)

            def step(u, s, ahead):
                pe.wait_ge(hnt.sem, hnt.at(u + 1))
                for c, (a, r) in enumerate(CHUNKS):
                    pe.wait_ge(prod.sem, prod.at(u * NC + c - 1))
                    for m in range(2):
                        mm = pe.matmul(bank[2 + 2 * ((s + c) % 2) + m][0:r, :], w["w1"][:, m, a:a + r], HNT[:, s, :], start=True, stop=True)
                    mm.then_inc(ag_up.sem, 1)
                if ahead > 1:
                    shifted(u + 2)
                if ahead:
                    turn(u + 1, 1 - s)
                pe.wait_ge(prod.sem, prod.at((u + 1) * NC))
                pe.wait_ge(added.sem, added.at(u))
                for j in range(UNIT):
                    for c, (a, r) in enumerate(CHUNKS):
                        r += c == NC - 1
                        mm = pe.matmul(bank[6][:, j * P:(j + 1) * P], PROD[0:r, s, c, j * P:(j + 1) * P], w["w2"][0:r, c, :],
                                       start=c == 0, stop=c == NC - 1)
                mm.then_inc(y_up.sem, 1)
            in_pairs(pe, UNITS, step)

        @block.scalar
        def _(act):
            def affine(u, s):
                act.wait_ge(t_up.sem, t_up.at(u + 1))
                act.wait_ge(ag_up.sem, ag_up.at(NC * (u - 1)))
                act.activation(HNT[:, s, :], bank[1], ACT.Identity, scale=w["ln"][:, 0:1], bias=w["ln"][:, 1:2]).then_inc(hnt.sem, 1)

            affine(0, 0)

            def step(u, s, ahead):
                for c, (a, r) in enumerate(CHUNKS):
                    n = u * NC + c
                    act.wait_ge(ag_up.sem, ag_up.at(n + 1))
                    act.wait_ge(prod.sem, prod.at(n - 1))
                    act.activation(GL[0:r, (s + c) % 2, :], bank[3 + 2 * ((s + c) % 2)][0:r, :], ACT.Gelu,
                                   bias=w["b1"][0:r, 1, c:c + 1]).then_inc(gelu.sem, 1)
                if ahead:
                    affine(u + 1, 1 - s)
            in_pairs(act, UNITS, step)

        @block.vector
        def _(dve):
            def normalise(u, s):
                dve.wait_ge(h_up.sem, h_up.at(u + 1))
                for j in range(UNIT):
                    st = dve.bn_stats(STATS[:, j, :], bank[0][:, j * P:(j + 1) * P])
                st.then_inc(stats.sem, 1)
                dve.wait_ge(stats.sem, stats.at(u + 1))
                dve.wait_ge(t_up.sem, t_up.at(u - 1))
                dve.sem_inc(held.sem, 1)
                for j in range(UNIT):
                    mv = dve.bn_aggr(MV[:, s, j, :], STATS[:, j, :])
                mv.then_inc(moments.sem, 1)
                dve.wait_ge(rstd.sem, rstd.at(2 * u + 2))
                for j in range(UNIT):
                    h = dve.tensor_scalar(HN[:, s, j, :], bank[0][:, j * P:(j + 1) * P], MV[:, s, j, 0:1], RSTD[:, s, j:j + 1],
                                          ALU.subtract, ALU.mult)
                h.then_inc(hn.sem, 1)

            normalise(0, 0)
            normalise(1, 1)

            def step(u, s, ahead):
                for c, (a, r) in enumerate(CHUNKS):
                    dve.wait_ge(gelu.sem, gelu.at(u * NC + c + 1))
                    dve.wait_ge(y_up.sem, y_up.at(u - 1))
                    dve.scalar_tensor_tensor(out=PROD[0:r, s, c, :], in0=bank[2 + 2 * ((s + c) % 2)][0:r, :],
                                             scalar=w["b1"][0:r, 0, c:c + 1], in1=GL[0:r, (s + c) % 2, :], op0=ALU.add,
                                             op1=ALU.mult).then_inc(prod.sem, 1)
                if ahead > 1:
                    normalise(u + 2, s)
                dve.wait_ge(y_up.sem, y_up.at(u + 1))
                z = k.Zpad[:, bass.ds(k.zindex(u * UNIT), UNIT), :]
                dve.tensor_tensor(z, z, bank[6].rearrange("p (j d) -> p j d", d=D), ALU.add).then_inc(added.sem, 1)
            in_pairs(dve, UNITS, step)

        @block.gpsimd
        def _(pool):
            with pool.Fori(0, UNITS // 2) as v:
                for s in range(2):
                    u = v * 2 + s
                    pool.wait_ge(moments.sem, moments.at(u + 1))
                    pool.sem_inc(held.sem, 1)
                    pool.tensor_scalar(VAR[:, s, :], MV[:, s, :, 1], 1.0, EPS, ALU.mult, ALU.add).then_inc(rstd.sem, 1)
                    pool.wait_ge(rstd.sem, rstd.at(2 * u + 1))
                    pool.tensor_tensor(RSTD[:, s, :], VAR[:, s, :], k.minus_half[:, 0:UNIT], ALU.pow).then_inc(rstd.sem, 1)

    for s in (h_up, stats, moments, hn, t_up, hnt, y_up, added):
        s.passed(UNITS)
    for s in (ag_up, gelu, prod):
        s.passed(UNITS * NC)
    rstd.passed(2 * UNITS)



def routed_ffn(k):
    nc, w, bank, psum = k.nc, k.w, k.bank, k.psum
    CAP, HEADS, HD, TOP = 64, 16, 8, 8
    T = BATCH * CAP // P
    PER = P // CAP
    N = BATCH * CAP
    EPS = 1e-6
    SCALE = float(1.0 / np.sqrt(HD))
    DFF = w["f_upT"].shape[2]
    CHUNKS = halves(DFF, P)
    GONE = -3.0e38
    A = k.arena
    layernorm(k)
    FT = A[0]
    HOTR = A[1][:, 0:T * SEQ].rearrange("p (t s) -> p t s", t=T)
    HOTT = A[1][:, T * SEQ:2 * T * SEQ].rearrange("p (t j r) -> p t j r", t=T, j=TPB)
    IOTA = A[2][:, 0:SEQ]
    SCORE = A[2][0:BATCH, SEQ:3 * SEQ].rearrange("p (s t) -> p s t", s=2)
    MASK = A[2][:, 3 * SEQ:3 * SEQ + BANK // 2].bitcast(BF16)
    QB = A[3].rearrange("p (b h q) -> p b h q", b=BATCH, h=HEADS)
    E = A[4][:, 0:BATCH * BANK].rearrange("p (b c t) -> p b c t", b=BATCH, c=TOP)
    PT = A[5][0:CAP, :].rearrange("p (b c r) -> p b c r", b=BATCH, c=HEADS // 2)
    at = [0]

    def place(*shape):
        n = int(np.prod(shape))
        names = "abcd"[:len(shape)]
        flat = k.arena6[:, at[0]:at[0] + n]
        at[0] += n
        return flat.rearrange(f"p ({' '.join(names)}) -> p {' '.join(names)}", **dict(zip(names, shape)))

    XS, XA, H, O, S2, H2, Y, SQ = (place(T, D) for _ in range(8))
    HT, QT, KT, OT, H2T = (place(N) for _ in range(5))
    V = place(BATCH, D)[0:CAP]
    SIL, PROD = place(len(CHUNKS), N), place(len(CHUNKS), N)
    HEADMASK = place(HEADS)
    IDX = place(T * CAP)[0:BATCH]
    IDXT = place(T)
    VALS = place(CAP)[0:BATCH]
    IDXU = place(CAP).bitcast(U32)[0:BATCH]
    SS, MS, RS = place(2, T), place(2, T), place(2, T)
    PEAK, SUM, INV = place(BATCH, TOP), place(BATCH, TOP), place(BATCH, TOP)
    names = ("loaded", "resid", "routed", "score", "rank", "idx", "idx_up", "idxT", "hotr", "hott_up", "hott", "picked", "xs", "ss",
             "rs", "h", "h_up", "ht", "qk_up", "qk", "v_up", "v", "qb", "s_up", "soft", "exp", "e", "pt_up", "pt", "pv", "o", "ot_up",
             "ot", "xa_up", "xa", "up", "sil", "prod", "down", "y", "spread", "added")
    c = {n: k.count("route_" + n) for n in names}

    def inc(ins, name):
        return ins.then_inc(c[name].sem, 16 if name == "loaded" else 1)

    def wait(eng, name, n):
        eng.wait_ge(c[name].sem, c[name].at(n))

    turn_stream(k, FT, SEQ, 0)
    with nc.Block() as block:
        @block.sync
        def _(sp):
            d = k.dram
            sp.dma_start(IOTA, d["c_iota"].partition_broadcast(P)).then_inc(c["loaded"].sem, 16)
            sp.dma_start(MASK, d["c_ranks"]).then_inc(c["loaded"].sem, 16)
            sp.dma_start(HEADMASK, d["c_heads"]).then_inc(c["loaded"].sem, 16)
            wait(sp, "loaded", 48)

        @block.gpsimd
        def _(pool):
            for b in range(BATCH):
                inc(pool.tensor_tensor(k.xpart(b), k.xpart(b), k.zpart(b), ALU.add), "resid")
            for n in range(2):
                wait(pool, "ss", T * (n + 1))
                inc(pool.tensor_scalar(MS[:, n, :], SS[:, n, :], 1.0 / D, EPS, ALU.mult, ALU.add), "rs")
                wait(pool, "rs", 2 * n + 1)
                inc(pool.tensor_tensor(RS[:, n, :], MS[:, n, :], k.minus_half[:, 0:T], ALU.pow), "rs")

        @block.tensor
        def _(pe):
            for h in range(2):
                for b in range(BATCH):
                    mm = pe.matmul(bank[h][0:BATCH, :], w["router4"][:, b, :], FT[:, b * SEQ + h * BANK:b * SEQ + (h + 1) * BANK],
                                   start=b == 0, stop=b == BATCH - 1)
            inc(mm, "routed")
            wait(pe, "idx", 2)
            inc(pe.matmul(bank[2][:, 0:BATCH], IDX, k.ident[0:BATCH, 0:BATCH], start=True, stop=True), "idx_up")
            for t in range(T):
                wait(pe, "hotr", t + 1)
                for j in range(TPB):
                    mm = pe.transpose(bank[4 + 2 * t + j // 4][:, (j % 4) * P:(j % 4 + 1) * P], HOTR[:, t, j * P:(j + 1) * P], k.ident)
                inc(mm, "hott_up")
            for t in range(T):
                wait(pe, "hott", t + 1)
                for i in range(PER):
                    for j in range(TPB):
                        mm = pe.matmul(bank[t][CAP * i:CAP * (i + 1), 0:D], HOTT[:, t, j, CAP * i:CAP * (i + 1)],
                                       k.Zpad[:, k.zindex((t * PER + i) * TPB + j), :], start=j == 0, stop=j == TPB - 1)
                inc(mm, "picked")
            for t in range(T):
                wait(pe, "h", t + 1)
                inc(pe.transpose(bank[2][:, t * P:(t + 1) * P], H[:, t, :], k.ident), "h_up")
            wait(pe, "ht", 1)
            for m in range(2):
                inc(pe.matmul(bank[3 + m][:, 0:N], w["qkvT"][:, m * D:(m + 1) * D], HT, start=True, stop=True), "qk_up")
            for b in range(BATCH):
                mm = pe.matmul(bank[5][0:CAP, b * D:(b + 1) * D], HT[:, b * CAP:(b + 1) * CAP], w["qkvT"][:, 2 * D:3 * D],
                               start=True, stop=True)
            inc(mm, "v_up")
            wait(pe, "qk", 2)
            wait(pe, "v", 1)
            wait(pe, "xs", T)
            for b in range(BATCH):
                wait(pe, "qb", b + 1)
                for n in range(HEADS // 2):
                    pe.matmul(bank[b][:, n * CAP:(n + 1) * CAP], QB[:, b, 2 * n:2 * n + 2, :].rearrange("p h q -> p (h q)"),
                              KT[:, b * CAP:(b + 1) * CAP], start=n == 0, stop=True, skip_group_check=True)
                inc(pe.matmul(bank[b], k.identb, MASK, start=False, stop=True, skip_group_check=True), "s_up")
            for b in range(BATCH):
                wait(pe, "e", b + 1)
                if b >= 2:
                    wait(pe, "pt", b - 1)
                for n in range(HEADS // 2):
                    mm = pe.transpose(bank[4 + 2 * (b % 2) + n // 4][0:CAP, (n % 4) * P:(n % 4 + 1) * P], E[:, b, n, :], k.ident)
                inc(mm, "pt_up")
            for b in range(BATCH):
                wait(pe, "pt", b + 1)
                for h in range(HEADS):
                    mm = pe.matmul(bank[b // PER][CAP * (b % PER):CAP * (b % PER + 1), h * HD:(h + 1) * HD],
                                   PT[:, b, h // 2, CAP * (h % 2):CAP * (h % 2 + 1)], V[:, b, h * HD:(h + 1) * HD], start=True, stop=True)
                inc(mm, "pv")
            for t in range(T):
                wait(pe, "o", t + 1)
                inc(pe.transpose(bank[2][:, t * P:(t + 1) * P], O[:, t, :], k.ident), "ot_up")
            wait(pe, "ot", 1)
            for t in range(T):
                inc(pe.matmul(bank[3][:, t * P:(t + 1) * P], OT[:, t * P:(t + 1) * P], w["f_outT"], start=True, stop=True), "xa_up")
            for t in range(T):
                wait(pe, "h", T + t + 1)
                inc(pe.transpose(bank[2][:, t * P:(t + 1) * P], H2[:, t, :], k.ident), "h_up")
            wait(pe, "ht", 2)
            for n, (a, r) in enumerate(CHUNKS):
                for m in range(2):
                    mm = pe.matmul(bank[4 + n][0:r, m * N:(m + 1) * N], w["f_upT"][:, m, a:a + r], H2T, start=True, stop=True)
                inc(mm, "up")
            for t in range(T):
                wait(pe, "prod", len(CHUNKS))
                for n, (a, r) in enumerate(CHUNKS):
                    mm = pe.matmul(bank[t][:, 0:D], PROD[0:r, n, t * P:(t + 1) * P], w["f_downT"][0:r, n, :], start=n == 0,
                                   stop=n == len(CHUNKS) - 1)
                inc(mm, "down")
            for b in range(BATCH):
                wait(pe, "y", b // PER + 1)
                wait(pe, "prod", len(CHUNKS))
                if b >= 3:
                    wait(pe, "added", b - 2)
                rows = slice(CAP * (b % PER), CAP * (b % PER + 1))
                for j in range(TPB):
                    mm = pe.matmul(bank[2 + 2 * (b % 3) + j // 4][:, (j % 4) * P:(j % 4 + 1) * P], HOTR[rows, b // PER, j * P:(j + 1) * P],
                                   Y[rows, b // PER, :], start=True, stop=True)
                inc(mm, "spread")

        @block.scalar
        def _(act):
            wait(act, "routed", 1)
            inc(act.copy(SCORE[:, 0, :], psum[0:BATCH, 0:SEQ]), "score")
            for t in range(T):
                wait(act, "hott_up", t + 1)
                inc(act.copy(HOTT[:, t].rearrange("p j r -> p (j r)"), psum[:, (4 + 2 * t) * BANK:(6 + 2 * t) * BANK]), "hott")
            for t in range(T):
                wait(act, "xs", t + 1)
                inc(act.activation(SQ[:, t, :], XS[:, t, :], ACT.Square, accum_out=SS[:, 0, t:t + 1]), "ss")
            wait(act, "h_up", T)
            inc(act.activation(HT, bank[2][:, 0:N], ACT.Copy, scale=w["f_g1"]), "ht")
            wait(act, "qk_up", 2)
            inc(act.copy(KT, bank[4][:, 0:N]), "qk")
            wait(act, "v_up", 1)
            inc(act.copy(V.rearrange("p b d -> p (b d)"), bank[5][0:CAP, :]), "v")
            for b in range(BATCH):
                wait(act, "soft", 2 * b + 2)
                e = E[:, b].rearrange("p c t -> p (c t)")
                inc(act.activation(e, e, ACT.Exp, scale=SCALE), "exp")
            for b in range(BATCH):
                wait(act, "pt_up", b + 1)
                first = 4 + 2 * (b % 2)
                inc(act.copy(PT[:, b].rearrange("p c r -> p (c r)"), psum[0:CAP, first * BANK:(first + 2) * BANK]), "pt")
            for t in range(T):
                wait(act, "xa", 2 * t + 2)
                inc(act.activation(SQ[:, t, :], S2[:, t, :], ACT.Square, accum_out=SS[:, 1, t:t + 1]), "ss")
            wait(act, "h_up", 2 * T)
            inc(act.activation(H2T, bank[2][:, 0:N], ACT.Copy, scale=w["f_g2"]), "ht")
            for n, (a, r) in enumerate(CHUNKS):
                wait(act, "up", n + 1)
                inc(act.activation(SIL[0:r, n, :], bank[4 + n][0:r, 0:N], ACT.Silu), "sil")

        @block.vector
        def _(dve):
            wait(dve, "score", 1)
            wait(dve, "loaded", 48)
            n = 0
            for r in range(CAP // TOP):
                cur, new = SCORE[:, r % 2, :], SCORE[:, (r + 1) % 2, :]
                part = slice(r * TOP, (r + 1) * TOP)
                if r:
                    wait(dve, "rank", 3 * r)
                inc(dve.max(VALS[:, part], cur), "rank")
                wait(dve, "rank", 3 * r + 1)
                inc(dve.max_index(IDXU[:, part], VALS[:, part], cur), "rank")
                inc(dve.match_replace(new, VALS[:, part], cur, GONE), "rank")
            wait(dve, "rank", 3 * CAP // TOP)
            for i in range(PER):
                inc(dve.tensor_copy(IDX[:, i * CAP:(i + 1) * CAP], IDXU), "idx")
            wait(dve, "idx_up", 1)
            for i in range(PER):
                rows = slice(i * CAP, (i + 1) * CAP)
                inc(dve.tensor_copy(IDXT[rows, :], bank[2][rows, i:BATCH:PER]), "idxT")
            wait(dve, "idxT", PER)
            for t in range(T):
                inc(dve.tensor_scalar(HOTR[:, t, :], IOTA, IDXT[:, t:t + 1], None, ALU.is_equal), "hotr")
            for t in range(T):
                wait(dve, "picked", t + 1)
                inc(dve.tensor_copy(XS[:, t, :], bank[t][:, 0:D]), "xs")
            wait(dve, "rs", 2)
            wait(dve, "xs", T)
            for t in range(T):
                inc(dve.tensor_scalar(H[:, t, :], XS[:, t, :], RS[:, 0, t:t + 1], None, ALU.mult), "h")
            wait(dve, "qk_up", 2)
            inc(dve.tensor_copy(QT, bank[3][:, 0:N]), "qk")
            wait(dve, "qk", 2)
            for b in range(BATCH):
                inc(dve.tensor_tensor(QB[:, b], QT[:, b * CAP:(b + 1) * CAP].unsqueeze(1).broadcast_to([P, HEADS, CAP]),
                                      HEADMASK.unsqueeze(2).broadcast_to([P, HEADS, CAP]), ALU.mult), "qb")
            for b in range(BATCH):
                s = bank[b].rearrange("p (c t) -> p c t", c=TOP)
                wait(dve, "s_up", b + 1)
                inc(dve.tensor_reduce(PEAK[:, b, :], s, AX_X, ALU.max), "soft")
                wait(dve, "soft", 2 * b + 1)
                inc(dve.tensor_tensor(E[:, b], s, PEAK[:, b, :].unsqueeze(2).broadcast_to([P, TOP, CAP]), ALU.subtract), "soft")
            for b in range(BATCH):
                wait(dve, "exp", b + 1)
                inc(dve.tensor_reduce(SUM[:, b, :], E[:, b], AX_X, ALU.add), "idx")
                wait(dve, "idx", 2 + 2 * b + 1)
                inc(dve.reciprocal(INV[:, b, :], SUM[:, b, :]), "idx")
                wait(dve, "idx", 2 + 2 * b + 2)
                inc(dve.tensor_tensor(E[:, b], E[:, b], INV[:, b, :].unsqueeze(2).broadcast_to([P, TOP, CAP]), ALU.mult), "e")
            for t in range(T):
                wait(dve, "pv", PER * (t + 1))
                inc(dve.tensor_copy(O[:, t, :], bank[t][:, 0:D]), "o")
            wait(dve, "ot_up", T)
            inc(dve.tensor_copy(OT, bank[2][:, 0:N]), "ot")
            wait(dve, "xa_up", T)
            for t in range(T):
                part = bank[3][:, t * P:(t + 1) * P]
                inc(dve.tensor_copy(XA[:, t, :], part), "xa")
                inc(dve.tensor_tensor(S2[:, t, :], XS[:, t, :], part, ALU.add), "xa")
            wait(dve, "rs", 4)
            wait(dve, "xa", 2 * T)
            for t in range(T):
                inc(dve.tensor_scalar(H2[:, t, :], S2[:, t, :], RS[:, 1, t:t + 1], None, ALU.mult), "h")
            for n, (a, r) in enumerate(CHUNKS):
                wait(dve, "sil", n + 1)
                inc(dve.tensor_tensor(PROD[0:r, n, :], SIL[0:r, n, :], bank[4 + n][0:r, N:2 * N], ALU.mult), "prod")
            for t in range(T):
                wait(dve, "down", t + 1)
                inc(dve.tensor_tensor(Y[:, t, :], XA[:, t, :], bank[t][:, 0:D], ALU.add), "y")
            wait(dve, "resid", BATCH)
            for b in range(BATCH):
                wait(dve, "spread", b + 1)
                first = 2 + 2 * (b % 3)
                inc(dve.tensor_tensor(k.xpart(b), k.xpart(b), psum[:, first * BANK:(first + 2) * BANK].rearrange(
                    "p (j d) -> p j d", d=D), ALU.add), "added")

    for n, total in (("loaded", 48), ("resid", BATCH), ("routed", 1), ("score", 1), ("rank", 3 * CAP // TOP), ("idx", 2 + 2 * BATCH),
                     ("idx_up", 1), ("idxT", PER), ("hotr", T), ("hott_up", T), ("hott", T), ("picked", T), ("xs", T), ("ss", 2 * T),
                     ("rs", 4), ("h", 2 * T), ("h_up", 2 * T), ("ht", 2), ("qk_up", 2), ("qk", 2), ("v_up", 1), ("v", 1),
                     ("qb", BATCH), ("s_up", BATCH), ("soft", 2 * BATCH), ("exp", BATCH), ("e", BATCH), ("pt_up", BATCH),
                     ("pt", BATCH), ("pv", BATCH), ("o", T), ("ot_up", T), ("ot", 1), ("xa_up", T), ("xa", 2 * T),
                     ("up", len(CHUNKS)), ("sil", len(CHUNKS)), ("prod", len(CHUNKS)), ("down", T), ("y", T), ("spread", BATCH),
                     ("added", BATCH)):
        c[n].passed(total)



def load(k):
    nc, d, w = k.nc, k.dram, k.w
    loads = []

    def keep(name, shape, *pairs, dt=F32):
        t = k.mem.enter_context(nc.sbuf_tensor("w_" + name, list(shape), dt))
        w[name] = t[tuple(slice(None) for _ in shape)]
        for into, source in pairs:
            loads.append((w[name] if into is None else t[into], source))
        return t

    def col(ap):
        return ap.rearrange("(p a) -> p a", a=1)

    def dup(name, ap):
        keep(name, (P, 1), ((slice(0, 64),), col(ap)), ((slice(64, 128),), col(ap)))

    x = k.dram["L0_attn_a_x"].rearrange("b s d -> (b s) d").rearrange("(t p) d -> p t d", p=P)
    for b in range(BATCH):
        loads.append((k.X[:, b * TPB:(b + 1) * TPB, :], x[:, b * TPB:(b + 1) * TPB, :]))
    keep("ident", (P, P), (None, d["c_ident"]))
    keep("identb", (P, P), (None, d["c_identb"]), dt=BF16)
    k.ident, k.identb = w["ident"], w["identb"]
    a = "L0_attn_a_"
    keep("W_up", (P, P), (None, d[a + "W_up"]))
    keep("up_left2", (P, P), ((slice(None), slice(0, 64)), d[a + "W_up"][:, 0:64]),
         ((slice(None), slice(64, 128)), d[a + "W_up"][:, 0:64]))
    keep("ln_gamma", (P, 1), (None, col(d[a + "ln_gamma"])))
    keep("ln_beta", (P, 1), (None, col(d[a + "ln_beta"])))
    dup("b_left2", d[a + "b_up"][0:64])
    keep("b_right", (64, 1), (None, col(d[a + "b_up"][64:128])))
    cw = d[a + "conv_w"].rearrange("d a c -> d (a c)")
    keep("conv_w2", (P, 3), ((slice(0, 64),), cw), ((slice(64, 128),), cw))
    dup("conv_b2", d[a + "conv_b"])
    dup("b_delta2", d[a + "b_delta"])
    keep("delta2", (64, P), ((slice(None), slice(0, 64)), d[a + "W_delta"]), ((slice(None), slice(64, 128)), d[a + "W_delta"]))
    keep("bc3", (64, 2, 96), *[((slice(None), m, slice(32 * r, 32 * r + 32)), d[a + n]) for m, n in enumerate(("W_B", "W_C"))
                               for r in range(3)])
    al = d[a + "A_log"].rearrange("d (n j) -> n d j", n=2)
    keep("A1", (P, 16), ((slice(0, 64),), al[0]), ((slice(64, 128),), al[1]))
    keep("D1col", (64, 1), (None, col(d[a + "D"])))
    keep("D1", (P, 64))
    keep("fold", (P, 64), (None, d["c_fold"]))
    keep("W_down", (64, P), (None, d[a + "W_down"]))
    keep("b_down_row", (P, P), (None, d[a + "b_down"].partition_broadcast(P)))
    keep("minus_half", (P, TILES))
    k.minus_half = w["minus_half"]
    keep_later(k, keep, loads, col)

    loaded, a_exp, made = k.count("loaded"), k.count("a_exp"), k.count("made")
    with nc.Block() as block:
        engines = ((block.sync, 0), (block.scalar, 1))

        def issue(eng, n):
            for into, source in loads[n::2]:
                eng.dma_start(into, source).then_inc(loaded.sem, 16)

        @block.sync
        def _(sp):
            issue(sp, 0)

        @block.scalar
        def _(act):
            issue(act, 1)
            act.wait_ge(loaded.sem, loaded.at(16 * len(loads)))
            act.activation(w["A1"], w["A1"], ACT.Exp).then_inc(a_exp.sem, 1)
            if 7 in STAGES:
                act.activation(w["A7"], w["A7"], ACT.Exp).then_inc(a_exp.sem, 1)

        @block.vector
        def _(dve):
            dve.memset(w["minus_half"], -0.5)
            dve.memset(k.Zpad[:, 0:TILES + BATCH + 1:TPB + 1, :], 0.0)
            dve.wait_ge(loaded.sem, loaded.at(16 * len(loads)))
            dve.memset(w["D1"][64:P, :], 0.0)
            dve.tensor_scalar(w["D1"][0:64, :], k.ident[0:64, 0:64], w["D1col"], None, ALU.mult)
            dve.wait_ge(a_exp.sem, a_exp.at(1))
            dve.tensor_scalar(w["A1"], w["A1"], -1.0, None, ALU.mult)
            if 7 in STAGES:
                for hf in range(2):
                    dve.tensor_scalar(w["D7"][:, hf, :], k.ident, w["D7col"][:, hf:hf + 1], None, ALU.mult)
                dve.wait_ge(a_exp.sem, a_exp.at(2))
                dve.tensor_scalar(w["A7"], w["A7"], -1.0, None, ALU.mult)

        @block.gpsimd
        def _(pool):
            pool.wait_ge(loaded.sem, loaded.at(16 * len(loads)))
    turn_weights(k)


def store(k):
    stored = k.count("stored")
    out = k.out.rearrange("b s d -> (b s) d").rearrange("(t p) d -> p t d", p=P)
    with k.nc.Block() as block:
        @block.sync
        def _(sp):
            for b in range(BATCH):
                part = slice(b * TPB, (b + 1) * TPB)
                sp.dma_start(out[:, part, :], k.X[:, part, :]).then_inc(stored.sem, 16)
            sp.wait_ge(stored.sem, 16 * BATCH)


def halves(n, size):
    return [(i, min(size, n - i)) for i in range(0, n, size)]


def keep_later(k, keep, loads, col):
    d, w = k.dram, k.w
    k.turn = turn = []
    natural = k.arena[1]
    at = [0]

    def turned(source, *pairs):
        r, c = source.shape
        place = natural[0:r, at[0]:at[0] + c]
        at[0] += c
        loads.append((place, source))
        turn.append((place, pairs or None))
        return len(turn) - 1

    def into(n, *pairs):
        turn[n] = (turn[n][0], pairs)

    full = slice(None)
    if {2, 4} & set(STAGES):
        f = "L0_ffn_"
        keep("qkvT", (P, 3 * D))
        for i, r in halves(3 * D, P):
            into(turned(d[f + "W_qkv"][i:i + r, :]), (w["qkvT"][:, i:i + r], full))
        keep("f_outT", (P, D))
        into(turned(d[f + "W_out"]), (w["f_outT"], full))
        DFF = d[f + "W1"].shape[0]
        keep("f_upT", (P, 2, DFF))
        for m, name in enumerate(("W1", "W2")):
            for i, r in halves(DFF, P):
                into(turned(d[f + name][i:i + r, :]), (w["f_upT"][:, m, i:i + r], full))
        keep("f_downT", (P, 3, D))
        for n, (i, r) in enumerate(halves(DFF, P)):
            into(turned(d[f + "W3"][:, i:i + r]), (w["f_downT"][0:r, n, :], full))
        keep("router", (P, 1), (None, col(d[f + "w_router"])))
        keep("router4", (P, BATCH, BATCH))
        keep("f_g1", (P, 1), (None, col(d[f + "g1"])))
        keep("f_g2", (P, 1), (None, col(d[f + "g2"])))
    if 3 in STAGES:
        keep("W_band", (P, P), (None, d["L0_attn_b_W"]))
    if 5 in STAGES:
        for n in "QKVO":
            keep("W" + n, (P, P), (None, d["L1_attn_a_W" + n]))
    if 7 in STAGES:
        f = "L1_attn_b_"
        keep("w7_inT", (P, 4 * P))
        for i, r in halves(4 * P, P):
            into(turned(d[f + "W_in"][i:i + r, :]), (w["w7_inT"][:, i:i + r], full))
        keep("w7_dtin", (P, 2, 64))
        keep("bc7", (P, 2, 2, 96))
        keep("w7_outT", (P, 2, P))
        for hf in range(2):
            into(turned(d[f + "W_x"][:, hf * P:(hf + 1) * P]), (w["w7_dtin"][:, hf, :], slice(0, 64)),
                 *[(w["bc7"][:, m, hf, 32 * r:32 * r + 16], slice(64 + 16 * m, 80 + 16 * m)) for m in range(2) for r in range(3)])
            into(turned(d[f + "W_out"][:, hf * P:(hf + 1) * P]), (w["w7_outT"][:, hf, :], full))
        keep("w7_dtT", (64, 2 * P))
        for i, r in halves(2 * P, P):
            into(turned(d[f + "W_dt"][i:i + r, :]), (w["w7_dtT"][:, i:i + r], full))

        def column2(ap):
            return [((full, slice(hf, hf + 1)), col(ap[hf * P:(hf + 1) * P])) for hf in range(2)]

        keep("ln7_g", (P, 1), (None, col(d[f + "ln_g"])))
        keep("ln7_b", (P, 1), (None, col(d[f + "ln_b"])))
        keep("conv7_w", (P, 2, 4), (None, d[f + "conv_w"].rearrange("(h p) a c -> p h (a c)", h=2)))
        keep("conv7_b", (P, 2), *column2(d[f + "conv_b"]))
        keep("b7_dt", (P, 2), *column2(d[f + "b_dt"]))
        keep("A7", (P, 2, 16), (None, d[f + "A_log"].rearrange("(h p) n -> p h n", h=2)))
        keep("D7col", (P, 2), *column2(d[f + "D_param"]))
        keep("D7", (P, 2, P))
        keep("alpha", (P, 1), (None, d[f + "alpha"].partition_broadcast(P)))
    if {6, 8} & set(STAGES):
        HID = d["L1_ffn_w2"].shape[1]
        k.layer = {}
        for name, shape in (("wqkv", (P, 3 * 512)), ("wo", (P, 4, D)), ("w1", (P, 2, HID)), ("w2", (P, 3, D)), ("ln", (P, 2)),
                            ("b1", (P, 2, 3))):
            keep("layer_" + name, shape)
            k.layer[name] = w["layer_" + name]
        keep("shift", (P, P), (None, d["c_shift"]))
        keep("carry", (P, P), (None, d["c_carry"]))


def turn_weights(k):
    nc, w = k.nc, k.w
    up, out, clear = k.count("turn_up"), k.count("turn_out"), k.count("turn_clear")
    if not k.turn:
        return
    with nc.Block() as block:
        @block.tensor
        def _(pe):
            for n, (place, _) in enumerate(k.turn):
                r, c = place.shape
                if n >= 8:
                    pe.wait_ge(out.sem, out.at(n - 7))
                pe.transpose(k.bank[n % 8][0:c, 0:r], place, k.ident[0:r, 0:r]).then_inc(up.sem, 1)

        @block.vector
        def _(dve):
            clears = 0
            if "bc7" in w:
                dve.memset(w["bc7"], 0.0).then_inc(clear.sem, 1)
                clears += 1
            if "router4" in w:
                dve.memset(w["router4"], 0.0).then_inc(clear.sem, 1)
                clears += 1
            if clears:
                dve.wait_ge(clear.sem, clear.at(clears))
            if "router4" in w:
                for b in range(BATCH):
                    dve.tensor_copy(w["router4"][:, b, b:b + 1], w["router"])
            for n, (place, pairs) in enumerate(k.turn):
                r, c = place.shape
                dve.wait_ge(up.sem, up.at(n + 1))
                for place2, cols in pairs:
                    cp = dve.tensor_copy(place2, k.bank[n % 8][0:c, 0:r][:, cols])
                cp.then_inc(out.sem, 1)


def more_constants(c, f32, bf16, eye):
    row = np.arange(96)
    state = np.where(row % 32 < 16, row % 32, -1)
    c["c_sel7"] = bf16(np.repeat(state[:, None] == np.arange(16)[None], P, axis=1))
    more_constants_attention(c, bf16)


def more_constants_attention(c, bf16):
    q, j, kk = np.arange(P)[:, None, None], np.arange(TPB)[None, :, None], np.arange(256)[None, None, :]
    key = j * P - 64 + kk
    ok = (np.abs(j * P + q - key) <= 64) & (key >= 0) & (key < SEQ)
    c["c_band"] = bf16(np.where(ok, 0.0, MASKED)).reshape(P, TPB * 256)
    i = np.arange(P)
    c["c_causal"] = bf16(np.where(i[:, None] >= i[None, :], 0.0, MASKED))
    HD, WIN = 64, 64
    c["c_shift"] = np.eye(P, k=1, dtype=np.float32)
    carry = np.zeros((P, P), np.float32)
    carry[P - 1, 0] = 1
    c["c_carry"] = carry
    f32 = np.float32
    half = np.arange(0, HD, 2, dtype=f32)
    freq = (f32(1.0) / f32(10000.0) ** (half / f32(HD))).astype(f32)
    t = np.arange(SEQ, dtype=f32)
    angle = np.concatenate([t[:, None] * freq[None]] * 2, axis=1)
    base = ((half + f32(0.4 * HD)) / f32(1.4 * HD)).astype(f32)
    power = ((t - SEQ // 2) / f32(WIN // 2)).astype(f32)
    scale = np.concatenate([base[None] ** power[:, None]] * 2, axis=1).astype(f32)
    sign = np.where(np.arange(HD) < HD // 2, f32(-1), f32(1))
    cos, sin = np.cos(angle), np.sin(angle) * sign
    rope = np.stack([np.stack([cos * scale * f32(8), cos / scale]), np.stack([sin * scale * f32(8), sin / scale])])
    c["c_rope"] = rope.astype(f32).reshape(2, 2, TPB, P, HD).transpose(3, 2, 0, 1, 4).reshape(P, -1).copy()
    q, kk = np.arange(P)[:, None], np.arange(WIN + P)[None]
    back = q - (kk - WIN)
    ok = (back >= 0) & (back <= WIN)
    c["c_local"] = bf16(np.concatenate([np.where(ok & (kk >= WIN), 0.0, MASKED), np.where(ok, 0.0, MASKED)], axis=1))
    c["c_iota"] = np.arange(SEQ, dtype=f32)
    rank = np.arange(P)[:, None, None] % 64
    c["c_ranks"] = bf16(np.broadcast_to(np.where(rank >= np.arange(64)[None, None], 0.0, MASKED), (P, 8, 64)).reshape(P, 512))
    c["c_heads"] = (np.arange(P)[:, None] // 8 == np.arange(16)[None]).astype(f32)


def build(nc, dram, out):
    k = Core()
    k.nc, k.dram, k.out, k.w = nc, dram, out, {}
    counts, free = {}, []
    with ExitStack() as mem:
        k.mem = mem

        def count(name):
            if name not in counts:
                sem = free.pop() if free else mem.enter_context(nc.semaphore(name))
                counts[name] = Count(sem)
            return counts[name]

        def end_stage():
            with nc.Block() as block:
                @block.sync
                def _(sp):
                    for c in counts.values():
                        sp.sem_clear(c.sem)
            free.extend(c.sem for c in counts.values())
            counts.clear()

        made = [0]

        def name(base):
            made[0] += 1
            return f"{base}_{made[0]}"

        k.count, k.name = count, name
        X = mem.enter_context(nc.sbuf_tensor("X", [P, TILES, D], F32))
        Zpad = mem.enter_context(nc.sbuf_tensor("Z", [P, TILES + BATCH + 1, D], F32))
        k.X, k.Zpad = X, Zpad[:, :, :]
        k.zindex = lambda i: i + i // TPB + 1
        k.zpart = lambda b: k.Zpad[:, b * (TPB + 1) + 1:(b + 1) * (TPB + 1), :]
        k.xpart = lambda b: k.X[:, b * TPB:(b + 1) * TPB, :]
        big = mem.enter_context(nc.sbuf_tensor("arena", [P, 6 * TOK + 16], F32))
        k.big = big
        k.arena = [big[:, (i * TOK + (16 if i > 2 else 0)):][:, 0:TOK] for i in range(6)]
        k.arena_wide = big[:, 2 * TOK:3 * TOK + 16]
        k.arena6 = mem.enter_context(nc.sbuf_tensor("arena6", [P, 6 * SEQ], F32))[:, :]
        k.ZZ = k.arena[0].rearrange("p (t d) -> p t d", d=D)
        psum = mem.enter_context(nc.psum_tensor("psum", [P, 8 * BANK], F32))
        k.psum = psum[:, :]
        k.bank = [psum[:, i * BANK:(i + 1) * BANK] for i in range(8)]
        load(k)
        stages = {1: mamba_small, 2: routed_ffn, 3: band_attention, 4: routed_ffn, 5: causal_attention,
                  6: local_transformer, 7: mamba_large, 8: local_transformer}
        for s in STAGES:
            stages[s](k)
            end_stage()
        store(k)


def upper_half(a):
    return (np.ascontiguousarray(a, dtype=np.float32).view(np.uint32) >> 16).astype(np.uint16)


def constants():
    f32, bf16 = np.float32, upper_half
    c = {}
    eye = np.eye(P, dtype=f32)
    c["c_ident"] = eye
    c["c_identb"] = bf16(eye)
    c["c_fold"] = np.concatenate([np.eye(64, dtype=f32)] * 2)
    row = np.arange(96) % 32
    lane = np.arange(16)[:, None] + 16 * (np.arange(P)[None, :] // 64)
    c["c_sel1"] = bf16((row[:, None, None] == lane[None]).reshape(96, 16 * P))
    more_constants(c, f32, bf16, eye)
    return c


def kernel(**inputs):
    import numpy as _np
    import concourse.bacc as _bacc
    from concourse import mybir as _mybir
    from concourse.bass_utils import run_bass_kernel_spmd as _run

    nc = _bacc.Bacc("TRN2", target_bir_lowering=False, num_devices=1)
    arrays, dram = {}, {}
    for source in (inputs, constants()):
        for name, value in source.items():
            a = _np.ascontiguousarray(value)
            arrays["in_" + name] = a
            dram[name] = nc.dram_tensor("in_" + name, a.shape, _mybir.dt.from_np(a.dtype), kind="ExternalInput").ap()
            if a.dtype == _np.uint16:
                dram[name] = dram[name].bitcast(_mybir.dt.bfloat16)
    out = nc.dram_tensor("out_x", (BATCH, SEQ, D), _mybir.dt.float32, kind="ExternalOutput").ap()
    build(nc, dram, out)
    r = _run(nc, [arrays], core_ids=[0])
    return r.results[0]["out_x"]
```

```python
from contextlib import ExitStack

import numpy as np

import concourse.bass as bass
from concourse import mybir

F32 = mybir.dt.float32
BF16 = mybir.dt.bfloat16
U32 = mybir.dt.uint32
ALU = mybir.AluOpType
ACT = mybir.ActivationFunctionType
AX_X = mybir.AxisListType.X

P = 128
D = 128
BATCH, SEQ = 4, 1024
TOK = BATCH * SEQ
TILES = TOK // P
TPB = SEQ // P
BANK = 512
MASKED = -1.0e30

STAGES = (1, 2, 3, 4, 5, 6, 7, 8)


class Count:

    def __init__(self, sem):
        self.sem, self.base = sem, 0

    def at(self, n):
        return self.base + n

    def passed(self, n):
        self.base += n


class Core:
    pass





def layernorm(k, second_eps=None):
    nc = k.nc
    EPS = 1e-5
    X = k.X
    total, centred, squared, var, factor, scaled = (
        k.count(n) for n in ("ln_total", "ln_centred", "ln_squared", "ln_var", "ln_factor", "ln_scaled"))
    STEPS = 2 if second_eps is None else 8
    with ExitStack() as mem:
        SQ = k.arena[4].rearrange("p (t d) -> p t d", d=D)
        st = mem.enter_context(nc.sbuf_tensor(k.name("ln_st"), [P, 8, TILES], F32))
        block = mem.enter_context(nc.Block())
        SUM, MEAN, VARSUM, VAR, RSTD, VAR2, T, RSTD2 = range(8)

        def row(r, q):
            return st[:, r, TPB * q:TPB * (q + 1)]

        def wide(r, q):
            return row(r, q).unsqueeze(2).broadcast_to([P, TPB, D])

        def part(m, q):
            return m[:, TPB * q:TPB * (q + 1), :]

        @block.vector
        def _(dve):
            for q in range(BATCH):
                dve.tensor_reduce(row(SUM, q), part(X, q), AX_X, ALU.add).then_inc(total.sem, 1)
                dve.wait_ge(total.sem, total.at(2 * q + 1))
                dve.tensor_scalar(row(MEAN, q), row(SUM, q), 1.0 / D, None, ALU.mult).then_inc(total.sem, 1)
                dve.wait_ge(total.sem, total.at(2 * q + 2))
                dve.tensor_tensor(k.zpart(q), part(X, q), wide(MEAN, q), ALU.subtract).then_inc(centred.sem, 1)
            for q in range(BATCH):
                dve.wait_ge(squared.sem, squared.at(q + 1))
                dve.tensor_reduce(row(VARSUM, q), part(SQ, q), AX_X, ALU.add).then_inc(var.sem, 1)
            for q in range(BATCH):
                dve.wait_ge(factor.sem, factor.at(STEPS * (q + 1)))
                if second_eps is not None:
                    dve.tensor_tensor(part(k.ZZ, q), k.zpart(q), wide(RSTD2, q), ALU.mult).then_inc(scaled.sem, 1)
                    dve.wait_ge(scaled.sem, scaled.at(q + 1))
                dve.tensor_tensor(k.zpart(q), k.zpart(q), wide(RSTD, q), ALU.mult)

        @block.scalar
        def _(act):
            for q in range(BATCH):
                act.wait_ge(centred.sem, centred.at(q + 1))
                act.activation(part(SQ, q), k.zpart(q), ACT.Square).then_inc(squared.sem, 1)

        @block.gpsimd
        def _(pool):
            half = k.minus_half[:, 0:TPB]
            for q in range(BATCH):
                s = STEPS * q
                pool.wait_ge(var.sem, var.at(q + 1))
                pool.tensor_scalar(row(VAR, q), row(VARSUM, q), 1.0 / D, EPS, ALU.mult, ALU.add).then_inc(factor.sem, 1)
                pool.wait_ge(factor.sem, factor.at(s + 1))
                pool.tensor_tensor(row(RSTD, q), row(VAR, q), half, ALU.pow).then_inc(factor.sem, 1)
                if second_eps is not None:
                    pool.tensor_scalar(row(VAR2, q), row(VARSUM, q), 1.0 / D, 0.0, ALU.mult, ALU.add).then_inc(factor.sem, 1)
                    pool.wait_ge(factor.sem, factor.at(s + 3))
                    pool.tensor_tensor(row(T, q), row(VAR2, q), row(RSTD, q), ALU.mult).then_inc(factor.sem, 1)
                    pool.wait_ge(factor.sem, factor.at(s + 4))
                    pool.tensor_tensor(row(VAR2, q), row(T, q), row(RSTD, q), ALU.mult).then_inc(factor.sem, 1)
                    pool.wait_ge(factor.sem, factor.at(s + 5))
                    pool.tensor_scalar(row(T, q), row(VAR2, q), 1.0, second_eps, ALU.mult, ALU.add).then_inc(factor.sem, 1)
                    pool.wait_ge(factor.sem, factor.at(s + 6))
                    pool.tensor_tensor(row(VAR2, q), row(T, q), half, ALU.pow).then_inc(factor.sem, 1)
                    pool.wait_ge(factor.sem, factor.at(s + 7))
                    pool.tensor_tensor(row(RSTD2, q), row(VAR2, q), row(RSTD, q), ALU.mult).then_inc(factor.sem, 1)

    total.passed(2 * BATCH)
    factor.passed(STEPS * BATCH)
    for s in (centred, squared, var):
        s.passed(BATCH)
    if second_eps is not None:
        scaled.passed(BATCH)



def scan(k, batches, halves_n, delta, du, parts, sel, a_col, fold, diag, u, out, gate, spare):
    nc = k.nc
    J, U = 16, 4
    LEAD = 5
    M = fold.shape[1]
    b_up, c_up, b_copied, decay_up, input_up, scanned, weighted, summed, y_taken = [
        k.count("scan_" + n) for n in ("b_up", "c_up", "b_copied", "decay_up", "input_up", "scanned", "weighted",
                                       "summed", "y_taken")]
    credited = (b_copied, input_up, scanned, weighted, summed, y_taken)
    for s in credited:
        s.passed(U)
    runs = [(b, hf) for b in range(batches) for hf in range(halves_n)]
    with ExitStack() as mem:
        ring = k.arena[4].rearrange("p (r s t) -> p r s t", r=2, t=SEQ)
        ring2 = k.arena6.rearrange("p (r s t) -> p r s t", r=3, t=SEQ)
        decay = ring[:, 0]
        b_lane = [ring[:, 1, 0], ring[:, 1, 1]] + spare
        inputs, weight = ring2[:, 0], ring2[:, 2]
        more = mem.enter_context(nc.sbuf_tensor(k.name("scan_state"), [P, U - 2, SEQ], F32))
        state = [ring2[:, 1, 0], ring2[:, 1, 1]] + [more[:, n, :] for n in range(U - 2)]
        bank = k.bank
        block = mem.enter_context(nc.Block())

        def two(first):
            return k.psum[:, first * BANK:(first + 2) * BANK]

        def ahead(o, j, n):
            if isinstance(j, int) and j + n >= J:
                return (o + 1, j + n - J) if o + 1 < len(runs) else None
            return o, j + n

        def steps(eng, body, begin=None):
            for o in range(len(runs)):
                if begin:
                    begin(o)
                with eng.Fori(0, J // U - 2) as jj:
                    for s in range(U):
                        body(o, jj * U + s, s)
                for j in range(J - 2 * U, J):
                    body(o, j, j % U)

        @block.sync
        def _(sp):
            for s in credited:
                sp.sem_inc(s.sem, U)

        @block.tensor
        def _(pe):
            def spread_b(o, j):
                pe.wait_ge(b_copied.sem, b_copied.at(o * J + j))
                for c in range(2):
                    mm = pe.matmul(bank[c], sel(j), parts(0, runs[o][0], c), start=True, stop=True)
                mm.then_inc(b_up.sem, 1)

            def spread_c(o, j, s):
                pe.wait_ge(weighted.sem, weighted.at(o * J + j - 1))
                for c in range(2):
                    mm = pe.matmul(bank[2 + 2 * (s % 2) + c], sel(j), parts(1, runs[o][0], c), start=True, stop=True)
                mm.then_inc(c_up.sem, 1)

            def begin(o):
                b, hf = runs[o]
                pe.wait_ge(y_taken.sem, y_taken.at(o))
                for c in range(2):
                    pe.matmul(bank[6 + c][0:M, :], diag(hf), u(b, hf, c), start=True, stop=False, skip_group_check=True)

            def body(o, j, s):
                if ahead(o, j, 2):
                    spread_c(*ahead(o, j, 2), s)
                pe.wait_ge(weighted.sem, weighted.at(o * J + j + 1))
                for c in range(2):
                    mm = pe.matmul(bank[6 + c][0:M, :], fold, weight[:, s % 2, c * BANK:(c + 1) * BANK], start=False,
                                   stop=isinstance(j, int) and j == J - 1, skip_group_check=True)
                mm.then_inc(summed.sem, 1)
                if ahead(o, j, LEAD):
                    spread_b(*ahead(o, j, LEAD))

            for j in range(2):
                spread_c(0, j, j)
            for j in range(LEAD):
                spread_b(0, j)
            steps(pe, body, begin)

        @block.scalar
        def _(act):
            def copy_b(o, j, s):
                i = o * J + j
                act.wait_ge(b_up.sem, b_up.at(i + 1))
                act.wait_ge(input_up.sem, input_up.at(i - 3))
                act.activation(b_lane[s % U], two(0), ACT.Copy).then_inc(b_copied.sem, 1)

            def decay_of(o, j, s):
                b, hf = runs[o]
                act.wait_ge(scanned.sem, scanned.at(o * J + j - 1))
                act.activation(decay[:, s % 2], delta(b, hf), ACT.Exp, scale=a_col(hf, j)).then_inc(decay_up.sem, 1)

            def body(o, j, s):
                if ahead(o, j, 2):
                    decay_of(*ahead(o, j, 2), s)
                if ahead(o, j, 3):
                    copy_b(*ahead(o, j, 3), s + 3)

            for j in range(3):
                copy_b(0, j, j)
                if j < 2:
                    decay_of(0, j, j)
            steps(act, body)

        @block.gpsimd
        def _(pool):
            def body(o, j, s):
                i = o * J + j
                pool.wait_ge(b_copied.sem, b_copied.at(i + 1))
                pool.wait_ge(scanned.sem, scanned.at(i - 1))
                pool.tensor_tensor(inputs[:, s % 2], b_lane[s], du(*runs[o]), ALU.mult).then_inc(input_up.sem, 1)
            steps(pool, body)

        @block.vector
        def _(dve):
            def scan_step(o, j, s):
                i = o * J + j
                dve.wait_ge(decay_up.sem, decay_up.at(i + 1))
                dve.wait_ge(input_up.sem, input_up.at(i + 1))
                dve.tensor_tensor_scan(state[s % U], decay[:, s % 2], inputs[:, s % 2], 0.0, ALU.mult, ALU.add).then_inc(
                    scanned.sem, 1)

            def take(o):
                b, hf = runs[o]
                dve.wait_ge(summed.sem, summed.at((o + 1) * J))
                dve.tensor_tensor(out(b, hf), two(6)[0:M, :], gate(b, hf), ALU.mult).then_inc(y_taken.sem, 1)

            def body(o, j, s):
                i = o * J + j
                if ahead(o, j, 1):
                    scan_step(*ahead(o, j, 1), s + 1)
                dve.wait_ge(scanned.sem, scanned.at(i + 1))
                dve.wait_ge(c_up.sem, c_up.at(i + 1))
                dve.wait_ge(summed.sem, summed.at(i - 1))
                dve.tensor_tensor(weight[:, s % 2], state[s % U], two(2 + 2 * (s % 2)), ALU.mult).then_inc(weighted.sem, 1)

            scan_step(0, 0, 0)
            steps(dve, body, lambda o: take(o - 1) if o else None)
            take(len(runs) - 1)

    n = len(runs)
    for s in (b_up, c_up, b_copied, decay_up, input_up, scanned, weighted, summed):
        s.passed(n * J)
    y_taken.passed(n)



def mamba_small(k):
    nc, w = k.nc, k.w
    DI, NS, KC = 64, 32, 3
    layernorm(k, second_eps=1e-5)
    A = k.arena
    FT = A[1]
    LEFT = k.arena_wide[:, 0:BATCH * (SEQ + KC - 1)].rearrange("p (b t) -> p b t", b=BATCH)
    R = A[3][0:DI].rearrange("p (b t) -> p b t", b=BATCH)
    DELTA = A[1].rearrange("p (b t) -> p b t", b=BATCH)
    U = A[0].rearrange("p (b t) -> p b t", b=BATCH)
    DU = A[2].rearrange("p (b t) -> p b t", b=BATCH)
    TMP = A[4].rearrange("p (s t) -> p s t", t=SEQ)
    PARTS = A[5].bitcast(BF16).rearrange("p (m b t) -> p m b t", m=2, b=BATCH)
    NPART = 3 * NS
    bank, psum = k.bank, k.psum

    def two(first):
        return psum[:, first * BANK:(first + 2) * BANK]

    names = ("turned", "normed", "left_up", "right_up", "left", "right", "conv", "u", "residual")
    turned, normed, left_up, right_up, left, right, conv, u_up, resid = cs = [k.count("m1_" + n) for n in names]
    with nc.Block() as block:
        @block.tensor
        def _(pe):
            for b in range(BATCH):
                if b:
                    pe.wait_ge(normed.sem, normed.at(b))
                for j in range(TPB):
                    mm = pe.transpose(bank[j // 4][:, P * (j % 4):P * (j % 4 + 1)], k.ZZ[:, b * TPB + j, :], k.ident)
                mm.then_inc(turned.sem, 1)
                pe.wait_ge(normed.sem, normed.at(b + 1))
                if b:
                    pe.wait_ge(left.sem, left.at(b + 1))
                for c in range(2):
                    mm = pe.matmul(bank[2 + c], w["up_left2"], FT[:, b * SEQ + c * BANK:][:, 0:BANK], start=True, stop=True)
                mm.then_inc(left_up.sem, 1)
                if b:
                    pe.wait_ge(right.sem, right.at(b))
                for c in range(2):
                    mm = pe.matmul(bank[4 + c][0:DI, :], w["W_up"][:, DI:2 * DI], FT[:, b * SEQ + c * BANK:][:, 0:BANK],
                                   start=True, stop=True)
                mm.then_inc(right_up.sem, 1)

        @block.vector
        def _(dve):
            dve.memset(LEFT[:, :, 0:KC - 1], 0.0).then_inc(left.sem, 1)
            for b in range(BATCH):
                dve.wait_ge(turned.sem, turned.at(b + 1))
                dve.tensor_scalar(FT[:, b * SEQ:(b + 1) * SEQ], two(0), w["ln_gamma"], w["ln_beta"], ALU.mult,
                                  ALU.add).then_inc(normed.sem, 1)
                dve.wait_ge(left_up.sem, left_up.at(b + 1))
                dve.tensor_scalar(LEFT[:, b, KC - 1:], two(2), w["b_left2"], None, ALU.add).then_inc(left.sem, 1)
                dve.wait_ge(left.sem, left.at(b + 2))
                if b >= 2:
                    dve.wait_ge(u_up.sem, u_up.at(b - 1))
                acc = TMP[:, b % 2]
                dve.tensor_scalar(acc, LEFT[:, b, 0:SEQ], w["conv_w2"][:, 0:1], None, ALU.mult).then_inc(conv.sem, 1)
                for tap in range(1, KC):
                    dve.wait_ge(conv.sem, conv.at(KC * b + tap))
                    dve.scalar_tensor_tensor(out=acc, in0=LEFT[:, b, tap:tap + SEQ], scalar=w["conv_w2"][:, tap:tap + 1],
                                             in1=acc, op0=ALU.mult, op1=ALU.add).then_inc(conv.sem, 1)

        @block.scalar
        def _(act):
            for b in range(BATCH):
                act.wait_ge(right_up.sem, right_up.at(b + 1))
                act.activation(R[:, b, :], two(4)[0:DI, :], ACT.Silu, bias=w["b_right"]).then_inc(right.sem, 1)
                act.wait_ge(conv.sem, conv.at(KC * (b + 1)))
                act.activation(U[:, b, :], TMP[:, b % 2], ACT.Silu, bias=w["conv_b2"]).then_inc(u_up.sem, 1)

        @block.gpsimd
        def _(pool):
            bias = w["b_down_row"].unsqueeze(1).broadcast_to([P, TPB, D])
            for b in range(BATCH):
                pool.tensor_tensor(k.zpart(b), k.zpart(b), bias, ALU.add).then_inc(resid.sem, 1)
            for b in range(BATCH):
                pool.wait_ge(resid.sem, resid.at(b + 1))
                pool.tensor_tensor(k.xpart(b), k.xpart(b), k.zpart(b), ALU.add)

    names = ("d_up", "b_up", "c_up", "soft", "d_taken", "first", "rest", "mid", "parts", "delta")
    d_up, b_up, c_up, soft, d_taken, first, rest, mid, done, delta_up = [k.count("m1p_" + n) for n in names]
    bc = (b_up, c_up)
    with nc.Block() as block:
        @block.tensor
        def _(pe):
            for b in range(BATCH):
                if b:
                    pe.wait_ge(d_taken.sem, d_taken.at(b))
                    pe.wait_ge(soft.sem, soft.at(3 * b))
                for c in range(2):
                    mm = pe.matmul(bank[c], w["delta2"], U[0:DI, b, c * BANK:(c + 1) * BANK], start=True, stop=True)
                mm.then_inc(d_up.sem, 1)
                for m in range(2):
                    if b:
                        pe.wait_ge(rest.sem, rest.at(2 * (b - 1) + m + 1))
                    for c in range(2):
                        mm = pe.matmul(bank[2 + 2 * m + c][0:NPART, :], w["bc3"][:, m, :], U[0:DI, b, c * BANK:(c + 1) * BANK],
                                       start=True, stop=True)
                    mm.then_inc(bc[m].sem, 1)

        @block.scalar
        def _(act):
            for b in range(BATCH):
                t = TMP[:, b % 2]
                act.wait_ge(d_up.sem, d_up.at(b + 1))
                if b >= 2:
                    act.wait_ge(delta_up.sem, delta_up.at(b - 1))
                act.activation(t, two(0), ACT.Abs, bias=w["b_delta2"]).then_inc(soft.sem, 1)
                act.wait_ge(soft.sem, soft.at(3 * b + 1))
                act.activation(t, t, ACT.Exp, scale=-1.0).then_inc(soft.sem, 1)
                act.wait_ge(soft.sem, soft.at(3 * b + 2))
                act.activation(t, t, ACT.Ln, bias=1.0).then_inc(soft.sem, 1)
                for m in range(2):
                    n = 2 * b + m
                    act.wait_ge(bc[m].sem, bc[m].at(b + 1))
                    act.activation(PARTS[0:NPART, m, b, :], two(2 + 2 * m)[0:NPART, :], ACT.Copy).then_inc(first.sem, 1)
                    act.wait_ge(rest.sem, rest.at(n + 1))
                    act.activation(PARTS[NS:2 * NS, m, b, :], TMP[NS:2 * NS, 2 + m, :], ACT.Copy)
                    act.activation(PARTS[2 * NS:NPART, m, b, :], TMP[2 * NS:NPART, 2 + m, :], ACT.Copy).then_inc(mid.sem, 1)

        @block.vector
        def _(dve):
            for b in range(BATCH):
                dve.wait_ge(soft.sem, soft.at(3 * b + 1))
                dve.tensor_scalar(DELTA[:, b, :], two(0), w["b_delta2"], 0.0, ALU.add, ALU.max).then_inc(d_taken.sem, 1)
                dve.wait_ge(d_taken.sem, d_taken.at(b + 1))
                dve.wait_ge(soft.sem, soft.at(3 * b + 3))
                dve.tensor_tensor(DELTA[:, b, :], DELTA[:, b, :], TMP[:, b % 2], ALU.add).then_inc(delta_up.sem, 1)
                for m in range(2):
                    n = 2 * b + m
                    dve.wait_ge(first.sem, first.at(n + 1))
                    if n >= 2:
                        dve.wait_ge(done.sem, done.at(n - 1))
                    dve.tensor_tensor(TMP[0:NPART, 2 + m, :], two(2 + 2 * m)[0:NPART, :], PARTS[0:NPART, m, b, :],
                                      ALU.subtract).then_inc(rest.sem, 1)
                    dve.wait_ge(mid.sem, mid.at(n + 1))
                    dve.tensor_tensor(PARTS[2 * NS:NPART, m, b, :], TMP[2 * NS:NPART, 2 + m, :],
                                      PARTS[2 * NS:NPART, m, b, :], ALU.subtract).then_inc(done.sem, 1)

        @block.gpsimd
        def _(pool):
            for b in range(BATCH):
                pool.wait_ge(delta_up.sem, delta_up.at(b + 1))
                pool.tensor_tensor(DU[:, b, :], DELTA[:, b, :], U[:, b, :], ALU.mult)

    with ExitStack() as mem:
        selt = mem.enter_context(nc.sbuf_tensor("m1_sel", [NPART, 16 * P], BF16))
        loaded = k.count("m1_sel_in")
        with nc.Block() as block:
            @block.sync
            def _(sp):
                sp.dma_start(selt[:, :], k.dram["c_sel1"]).then_inc(loaded.sem, 16)
                sp.wait_ge(loaded.sem, loaded.at(16))
        scan(k, BATCH, 1, lambda b, hf: DELTA[:, b, :], lambda b, hf: DU[:, b, :],
             lambda m, b, c: PARTS[0:NPART, m, b, c * BANK:(c + 1) * BANK],
             lambda j: selt[:, bass.ds(j * P, P)], lambda hf, j: w["A1"][:, bass.ds(j, 1)], w["fold"], lambda hf: w["D1"],
             lambda b, hf, c: U[:, b, c * BANK:(c + 1) * BANK], lambda b, hf: R[:, b, :], lambda b, hf: R[:, b, :],
             [k.zpart(b).rearrange("p j d -> p (j d)") for b in range(2)])

    project_back(k, [R.rearrange("p b t -> p (b t)")], [w["W_down"]])


def project_back(k, sources, weights, batches=range(BATCH), scale=None):
    nc = k.nc
    up, added = k.count("back_up"), k.count("back_added")
    with nc.Block() as block:
        @block.tensor
        def _(pe):
            for b in range(len(batches)):
                if b >= 2:
                    pe.wait_ge(added.sem, added.at(b - 1))
                for j in range(TPB):
                    o = k.bank[2 * (b % 2) + j // 4][:, P * (j % 4):P * (j % 4 + 1)]
                    t = (b * TPB + j) * P
                    for n, (src, wt) in enumerate(zip(sources, weights)):
                        mm = pe.matmul(o, src[:, t:t + P], wt, start=n == 0, stop=n == len(sources) - 1)
                mm.then_inc(up.sem, 1)

        @block.vector
        def _(dve):
            for b, seq in enumerate(batches):
                x = k.X[:, seq * TPB:(seq + 1) * TPB, :]
                y = k.psum[:, 2 * (b % 2) * BANK:(2 * (b % 2) + 2) * BANK].rearrange("p (j d) -> p j d", d=D)
                dve.wait_ge(up.sem, up.at(b + 1))
                if scale is None:
                    dve.tensor_tensor(x, x, y, ALU.add).then_inc(added.sem, 1)
                else:
                    dve.scalar_tensor_tensor(out=x, in0=y, scalar=scale, in1=x, op0=ALU.mult,
                                             op1=ALU.add).then_inc(added.sem, 1)
    for s in (up, added):
        s.passed(len(batches))



def mamba_large(k):
    nc, w, bank, psum = k.nc, k.w, k.bank, k.psum
    HV, KC, NS = 2, 4, 16
    RANK, GAP = 64, 32
    NPART = 3 * GAP
    PAIR = 2
    layernorm(k, second_eps=1e-5)
    FT = k.Zpad.rearrange("p t d -> p (t d)")[:, 0:TOK]
    turned, normed, resid = k.count("m7_turned"), k.count("m7_normed"), k.count("m7_residual")
    with nc.Block() as block:
        @block.gpsimd
        def _(pool):
            for b in range(BATCH):
                pool.tensor_tensor(k.xpart(b), k.xpart(b), k.zpart(b), ALU.add).then_inc(resid.sem, 1)

        @block.tensor
        def _(pe):
            for b in range(BATCH):
                for j in range(TPB):
                    mm = pe.transpose(bank[2 * b + j // 4][:, P * (j % 4):P * (j % 4 + 1)], k.ZZ[:, b * TPB + j, :], k.ident)
                mm.then_inc(turned.sem, 1)

        @block.vector
        def _(dve):
            for b in range(BATCH):
                dve.wait_ge(turned.sem, turned.at(b + 1))
                dve.wait_ge(resid.sem, resid.at(BATCH))
                dve.tensor_scalar(FT[:, b * SEQ:(b + 1) * SEQ], psum[:, 2 * b * BANK:(2 * b + 2) * BANK], w["ln7_g"], w["ln7_b"],
                                  ALU.mult, ALU.add).then_inc(normed.sem, 1)

    def quad(a):
        return a.rearrange("p (h b t) -> p h b t", h=HV, b=PAIR)

    U, DELTA, DU, R = (quad(k.arena[n]) for n in (0, 1, 2, 3))
    LEFT = k.arena_wide[:, 0:HV * PAIR * (SEQ + KC - 1)].rearrange("p (h b t) -> p h b t", h=HV, b=PAIR)
    TMP = quad(k.arena[4])
    REST = k.arena6.rearrange("p (s t) -> p s t", t=SEQ)
    PARTS = k.arena[5].bitcast(BF16)[:, 0:2 * PAIR * SEQ].rearrange("p (m b t) -> p m b t", m=2, b=PAIR)

    def two(first):
        return psum[:, first * BANK:(first + 2) * BANK]

    with ExitStack() as mem:
        selt = mem.enter_context(nc.sbuf_tensor("m7_sel", [NPART, NS * P], BF16))
        loaded = k.count("m7_sel_in")
        with nc.Block() as block:
            @block.sync
            def _(sp):
                sp.dma_start(selt[:, :], k.dram["c_sel7"]).then_inc(loaded.sem, 16)
                sp.wait_ge(loaded.sem, loaded.at(16))
        for pair in range(BATCH // PAIR):
            channels(k, pair, two, FT, LEFT, U, R, TMP, HV, KC, PAIR)
            deltas(k, two, U, DELTA, DU, TMP, REST, PARTS, HV, PAIR, RANK, GAP, NPART)
            scan(k, PAIR, HV, lambda b, hf: DELTA[:, hf, b, :], lambda b, hf: DU[:, hf, b, :],
                 lambda m, b, c: PARTS[0:NPART, m, b, c * BANK:(c + 1) * BANK],
                 lambda j: selt[:, bass.ds(j * P, P)], lambda hf, j: w["A7"][:, hf, bass.ds(j, 1)], k.ident,
                 lambda hf: w["D7"][:, hf, :], lambda b, hf, c: U[:, hf, b, c * BANK:(c + 1) * BANK],
                 lambda b, hf: R[:, hf, b, :], lambda b, hf: R[:, hf, b, :],
                 [k.arena[5][:, n * SEQ:(n + 1) * SEQ] for n in (2, 3)])
            project_back(k, [R[:, hf].rearrange("p b t -> p (b t)") for hf in range(HV)],
                         [w["w7_outT"][:, hf, :] for hf in range(HV)], range(pair * PAIR, (pair + 1) * PAIR), w["alpha"])


def channels(k, pair, two, FT, LEFT, U, R, TMP, HV, KC, PAIR):
    nc, w, bank = k.nc, k.w, k.bank
    left_up, right_up, left, right, conv = cs = [k.count("m7c_" + n) for n in ("left_up", "right_up", "left", "right", "conv")]
    with nc.Block() as block:
        @block.tensor
        def _(pe):
            for b in range(PAIR):
                for q in range(2 * HV):
                    n = b * HV + q % HV
                    if b:
                        done = left if q < HV else right
                        pe.wait_ge(done.sem, done.at((1 if q < HV else 0) + n - HV + 1))
                    for c in range(2):
                        at = (pair * PAIR + b) * SEQ + c * BANK
                        mm = pe.matmul(bank[2 * q + c], w["w7_inT"][:, q * P:(q + 1) * P], FT[:, at:at + BANK], start=True, stop=True)
                    mm.then_inc((left_up if q < HV else right_up).sem, 1)

        @block.vector
        def _(dve):
            dve.memset(LEFT[:, :, :, 0:KC - 1], 0.0).then_inc(left.sem, 1)
            for b in range(PAIR):
                for hf in range(HV):
                    n = b * HV + hf
                    dve.wait_ge(left_up.sem, left_up.at(n + 1))
                    dve.tensor_copy(LEFT[:, hf, b, KC - 1:], two(2 * hf)).then_inc(left.sem, 1)
                    dve.wait_ge(left.sem, left.at(n + 2))
                    acc, taps = TMP[:, hf, b, :], w["conv7_w"][:, hf, :]
                    dve.tensor_scalar(acc, LEFT[:, hf, b, 0:SEQ], taps[:, 0:1], None, ALU.mult).then_inc(conv.sem, 1)
                    for tap in range(1, KC):
                        dve.wait_ge(conv.sem, conv.at(KC * n + tap))
                        dve.scalar_tensor_tensor(out=acc, in0=LEFT[:, hf, b, tap:tap + SEQ], scalar=taps[:, tap:tap + 1],
                                                 in1=acc, op0=ALU.mult, op1=ALU.add).then_inc(conv.sem, 1)

        @block.scalar
        def _(act):
            for b in range(PAIR):
                for hf in range(HV):
                    act.wait_ge(right_up.sem, right_up.at(b * HV + hf + 1))
                    act.activation(R[:, hf, b, :], two(4 + 2 * hf), ACT.Silu).then_inc(right.sem, 1)
                for hf in range(HV):
                    act.wait_ge(conv.sem, conv.at(KC * (b * HV + hf + 1)))
                    act.activation(U[:, hf, b, :], TMP[:, hf, b, :], ACT.Silu, bias=w["conv7_b"][:, hf:hf + 1])
    for s in (left_up, right_up, right):
        s.passed(HV * PAIR)
    left.passed(HV * PAIR + 1)
    conv.passed(KC * HV * PAIR)


def deltas(k, two, U, DELTA, DU, TMP, REST, PARTS, HV, PAIR, RANK, GAP, NPART):
    nc, w, bank = k.nc, k.w, k.bank
    names = ("t_up", "dt", "d_up", "b_up", "c_up", "soft", "d_taken", "first", "rest", "mid", "parts", "delta")
    t_up, dt_in, d_up, b_up, c_up, soft, d_taken, first, rest, mid, done, delta_up = [k.count("m7d_" + n) for n in names]
    bc = (b_up, c_up)
    DT = REST[0:RANK, 2:2 + PAIR, :]
    with nc.Block() as block:
        @block.tensor
        def _(pe):
            for b in range(PAIR):
                if b:
                    pe.wait_ge(d_taken.sem, d_taken.at(HV * (b - 1) + 1))
                    pe.wait_ge(soft.sem, soft.at(3 * HV * (b - 1) + 3))
                for c in range(2):
                    for hf in range(HV):
                        mm = pe.matmul(bank[c][0:RANK, :], w["w7_dtin"][:, hf, :], U[:, hf, b, c * BANK:(c + 1) * BANK],
                                       start=hf == 0, stop=hf == HV - 1)
                mm.then_inc(t_up.sem, 1)
                for m in range(2):
                    if b:
                        pe.wait_ge(rest.sem, rest.at(2 * (b - 1) + m + 1))
                    for c in range(2):
                        for hf in range(HV):
                            mm = pe.matmul(bank[2 + 2 * m + c][0:NPART, :], w["bc7"][:, m, hf, :],
                                           U[:, hf, b, c * BANK:(c + 1) * BANK], start=hf == 0, stop=hf == HV - 1)
                    mm.then_inc(bc[m].sem, 1)
                pe.wait_ge(dt_in.sem, dt_in.at(b + 1))
                for hf in range(HV):
                    if b and hf:
                        pe.wait_ge(d_taken.sem, d_taken.at(HV * b))
                        pe.wait_ge(soft.sem, soft.at(3 * HV * b))
                    for c in range(2):
                        mm = pe.matmul(bank[6 * hf + c], w["w7_dtT"][:, hf * P:(hf + 1) * P], DT[:, b, c * BANK:(c + 1) * BANK],
                                       start=True, stop=True)
                    mm.then_inc(d_up.sem, 1)

        @block.scalar
        def _(act):
            for b in range(PAIR):
                for m in range(2):
                    n = 2 * b + m
                    act.wait_ge(bc[m].sem, bc[m].at(b + 1))
                    act.activation(PARTS[0:NPART, m, b, :], two(2 + 2 * m)[0:NPART, :], ACT.Copy).then_inc(first.sem, 1)
                    act.wait_ge(rest.sem, rest.at(n + 1))
                    act.activation(PARTS[GAP:2 * GAP, m, b, :], REST[GAP:2 * GAP, m, :], ACT.Copy)
                    act.activation(PARTS[2 * GAP:NPART, m, b, :], REST[2 * GAP:NPART, m, :], ACT.Copy).then_inc(mid.sem, 1)
                for hf in range(HV):
                    t, n, bias = TMP[:, hf, b, :], 3 * (HV * b + hf), w["b7_dt"][:, hf:hf + 1]
                    act.wait_ge(d_up.sem, d_up.at(HV * b + hf + 1))
                    act.activation(t, two(6 * hf), ACT.Abs, bias=bias).then_inc(soft.sem, 1)
                    act.wait_ge(soft.sem, soft.at(n + 1))
                    act.activation(t, t, ACT.Exp, scale=-1.0).then_inc(soft.sem, 1)
                    act.wait_ge(soft.sem, soft.at(n + 2))
                    act.activation(t, t, ACT.Ln, bias=1.0).then_inc(soft.sem, 1)

        @block.vector
        def _(dve):
            for b in range(PAIR):
                dve.wait_ge(t_up.sem, t_up.at(b + 1))
                dve.tensor_copy(DT[:, b, :], two(0)[0:RANK, :]).then_inc(dt_in.sem, 1)
                for m in range(2):
                    n = 2 * b + m
                    dve.wait_ge(first.sem, first.at(n + 1))
                    if n >= 2:
                        dve.wait_ge(done.sem, done.at(n - 1))
                    dve.tensor_tensor(REST[0:NPART, m, :], two(2 + 2 * m)[0:NPART, :], PARTS[0:NPART, m, b, :],
                                      ALU.subtract).then_inc(rest.sem, 1)
                    dve.wait_ge(mid.sem, mid.at(n + 1))
                    dve.tensor_tensor(PARTS[2 * GAP:NPART, m, b, :], REST[2 * GAP:NPART, m, :],
                                      PARTS[2 * GAP:NPART, m, b, :], ALU.subtract).then_inc(done.sem, 1)
                for hf in range(HV):
                    n = HV * b + hf
                    dve.wait_ge(soft.sem, soft.at(3 * n + 1))
                    dve.tensor_scalar(DELTA[:, hf, b, :], two(6 * hf), w["b7_dt"][:, hf:hf + 1], 0.0, ALU.add,
                                      ALU.max).then_inc(d_taken.sem, 1)
                    dve.wait_ge(d_taken.sem, d_taken.at(n + 1))
                    dve.wait_ge(soft.sem, soft.at(3 * n + 3))
                    dve.tensor_tensor(DELTA[:, hf, b, :], DELTA[:, hf, b, :], TMP[:, hf, b, :], ALU.add).then_inc(delta_up.sem, 1)

        @block.gpsimd
        def _(pool):
            for b in range(PAIR):
                for hf in range(HV):
                    pool.wait_ge(delta_up.sem, delta_up.at(HV * b + hf + 1))
                    pool.tensor_tensor(DU[:, hf, b, :], DELTA[:, hf, b, :], U[:, hf, b, :], ALU.mult)
    for s in (t_up, dt_in, b_up, c_up):
        s.passed(PAIR)
    for s in (d_up, d_taken, delta_up):
        s.passed(HV * PAIR)
    for s in (first, rest, mid, done):
        s.passed(2 * PAIR)
    soft.passed(3 * HV * PAIR)



def in_pairs(eng, n, step, reach=2):
    loops = (n - reach) // 2
    with eng.Fori(0, loops) as p:
        for s in range(2):
            step(p * 2 + s, s, reach)
    for i in range(2 * loops, n):
        step(i, i % 2, n - 1 - i)


def turn_stream(k, into, stride, lead):
    nc, bank = k.nc, k.bank
    turned, taken = k.count("turned"), k.count("turned_taken")
    with nc.Block() as block:
        @block.tensor
        def _(pe):
            for b in range(BATCH):
                for j in range(TPB):
                    mm = pe.transpose(bank[2 * b + j // 4][:, P * (j % 4):P * (j % 4 + 1)], k.Zpad[:, k.zindex(b * TPB + j), :], k.ident)
                mm.then_inc(turned.sem, 1)

        def take(eng, copy, b):
            eng.wait_ge(turned.sem, turned.at(b + 1))
            copy(into[:, b * stride + lead:b * stride + lead + SEQ], k.psum[:, 2 * b * BANK:(2 * b + 2) * BANK])

        @block.vector
        def _(dve):
            for b in range(0, BATCH, 2):
                take(dve, dve.tensor_copy, b)

        @block.scalar
        def _(act):
            for b in range(1, BATCH, 2):
                take(act, act.copy, b)
    turned.passed(BATCH)



def band_attention(k):
    nc, w, bank = k.nc, k.w, k.bank
    WIN, KEYS = 64, 256
    layernorm(k)
    stride = SEQ + 2 * WIN
    ZT = k.big[:, TOK:TOK + BATCH * stride]
    names = ("qw", "q", "scores", "peak", "probs", "pt", "pts", "o", "inverse", "relu", "added", "cleared", "resid")
    qw, q_up, scores, peak, probs, pt, pts, o_up, inverse, relu, added, cleared, resid = [k.count("band_" + n) for n in names]
    credited = (q_up, pts, relu, added, pt, o_up)
    with ExitStack() as mem:
        def sb(name, shape, dt=F32):
            return mem.enter_context(nc.sbuf_tensor("band_" + name, shape, dt))

        mask = sb("mask", [P, TPB, KEYS], BF16)
        Q = sb("q", [P, 2, P])
        PR = sb("probs", [P, 2, KEYS + 2 * WIN])
        PT = sb("pt", [P, 2, 3 * P])
        RO = sb("relu", [P, 2, D])
        top, low, total, inv = (sb(n, [P, 2]) for n in ("top", "low", "total", "inv"))
        with nc.Block() as block:
            @block.sync
            def _(sp):
                sp.dma_start(mask[:, :, :], k.dram["c_band"].rearrange("p (j c) -> p j c", j=TPB)).then_inc(cleared.sem, 16)
                for s in credited:
                    sp.sem_inc(s.sem, 2)
                sp.wait_ge(cleared.sem, cleared.at(16))

            @block.gpsimd
            def _(pool):
                pool.memset(PR[:, :, :], 0.0)
                pool.memset(ZT, 0.0)
        for s in credited:
            s.passed(2)
        turn_stream(k, ZT, stride, WIN)

        with nc.Block() as block:
            @block.tensor
            def _(pe):
                def column(i):
                    return i * P + (i // TPB) * (2 * WIN)

                def query(i, s):
                    pe.wait_ge(q_up.sem, q_up.at(i - 1))
                    pe.matmul(bank[s][:, 0:P], w["W_band"], ZT[:, bass.ds(column(i) + WIN, P)], start=True,
                              stop=True).then_inc(qw.sem, 1)

                def score(i, s):
                    pe.wait_ge(q_up.sem, q_up.at(i + 1))
                    pe.matmul(bank[2 + s][:, 0:KEYS], Q[:, s, :], ZT[:, bass.ds(column(i), KEYS)], start=True, stop=False)
                    pe.matmul(bank[2 + s][:, 0:KEYS], k.identb, mask[:, i % TPB, :], start=False,
                              stop=True).then_inc(scores.sem, 1)

                query(0, 0)
                query(1, 1)
                score(0, 0)

                def step(i, s, ahead):
                    pe.wait_ge(probs.sem, probs.at(i + 1))
                    pe.wait_ge(pts.sem, pts.at(i - 1))
                    for n in range(3):
                        mm = pe.transpose(bank[4 + s][:, n * P:(n + 1) * P], PR[:, s, n * P:(n + 1) * P], k.ident)
                    mm.then_inc(pt.sem, 1)
                    if ahead > 1:
                        query(i + 2, s)
                    if ahead:
                        score(i + 1, 1 - s)
                    pe.wait_ge(relu.sem, relu.at(i - 1))
                    pe.wait_ge(pts.sem, pts.at(i + 1))
                    for n in range(3):
                        mm = pe.matmul(bank[6 + s][:, 0:D], PT[:, s, n * P:(n + 1) * P], k.Zpad[:, k.zindex(i) - 1 + n, :], start=n == 0, stop=n == 2)
                    mm.then_inc(o_up.sem, 1)
                in_pairs(pe, TILES, step)

            @block.scalar
            def _(act):
                def copy_q(i, s):
                    act.wait_ge(qw.sem, qw.at(i + 1))
                    act.copy(Q[:, s, :], bank[s][:, 0:P]).then_inc(q_up.sem, 1)

                copy_q(0, 0)

                def step(i, s, ahead):
                    act.wait_ge(pt.sem, pt.at(i - 1))
                    act.wait_ge(peak.sem, peak.at(2 * i + 2))
                    act.activation(PR[:, s, WIN:WIN + KEYS], bank[2 + s][:, 0:KEYS], ACT.Exp, bias=low[:, s:s + 1],
                                   accum_out=total[:, s:s + 1]).then_inc(probs.sem, 1)
                    if ahead:
                        copy_q(i + 1, 1 - s)
                    act.wait_ge(o_up.sem, o_up.at(i + 1))
                    act.wait_ge(inverse.sem, inverse.at(i + 1))
                    act.wait_ge(added.sem, added.at(i - 1))
                    act.activation(RO[:, s, :], bank[6 + s][:, 0:D], ACT.Relu, scale=inv[:, s:s + 1]).then_inc(relu.sem, 1)
                in_pairs(act, TILES, step)

            @block.vector
            def _(dve):
                def maximum(i, s):
                    dve.wait_ge(scores.sem, scores.at(i + 1))
                    dve.tensor_reduce(top[:, s:s + 1], bank[2 + s][:, 0:KEYS], AX_X, ALU.max).then_inc(peak.sem, 1)
                    dve.wait_ge(peak.sem, peak.at(2 * i + 1))
                    dve.tensor_scalar(low[:, s:s + 1], top[:, s:s + 1], -1.0, None, ALU.mult).then_inc(peak.sem, 1)

                dve.wait_ge(resid.sem, resid.at(1))
                maximum(0, 0)

                def step(i, s, ahead):
                    dve.wait_ge(pt.sem, pt.at(i + 1))
                    dve.wait_ge(o_up.sem, o_up.at(i - 1))
                    dve.tensor_copy(PT[:, s, :], bank[4 + s][:, 0:3 * P]).then_inc(pts.sem, 1)
                    dve.reciprocal(inv[:, s:s + 1], total[:, s:s + 1]).then_inc(inverse.sem, 1)
                    if ahead:
                        maximum(i + 1, 1 - s)
                    dve.wait_ge(relu.sem, relu.at(i + 1))
                    dve.tensor_tensor(k.X[:, i, :], k.X[:, i, :], RO[:, s, :], ALU.add).then_inc(added.sem, 1)
                in_pairs(dve, TILES, step)

            @block.gpsimd
            def _(pool):
                for b in range(BATCH):
                    add = pool.tensor_tensor(k.xpart(b), k.xpart(b), k.zpart(b), ALU.add)
                add.then_inc(resid.sem, 1)



def causal_attention(k):
    nc, w, bank = k.nc, k.w, k.bank
    HEADS, HD, STRIP = 16, 8, 32
    GROUPS, IN, PARTS = 4, 4, 3
    ROUNDS, SLOTS = BATCH * GROUPS, 4
    ROWS = PARTS * HD
    PEAK = 96
    SCALE = float(1.0 / np.sqrt(HD))
    GROUP = IN * SEQ
    layernorm(k)

    QK = k.big[:, 0:SLOTS * GROUP].bitcast(BF16).rearrange("p (s m t) -> p s m t", s=SLOTS, m=2)
    PT = k.big[:, SLOTS * GROUP:(SLOTS + 2) * GROUP].rearrange("p (s h t) -> p s h t", s=2, h=IN)
    FT = k.big[:, SLOTS * GROUP:(SLOTS + 1) * GROUP]
    REST = k.big[:, (SLOTS + 1) * GROUP:(SLOTS + 1) * GROUP + 4 * BANK].rearrange("p (s t) -> p s t", s=4)
    parts = k.big[:, 0:PARTS * TOK].bitcast(BF16).rearrange("p (b m a t) -> p b m a t", b=BATCH, m=2, a=PARTS)
    V = k.arena6[:, 0:TOK].rearrange("p (r j c) -> p r j c", r=ROUNDS, j=TPB)
    zt = [k.Zpad[:, b * (TPB + 1) + 1:(b + 1) * (TPB + 1), :] for b in range(BATCH)]
    VS = zt[0].rearrange("p j (h e) -> p j h e", h=IN)
    OT, INV, ON = (z.rearrange("p j d -> p (j d)") for z in zt[1:])
    turn_stream(k, FT, SEQ, 0)
    kept = nc.dram_tensor("causal_parts", (2, ROUNDS, PARTS, HD * IN, SEQ), BF16).ap()

    names = ("qk_up", "first", "second", "left", "third", "v_up", "v_in", "written", "cleared", "fed", "s1_up", "s1_free", "s2_up", "probs",
             "pv", "vs_in", "o_in", "sums_out", "inverse", "sums_in", "peak", "split", "zeroed")
    (qk_up, first, second, left, third, v_up, v_in, written, cleared, fed, s1_up, s1_free, s2_up, probs, pv, vs_in, o_in, sums_out,
     inverse, sums_in, peak, split, zeroed) = [k.count("causal_" + n) for n in names]
    loaded = [k.count(f"causal_loaded{s}") for s in range(SLOTS)]
    peaks_in = [k.count(f"causal_peaks_in{s}") for s in range(SLOTS)]
    with ExitStack() as mem:
        def sb(name, shape, dt=F32):
            return mem.enter_context(nc.sbuf_tensor("causal_" + name, shape, dt))

        mask = sb("mask", [P, 2, P], BF16)
        WP = sb("wp", [P, 2, P])
        WS = sb("wo", [P, GROUPS, D])
        sums = sb("sums", [P, P])
        part = sb("peak_parts", [P, IN, TPB, 2])
        top = sb("top", [P, IN, TPB])
        total, inv = (sb(n, [P, SEQ // STRIP]) for n in ("total", "inv"))
        low = sb("low", [IN * TPB, 2, P])
        lowb = sb("low_parts", [IN * TPB, PARTS, P], BF16)

        CH = [(c, m) for c in range(TOK // BANK) for m in range(2)]
        with nc.Block() as block:
            @block.sync
            def _(sp):
                n = 0
                for m in range(2):
                    sp.dma_start(mask[:, m, :], k.dram["c_causal"] if m == 0 else k.dram["c_causal_turned"]).then_inc(cleared.sem, 16)
                sp.dma_start(sums[:, :], k.dram["c_sums"]).then_inc(cleared.sem, 16)
                sp.wait_ge(vs_in.sem, vs_in.at(1))
                for hh in range(IN):
                    sp.dma_start(WS[STRIP * hh:STRIP * hh + HD, :, :],
                                 k.dram["L1_attn_a_WO"].rearrange("(g h e) d -> h e g d", g=GROUPS, h=IN)[hh]).then_inc(cleared.sem, 16)
                for i, (c, m) in enumerate(CH):
                    if c % 2:
                        b = c // 2
                        sp.wait_ge(first.sem, first.at(i + 1))
                        sp.wait_ge(second.sem, second.at(i + 1))
                        sp.wait_ge(third.sem, third.at(i + 1))
                        for g in range(GROUPS):
                            for a in range(PARTS):
                                sp.dma_start(kept[m, b * GROUPS + g, a], parts[STRIP * g:STRIP * (g + 1), b, m, a, :]).then_inc(written.sem, 16)
                                n += 1
                sp.wait_ge(written.sem, written.at(16 * n))
                sp.wait_ge(cleared.sem, cleared.at(16 * 7))
                for s, v in ((s1_free, 2), (probs, 2), (pv, 2), (o_in, 1)):
                    sp.sem_inc(s.sem, v)

            @block.gpsimd
            def _(pool):
                pool.memset(WS[:, :, :], 0.0).then_inc(vs_in.sem, 1)
                for m, n in enumerate("QK"):
                    cp = pool.tensor_copy(WP[:, m, :].rearrange("p (g e h) -> p g e h", g=GROUPS, e=HD),
                                          w["W" + n].rearrange("p (g h e) -> p g e h", g=GROUPS, h=IN))
                cp.then_inc(vs_in.sem, 1)
                pool.memset(VS, 0.0)
                pool.memset(part[:, :, :, :], MASKED)
                for i, (c, m) in enumerate(CH):
                    b, t = c // 2, (c % 2) * BANK
                    pool.wait_ge(second.sem, second.at(i + 1))
                    pool.tensor_tensor(parts[:, b, m, 2, t:t + BANK], REST[:, i % 4, :], parts[:, b, m, 1, t:t + BANK], ALU.subtract).then_inc(third.sem, 1)

            @block.tensor
            def _(pe):
                pe.wait_ge(vs_in.sem, vs_in.at(2))
                for i, (c, m) in enumerate(CH):
                    if i >= 4:
                        pe.wait_ge(left.sem, left.at(i - 3))
                    pe.matmul(bank[i % 4], WP[:, m, :], FT[:, c * BANK:(c + 1) * BANK], start=True, stop=True).then_inc(qk_up.sem, 1)
                    if m:
                        if c >= 4:
                            pe.wait_ge(v_in.sem, v_in.at(c - 3))
                        for j in range(4):
                            mm = pe.matmul(bank[4 + c % 4][:, j * P:(j + 1) * P], FT[:, c * BANK + j * P:c * BANK + (j + 1) * P], w["WV"],
                                           start=True, stop=True)
                        mm.then_inc(v_up.sem, 1)

            @block.scalar
            def _(act):
                def part_two(i):
                    c, m = CH[i]
                    act.wait_ge(left.sem, left.at(i + 1))
                    act.copy(parts[:, c // 2, m, 1, (c % 2) * BANK:][:, 0:BANK], REST[:, i % 4, :]).then_inc(second.sem, 1)

                for i, (c, m) in enumerate(CH):
                    act.wait_ge(qk_up.sem, qk_up.at(i + 1))
                    act.copy(parts[:, c // 2, m, 0, (c % 2) * BANK:][:, 0:BANK], bank[i % 4]).then_inc(first.sem, 1)
                    if i:
                        part_two(i - 1)
                part_two(len(CH) - 1)

            @block.vector
            def _(dve):
                for i, (c, m) in enumerate(CH):
                    dve.wait_ge(first.sem, first.at(i + 1))
                    if i >= 4:
                        dve.wait_ge(third.sem, third.at(i - 3))
                    dve.tensor_tensor(REST[:, i % 4, :], bank[i % 4], parts[:, c // 2, m, 0, (c % 2) * BANK:][:, 0:BANK],
                                      ALU.subtract).then_inc(left.sem, 1)
                    if m:
                        dve.wait_ge(v_up.sem, v_up.at(c + 1))
                        dve.tensor_copy(V.rearrange("p (b g) j c -> p b j g c", b=BATCH)[:, c // 2, 4 * (c % 2):4 * (c % 2) + 4, :, :],
                                        bank[4 + c % 4].rearrange("p (j g c) -> p j g c", j=4, g=GROUPS)).then_inc(v_in.sem, 1)
        vs_in.passed(2)
        for s, v in ((s1_free, 2), (probs, 2), (pv, 2), (o_in, 1)):
            s.passed(v)
        with nc.Block() as block:
            @block.vector
            def _(dve):
                for s in range(2):
                    dve.memset(k.big[:, s * GROUP:(s + 1) * GROUP], 0.0).then_inc(zeroed.sem, 1)
                dve.wait_ge(zeroed.sem, zeroed.at(4))
                for s in range(SLOTS):
                    dve.memset(QK[PEAK:PEAK + PARTS, s, 1, :], 1.0)
                dve.memset(VS[:, :, :, HD:HD + 1], 1.0)
                dve.memset(INV, 0.0)

            @block.gpsimd
            def _(pool):
                for s in range(2, 4):
                    pool.memset(k.big[:, s * GROUP:(s + 1) * GROUP], 0.0).then_inc(zeroed.sem, 1)
        zeroed.passed(4)

        first_units = []
        for qt in range(TPB):
            for half, (_, n) in enumerate(halves((qt + 1) * P, BANK)):
                per = BANK // n
                first_units += [(qt, half, range(h, min(h + per, IN)), n) for h in range(0, IN, per)]
        second_units, after = [], {}
        for kt in range(TPB):
            n = SEQ - kt * P
            per = 1 if n > BANK else 2 if 2 * n > BANK else 4
            second_units += [(kt, range(h, h + per), n) for h in range(0, IN, per)]
            after[kt] = len(second_units)
        N1, N2 = len(first_units), len(second_units)
        ONES, OUT = [("sum", 0), ("sum", 1)], [("out", 0), ("out", 1)]
        scoring = [("score", i) for i in range(N1)]
        LEAD = 18
        SHORT, LONG = N1 + 1, N1 + 5
        soon = [("soon", i) for i in range(LEAD)]

        def ring_steps(before, more):
            steps = scoring[LEAD:] + [("turn", 0)] if more else []
            if more > 1:
                steps = steps + soon
            if before:
                steps = steps[0:SUMS_AT] + ONES + steps[SUMS_AT:OUT_AT] + OUT + steps[OUT_AT:]
            return steps

        def sums_step(r):
            return ring_start(r) + (SUMS_AT if not isinstance(r, int) or r + 1 < ROUNDS else 0)

        def ring_start(r):
            if isinstance(r, int) and r == ROUNDS - 1:
                return 2 * SHORT + LEAD + (r - 1) * LONG - LEAD
            return 2 * SHORT + LEAD + (r - 1) * LONG

        INVERSE_AT, SUMS_AT, OUT_AT = 10, 18, 26
        values_after = {5: 0, 9: 1, 13: 2, 17: 3, 19: 4, 21: 5}
        TURN = 18

        def rounds(eng, body):
            body(0, 0, False, 2, 0, 0)
            with eng.Fori(0, BATCH - 1) as b:
                for j in range(1, GROUPS + 1):
                    body(b * GROUPS + j, j % SLOTS, True, 2, b, j - 1)
            for r in range((BATCH - 1) * GROUPS + 1, ROUNDS):
                body(r, r % SLOTS, True, min(2, ROUNDS - 1 - r), BATCH - 1, r - 1 - (BATCH - 1) * GROUPS)

        with nc.Block() as block:
            @block.sync
            def _(sp):
                def load_round(r, s):
                    for a in range(PARTS):
                        for c in range(PARTS):
                            rows = slice((a * PARTS + c) * HD, (a * PARTS + c + 1) * HD)
                            sp.dma_start(QK[rows, s, 1, :], keys(r, a)).then_inc(loaded[s].sem, 16)
                        sp.dma_start(QK[a * ROWS:(a + 1) * ROWS, s, 0, :], queries(r)).then_inc(loaded[s].sem, 16)

                def of_round(m, r):
                    x = kept[m].rearrange("r a (e h) t -> r (a e) (h t)", e=HD)
                    return (x[r:r + 1] if isinstance(r, int) else x[bass.ds(r, 1)]).rearrange("r q t -> (r q) t")

                def queries(r):
                    return of_round(0, r)

                def keys(r, a):
                    return of_round(1, r)[a * HD:(a + 1) * HD, :]

                def maxima(r, s):
                    sp.wait_ge(split.sem, split.at(4 * r + 4))
                    for a in range(PARTS):
                        sp.dma_start(QK[PEAK + a:PEAK + a + 1, s, 0, :].rearrange("a (p c) -> a p c", p=IN * TPB), lowb[:, a, :]).then_inc(peaks_in[s].sem, 16)

                def invert(r):
                    sp.wait_ge(o_in.sem, o_in.at(r + 1))
                    for hh in range(IN):
                        strip = slice(STRIP * hh, STRIP * (hh + 1))
                        row = STRIP * hh + HD
                        sp.dma_start(total[strip, :], OT[row:row + 1, :].rearrange("a (p c) -> a p c", p=STRIP)).then_inc(sums_out.sem, 16)
                    sp.wait_ge(inverse.sem, inverse.at(r + 1))
                    for hh in range(IN):
                        strip = slice(STRIP * hh, STRIP * (hh + 1))
                        row = STRIP * hh + HD
                        sp.dma_start(INV[row:row + 1, :].rearrange("a (p c) -> a p c", p=STRIP), inv[strip, :]).then_inc(sums_in.sem, 16)

                for r in range(SLOTS):
                    load_round(r, r)
                maxima(0, 0)

                def body(r, s, before, more, b, g):
                    if before and (not isinstance(r, int) or r + 3 < ROUNDS):
                        sp.wait_ge(s2_up.sem, s2_up.at(r * N2))
                        load_round(r + 3, (s + 3) % SLOTS)
                    if before:
                        invert(r - 1)
                    if more:
                        maxima(r + 1, (s + 1) % SLOTS)
                rounds(sp, body)
                invert(ROUNDS - 1)

            @block.gpsimd
            def _(pool):
                def split_maxima(r, n, s, count):
                    pool.wait_ge(s1_free.sem, s1_free.at(n + 1))
                    if count is not None:
                        pool.wait_ge(*count)
                    pool.sem_inc(fed.sem, 1)
                    pool.tensor_copy(lowb[:, 0, :], low[:, 0, :]).then_inc(split.sem, 1)
                    pool.wait_ge(split.sem, split.at(4 * r + 1))
                    pool.tensor_tensor(low[:, 1, :], low[:, 0, :], lowb[:, 0, :], ALU.subtract).then_inc(split.sem, 1)
                    pool.wait_ge(split.sem, split.at(4 * r + 2))
                    pool.sem_inc(fed.sem, 1)
                    pool.tensor_copy(lowb[:, 1, :], low[:, 1, :]).then_inc(split.sem, 1)
                    pool.wait_ge(split.sem, split.at(4 * r + 3))
                    pool.tensor_tensor(lowb[:, 2, :], low[:, 1, :], lowb[:, 1, :], ALU.subtract).then_inc(split.sem, 1)

                def values(r):
                    pool.wait_ge(pv.sem, pv.at(r * TPB))
                    pool.wait_ge(split.sem, split.at(4 * r + 4))
                    pool.sem_inc(fed.sem, 1)
                    rr = slice(r, r + 1) if isinstance(r, int) else bass.ds(r, 1)
                    pool.tensor_copy(VS[:, :, :, 0:HD], V[:, rr, :, :].rearrange("p r j (h e) -> p (r j) h e", h=IN)).then_inc(vs_in.sem, 1)

                split_maxima(0, SHORT - 1, 0, None)

                def body(r, s, before, more, b, g):
                    steps = ring_steps(before, more)
                    start = ring_start(r) if before else SHORT + LEAD
                    values(r)
                    if before and (not isinstance(r, int) or r + 3 < ROUNDS):
                        pool.wait_ge(s2_up.sem, s2_up.at(r * N2))
                        pool.wait_ge(vs_in.sem, vs_in.at(r + 1))
                        pool.sem_inc(fed.sem, 1)
                        pool.memset(QK[PEAK:PEAK + PARTS, (s + 3) % SLOTS, 0, :], 0.0).then_inc(zeroed.sem, 1)
                        pool.wait_ge(zeroed.sem, zeroed.at(r))
                    else:
                        pool.wait_ge(vs_in.sem, vs_in.at(r + 1))
                    if more:
                        turn = b + 1 + (1 if s == 0 and before else 0)
                        split_maxima(r + 1, start + steps.index(("turn", 0)), s, (peaks_in[s].sem, peaks_in[s].at(turn * 16 * PARTS)))
                rounds(pool, body)

            @block.tensor
            def _(pe):
                ring = [0]

                def enter(n):
                    pe.wait_ge(s1_free.sem, s1_free.at(n - 1))
                    place = bank[ring[0]]
                    ring[0] = 1 - ring[0]
                    return place

                def ring_step(step, n, r, s, g):
                    kind, i = step
                    if kind in ("score", "soon"):
                        s = (s + 1 + (kind == "soon")) % SLOTS
                        qt, half, heads, size = first_units[i]
                        out = enter(n)
                        for at, hh in enumerate(heads):
                            col = hh * SEQ
                            o = out[:, at * size:(at + 1) * size]
                            diag = half == (qt * P) // BANK
                            mm = pe.matmul(o, QK[:, s, 0, col + qt * P:col + (qt + 1) * P], QK[:, s, 1, col + half * BANK:col + half * BANK + size],
                                           start=True, stop=True)
                            if diag:
                                mm = pe.matmul(o[:, size - P:size], k.identb, mask[:, 0, :], start=False, stop=True, skip_group_check=True)
                        mm.then_inc(s1_up.sem, 1)
                    elif kind == "turn":
                        pe.wait_ge(peak.sem, peak.at(r + 2))
                        out = enter(n)
                        pe.matmul(out[0:IN * TPB, 0:P], top[:, :, :].rearrange("p h j -> p (h j)"), k.ident, start=True, stop=True).then_inc(s1_up.sem, 1)
                    elif kind == "sum":
                        pe.wait_ge(sums_in.sem, sums_in.at(16 * IN * r))
                        out = enter(n)
                        pe.matmul(out, sums[:, :], INV[:, i * BANK:(i + 1) * BANK], start=True, stop=True).then_inc(s1_up.sem, 1)
                    else:
                        out = enter(n)
                        for j in range(4):
                            mm = pe.matmul(out[:, j * P:(j + 1) * P], ON[:, i * BANK + j * P:i * BANK + (j + 1) * P], WS[:, g, :], start=True, stop=True)
                        mm.then_inc(s1_up.sem, 1)

                def second(i, r, s):
                    kt, heads, size = second_units[i]
                    pe.wait_ge(probs.sem, probs.at(r * N2 + i - 1))
                    base = 2 + 2 * (i % 2)
                    for at, hh in enumerate(heads):
                        col = hh * SEQ
                        keys = QK[:, s, 1, col + kt * P:col + (kt + 1) * P]
                        if size > BANK:
                            places = [(base, kt * P, BANK), (base + 1, 0, BANK)]
                        else:
                            stride = 2 * BANK // len(heads) if size > P else P
                            lead = stride - size
                            places = [(base + at * stride // BANK, at * stride % BANK + lead, at * stride % BANK + lead + size)]
                        q = col + kt * P
                        for n, (bk, lo, hi) in enumerate(places):
                            mm = pe.matmul(bank[bk][:, lo:hi], keys, QK[:, s, 0, q:q + hi - lo], start=True, stop=True)
                            if n == 0:
                                mm = pe.matmul(bank[bk][:, lo:lo + P], k.identb, mask[:, 1, :], start=False, stop=True, skip_group_check=True)
                            q += hi - lo
                    mm.then_inc(s2_up.sem, 1)

                def values(kt, r):
                    pe.wait_ge(probs.sem, probs.at(r * N2 + after[kt]))
                    if kt == 0:
                        pe.wait_ge(vs_in.sem, vs_in.at(r + 1))
                        pe.wait_ge(o_in.sem, o_in.at(r))
                    for half in range(2):
                        lo = max(kt * P, half * BANK)
                        if lo < (half + 1) * BANK:
                            for hh in range(IN):
                                mm = pe.matmul(bank[6 + half][STRIP * hh:STRIP * (hh + 1), lo - half * BANK:BANK], VS[:, kt, hh, :],
                                               PT[:, kt % 2, hh, lo:(half + 1) * BANK], start=kt == 0, stop=(kt + 1) * P == (half + 1) * BANK)
                    mm.then_inc(pv.sem, 1)

                def feed(r, s, fill):
                    pe.wait_ge(loaded[s].sem, loaded[s].at(fill * 16 * PARTS * (PARTS + 1)))
                    if not isinstance(r, int) or r >= SLOTS:
                        pe.wait_ge(zeroed.sem, zeroed.at(r - SLOTS + 1))

                feed(0, 0, 1)
                for n, step in enumerate(scoring + [("turn", 0)]):
                    ring_step(step, n, -1, SLOTS - 1, 0)
                feed(1, 1, 1)
                for n, step in enumerate(soon):
                    ring_step(step, SHORT + n, -1, SLOTS - 1, 0)

                def body(r, s, before, more, b, g):
                    steps = ring_steps(before, more)
                    start = ring_start(r) if before else SHORT + LEAD
                    done = 0
                    fill = b + 1 + (1 if s == 0 and before else 0)
                    for i in range(N2):
                        if i == 0:
                            pe.wait_ge(peaks_in[s].sem, peaks_in[s].at(fill * 16 * PARTS))
                        second(i, r, s)
                        if before and i < 2:
                            values(6 + i, r - 1)
                        goal = len(steps) * (i + 1) // N2 if more else len(steps) * i // TURN
                        while done < goal:
                            if steps[done] == soon[0]:
                                feed(r + 2, (s + 2) % SLOTS, b + 1 + (1 if s + 2 >= SLOTS or (s == 0 and before) else 0))
                            ring_step(steps[done], start + done, r, s, g)
                            done += 1
                        if i in values_after:
                            values(values_after[i], r)
                rounds(pe, body)
                values(6, ROUNDS - 1)
                values(7, ROUNDS - 1)
                for i, step in enumerate(ONES + OUT):
                    ring_step(step, ring_start(ROUNDS - 1) + 4 + i, ROUNDS, 0, GROUPS - 1)

            @block.scalar
            def _(act):
                def outputs(r):
                    act.wait_ge(pv.sem, pv.at(TPB * (r + 1)))
                    if not isinstance(r, int) or r:
                        act.wait_ge(s1_free.sem, s1_free.at(sums_step(r) + 2))
                    act.copy(OT, k.psum[:, 6 * BANK:8 * BANK]).then_inc(o_in.sem, 1)

                def body(r, s, before, more, b, g):
                    for i, (kt, heads, size) in enumerate(second_units):
                        act.wait_ge(s2_up.sem, s2_up.at(r * N2 + i + 1))
                        if i == 0 or kt and after[kt - 1] == i:
                            act.wait_ge(pv.sem, pv.at(r * TPB + kt - 1))
                        base = (2 + 2 * (i % 2)) * BANK
                        if size > BANK:
                            place, into = k.psum[:, base + kt * P:base + 2 * BANK], PT[:, kt % 2, heads[0], kt * P:SEQ]
                        else:
                            stride = 2 * BANK // len(heads) if size > P else P
                            place = k.psum[:, base:base + len(heads) * stride].rearrange("p (h t) -> p h t", t=stride)[:, :, stride - size:]
                            into = PT[:, kt % 2, heads[0]:heads[0] + len(heads), kt * P:SEQ]
                        act.activation(into, place, ACT.Exp, scale=SCALE).then_inc(probs.sem, 1)
                        if i == 2 and before:
                            outputs(r - 1)
                rounds(act, body)
                outputs(ROUNDS - 1)

            @block.vector
            def _(dve):
                ring = [0]

                def ring_step(step, n, r, b, g):
                    kind, i = step
                    place = bank[ring[0]]
                    ring[0] = 1 - ring[0]
                    dve.wait_ge(s1_up.sem, s1_up.at(n + 1))
                    if kind in ("score", "soon"):
                        qt, half, heads, size = first_units[i]
                        dve.tensor_reduce(part[:, heads[0]:heads[0] + len(heads), qt, half:half + 1].rearrange("p h a -> p (h a)"),
                                          place[:, 0:len(heads) * size].rearrange("p (h t) -> p h t", t=size), AX_X, ALU.max).then_inc(s1_free.sem, 1)
                        if i == N1 - 1:
                            dve.wait_ge(s1_free.sem, s1_free.at(n + 1))
                            dve.tensor_tensor(top[:, :, :], part[:, :, :, 0], part[:, :, :, 1], ALU.max).then_inc(peak.sem, 1)
                    elif kind == "turn":
                        dve.tensor_scalar(low[:, 0, :], place[0:IN * TPB, 0:P], -1.0, None, ALU.mult).then_inc(s1_free.sem, 1)
                    elif kind == "sum":
                        half = slice(i * BANK, (i + 1) * BANK)
                        dve.tensor_tensor(ON[:, half], OT[:, half], place, ALU.mult).then_inc(s1_free.sem, 1)
                    else:
                        t = b * TPB + 4 * i
                        x = k.X[:, t:t + 4, :] if isinstance(t, int) else k.X[:, bass.ds(t, 4), :]
                        dve.tensor_tensor(x, x, place.rearrange("p (j d) -> p j d", d=D), ALU.add).then_inc(s1_free.sem, 1)

                def invert(r):
                    dve.wait_ge(sums_out.sem, sums_out.at(16 * IN * (r + 1)))
                    dve.reciprocal(inv[:, :], total[:, :]).then_inc(inverse.sem, 1)

                for n, step in enumerate(scoring + [("turn", 0)] + soon):
                    ring_step(step, n, -1, 0, 0)

                def body(r, s, before, more, b, g):
                    start = ring_start(r) if before else SHORT + LEAD
                    for n, step in enumerate(ring_steps(before, more)):
                        if before and n == (INVERSE_AT if more else 0):
                            invert(r - 1)
                        ring_step(step, start + n, r, b, g)
                rounds(dve, body)
                invert(ROUNDS - 1)
                for i, step in enumerate(ONES + OUT):
                    ring_step(step, ring_start(ROUNDS - 1) + 4 + i, ROUNDS, BATCH - 1, GROUPS - 1)



def local_transformer(k):
    nc = k.nc
    layernorm(k)
    for depth in range(2):
        local_attention(k, depth)
        gated_units(k, depth)
    with nc.Block() as block:
        @block.vector
        def _(dve):
            for b in range(0, BATCH, 2):
                dve.tensor_tensor(k.xpart(b), k.xpart(b), k.zpart(b), ALU.add)

        @block.gpsimd
        def _(pool):
            for b in range(1, BATCH, 2):
                pool.tensor_tensor(k.xpart(b), k.xpart(b), k.zpart(b), ALU.add)


def local_attention(k, depth):
    nc, bank, psum = k.nc, k.bank, k.psum
    HEADS, HD, WIN = 8, 64, 64
    PAIRS, KEYS = HEADS // 2, WIN + P
    INNER = HEADS * HD
    A = k.arena
    w = k.layer
    names = ("zs", "ht_up", "ht", "qkv_up", "raw", "v_in", "sq", "ss", "ab", "rn", "rot", "tr_up", "qkt", "s_up", "peak", "probs",
             "pt_up", "pt_a", "pt_b", "pv_up", "o_in", "ot_up", "ot", "y_up", "added", "loaded", "ready", "ready2", "held")
    (zs_in, ht_up, ht_in, qkv_up, raw_in, v_in, sq_in, ss_in, ab_in, rn_in, rot, tr_up, qkt, s_up, peak, probs, pt_up, pt_a, pt_b,
     pv_up, o_in, ot_up, ot_in, y_up, added, loaded, ready, ready2, held) = [k.count("local_" + n) for n in names]

    def cut(i, size, first, shape):
        n = int(np.prod(shape))
        flat = A[i][:, first:first + n]
        names = "abcd"[:len(shape)]
        return flat.rearrange(f"p ({' '.join(names)}) -> p {' '.join(names)}", **dict(zip(names, shape)))

    TABLE = cut(0, 0, 0, (TPB, 2, 2, HD))
    BASE = cut(0, 0, 2048, (TPB, 2, 2, HD))
    RAW = cut(1, 0, 0, (2, 2 * INNER))
    SQ = cut(1, 0, 2048, (2 * INNER,))
    HT = cut(1, 0, 3072, (2, P))
    ZS = cut(1, 0, 3328, (2, KEYS))
    COS = cut(2, 0, 0, (2, 2 * INNER))
    SIN = cut(2, 0, 2048, (2, 2 * INNER))
    QT = k.arena6[:, 1024:1024 + 4 * PAIRS * P].rearrange("p (s a c t) -> p s a c t", s=2, a=2, c=PAIRS)
    KT = cut(3, 0, 1024, (2, PAIRS, KEYS))
    O = cut(3, 0, 2560, (INNER,))
    OT = cut(3, 0, 3072, (PAIRS, P))
    MASK = A[3][:, 3584:4096].bitcast(BF16)[:, 0:2 * KEYS].rearrange("p (m c) -> p m c", m=2)
    PR = cut(4, 0, 0, (2, HEADS, 2 * P))
    PT = cut(5, 0, 0, (HEADS, 2, P))
    V = cut(5, 0, 2048, (4, INNER))
    small = k.arena6[:, 0:512].rearrange("p (s c) -> p s c", c=16)
    SS, RN, LOW, SUM, INV = (small[:, 2 * n:2 * n + 2, :] for n in range(5))
    SC = k.arena6[:, 512:768].rearrange("p (m a d) -> p m a d", m=2, a=2)
    SHIFT, CARRY = k.w["shift"], k.w["carry"]

    credited = (ht_in, v_in, qkt, added, ot_in, pt_a, pt_b, ht_up, tr_up, rot, ab_in, s_up, pv_up, probs, pt_up, o_in, y_up, ot_up,
                raw_in, ss_in, sq_in, zs_in, qkv_up, rn_in)
    CREDIT = 4
    with nc.Block() as block:
        @block.sync
        def _(sp):
            d = k.dram
            n = 0
            sp.dma_start(BASE, d["c_rope"].rearrange("p (j a m d) -> p j a m d", j=TPB, a=2, m=2)).then_inc(loaded.sem, 16)
            sp.dma_start(MASK, d["c_local"].rearrange("p (m c) -> p m c", m=2)).then_inc(loaded.sem, 16)
            half = HD // 2
            for m, name in enumerate(("q_scale", "k_scale")):
                row = d["L1_ffn_" + name][depth]
                sp.dma_start(SC[:, 0, m, :], row.partition_broadcast(P)).then_inc(loaded.sem, 16)
                sp.dma_start(SC[:, 1, m, 0:half], row[half:HD].partition_broadcast(P)).then_inc(loaded.sem, 16)
                sp.dma_start(SC[:, 1, m, half:HD], row[0:half].partition_broadcast(P)).then_inc(loaded.sem, 16)
            load_layer(k, sp, depth, loaded)
            for s in credited:
                sp.sem_inc(s.sem, CREDIT)
            sp.wait_ge(loaded.sem, loaded.at(16 * (8 + LAYER_LOADS)))

        @block.vector
        def _(dve):
            dve.memset(KT, 0.0)
            dve.memset(QT, 0.0)
            dve.memset(V, 0.0)
            dve.memset(k.Zpad[:, 0:TILES + BATCH + 1:TPB + 1, :], 0.0)
            dve.wait_ge(loaded.sem, loaded.at(16 * (8 + LAYER_LOADS)))
            scales = SC.rearrange("p m a d -> p (m a) d")
            for j in range(TPB):
                dve.tensor_tensor(TABLE[:, j].rearrange("p m a d -> p (m a) d"), BASE[:, j].rearrange("p m a d -> p (m a) d"),
                                  scales, ALU.mult)

        @block.gpsimd
        def _(pool):
            pool.memset(PR, 0.0)
    for s in credited:
        s.passed(CREDIT)
    loaded.passed(16 * (8 + LAYER_LOADS))

    REACH = 3

    def group_of(g):
        return psum[:, (3 + 2 * g) * BANK:(5 + 2 * g) * BANK].rearrange("p (r c) -> p r c", c=2 * P)[:, :, 0:KEYS]

    def in_steps(eng, step, finish):
        loops = (TILES - 2 - REACH) // 2
        for i in range(2):
            step(i, i, REACH, i > 0)
        with eng.Fori(1, 1 + loops) as p:
            for s in range(2):
                step(p * 2 + s, s, REACH, True)
        for i in range(2 + 2 * loops, TILES):
            step(i, i % 2, TILES - 1 - i, True)
        finish(TILES - 1, (TILES - 1) % 2)

    with nc.Block() as block:
        @block.tensor
        def _(pe):
            def turn_in(i, s):
                pe.wait_ge(zs_in.sem, zs_in.at(i + 1))
                pe.wait_ge(ht_in.sem, ht_in.at(i))
                pe.wait_ge(ot_in.sem, ot_in.at(i - REACH))
                pe.matmul(bank[7][0:64, 0:P], ZS[:, s, 64:128], k.ident, start=True, stop=True)
                pe.matmul(bank[7][64:P, 0:P], ZS[:, s, 128:192], SHIFT, start=True, stop=False)
                pe.matmul(bank[7][64:P, 0:P], ZS[:, s, 0:64], CARRY, start=False, stop=True).then_inc(ht_up.sem, 1)

            def project(i, s):
                pe.wait_ge(ht_in.sem, ht_in.at(i + 1))
                pe.wait_ge(qkt.sem, qkt.at(i - 1))
                pe.wait_ge(added.sem, added.at(i - 3))
                for m in range(3):
                    mm = pe.matmul(bank[m], HT[:, s, :], w["wqkv"][:, m * INNER:(m + 1) * INNER], start=True, stop=True)
                mm.then_inc(qkv_up.sem, 1)

            def turn_qk(i, s):
                pe.wait_ge(rot.sem, rot.at(i + 1))
                for m in range(2):
                    for c in range(PAIRS):
                        mm = pe.transpose(bank[m][:, c * P:(c + 1) * P], COS[:, s, m * INNER + c * P:m * INNER + (c + 1) * P], k.ident)
                mm.then_inc(tr_up.sem, 1)

            def scores(i, s, g):
                pe.wait_ge(qkt.sem, qkt.at(i + 1))
                pe.wait_ge((pt_a, pt_b)[g].sem, (pt_a, pt_b)[g].at(i))
                for c in range(PAIRS):
                    o = bank[3 + 2 * g + c // 2][:, 2 * P * (c % 2):2 * P * (c % 2) + KEYS]
                    pe.matmul(o, QT[:, s, g, c, :], KT[:, s, c, :], start=c % 2 == 0, stop=True, skip_group_check=True)
                for n in range(2):
                    o = bank[3 + 2 * g + n].rearrange("p (a c) -> p a c", a=2)[:, :, 0:KEYS]
                    rows = MASK[:, bass.ds((i % TPB + TPB - 1) // TPB, 1), :].broadcast_to([P, 2, KEYS])
                    mm = pe.matmul(o, k.identb, rows, start=False, stop=True, skip_group_check=True)
                mm.then_inc(s_up.sem, 1)

            def turn_probs(i, s, g):
                pe.wait_ge(probs.sem, probs.at(2 * i + g + 1))
                for c in range(PAIRS):
                    for n in range(2):
                        mm = pe.transpose(bank[3 + 2 * g + c // 2][:, P * (2 * (c % 2) + n):P * (2 * (c % 2) + n + 1)],
                                          PR[:, s, g * PAIRS + c, n * P:(n + 1) * P], k.ident)
                mm.then_inc(pt_up.sem, 1)

            def values(i, copied):
                pe.wait_ge(ht_in.sem, ht_in.at(copied))
                pe.wait_ge(pt_a.sem, pt_a.at(i + 1))
                pe.wait_ge(pt_b.sem, pt_b.at(i + 1))
                for r in range(HEADS):
                    h = 2 * (r % PAIRS) + r // PAIRS
                    for n in range(2):
                        mm = pe.matmul(bank[7][:, h * HD:(h + 1) * HD], PT[:, r, n, :], V[:, (i + 3 + n) % 4, h * HD:(h + 1) * HD],
                                       start=n == 0, stop=n == 1)
                mm.then_inc(pv_up.sem, 1)

            def turn_out(i):
                pe.wait_ge(o_in.sem, o_in.at(i + 1))
                for c in range(PAIRS):
                    mm = pe.transpose(bank[7][:, c * P:(c + 1) * P], O[:, c * P:(c + 1) * P], k.ident)
                mm.then_inc(ot_up.sem, 1)

            def output(i, copied):
                pe.wait_ge(v_in.sem, v_in.at(copied))
                pe.wait_ge(ot_in.sem, ot_in.at(i + 1))
                for c in range(PAIRS):
                    mm = pe.matmul(bank[2][:, 0:D], OT[:, c, :], w["wo"][:, c, :], start=c == 0, stop=c == PAIRS - 1)
                mm.then_inc(y_up.sem, 1)

            turn_in(0, 0)
            project(0, 0)
            turn_in(1, 1)
            pe.wait_ge(raw_in.sem, raw_in.at(1))
            pe.wait_ge(v_in.sem, v_in.at(1))
            turn_qk(0, 0)
            pe.wait_ge(qkt.sem, qkt.at(1))
            project(1, 1)
            turn_in(2, 0)

            def step(i, s, ahead, before):
                scores(i, s, 0)
                scores(i, s, 1)
                if before:
                    values(i - 1, i + 3 if ahead > 1 else TILES)
                if ahead > 1:
                    if not before:
                        pe.wait_ge(v_in.sem, v_in.at(2))
                    project(i + 2, s)
                if before:
                    turn_out(i - 1)
                turn_probs(i, s, 0)
                if ahead > 1:
                    pe.wait_ge(raw_in.sem, raw_in.at(i + 3))
                if ahead:
                    turn_qk(i + 1, 1 - s)
                if before:
                    output(i - 1, i + 3 if ahead > 1 else TILES)
                if ahead > 2:
                    turn_in(i + 3, 1 - s)
                turn_probs(i, s, 1)

            def finish(i, s):
                values(i, TILES)
                turn_out(i)
                pe.wait_ge(added.sem, added.at(i))
                output(i, TILES)
            in_steps(pe, step, finish)

        @block.scalar
        def _(act):
            def copy_h(i, s):
                act.wait_ge(ht_up.sem, ht_up.at(i + 1))
                act.wait_ge(qkv_up.sem, qkv_up.at(i - 1))
                act.copy(HT[:, s, :], bank[7][:, 0:P]).then_inc(ht_in.sem, 1)

            def take(i, s):
                act.wait_ge(qkv_up.sem, qkv_up.at(i + 1))
                act.wait_ge(ab_in.sem, ab_in.at(i - 1))
                act.copy(RAW[:, s, :], psum[:, 0:2 * BANK]).then_inc(raw_in.sem, 1)

            def take_v(i):
                act.wait_ge(pv_up.sem, pv_up.at(i - 2))
                act.sem_inc(held.sem, 1)
                act.copy(V[:, i % 4, :], bank[2]).then_inc(v_in.sem, 1)

            def square(i, s):
                act.wait_ge(raw_in.sem, raw_in.at(i + 1))
                act.wait_ge(ss_in.sem, ss_in.at(i))
                act.activation(SQ, RAW[:, s, :], ACT.Square).then_inc(sq_in.sem, 1)

            def exponential(i, s, g):
                act.wait_ge(peak.sem, peak.at(2 * i + g + 1))
                act.wait_ge(pt_up.sem, pt_up.at(2 * (i - 1) + g - 1))
                for c in range(PAIRS):
                    r = g * PAIRS + c
                    e = act.activation(PR[:, s, r, WIN:], group_of(g)[:, c, :], ACT.Exp, bias=LOW[:, s, r:r + 1],
                                       accum_out=SUM[:, s, r:r + 1])
                e.then_inc(probs.sem, 1)

            copy_h(0, 0)
            for i in range(2):
                take(i, i)
                take_v(i)
                square(i, i)
                copy_h(i + 1, 1 - i)

            def step(i, s, ahead, before):
                exponential(i, s, 0)
                exponential(i, s, 1)
                if ahead > 1:
                    take(i + 2, s)
                    take_v(i + 2)
                    square(i + 2, s)
                act.wait_ge(pt_up.sem, pt_up.at(2 * i + 1))
                act.wait_ge(pv_up.sem, pv_up.at(i))
                act.copy(PT[:, 0:4].rearrange("p r n t -> p (r n t)"), psum[:, 3 * BANK:5 * BANK]).then_inc(pt_a.sem, 1)
                if ahead > 2:
                    copy_h(i + 3, 1 - s)
                act.wait_ge(pt_up.sem, pt_up.at(2 * i + 2))
                act.copy(PT[:, 4:8].rearrange("p r n t -> p (r n t)"), psum[:, 5 * BANK:7 * BANK]).then_inc(pt_b.sem, 1)
            in_steps(act, step, lambda i, s: None)

        @block.vector
        def _(dve):
            def rotate(i, s, part):
                j = i % TPB
                raw = RAW[:, s, :].rearrange("p (m h d) -> p m h d", m=2, d=HD)
                cos = COS[:, s, :].rearrange("p (m h d) -> p m h d", m=2, d=HD)
                sin = SIN[:, s, :].rearrange("p (m h d) -> p m h d", m=2, d=HD)

                def table(a, lo, hi):
                    t = TABLE[:, bass.ds(j, 1), a, :, lo:hi].rearrange("p a m d -> p (a m) d")
                    return t.unsqueeze(2).broadcast_to([P, 2, HEADS, hi - lo])

                half = HD // 2
                if part == 0:
                    dve.wait_ge(raw_in.sem, raw_in.at(i + 1))
                    dve.wait_ge(tr_up.sem, tr_up.at(i - 1))
                    dve.tensor_tensor(cos, raw, table(0, 0, HD), ALU.mult)
                    return
                dve.tensor_tensor(sin[:, :, :, 0:half], raw[:, :, :, half:HD], table(1, 0, half), ALU.mult)
                dve.tensor_tensor(sin[:, :, :, half:HD], raw[:, :, :, 0:half], table(1, half, HD), ALU.mult).then_inc(ab_in.sem, 1)
                dve.wait_ge(sq_in.sem, sq_in.at(i + 1))
                dve.wait_ge(rn_in.sem, rn_in.at(2 * (i - 1)))
                dve.tensor_reduce(SS[:, s, :], SQ.rearrange("p (h d) -> p h d", d=HD), AX_X, ALU.add).then_inc(ss_in.sem, 1)

            def copy_qk(i, s):
                dve.wait_ge(tr_up.sem, tr_up.at(i + 1))
                dve.wait_ge(s_up.sem, s_up.at(2 * i))
                keys = bank[1].rearrange("p (c t) -> p c t", t=P)
                for a in range(2):
                    half = slice(64 * a, 64 * a + 64)
                    dve.tensor_copy(QT[half, s, a].rearrange("p c t -> p (c t)"), bank[0][half, :])
                dve.tensor_copy(KT[:, s, :, WIN:], keys)
                dve.tensor_copy(KT[:, 1 - s, :, 0:WIN], keys[:, :, P - WIN:P]).then_inc(qkt.sem, 1)

            def maximum(i, s, g):
                dve.wait_ge(s_up.sem, s_up.at(2 * i + g + 1))
                dve.tensor_reduce(LOW[:, s, g * PAIRS:(g + 1) * PAIRS], group_of(g), AX_X, ALU.max, negate=True).then_inc(peak.sem, 1)

            def normal(i, s):
                dve.wait_ge(pv_up.sem, pv_up.at(i + 1))
                dve.wait_ge(ready.sem, ready.at(i + 1))
                dve.wait_ge(ot_up.sem, ot_up.at(i))
                inv = INV[:, s, 0:HEADS].rearrange("p (a c) -> p c a", a=2).unsqueeze(3).broadcast_to([P, PAIRS, 2, HD])
                dve.tensor_tensor(O.rearrange("p (c a d) -> p c a d", a=2, d=HD), bank[7].rearrange("p (c a d) -> p c a d", a=2, d=HD),
                                  inv, ALU.mult).then_inc(o_in.sem, 1)

            def copy_out(i):
                dve.wait_ge(ot_up.sem, ot_up.at(i + 1))
                dve.wait_ge(y_up.sem, y_up.at(i))
                dve.tensor_copy(OT.rearrange("p c t -> p (c t)"), bank[7]).then_inc(ot_in.sem, 1)

            def add(i):
                dve.wait_ge(y_up.sem, y_up.at(i + 1))
                z = k.Zpad[:, bass.ds(k.zindex(i), 1), :].rearrange("p a d -> p (a d)")
                dve.tensor_tensor(z, z, bank[2][:, 0:D], ALU.add).then_inc(added.sem, 1)

            rotate(0, 0, 0)
            rotate(0, 0, 1)
            copy_qk(0, 0)
            rotate(1, 1, 0)
            rotate(1, 1, 1)

            def step(i, s, ahead, before):
                maximum(i, s, 0)
                maximum(i, s, 1)
                if before:
                    normal(i - 1, 1 - s)
                    copy_out(i - 1)
                if ahead > 1:
                    rotate(i + 2, s, 0)
                if ahead:
                    copy_qk(i + 1, 1 - s)
                if ahead > 1:
                    rotate(i + 2, s, 1)
                if before:
                    add(i - 1)
                dve.wait_ge(probs.sem, probs.at(2 * i + 2))
                dve.reciprocal(INV[:, s, 0:HEADS], SUM[:, s, 0:HEADS]).then_inc(ready.sem, 1)

            def finish(i, s):
                normal(i, s)
                copy_out(i)
                add(i)
            in_steps(dve, step, finish)

        @block.gpsimd
        def _(pool):
            def fetch(i, s):
                pool.wait_ge(ht_up.sem, ht_up.at(i - 1))
                pool.sem_inc(held.sem, 1)
                flat = k.Zpad.rearrange("p t d -> p (t d)")
                pool.tensor_copy(ZS[:, s, :], flat[:, bass.ds(k.zindex(i) * D - 64, KEYS)]).then_inc(zs_in.sem, 1)

            def norm(i, s):
                pool.wait_ge(ab_in.sem, ab_in.at(i + 1))
                pool.tensor_tensor(COS[:, s, :], COS[:, s, :], SIN[:, s, :], ALU.add).then_inc(ready2.sem, 1)
                pool.wait_ge(ss_in.sem, ss_in.at(i + 1))
                pool.tensor_tensor(RN[:, s, :], SS[:, s, :], k.minus_half[:, 0:2 * HEADS], ALU.pow).then_inc(rn_in.sem, 1)
                pool.wait_ge(rn_in.sem, rn_in.at(2 * i + 1))
                pool.sem_inc(held.sem, 1)
                pool.tensor_scalar(RN[:, s, :], RN[:, s, :], 1e12, 0.0, ALU.min, ALU.max).then_inc(rn_in.sem, 1)
                pool.wait_ge(ready2.sem, ready2.at(i + 1))
                pool.wait_ge(rn_in.sem, rn_in.at(2 * i + 2))
                heads = COS[:, s, :].rearrange("p (h d) -> p h d", d=HD)
                pool.tensor_tensor(heads, heads, RN[:, s, :].unsqueeze(2).broadcast_to([P, 2 * HEADS, HD]), ALU.mult).then_inc(
                    rot.sem, 1)

            for i in range(3):
                fetch(i, i % 2)
            norm(0, 0)
            norm(1, 1)

            def step(i, s, ahead, before):
                if ahead > 2:
                    fetch(i + 3, 1 - s)
                if ahead > 1:
                    norm(i + 2, s)
            in_steps(pool, step, lambda i, s: None)

    for s in (zs_in, ht_up, ht_in, qkv_up, raw_in, v_in, sq_in, ss_in, ab_in, rot, tr_up, qkt, pt_a, pt_b, pv_up,
              o_in, ot_up, ot_in, y_up, added, ready, ready2):
        s.passed(TILES)
    for s in (peak, rn_in, s_up, probs, pt_up):
        s.passed(2 * TILES)


LAYER_LOADS = 14


def load_layer(k, sp, depth, loaded):
    d, w, f = k.dram, k.layer, "L1_ffn_"
    HID = d[f + "w2"].shape[1]
    whole = HID // P
    rest = HID - whole * P
    pairs = [
        (w["wqkv"], d[f + "wqkv"][depth]),
        (w["wo"], d[f + "wo"][depth].rearrange("(c p) d -> p c d", p=P)),
        (w["w1"], d[f + "w1"][depth].rearrange("p (m h) -> p m h", m=2)),
        (w["w2"][:, 0:whole, :], d[f + "w2"][depth][0:whole * P].rearrange("(c p) d -> p c d", p=P)),
        (w["w2"][0:rest, whole, :], d[f + "w2"][depth][whole * P:HID]),
        (w["w2"][rest:rest + 1, whole, :], d[f + "b2"][depth].rearrange("(a d) -> a d", a=1)),
        (w["ln"][:, 0:1], d[f + "ln_g"][depth].rearrange("(p a) -> p a", a=1)),
        (w["ln"][:, 1:2], d[f + "ln_b"][depth].rearrange("(p a) -> p a", a=1))]
    for m in range(2):
        for c, (a, r) in enumerate(halves(HID, P)):
            pairs.append((w["b1"][0:r, m, c:c + 1], d[f + "b1"][depth][m * HID + a:m * HID + a + r].rearrange("(p a) -> p a", a=1)))
    assert len(pairs) == LAYER_LOADS
    for into, source in pairs:
        sp.dma_start(into, source).then_inc(loaded.sem, 16)


def gated_units(k, depth):
    nc, bank, w = k.nc, k.bank, k.layer
    EPS = 1e-5
    UNIT = 4
    UNITS = TILES // UNIT
    HID = w["w1"].shape[2]
    CHUNKS = halves(HID, P)
    NC = len(CHUNKS)
    A = k.arena
    HN = A[0][:, 0:2 * BANK].rearrange("p (s j d) -> p s j d", s=2, d=D)
    HNT = A[0][:, 2 * BANK:4 * BANK].rearrange("p (s t) -> p s t", s=2)
    GL = A[1][:, 0:2 * BANK].rearrange("p (s t) -> p s t", s=2)
    PROD = A[2][:, 0:2 * NC * BANK].rearrange("p (s c t) -> p s c t", s=2, c=NC)
    small = k.arena6[:, 0:128]
    STATS = small[:, 0:24].rearrange("p (j c) -> p j c", j=UNIT)
    MV = small[:, 32:48].rearrange("p (s j c) -> p s j c", s=2, j=UNIT)
    RSTD = small[:, 48:56].rearrange("p (s j) -> p s j", s=2)
    VAR = small[:, 56:64].rearrange("p (s j) -> p s j", s=2)
    names = ("h_up", "stats", "moments", "rstd", "hn", "t_up", "hnt", "ag_up", "gelu", "prod", "y_up", "added", "held")
    h_up, stats, moments, rstd, hn, t_up, hnt, ag_up, gelu, prod, y_up, added, held = [k.count("units_" + n) for n in names]
    credited = (hn, hnt, prod, gelu, y_up, added, t_up, ag_up, h_up, rstd, moments, stats)
    CREDIT = 8
    for s in credited:
        s.passed(CREDIT)
    with nc.Block() as block:
        @block.sync
        def _(sp):
            for s in credited:
                sp.sem_inc(s.sem, CREDIT)

        @block.vector
        def _(dve):
            dve.memset(PROD, 1.0)

    with nc.Block() as block:
        @block.tensor
        def _(pe):
            def shifted(u):
                pe.wait_ge(hn.sem, hn.at(u))
                for j in range(UNIT):
                    i = u * UNIT + j
                    z = k.zindex(i)
                    o = bank[0][:, j * P:(j + 1) * P]
                    pe.matmul(o[:, 0:64], k.ident, k.Zpad[:, z, 0:64], start=j == 0, stop=True, skip_group_check=True)
                    pe.matmul(o[:, 64:P], k.w["shift"], k.Zpad[:, z, 64:P], start=False, stop=False, skip_group_check=True)
                    mm = pe.matmul(o[:, 64:P], k.w["carry"], k.Zpad[:, z - 1, 64:P], start=False, stop=True, skip_group_check=True)
                mm.then_inc(h_up.sem, 1)

            def turn(u, s):
                pe.wait_ge(hn.sem, hn.at(u + 1))
                pe.wait_ge(hnt.sem, hnt.at(u))
                for j in range(UNIT):
                    mm = pe.transpose(bank[1][:, j * P:(j + 1) * P], HN[:, s, j, :], k.ident)
                mm.then_inc(t_up.sem, 1)

            shifted(0)
            turn(0, 0)
            shifted(1)

            def step(u, s, ahead):
                pe.wait_ge(hnt.sem, hnt.at(u + 1))
                for c, (a, r) in enumerate(CHUNKS):
                    pe.wait_ge(prod.sem, prod.at(u * NC + c - 1))
                    for m in range(2):
                        mm = pe.matmul(bank[2 + 2 * ((s + c) % 2) + m][0:r, :], w["w1"][:, m, a:a + r], HNT[:, s, :], start=True, stop=True)
                    mm.then_inc(ag_up.sem, 1)
                if ahead > 1:
                    shifted(u + 2)
                if ahead:
                    turn(u + 1, 1 - s)
                pe.wait_ge(prod.sem, prod.at((u + 1) * NC))
                pe.wait_ge(added.sem, added.at(u))
                for j in range(UNIT):
                    for c, (a, r) in enumerate(CHUNKS):
                        r += c == NC - 1
                        mm = pe.matmul(bank[6][:, j * P:(j + 1) * P], PROD[0:r, s, c, j * P:(j + 1) * P], w["w2"][0:r, c, :],
                                       start=c == 0, stop=c == NC - 1)
                mm.then_inc(y_up.sem, 1)
            in_pairs(pe, UNITS, step)

        @block.scalar
        def _(act):
            def affine(u, s):
                act.wait_ge(t_up.sem, t_up.at(u + 1))
                act.wait_ge(ag_up.sem, ag_up.at(NC * (u - 1)))
                act.activation(HNT[:, s, :], bank[1], ACT.Identity, scale=w["ln"][:, 0:1], bias=w["ln"][:, 1:2]).then_inc(hnt.sem, 1)

            affine(0, 0)

            def step(u, s, ahead):
                for c, (a, r) in enumerate(CHUNKS):
                    n = u * NC + c
                    act.wait_ge(ag_up.sem, ag_up.at(n + 1))
                    act.wait_ge(prod.sem, prod.at(n - 1))
                    act.activation(GL[0:r, (s + c) % 2, :], bank[3 + 2 * ((s + c) % 2)][0:r, :], ACT.Gelu,
                                   bias=w["b1"][0:r, 1, c:c + 1]).then_inc(gelu.sem, 1)
                if ahead:
                    affine(u + 1, 1 - s)
            in_pairs(act, UNITS, step)

        @block.vector
        def _(dve):
            def normalise(u, s):
                dve.wait_ge(h_up.sem, h_up.at(u + 1))
                for j in range(UNIT):
                    st = dve.bn_stats(STATS[:, j, :], bank[0][:, j * P:(j + 1) * P])
                st.then_inc(stats.sem, 1)
                dve.wait_ge(stats.sem, stats.at(u + 1))
                dve.wait_ge(t_up.sem, t_up.at(u - 1))
                dve.sem_inc(held.sem, 1)
                for j in range(UNIT):
                    mv = dve.bn_aggr(MV[:, s, j, :], STATS[:, j, :])
                mv.then_inc(moments.sem, 1)
                dve.wait_ge(rstd.sem, rstd.at(2 * u + 2))
                for j in range(UNIT):
                    h = dve.tensor_scalar(HN[:, s, j, :], bank[0][:, j * P:(j + 1) * P], MV[:, s, j, 0:1], RSTD[:, s, j:j + 1],
                                          ALU.subtract, ALU.mult)
                h.then_inc(hn.sem, 1)

            normalise(0, 0)
            normalise(1, 1)

            def step(u, s, ahead):
                for c, (a, r) in enumerate(CHUNKS):
                    dve.wait_ge(gelu.sem, gelu.at(u * NC + c + 1))
                    dve.wait_ge(y_up.sem, y_up.at(u - 1))
                    dve.scalar_tensor_tensor(out=PROD[0:r, s, c, :], in0=bank[2 + 2 * ((s + c) % 2)][0:r, :],
                                             scalar=w["b1"][0:r, 0, c:c + 1], in1=GL[0:r, (s + c) % 2, :], op0=ALU.add,
                                             op1=ALU.mult).then_inc(prod.sem, 1)
                if ahead > 1:
                    normalise(u + 2, s)
                dve.wait_ge(y_up.sem, y_up.at(u + 1))
                z = k.Zpad[:, bass.ds(k.zindex(u * UNIT), UNIT), :]
                dve.tensor_tensor(z, z, bank[6].rearrange("p (j d) -> p j d", d=D), ALU.add).then_inc(added.sem, 1)
            in_pairs(dve, UNITS, step)

        @block.gpsimd
        def _(pool):
            with pool.Fori(0, UNITS // 2) as v:
                for s in range(2):
                    u = v * 2 + s
                    pool.wait_ge(moments.sem, moments.at(u + 1))
                    pool.sem_inc(held.sem, 1)
                    pool.tensor_scalar(VAR[:, s, :], MV[:, s, :, 1], 1.0, EPS, ALU.mult, ALU.add).then_inc(rstd.sem, 1)
                    pool.wait_ge(rstd.sem, rstd.at(2 * u + 1))
                    pool.tensor_tensor(RSTD[:, s, :], VAR[:, s, :], k.minus_half[:, 0:UNIT], ALU.pow).then_inc(rstd.sem, 1)

    for s in (h_up, stats, moments, hn, t_up, hnt, y_up, added):
        s.passed(UNITS)
    for s in (ag_up, gelu, prod):
        s.passed(UNITS * NC)
    rstd.passed(2 * UNITS)



def routed_ffn(k):
    nc, w, bank, psum = k.nc, k.w, k.bank, k.psum
    CAP, HEADS, HD, TOP = 64, 16, 8, 8
    T = BATCH * CAP // P
    PER = P // CAP
    N = BATCH * CAP
    EPS = 1e-6
    SCALE = float(1.0 / np.sqrt(HD))
    DFF = w["f_upT"].shape[2]
    CHUNKS = halves(DFF, P)
    GONE = -3.0e38
    A = k.arena
    layernorm(k)
    FT = A[0]
    HOTR = A[1][:, 0:T * SEQ].rearrange("p (t s) -> p t s", t=T)
    HOTT = A[1][:, T * SEQ:2 * T * SEQ].rearrange("p (t j r) -> p t j r", t=T, j=TPB)
    IOTA = A[2][:, 0:SEQ]
    SCORE = A[2][0:BATCH, SEQ:3 * SEQ].rearrange("p (s t) -> p s t", s=2)
    MASK = A[2][:, 3 * SEQ:3 * SEQ + BANK // 2].bitcast(BF16)
    QB = A[3].rearrange("p (b h q) -> p b h q", b=BATCH, h=HEADS)
    E = A[4][:, 0:BATCH * BANK].rearrange("p (b c t) -> p b c t", b=BATCH, c=TOP)
    PT = A[5][0:CAP, :].rearrange("p (b c r) -> p b c r", b=BATCH, c=HEADS // 2)
    at = [0]

    def place(*shape):
        n = int(np.prod(shape))
        names = "abcd"[:len(shape)]
        flat = k.arena6[:, at[0]:at[0] + n]
        at[0] += n
        return flat.rearrange(f"p ({' '.join(names)}) -> p {' '.join(names)}", **dict(zip(names, shape)))

    XS, XA, H, O, S2, H2, Y, SQ = (place(T, D) for _ in range(8))
    HT, QT, KT, OT, H2T = (place(N) for _ in range(5))
    V = place(BATCH, D)[0:CAP]
    SIL, PROD = place(len(CHUNKS), N), place(len(CHUNKS), N)
    HEADMASK = place(HEADS)
    IDX = place(T * CAP)[0:BATCH]
    IDXT = place(T)
    VALS = place(CAP)[0:BATCH]
    IDXU = place(CAP).bitcast(U32)[0:BATCH]
    SS, MS, RS = place(2, T), place(2, T), place(2, T)
    PEAK, SUM, INV = place(BATCH, TOP), place(BATCH, TOP), place(BATCH, TOP)
    names = ("loaded", "resid", "routed", "score", "rank", "idx", "idx_up", "idxT", "hotr", "hott_up", "hott", "picked", "xs", "ss",
             "rs", "h", "h_up", "ht", "qk_up", "qk", "v_up", "v", "qb", "s_up", "soft", "exp", "e", "pt_up", "pt", "pv", "o", "ot_up",
             "ot", "xa_up", "xa", "up", "sil", "prod", "down", "y", "spread", "added")
    c = {n: k.count("route_" + n) for n in names}

    def inc(ins, name):
        return ins.then_inc(c[name].sem, 16 if name == "loaded" else 1)

    def wait(eng, name, n):
        eng.wait_ge(c[name].sem, c[name].at(n))

    turn_stream(k, FT, SEQ, 0)
    with nc.Block() as block:
        @block.sync
        def _(sp):
            d = k.dram
            sp.dma_start(IOTA, d["c_iota"].partition_broadcast(P)).then_inc(c["loaded"].sem, 16)
            sp.dma_start(MASK, d["c_ranks"]).then_inc(c["loaded"].sem, 16)
            sp.dma_start(HEADMASK, d["c_heads"]).then_inc(c["loaded"].sem, 16)
            wait(sp, "loaded", 48)

        @block.gpsimd
        def _(pool):
            for b in range(BATCH):
                inc(pool.tensor_tensor(k.xpart(b), k.xpart(b), k.zpart(b), ALU.add), "resid")
            for n in range(2):
                wait(pool, "ss", T * (n + 1))
                inc(pool.tensor_scalar(MS[:, n, :], SS[:, n, :], 1.0 / D, EPS, ALU.mult, ALU.add), "rs")
                wait(pool, "rs", 2 * n + 1)
                inc(pool.tensor_tensor(RS[:, n, :], MS[:, n, :], k.minus_half[:, 0:T], ALU.pow), "rs")

        @block.tensor
        def _(pe):
            for h in range(2):
                for b in range(BATCH):
                    mm = pe.matmul(bank[h][0:BATCH, :], w["router4"][:, b, :], FT[:, b * SEQ + h * BANK:b * SEQ + (h + 1) * BANK],
                                   start=b == 0, stop=b == BATCH - 1)
            inc(mm, "routed")
            wait(pe, "idx", 2)
            inc(pe.matmul(bank[2][:, 0:BATCH], IDX, k.ident[0:BATCH, 0:BATCH], start=True, stop=True), "idx_up")
            for t in range(T):
                wait(pe, "hotr", t + 1)
                for j in range(TPB):
                    mm = pe.transpose(bank[4 + 2 * t + j // 4][:, (j % 4) * P:(j % 4 + 1) * P], HOTR[:, t, j * P:(j + 1) * P], k.ident)
                inc(mm, "hott_up")
            for t in range(T):
                wait(pe, "hott", t + 1)
                for i in range(PER):
                    for j in range(TPB):
                        mm = pe.matmul(bank[t][CAP * i:CAP * (i + 1), 0:D], HOTT[:, t, j, CAP * i:CAP * (i + 1)],
                                       k.Zpad[:, k.zindex((t * PER + i) * TPB + j), :], start=j == 0, stop=j == TPB - 1)
                inc(mm, "picked")
            for t in range(T):
                wait(pe, "h", t + 1)
                inc(pe.transpose(bank[2][:, t * P:(t + 1) * P], H[:, t, :], k.ident), "h_up")
            wait(pe, "ht", 1)
            for m in range(2):
                inc(pe.matmul(bank[3 + m][:, 0:N], w["qkvT"][:, m * D:(m + 1) * D], HT, start=True, stop=True), "qk_up")
            for b in range(BATCH):
                mm = pe.matmul(bank[5][0:CAP, b * D:(b + 1) * D], HT[:, b * CAP:(b + 1) * CAP], w["qkvT"][:, 2 * D:3 * D],
                               start=True, stop=True)
            inc(mm, "v_up")
            wait(pe, "qk", 2)
            wait(pe, "v", 1)
            wait(pe, "xs", T)
            for b in range(BATCH):
                wait(pe, "qb", b + 1)
                for n in range(HEADS // 2):
                    pe.matmul(bank[b][:, n * CAP:(n + 1) * CAP], QB[:, b, 2 * n:2 * n + 2, :].rearrange("p h q -> p (h q)"),
                              KT[:, b * CAP:(b + 1) * CAP], start=n == 0, stop=True, skip_group_check=True)
                inc(pe.matmul(bank[b], k.identb, MASK, start=False, stop=True, skip_group_check=True), "s_up")
            for b in range(BATCH):
                wait(pe, "e", b + 1)
                if b >= 2:
                    wait(pe, "pt", b - 1)
                for n in range(HEADS // 2):
                    mm = pe.transpose(bank[4 + 2 * (b % 2) + n // 4][0:CAP, (n % 4) * P:(n % 4 + 1) * P], E[:, b, n, :], k.ident)
                inc(mm, "pt_up")
            for b in range(BATCH):
                wait(pe, "pt", b + 1)
                for h in range(HEADS):
                    mm = pe.matmul(bank[b // PER][CAP * (b % PER):CAP * (b % PER + 1), h * HD:(h + 1) * HD],
                                   PT[:, b, h // 2, CAP * (h % 2):CAP * (h % 2 + 1)], V[:, b, h * HD:(h + 1) * HD], start=True, stop=True)
                inc(mm, "pv")
            for t in range(T):
                wait(pe, "o", t + 1)
                inc(pe.transpose(bank[2][:, t * P:(t + 1) * P], O[:, t, :], k.ident), "ot_up")
            wait(pe, "ot", 1)
            for t in range(T):
                inc(pe.matmul(bank[3][:, t * P:(t + 1) * P], OT[:, t * P:(t + 1) * P], w["f_outT"], start=True, stop=True), "xa_up")
            for t in range(T):
                wait(pe, "h", T + t + 1)
                inc(pe.transpose(bank[2][:, t * P:(t + 1) * P], H2[:, t, :], k.ident), "h_up")
            wait(pe, "ht", 2)
            for n, (a, r) in enumerate(CHUNKS):
                for m in range(2):
                    mm = pe.matmul(bank[4 + n][0:r, m * N:(m + 1) * N], w["f_upT"][:, m, a:a + r], H2T, start=True, stop=True)
                inc(mm, "up")
            for t in range(T):
                wait(pe, "prod", len(CHUNKS))
                for n, (a, r) in enumerate(CHUNKS):
                    mm = pe.matmul(bank[t][:, 0:D], PROD[0:r, n, t * P:(t + 1) * P], w["f_downT"][0:r, n, :], start=n == 0,
                                   stop=n == len(CHUNKS) - 1)
                inc(mm, "down")
            for b in range(BATCH):
                wait(pe, "y", b // PER + 1)
                wait(pe, "prod", len(CHUNKS))
                if b >= 3:
                    wait(pe, "added", b - 2)
                rows = slice(CAP * (b % PER), CAP * (b % PER + 1))
                for j in range(TPB):
                    mm = pe.matmul(bank[2 + 2 * (b % 3) + j // 4][:, (j % 4) * P:(j % 4 + 1) * P], HOTR[rows, b // PER, j * P:(j + 1) * P],
                                   Y[rows, b // PER, :], start=True, stop=True)
                inc(mm, "spread")

        @block.scalar
        def _(act):
            wait(act, "routed", 1)
            inc(act.copy(SCORE[:, 0, :], psum[0:BATCH, 0:SEQ]), "score")
            for t in range(T):
                wait(act, "hott_up", t + 1)
                inc(act.copy(HOTT[:, t].rearrange("p j r -> p (j r)"), psum[:, (4 + 2 * t) * BANK:(6 + 2 * t) * BANK]), "hott")
            for t in range(T):
                wait(act, "xs", t + 1)
                inc(act.activation(SQ[:, t, :], XS[:, t, :], ACT.Square, accum_out=SS[:, 0, t:t + 1]), "ss")
            wait(act, "h_up", T)
            inc(act.activation(HT, bank[2][:, 0:N], ACT.Copy, scale=w["f_g1"]), "ht")
            wait(act, "qk_up", 2)
            inc(act.copy(KT, bank[4][:, 0:N]), "qk")
            wait(act, "v_up", 1)
            inc(act.copy(V.rearrange("p b d -> p (b d)"), bank[5][0:CAP, :]), "v")
            for b in range(BATCH):
                wait(act, "soft", 2 * b + 2)
                e = E[:, b].rearrange("p c t -> p (c t)")
                inc(act.activation(e, e, ACT.Exp, scale=SCALE), "exp")
            for b in range(BATCH):
                wait(act, "pt_up", b + 1)
                first = 4 + 2 * (b % 2)
                inc(act.copy(PT[:, b].rearrange("p c r -> p (c r)"), psum[0:CAP, first * BANK:(first + 2) * BANK]), "pt")
            for t in range(T):
                wait(act, "xa", 2 * t + 2)
                inc(act.activation(SQ[:, t, :], S2[:, t, :], ACT.Square, accum_out=SS[:, 1, t:t + 1]), "ss")
            wait(act, "h_up", 2 * T)
            inc(act.activation(H2T, bank[2][:, 0:N], ACT.Copy, scale=w["f_g2"]), "ht")
            for n, (a, r) in enumerate(CHUNKS):
                wait(act, "up", n + 1)
                inc(act.activation(SIL[0:r, n, :], bank[4 + n][0:r, 0:N], ACT.Silu), "sil")

        @block.vector
        def _(dve):
            wait(dve, "score", 1)
            wait(dve, "loaded", 48)
            n = 0
            for r in range(CAP // TOP):
                cur, new = SCORE[:, r % 2, :], SCORE[:, (r + 1) % 2, :]
                part = slice(r * TOP, (r + 1) * TOP)
                if r:
                    wait(dve, "rank", 3 * r)
                inc(dve.max(VALS[:, part], cur), "rank")
                wait(dve, "rank", 3 * r + 1)
                inc(dve.max_index(IDXU[:, part], VALS[:, part], cur), "rank")
                inc(dve.match_replace(new, VALS[:, part], cur, GONE), "rank")
            wait(dve, "rank", 3 * CAP // TOP)
            for i in range(PER):
                inc(dve.tensor_copy(IDX[:, i * CAP:(i + 1) * CAP], IDXU), "idx")
            wait(dve, "idx_up", 1)
            for i in range(PER):
                rows = slice(i * CAP, (i + 1) * CAP)
                inc(dve.tensor_copy(IDXT[rows, :], bank[2][rows, i:BATCH:PER]), "idxT")
            wait(dve, "idxT", PER)
            for t in range(T):
                inc(dve.tensor_scalar(HOTR[:, t, :], IOTA, IDXT[:, t:t + 1], None, ALU.is_equal), "hotr")
            for t in range(T):
                wait(dve, "picked", t + 1)
                inc(dve.tensor_copy(XS[:, t, :], bank[t][:, 0:D]), "xs")
            wait(dve, "rs", 2)
            wait(dve, "xs", T)
            for t in range(T):
                inc(dve.tensor_scalar(H[:, t, :], XS[:, t, :], RS[:, 0, t:t + 1], None, ALU.mult), "h")
            wait(dve, "qk_up", 2)
            inc(dve.tensor_copy(QT, bank[3][:, 0:N]), "qk")
            wait(dve, "qk", 2)
            for b in range(BATCH):
                inc(dve.tensor_tensor(QB[:, b], QT[:, b * CAP:(b + 1) * CAP].unsqueeze(1).broadcast_to([P, HEADS, CAP]),
                                      HEADMASK.unsqueeze(2).broadcast_to([P, HEADS, CAP]), ALU.mult), "qb")
            for b in range(BATCH):
                s = bank[b].rearrange("p (c t) -> p c t", c=TOP)
                wait(dve, "s_up", b + 1)
                inc(dve.tensor_reduce(PEAK[:, b, :], s, AX_X, ALU.max), "soft")
                wait(dve, "soft", 2 * b + 1)
                inc(dve.tensor_tensor(E[:, b], s, PEAK[:, b, :].unsqueeze(2).broadcast_to([P, TOP, CAP]), ALU.subtract), "soft")
            for b in range(BATCH):
                wait(dve, "exp", b + 1)
                inc(dve.tensor_reduce(SUM[:, b, :], E[:, b], AX_X, ALU.add), "idx")
                wait(dve, "idx", 2 + 2 * b + 1)
                inc(dve.reciprocal(INV[:, b, :], SUM[:, b, :]), "idx")
                wait(dve, "idx", 2 + 2 * b + 2)
                inc(dve.tensor_tensor(E[:, b], E[:, b], INV[:, b, :].unsqueeze(2).broadcast_to([P, TOP, CAP]), ALU.mult), "e")
            for t in range(T):
                wait(dve, "pv", PER * (t + 1))
                inc(dve.tensor_copy(O[:, t, :], bank[t][:, 0:D]), "o")
            wait(dve, "ot_up", T)
            inc(dve.tensor_copy(OT, bank[2][:, 0:N]), "ot")
            wait(dve, "xa_up", T)
            for t in range(T):
                part = bank[3][:, t * P:(t + 1) * P]
                inc(dve.tensor_copy(XA[:, t, :], part), "xa")
                inc(dve.tensor_tensor(S2[:, t, :], XS[:, t, :], part, ALU.add), "xa")
            wait(dve, "rs", 4)
            wait(dve, "xa", 2 * T)
            for t in range(T):
                inc(dve.tensor_scalar(H2[:, t, :], S2[:, t, :], RS[:, 1, t:t + 1], None, ALU.mult), "h")
            for n, (a, r) in enumerate(CHUNKS):
                wait(dve, "sil", n + 1)
                inc(dve.tensor_tensor(PROD[0:r, n, :], SIL[0:r, n, :], bank[4 + n][0:r, N:2 * N], ALU.mult), "prod")
            for t in range(T):
                wait(dve, "down", t + 1)
                inc(dve.tensor_tensor(Y[:, t, :], XA[:, t, :], bank[t][:, 0:D], ALU.add), "y")
            wait(dve, "resid", BATCH)
            for b in range(BATCH):
                wait(dve, "spread", b + 1)
                first = 2 + 2 * (b % 3)
                inc(dve.tensor_tensor(k.xpart(b), k.xpart(b), psum[:, first * BANK:(first + 2) * BANK].rearrange(
                    "p (j d) -> p j d", d=D), ALU.add), "added")

    for n, total in (("loaded", 48), ("resid", BATCH), ("routed", 1), ("score", 1), ("rank", 3 * CAP // TOP), ("idx", 2 + 2 * BATCH),
                     ("idx_up", 1), ("idxT", PER), ("hotr", T), ("hott_up", T), ("hott", T), ("picked", T), ("xs", T), ("ss", 2 * T),
                     ("rs", 4), ("h", 2 * T), ("h_up", 2 * T), ("ht", 2), ("qk_up", 2), ("qk", 2), ("v_up", 1), ("v", 1),
                     ("qb", BATCH), ("s_up", BATCH), ("soft", 2 * BATCH), ("exp", BATCH), ("e", BATCH), ("pt_up", BATCH),
                     ("pt", BATCH), ("pv", BATCH), ("o", T), ("ot_up", T), ("ot", 1), ("xa_up", T), ("xa", 2 * T),
                     ("up", len(CHUNKS)), ("sil", len(CHUNKS)), ("prod", len(CHUNKS)), ("down", T), ("y", T), ("spread", BATCH),
                     ("added", BATCH)):
        c[n].passed(total)



def load(k):
    nc, d, w = k.nc, k.dram, k.w
    loads = []

    def keep(name, shape, *pairs, dt=F32):
        t = k.mem.enter_context(nc.sbuf_tensor("w_" + name, list(shape), dt))
        w[name] = t[tuple(slice(None) for _ in shape)]
        for into, source in pairs:
            loads.append((w[name] if into is None else t[into], source))
        return t

    def col(ap):
        return ap.rearrange("(p a) -> p a", a=1)

    def dup(name, ap):
        keep(name, (P, 1), ((slice(0, 64),), col(ap)), ((slice(64, 128),), col(ap)))

    x = k.dram["L0_attn_a_x"].rearrange("b s d -> (b s) d").rearrange("(t p) d -> p t d", p=P)
    for b in range(BATCH):
        loads.append((k.X[:, b * TPB:(b + 1) * TPB, :], x[:, b * TPB:(b + 1) * TPB, :]))
    keep("ident", (P, P), (None, d["c_ident"]))
    keep("identb", (P, P), (None, d["c_identb"]), dt=BF16)
    k.ident, k.identb = w["ident"], w["identb"]
    a = "L0_attn_a_"
    keep("W_up", (P, P), (None, d[a + "W_up"]))
    keep("up_left2", (P, P), ((slice(None), slice(0, 64)), d[a + "W_up"][:, 0:64]),
         ((slice(None), slice(64, 128)), d[a + "W_up"][:, 0:64]))
    keep("ln_gamma", (P, 1), (None, col(d[a + "ln_gamma"])))
    keep("ln_beta", (P, 1), (None, col(d[a + "ln_beta"])))
    dup("b_left2", d[a + "b_up"][0:64])
    keep("b_right", (64, 1), (None, col(d[a + "b_up"][64:128])))
    cw = d[a + "conv_w"].rearrange("d a c -> d (a c)")
    keep("conv_w2", (P, 3), ((slice(0, 64),), cw), ((slice(64, 128),), cw))
    dup("conv_b2", d[a + "conv_b"])
    dup("b_delta2", d[a + "b_delta"])
    keep("delta2", (64, P), ((slice(None), slice(0, 64)), d[a + "W_delta"]), ((slice(None), slice(64, 128)), d[a + "W_delta"]))
    keep("bc3", (64, 2, 96), *[((slice(None), m, slice(32 * r, 32 * r + 32)), d[a + n]) for m, n in enumerate(("W_B", "W_C"))
                               for r in range(3)])
    al = d[a + "A_log"].rearrange("d (n j) -> n d j", n=2)
    keep("A1", (P, 16), ((slice(0, 64),), al[0]), ((slice(64, 128),), al[1]))
    keep("D1col", (64, 1), (None, col(d[a + "D"])))
    keep("D1", (P, 64))
    keep("fold", (P, 64), (None, d["c_fold"]))
    keep("W_down", (64, P), (None, d[a + "W_down"]))
    keep("b_down_row", (P, P), (None, d[a + "b_down"].partition_broadcast(P)))
    keep("minus_half", (P, TILES))
    k.minus_half = w["minus_half"]
    keep_later(k, keep, loads, col)

    loaded, a_exp, made = k.count("loaded"), k.count("a_exp"), k.count("made")
    with nc.Block() as block:
        engines = ((block.sync, 0), (block.scalar, 1))

        def issue(eng, n):
            for into, source in loads[n::2]:
                eng.dma_start(into, source).then_inc(loaded.sem, 16)

        @block.sync
        def _(sp):
            issue(sp, 0)

        @block.scalar
        def _(act):
            issue(act, 1)
            act.wait_ge(loaded.sem, loaded.at(16 * len(loads)))
            act.activation(w["A1"], w["A1"], ACT.Exp).then_inc(a_exp.sem, 1)
            if 7 in STAGES:
                act.activation(w["A7"], w["A7"], ACT.Exp).then_inc(a_exp.sem, 1)

        @block.vector
        def _(dve):
            dve.memset(w["minus_half"], -0.5)
            dve.memset(k.Zpad[:, 0:TILES + BATCH + 1:TPB + 1, :], 0.0)
            dve.wait_ge(loaded.sem, loaded.at(16 * len(loads)))
            dve.memset(w["D1"][64:P, :], 0.0)
            dve.tensor_scalar(w["D1"][0:64, :], k.ident[0:64, 0:64], w["D1col"], None, ALU.mult)
            dve.wait_ge(a_exp.sem, a_exp.at(1))
            dve.tensor_scalar(w["A1"], w["A1"], -1.0, None, ALU.mult)
            if 7 in STAGES:
                for hf in range(2):
                    dve.tensor_scalar(w["D7"][:, hf, :], k.ident, w["D7col"][:, hf:hf + 1], None, ALU.mult)
                dve.wait_ge(a_exp.sem, a_exp.at(2))
                dve.tensor_scalar(w["A7"], w["A7"], -1.0, None, ALU.mult)

        @block.gpsimd
        def _(pool):
            pool.wait_ge(loaded.sem, loaded.at(16 * len(loads)))
    turn_weights(k)


def store(k):
    stored = k.count("stored")
    out = k.out.rearrange("b s d -> (b s) d").rearrange("(t p) d -> p t d", p=P)
    with k.nc.Block() as block:
        @block.sync
        def _(sp):
            for b in range(BATCH):
                part = slice(b * TPB, (b + 1) * TPB)
                sp.dma_start(out[:, part, :], k.X[:, part, :]).then_inc(stored.sem, 16)
            sp.wait_ge(stored.sem, 16 * BATCH)


def halves(n, size):
    return [(i, min(size, n - i)) for i in range(0, n, size)]


def keep_later(k, keep, loads, col):
    d, w = k.dram, k.w
    k.turn = turn = []
    natural = k.arena[1]
    at = [0]

    def turned(source, *pairs):
        r, c = source.shape
        place = natural[0:r, at[0]:at[0] + c]
        at[0] += c
        loads.append((place, source))
        turn.append((place, pairs or None))
        return len(turn) - 1

    def into(n, *pairs):
        turn[n] = (turn[n][0], pairs)

    full = slice(None)
    if {2, 4} & set(STAGES):
        f = "L0_ffn_"
        keep("qkvT", (P, 3 * D))
        for i, r in halves(3 * D, P):
            into(turned(d[f + "W_qkv"][i:i + r, :]), (w["qkvT"][:, i:i + r], full))
        keep("f_outT", (P, D))
        into(turned(d[f + "W_out"]), (w["f_outT"], full))
        DFF = d[f + "W1"].shape[0]
        keep("f_upT", (P, 2, DFF))
        for m, name in enumerate(("W1", "W2")):
            for i, r in halves(DFF, P):
                into(turned(d[f + name][i:i + r, :]), (w["f_upT"][:, m, i:i + r], full))
        keep("f_downT", (P, 3, D))
        for n, (i, r) in enumerate(halves(DFF, P)):
            into(turned(d[f + "W3"][:, i:i + r]), (w["f_downT"][0:r, n, :], full))
        keep("router", (P, 1), (None, col(d[f + "w_router"])))
        keep("router4", (P, BATCH, BATCH))
        keep("f_g1", (P, 1), (None, col(d[f + "g1"])))
        keep("f_g2", (P, 1), (None, col(d[f + "g2"])))
    if 3 in STAGES:
        keep("W_band", (P, P), (None, d["L0_attn_b_W"]))
    if 5 in STAGES:
        for n in "QKVO":
            keep("W" + n, (P, P), (None, d["L1_attn_a_W" + n]))
    if 7 in STAGES:
        f = "L1_attn_b_"
        keep("w7_inT", (P, 4 * P))
        for i, r in halves(4 * P, P):
            into(turned(d[f + "W_in"][i:i + r, :]), (w["w7_inT"][:, i:i + r], full))
        keep("w7_dtin", (P, 2, 64))
        keep("bc7", (P, 2, 2, 96))
        keep("w7_outT", (P, 2, P))
        for hf in range(2):
            into(turned(d[f + "W_x"][:, hf * P:(hf + 1) * P]), (w["w7_dtin"][:, hf, :], slice(0, 64)),
                 *[(w["bc7"][:, m, hf, 32 * r:32 * r + 16], slice(64 + 16 * m, 80 + 16 * m)) for m in range(2) for r in range(3)])
            into(turned(d[f + "W_out"][:, hf * P:(hf + 1) * P]), (w["w7_outT"][:, hf, :], full))
        keep("w7_dtT", (64, 2 * P))
        for i, r in halves(2 * P, P):
            into(turned(d[f + "W_dt"][i:i + r, :]), (w["w7_dtT"][:, i:i + r], full))

        def column2(ap):
            return [((full, slice(hf, hf + 1)), col(ap[hf * P:(hf + 1) * P])) for hf in range(2)]

        keep("ln7_g", (P, 1), (None, col(d[f + "ln_g"])))
        keep("ln7_b", (P, 1), (None, col(d[f + "ln_b"])))
        keep("conv7_w", (P, 2, 4), (None, d[f + "conv_w"].rearrange("(h p) a c -> p h (a c)", h=2)))
        keep("conv7_b", (P, 2), *column2(d[f + "conv_b"]))
        keep("b7_dt", (P, 2), *column2(d[f + "b_dt"]))
        keep("A7", (P, 2, 16), (None, d[f + "A_log"].rearrange("(h p) n -> p h n", h=2)))
        keep("D7col", (P, 2), *column2(d[f + "D_param"]))
        keep("D7", (P, 2, P))
        keep("alpha", (P, 1), (None, d[f + "alpha"].partition_broadcast(P)))
    if {6, 8} & set(STAGES):
        HID = d["L1_ffn_w2"].shape[1]
        k.layer = {}
        for name, shape in (("wqkv", (P, 3 * 512)), ("wo", (P, 4, D)), ("w1", (P, 2, HID)), ("w2", (P, 3, D)), ("ln", (P, 2)),
                            ("b1", (P, 2, 3))):
            keep("layer_" + name, shape)
            k.layer[name] = w["layer_" + name]
        keep("shift", (P, P), (None, d["c_shift"]))
        keep("carry", (P, P), (None, d["c_carry"]))


def turn_weights(k):
    nc, w = k.nc, k.w
    up, out, clear = k.count("turn_up"), k.count("turn_out"), k.count("turn_clear")
    if not k.turn:
        return
    with nc.Block() as block:
        @block.tensor
        def _(pe):
            for n, (place, _) in enumerate(k.turn):
                r, c = place.shape
                if n >= 8:
                    pe.wait_ge(out.sem, out.at(n - 7))
                pe.transpose(k.bank[n % 8][0:c, 0:r], place, k.ident[0:r, 0:r]).then_inc(up.sem, 1)

        @block.vector
        def _(dve):
            clears = 0
            if "bc7" in w:
                dve.memset(w["bc7"], 0.0).then_inc(clear.sem, 1)
                clears += 1
            if "router4" in w:
                dve.memset(w["router4"], 0.0).then_inc(clear.sem, 1)
                clears += 1
            if clears:
                dve.wait_ge(clear.sem, clear.at(clears))
            if "router4" in w:
                for b in range(BATCH):
                    dve.tensor_copy(w["router4"][:, b, b:b + 1], w["router"])
            for n, (place, pairs) in enumerate(k.turn):
                r, c = place.shape
                dve.wait_ge(up.sem, up.at(n + 1))
                for place2, cols in pairs:
                    cp = dve.tensor_copy(place2, k.bank[n % 8][0:c, 0:r][:, cols])
                cp.then_inc(out.sem, 1)


def more_constants(c, f32, bf16, eye):
    row = np.arange(96)
    state = np.where(row % 32 < 16, row % 32, -1)
    c["c_sel7"] = bf16(np.repeat(state[:, None] == np.arange(16)[None], P, axis=1))
    more_constants_attention(c, bf16)


def more_constants_attention(c, bf16):
    q, j, kk = np.arange(P)[:, None, None], np.arange(TPB)[None, :, None], np.arange(256)[None, None, :]
    key = j * P - 64 + kk
    ok = (np.abs(j * P + q - key) <= 64) & (key >= 0) & (key < SEQ)
    c["c_band"] = bf16(np.where(ok, 0.0, MASKED)).reshape(P, TPB * 256)
    i = np.arange(P)
    c["c_causal"] = bf16(np.where(i[:, None] >= i[None, :], 0.0, MASKED))
    c["c_causal_turned"] = bf16(np.where(i[:, None] <= i[None, :], 0.0, MASKED))
    c["c_sums"] = (i[:, None] == i[None, :] // 32 * 32 + 8).astype(np.float32)
    HD, WIN = 64, 64
    c["c_shift"] = np.eye(P, k=1, dtype=np.float32)
    carry = np.zeros((P, P), np.float32)
    carry[P - 1, 0] = 1
    c["c_carry"] = carry
    f32 = np.float32
    half = np.arange(0, HD, 2, dtype=f32)
    freq = (f32(1.0) / f32(10000.0) ** (half / f32(HD))).astype(f32)
    t = np.arange(SEQ, dtype=f32)
    angle = np.concatenate([t[:, None] * freq[None]] * 2, axis=1)
    base = ((half + f32(0.4 * HD)) / f32(1.4 * HD)).astype(f32)
    power = ((t - SEQ // 2) / f32(WIN // 2)).astype(f32)
    scale = np.concatenate([base[None] ** power[:, None]] * 2, axis=1).astype(f32)
    sign = np.where(np.arange(HD) < HD // 2, f32(-1), f32(1))
    cos, sin = np.cos(angle), np.sin(angle) * sign
    rope = np.stack([np.stack([cos * scale * f32(8), cos / scale]), np.stack([sin * scale * f32(8), sin / scale])])
    c["c_rope"] = rope.astype(f32).reshape(2, 2, TPB, P, HD).transpose(3, 2, 0, 1, 4).reshape(P, -1).copy()
    q, kk = np.arange(P)[:, None], np.arange(WIN + P)[None]
    back = q - (kk - WIN)
    ok = (back >= 0) & (back <= WIN)
    c["c_local"] = bf16(np.concatenate([np.where(ok & (kk >= WIN), 0.0, MASKED), np.where(ok, 0.0, MASKED)], axis=1))
    c["c_iota"] = np.arange(SEQ, dtype=f32)
    rank = np.arange(P)[:, None, None] % 64
    c["c_ranks"] = bf16(np.broadcast_to(np.where(rank >= np.arange(64)[None, None], 0.0, MASKED), (P, 8, 64)).reshape(P, 512))
    c["c_heads"] = (np.arange(P)[:, None] // 8 == np.arange(16)[None]).astype(f32)


def build(nc, dram, out):
    k = Core()
    k.nc, k.dram, k.out, k.w = nc, dram, out, {}
    counts, free = {}, []
    with ExitStack() as mem:
        k.mem = mem

        def count(name):
            if name not in counts:
                sem = free.pop() if free else mem.enter_context(nc.semaphore(name))
                counts[name] = Count(sem)
            return counts[name]

        def end_stage():
            with nc.Block() as block:
                @block.sync
                def _(sp):
                    for c in counts.values():
                        sp.sem_clear(c.sem)
            free.extend(c.sem for c in counts.values())
            counts.clear()

        made = [0]

        def name(base):
            made[0] += 1
            return f"{base}_{made[0]}"

        k.count, k.name = count, name
        X = mem.enter_context(nc.sbuf_tensor("X", [P, TILES, D], F32))
        Zpad = mem.enter_context(nc.sbuf_tensor("Z", [P, TILES + BATCH + 1, D], F32))
        k.X, k.Zpad = X, Zpad[:, :, :]
        k.zindex = lambda i: i + i // TPB + 1
        k.zpart = lambda b: k.Zpad[:, b * (TPB + 1) + 1:(b + 1) * (TPB + 1), :]
        k.xpart = lambda b: k.X[:, b * TPB:(b + 1) * TPB, :]
        big = mem.enter_context(nc.sbuf_tensor("arena", [P, 6 * TOK + 16], F32))
        k.big = big
        k.arena = [big[:, (i * TOK + (16 if i > 2 else 0)):][:, 0:TOK] for i in range(6)]
        k.arena_wide = big[:, 2 * TOK:3 * TOK + 16]
        k.arena6 = mem.enter_context(nc.sbuf_tensor("arena6", [P, 6 * SEQ], F32))[:, :]
        k.ZZ = k.arena[0].rearrange("p (t d) -> p t d", d=D)
        psum = mem.enter_context(nc.psum_tensor("psum", [P, 8 * BANK], F32))
        k.psum = psum[:, :]
        k.bank = [psum[:, i * BANK:(i + 1) * BANK] for i in range(8)]
        load(k)
        stages = {1: mamba_small, 2: routed_ffn, 3: band_attention, 4: routed_ffn, 5: causal_attention,
                  6: local_transformer, 7: mamba_large, 8: local_transformer}
        for s in STAGES:
            stages[s](k)
            end_stage()
        store(k)


def upper_half(a):
    return (np.ascontiguousarray(a, dtype=np.float32).view(np.uint32) >> 16).astype(np.uint16)


def constants():
    f32, bf16 = np.float32, upper_half
    c = {}
    eye = np.eye(P, dtype=f32)
    c["c_ident"] = eye
    c["c_identb"] = bf16(eye)
    c["c_fold"] = np.concatenate([np.eye(64, dtype=f32)] * 2)
    row = np.arange(96) % 32
    lane = np.arange(16)[:, None] + 16 * (np.arange(P)[None, :] // 64)
    c["c_sel1"] = bf16((row[:, None, None] == lane[None]).reshape(96, 16 * P))
    more_constants(c, f32, bf16, eye)
    return c


def kernel(**inputs):
    import numpy as _np
    import concourse.bacc as _bacc
    from concourse import mybir as _mybir
    from concourse.bass_utils import run_bass_kernel_spmd as _run

    nc = _bacc.Bacc("TRN2", target_bir_lowering=False, num_devices=1)
    arrays, dram = {}, {}
    for source in (inputs, constants()):
        for name, value in source.items():
            a = _np.ascontiguousarray(value)
            arrays["in_" + name] = a
            dram[name] = nc.dram_tensor("in_" + name, a.shape, _mybir.dt.from_np(a.dtype), kind="ExternalInput").ap()
            if a.dtype == _np.uint16:
                dram[name] = dram[name].bitcast(_mybir.dt.bfloat16)
    out = nc.dram_tensor("out_x", (BATCH, SEQ, D), _mybir.dt.float32, kind="ExternalOutput").ap()
    build(nc, dram, out)
    r = _run(nc, [arrays], core_ids=[0])
    return r.results[0]["out_x"]
```

```python
from contextlib import ExitStack

import numpy as np

import concourse.bass as bass
from concourse import mybir

F32 = mybir.dt.float32
BF16 = mybir.dt.bfloat16
U32 = mybir.dt.uint32
ALU = mybir.AluOpType
ACT = mybir.ActivationFunctionType
AX_X = mybir.AxisListType.X

P = 128
D = 128
BATCH, SEQ = 4, 1024
TOK = BATCH * SEQ
TILES = TOK // P
TPB = SEQ // P
BANK = 512
MASKED = -1.0e30

STAGES = (1, 2, 3, 4, 5, 6, 7, 8)


class Count:

    def __init__(self, sem):
        self.sem, self.base = sem, 0

    def at(self, n):
        return self.base + n

    def passed(self, n):
        self.base += n


class Core:
    pass





def layernorm(k, second_eps=None, pool_first=None, sp_first=None):
    nc = k.nc
    EPS = 1e-5
    X = k.X
    stats, moments, factor = (k.count(n) for n in ("ln_stats", "ln_moments", "ln_factor"))
    STEPS = 4 if second_eps is None else 9
    with ExitStack() as mem:
        def sb(name, shape):
            return mem.enter_context(nc.sbuf_tensor(k.name("ln_" + name), [P, TILES] + shape, F32))

        ST, MV = sb("stats", [6]), sb("moments", [2])
        VAR, RSTD, VAR2, RSTD2, LESS, SHIFT = (sb(n, []) for n in ("var", "rstd", "var2", "rstd2", "less", "shift"))
        block = mem.enter_context(nc.Block())

        def row(r, q):
            return r[:, TPB * q:TPB * (q + 1)]

        def tiles(q):
            return range(TPB * q, TPB * (q + 1))

        def of_act(t):
            return second_eps is None and t % 2 == 1

        @block.vector
        def _(dve):
            def aggregate(q):
                dve.wait_ge(stats.sem, stats.at(q + 1))
                for t in tiles(q):
                    mv = dve.bn_aggr(MV[:, t, :], ST[:, t, :])
                mv.then_inc(moments.sem, 1)

            for q in range(BATCH):
                for t in tiles(q):
                    st = dve.bn_stats(ST[:, t, :], X[:, t, :])
                st.then_inc(stats.sem, 1)
                if q:
                    aggregate(q - 1)
            aggregate(BATCH - 1)
            for q in range(BATCH):
                dve.wait_ge(factor.sem, factor.at(STEPS * q + 2))
                for t in tiles(q):
                    if not of_act(t):
                        dve.tensor_scalar(k.Zpad[:, k.zindex(t), :], X[:, t, :], MV[:, t, 0:1], RSTD[:, t:t + 1], ALU.subtract, ALU.mult)

        @block.sync
        def _(sp):
            if sp_first:
                sp_first(sp)

        @block.scalar
        def _(act):
            for q in range(BATCH):
                act.wait_ge(factor.sem, factor.at(STEPS * (q + 1)))
                for t in tiles(q):
                    if second_eps is not None:
                        act.activation(k.ZZ[:, t, :], X[:, t, :], ACT.Identity, scale=RSTD2[:, t:t + 1], bias=SHIFT[:, t:t + 1])
                    elif of_act(t):
                        act.activation(k.Zpad[:, k.zindex(t), :], X[:, t, :], ACT.Identity, scale=RSTD[:, t:t + 1], bias=SHIFT[:, t:t + 1])

        @block.gpsimd
        def _(pool):
            half = k.minus_half[:, 0:TPB]
            if pool_first:
                pool_first(pool)
            for q in range(BATCH):
                s = STEPS * q
                var = MV[:, TPB * q:TPB * (q + 1), 1]
                pool.wait_ge(moments.sem, moments.at(q + 1))
                pool.tensor_scalar(row(VAR, q), var, 1.0, EPS, ALU.mult, ALU.add).then_inc(factor.sem, 1)
                pool.wait_ge(factor.sem, factor.at(s + 1))
                pool.tensor_tensor(row(RSTD, q), row(VAR, q), half, ALU.pow).then_inc(factor.sem, 1)
                if second_eps is not None:
                    pool.wait_ge(factor.sem, factor.at(s + 2))
                    pool.tensor_tensor(row(VAR, q), var, row(RSTD, q), ALU.mult).then_inc(factor.sem, 1)
                    pool.wait_ge(factor.sem, factor.at(s + 3))
                    pool.tensor_tensor(row(VAR2, q), row(VAR, q), row(RSTD, q), ALU.mult).then_inc(factor.sem, 1)
                    pool.wait_ge(factor.sem, factor.at(s + 4))
                    pool.tensor_scalar(row(VAR, q), row(VAR2, q), 1.0, second_eps, ALU.mult, ALU.add).then_inc(factor.sem, 1)
                    pool.wait_ge(factor.sem, factor.at(s + 5))
                    pool.tensor_tensor(row(VAR2, q), row(VAR, q), half, ALU.pow).then_inc(factor.sem, 1)
                    pool.wait_ge(factor.sem, factor.at(s + 6))
                    pool.tensor_tensor(row(RSTD2, q), row(VAR2, q), row(RSTD, q), ALU.mult).then_inc(factor.sem, 1)
                pool.tensor_scalar(row(LESS, q), MV[:, TPB * q:TPB * (q + 1), 0], -1.0, 0.0, ALU.mult, ALU.add).then_inc(factor.sem, 1)
                pool.wait_ge(factor.sem, factor.at(s + STEPS - 1))
                pool.tensor_tensor(row(SHIFT, q), row(LESS, q), row(RSTD if second_eps is None else RSTD2, q), ALU.mult).then_inc(factor.sem, 1)

    for s in (stats, moments):
        s.passed(BATCH)
    factor.passed(STEPS * BATCH)



def scan(k, batches, halves_n, delta, du, parts, sel, a_col, fold, diag, u, out, gate, spare):
    nc = k.nc
    J, U = 16, 4
    LEAD = 5
    M = fold.shape[1]
    b_up, c_up, b_copied, decay_up, input_up, scanned, weighted, summed, y_taken = [
        k.count("scan_" + n) for n in ("b_up", "c_up", "b_copied", "decay_up", "input_up", "scanned", "weighted",
                                       "summed", "y_taken")]
    credited = (b_copied, input_up, scanned, weighted, summed, y_taken)
    for s in credited:
        s.passed(U)
    runs = [(b, hf) for b in range(batches) for hf in range(halves_n)]
    with ExitStack() as mem:
        ring = k.arena[4].rearrange("p (r s t) -> p r s t", r=2, t=SEQ)
        ring2 = k.arena6.rearrange("p (r s t) -> p r s t", r=3, t=SEQ)
        decay = ring[:, 0]
        b_lane = ring[:, 1]
        inputs, weight = ring2[:, 0], ring2[:, 2]
        state = [ring2[:, 1, 0], ring2[:, 1, 1]] + spare
        bank = k.bank
        block = mem.enter_context(nc.Block())

        def two(first):
            return k.psum[:, first * BANK:(first + 2) * BANK]

        def ahead(o, j, n):
            if isinstance(j, int) and j + n >= J:
                return (o + 1, j + n - J) if o + 1 < len(runs) else None
            return o, j + n

        def steps(eng, body, begin=None):
            for o in range(len(runs)):
                if begin:
                    begin(o)
                with eng.Fori(0, J // U - 2) as jj:
                    for s in range(U):
                        body(o, jj * U + s, s)
                for j in range(J - 2 * U, J):
                    body(o, j, j % U)

        @block.sync
        def _(sp):
            for s in credited:
                sp.sem_inc(s.sem, U)

        @block.tensor
        def _(pe):
            def spread_b(o, j):
                pe.wait_ge(b_copied.sem, b_copied.at(o * J + j))
                for c in range(2):
                    mm = pe.matmul(bank[c], sel(j), parts(0, runs[o][0], c), start=True, stop=True)
                mm.then_inc(b_up.sem, 1)

            def spread_c(o, j, s):
                pe.wait_ge(weighted.sem, weighted.at(o * J + j - 1))
                for c in range(2):
                    mm = pe.matmul(bank[2 + 2 * (s % 2) + c], sel(j), parts(1, runs[o][0], c), start=True, stop=True)
                mm.then_inc(c_up.sem, 1)

            def begin(o):
                b, hf = runs[o]
                pe.wait_ge(y_taken.sem, y_taken.at(o))
                for c in range(2):
                    pe.matmul(bank[6 + c][0:M, :], diag(hf), u(b, hf, c), start=True, stop=False, skip_group_check=True)

            def body(o, j, s):
                if ahead(o, j, 2):
                    spread_c(*ahead(o, j, 2), s)
                pe.wait_ge(weighted.sem, weighted.at(o * J + j + 1))
                for c in range(2):
                    mm = pe.matmul(bank[6 + c][0:M, :], fold, weight[:, s % 2, c * BANK:(c + 1) * BANK], start=False,
                                   stop=isinstance(j, int) and j == J - 1, skip_group_check=True)
                mm.then_inc(summed.sem, 1)
                if ahead(o, j, LEAD):
                    spread_b(*ahead(o, j, LEAD))

            for j in range(2):
                spread_c(0, j, j)
            for j in range(LEAD):
                spread_b(0, j)
            steps(pe, body, begin)

        @block.scalar
        def _(act):
            def copy_b(o, j, s):
                i = o * J + j
                act.wait_ge(b_up.sem, b_up.at(i + 1))
                act.wait_ge(input_up.sem, input_up.at(i - 1))
                act.activation(b_lane[:, s % 2], two(0), ACT.Copy).then_inc(b_copied.sem, 1)

            def decay_of(o, j, s):
                b, hf = runs[o]
                act.wait_ge(scanned.sem, scanned.at(o * J + j - 1))
                act.activation(decay[:, s % 2], delta(b, hf), ACT.Exp, scale=a_col(hf, j)).then_inc(decay_up.sem, 1)

            def body(o, j, s):
                if ahead(o, j, 2):
                    decay_of(*ahead(o, j, 2), s)
                if ahead(o, j, 3):
                    copy_b(*ahead(o, j, 3), s + 3)

            for j in range(3):
                copy_b(0, j, j)
                if j < 2:
                    decay_of(0, j, j)
            steps(act, body)

        @block.gpsimd
        def _(pool):
            def body(o, j, s):
                i = o * J + j
                pool.wait_ge(b_copied.sem, b_copied.at(i + 1))
                pool.wait_ge(scanned.sem, scanned.at(i - 1))
                pool.tensor_tensor(inputs[:, s % 2], b_lane[:, s % 2], du(*runs[o]), ALU.mult).then_inc(input_up.sem, 1)
            steps(pool, body)

        @block.vector
        def _(dve):
            def scan_step(o, j, s):
                i = o * J + j
                dve.wait_ge(decay_up.sem, decay_up.at(i + 1))
                dve.wait_ge(input_up.sem, input_up.at(i + 1))
                dve.tensor_tensor_scan(state[s % U], decay[:, s % 2], inputs[:, s % 2], 0.0, ALU.mult, ALU.add).then_inc(
                    scanned.sem, 1)

            def take(o):
                b, hf = runs[o]
                dve.wait_ge(summed.sem, summed.at((o + 1) * J))
                dve.tensor_tensor(out(b, hf), two(6)[0:M, :], gate(b, hf), ALU.mult).then_inc(y_taken.sem, 1)

            def body(o, j, s):
                i = o * J + j
                if ahead(o, j, 1):
                    scan_step(*ahead(o, j, 1), s + 1)
                dve.wait_ge(scanned.sem, scanned.at(i + 1))
                dve.wait_ge(c_up.sem, c_up.at(i + 1))
                dve.wait_ge(summed.sem, summed.at(i - 1))
                dve.tensor_tensor(weight[:, s % 2], state[s % U], two(2 + 2 * (s % 2)), ALU.mult).then_inc(weighted.sem, 1)

            scan_step(0, 0, 0)
            steps(dve, body, lambda o: take(o - 1) if o else None)
            take(len(runs) - 1)

    n = len(runs)
    for s in (b_up, c_up, b_copied, decay_up, input_up, scanned, weighted, summed):
        s.passed(n * J)
    y_taken.passed(n)



def mamba_small(k):
    nc, w = k.nc, k.w
    DI, NS, KC = 64, 32, 3
    layernorm(k, second_eps=1e-5, sp_first=k.load_first)
    first_weights(k)
    A = k.arena
    FT = A[1]
    LEFT = k.arena_wide[:, 0:BATCH * (SEQ + KC - 1)].rearrange("p (b t) -> p b t", b=BATCH)
    R = A[3][0:DI].rearrange("p (b t) -> p b t", b=BATCH)
    DELTA = A[1].rearrange("p (b t) -> p b t", b=BATCH)
    U = A[0].rearrange("p (b t) -> p b t", b=BATCH)
    DU = A[2].rearrange("p (b t) -> p b t", b=BATCH)
    TMP = A[4].rearrange("p (s t) -> p s t", t=SEQ)
    PARTS = A[5].bitcast(BF16).rearrange("p (m b t) -> p m b t", m=2, b=BATCH)
    NPART = 3 * NS
    bank, psum = k.bank, k.psum

    def two(first):
        return psum[:, first * BANK:(first + 2) * BANK]

    names = ("turned", "normed", "left_up", "right_up", "left", "right", "conv", "u", "residual")
    turned, normed, left_up, right_up, left, right, conv, u_up, resid = cs = [k.count("m1_" + n) for n in names]
    mem = ExitStack()
    selt = mem.enter_context(nc.sbuf_tensor("m1_sel", [NPART, 16 * P], BF16))
    loaded, later = k.count("m1_sel_in"), k.count("later")
    with nc.Block() as block:
        @block.sync
        def _(sp):
            sp.dma_start(selt[:, :], k.dram["c_sel1"]).then_inc(loaded.sem, 16)
            k.load_later(sp, later)
            sp.wait_ge(loaded.sem, loaded.at(16))

        @block.tensor
        def _(pe):
            for b in range(BATCH):
                if b:
                    pe.wait_ge(normed.sem, normed.at(b))
                for j in range(TPB):
                    mm = pe.transpose(bank[j // 4][:, P * (j % 4):P * (j % 4 + 1)], k.ZZ[:, b * TPB + j, :], k.ident)
                mm.then_inc(turned.sem, 1)
                pe.wait_ge(normed.sem, normed.at(b + 1))
                if b:
                    pe.wait_ge(left.sem, left.at(b + 1))
                for c in range(2):
                    mm = pe.matmul(bank[2 + c], w["up_left2"], FT[:, b * SEQ + c * BANK:][:, 0:BANK], start=True, stop=True)
                mm.then_inc(left_up.sem, 1)
                if b:
                    pe.wait_ge(right.sem, right.at(b))
                for c in range(2):
                    mm = pe.matmul(bank[4 + c][0:DI, :], w["W_up"][:, DI:2 * DI], FT[:, b * SEQ + c * BANK:][:, 0:BANK],
                                   start=True, stop=True)
                mm.then_inc(right_up.sem, 1)

        @block.vector
        def _(dve):
            dve.memset(LEFT[:, :, 0:KC - 1], 0.0).then_inc(left.sem, 1)
            for b in range(BATCH):
                dve.wait_ge(turned.sem, turned.at(b + 1))
                dve.tensor_scalar(FT[:, b * SEQ:(b + 1) * SEQ], two(0), w["ln_gamma"], w["ln_beta"], ALU.mult,
                                  ALU.add).then_inc(normed.sem, 1)
                dve.wait_ge(left_up.sem, left_up.at(b + 1))
                dve.tensor_scalar(LEFT[:, b, KC - 1:], two(2), w["b_left2"], None, ALU.add).then_inc(left.sem, 1)
                dve.wait_ge(left.sem, left.at(b + 2))
                if b >= 2:
                    dve.wait_ge(u_up.sem, u_up.at(b - 1))
                acc = TMP[:, b % 2]
                dve.tensor_scalar(acc, LEFT[:, b, 0:SEQ], w["conv_w2"][:, 0:1], None, ALU.mult).then_inc(conv.sem, 1)
                for tap in range(1, KC):
                    dve.wait_ge(conv.sem, conv.at(KC * b + tap))
                    dve.scalar_tensor_tensor(out=acc, in0=LEFT[:, b, tap:tap + SEQ], scalar=w["conv_w2"][:, tap:tap + 1],
                                             in1=acc, op0=ALU.mult, op1=ALU.add).then_inc(conv.sem, 1)

        @block.scalar
        def _(act):
            for b in range(BATCH):
                act.wait_ge(right_up.sem, right_up.at(b + 1))
                act.activation(R[:, b, :], two(4)[0:DI, :], ACT.Silu, bias=w["b_right"]).then_inc(right.sem, 1)
                act.wait_ge(conv.sem, conv.at(KC * (b + 1)))
                act.activation(U[:, b, :], TMP[:, b % 2], ACT.Silu, bias=w["conv_b2"]).then_inc(u_up.sem, 1)

        @block.gpsimd
        def _(pool):
            bias = w["b_down_row"].unsqueeze(1).broadcast_to([P, TPB, D])
            for b in range(BATCH):
                pool.tensor_tensor(k.zpart(b), k.zpart(b), bias, ALU.add).then_inc(resid.sem, 1)
            for b in range(BATCH):
                pool.wait_ge(resid.sem, resid.at(b + 1))
                pool.tensor_tensor(k.xpart(b), k.xpart(b), k.zpart(b), ALU.add)

    names = ("d_up", "b_up", "c_up", "soft", "d_taken", "first", "rest", "mid", "parts", "delta")
    d_up, b_up, c_up, soft, d_taken, first, rest, mid, done, delta_up = [k.count("m1p_" + n) for n in names]
    bc = (b_up, c_up)
    with nc.Block() as block:
        @block.sync
        def _(sp):
            sp.wait_ge(later.sem, later.at(k.later_loads))

        @block.tensor
        def _(pe):
            for b in range(BATCH):
                if b:
                    pe.wait_ge(d_taken.sem, d_taken.at(b))
                    pe.wait_ge(soft.sem, soft.at(3 * b - 2))
                for c in range(2):
                    mm = pe.matmul(bank[c], w["delta2"], U[0:DI, b, c * BANK:(c + 1) * BANK], start=True, stop=True)
                mm.then_inc(d_up.sem, 1)
                for m in range(2):
                    if b:
                        pe.wait_ge(rest.sem, rest.at(2 * (b - 1) + m + 1))
                    for c in range(2):
                        mm = pe.matmul(bank[2 + 2 * m + c][0:NPART, :], w["bc3"][:, m, :], U[0:DI, b, c * BANK:(c + 1) * BANK],
                                       start=True, stop=True)
                    mm.then_inc(bc[m].sem, 1)

        @block.scalar
        def _(act):
            for b in range(BATCH):
                t = TMP[:, b % 2]
                act.wait_ge(d_up.sem, d_up.at(b + 1))
                if b >= 2:
                    act.wait_ge(delta_up.sem, delta_up.at(b - 1))
                act.activation(t, two(0), ACT.Abs, bias=w["b_delta2"]).then_inc(soft.sem, 1)
                act.wait_ge(soft.sem, soft.at(3 * b + 1))
                act.activation(t, t, ACT.Exp, scale=-1.0).then_inc(soft.sem, 1)
                for m in range(2):
                    act.wait_ge(bc[m].sem, bc[m].at(b + 1))
                    act.activation(PARTS[0:NPART, m, b, :], two(2 + 2 * m)[0:NPART, :], ACT.Copy).then_inc(first.sem, 1)
                for m in range(2):
                    act.wait_ge(rest.sem, rest.at(2 * b + m + 1))
                    act.activation(PARTS[NS:2 * NS, m, b, :], TMP[NS:2 * NS, 2 + m, :], ACT.Copy)
                    act.activation(PARTS[2 * NS:NPART, m, b, :], TMP[2 * NS:NPART, 2 + m, :], ACT.Copy).then_inc(mid.sem, 1)
                act.wait_ge(soft.sem, soft.at(3 * b + 2))
                act.activation(t, t, ACT.Ln, bias=1.0).then_inc(soft.sem, 1)

        @block.vector
        def _(dve):
            for b in range(BATCH):
                dve.wait_ge(soft.sem, soft.at(3 * b + 1))
                dve.tensor_scalar(DELTA[:, b, :], two(0), w["b_delta2"], 0.0, ALU.add, ALU.max).then_inc(d_taken.sem, 1)
                for m in range(2):
                    n = 2 * b + m
                    dve.wait_ge(first.sem, first.at(n + 1))
                    if n >= 2:
                        dve.wait_ge(done.sem, done.at(n - 1))
                    dve.tensor_tensor(TMP[0:NPART, 2 + m, :], two(2 + 2 * m)[0:NPART, :], PARTS[0:NPART, m, b, :],
                                      ALU.subtract).then_inc(rest.sem, 1)
                for m in range(2):
                    dve.wait_ge(mid.sem, mid.at(2 * b + m + 1))
                    dve.tensor_tensor(PARTS[2 * NS:NPART, m, b, :], TMP[2 * NS:NPART, 2 + m, :],
                                      PARTS[2 * NS:NPART, m, b, :], ALU.subtract).then_inc(done.sem, 1)
                dve.wait_ge(d_taken.sem, d_taken.at(b + 1))
                dve.wait_ge(soft.sem, soft.at(3 * b + 3))
                dve.tensor_tensor(DELTA[:, b, :], DELTA[:, b, :], TMP[:, b % 2], ALU.add).then_inc(delta_up.sem, 1)

        @block.gpsimd
        def _(pool):
            for b in range(BATCH):
                pool.wait_ge(delta_up.sem, delta_up.at(b + 1))
                pool.tensor_tensor(DU[:, b, :], DELTA[:, b, :], U[:, b, :], ALU.mult)

    later_weights(k)
    scan(k, BATCH, 1, lambda b, hf: DELTA[:, b, :], lambda b, hf: DU[:, b, :],
         lambda m, b, c: PARTS[0:NPART, m, b, c * BANK:(c + 1) * BANK],
         lambda j: selt[:, bass.ds(j * P, P)], lambda hf, j: w["A1"][:, bass.ds(j, 1)], w["fold"], lambda hf: w["D1"],
         lambda b, hf, c: U[:, b, c * BANK:(c + 1) * BANK], lambda b, hf: R[:, b, :], lambda b, hf: R[:, b, :],
         [k.zpart(b).rearrange("p j d -> p (j d)") for b in range(2)])
    mem.close()

    project_back(k, [R.rearrange("p b t -> p (b t)")], [w["W_down"]])


def project_back(k, sources, weights, batches=range(BATCH), scale=None):
    nc = k.nc
    up, added = k.count("back_up"), k.count("back_added")
    with nc.Block() as block:
        @block.tensor
        def _(pe):
            for b in range(len(batches)):
                if b >= 2:
                    pe.wait_ge(added.sem, added.at(b - 1))
                for j in range(TPB):
                    o = k.bank[2 * (b % 2) + j // 4][:, P * (j % 4):P * (j % 4 + 1)]
                    t = (b * TPB + j) * P
                    for n, (src, wt) in enumerate(zip(sources, weights)):
                        mm = pe.matmul(o, src[:, t:t + P], wt, start=n == 0, stop=n == len(sources) - 1)
                mm.then_inc(up.sem, 1)

        @block.vector
        def _(dve):
            for b, seq in enumerate(batches):
                x = k.X[:, seq * TPB:(seq + 1) * TPB, :]
                y = k.psum[:, 2 * (b % 2) * BANK:(2 * (b % 2) + 2) * BANK].rearrange("p (j d) -> p j d", d=D)
                dve.wait_ge(up.sem, up.at(b + 1))
                if scale is None:
                    dve.tensor_tensor(x, x, y, ALU.add).then_inc(added.sem, 1)
                else:
                    dve.scalar_tensor_tensor(out=x, in0=y, scalar=scale, in1=x, op0=ALU.mult,
                                             op1=ALU.add).then_inc(added.sem, 1)
    for s in (up, added):
        s.passed(len(batches))



def mamba_large(k):
    nc, w, bank, psum = k.nc, k.w, k.bank, k.psum
    HV, KC, NS = 2, 4, 16
    RANK, GAP = 64, 32
    NPART = 3 * GAP
    PAIR = 2
    layernorm(k, second_eps=1e-5)
    FT = k.Zpad.rearrange("p t d -> p (t d)")[:, 0:TOK]
    turned, normed, resid = k.count("m7_turned"), k.count("m7_normed"), k.count("m7_residual")
    with nc.Block() as block:
        @block.gpsimd
        def _(pool):
            for b in range(BATCH):
                pool.tensor_tensor(k.xpart(b), k.xpart(b), k.zpart(b), ALU.add).then_inc(resid.sem, 1)

        @block.tensor
        def _(pe):
            for b in range(BATCH):
                for j in range(TPB):
                    mm = pe.transpose(bank[2 * b + j // 4][:, P * (j % 4):P * (j % 4 + 1)], k.ZZ[:, b * TPB + j, :], k.ident)
                mm.then_inc(turned.sem, 1)

        @block.vector
        def _(dve):
            for b in range(BATCH):
                dve.wait_ge(turned.sem, turned.at(b + 1))
                dve.wait_ge(resid.sem, resid.at(BATCH))
                dve.tensor_scalar(FT[:, b * SEQ:(b + 1) * SEQ], psum[:, 2 * b * BANK:(2 * b + 2) * BANK], w["ln7_g"], w["ln7_b"],
                                  ALU.mult, ALU.add).then_inc(normed.sem, 1)

    def quad(a):
        return a.rearrange("p (h b t) -> p h b t", h=HV, b=PAIR)

    U, DELTA, DU, R = (quad(k.arena[n]) for n in (0, 1, 2, 3))
    LEFT = k.arena_wide[:, 0:HV * PAIR * (SEQ + KC - 1)].rearrange("p (h b t) -> p h b t", h=HV, b=PAIR)
    TMP = quad(k.arena[4])
    REST = k.arena6.rearrange("p (s t) -> p s t", t=SEQ)
    PARTS = k.arena[5].bitcast(BF16)[:, 0:2 * PAIR * SEQ].rearrange("p (m b t) -> p m b t", m=2, b=PAIR)

    def two(first):
        return psum[:, first * BANK:(first + 2) * BANK]

    with ExitStack() as mem:
        selt = mem.enter_context(nc.sbuf_tensor("m7_sel", [NPART, NS * P], BF16))
        loaded = k.count("m7_sel_in")
        with nc.Block() as block:
            @block.sync
            def _(sp):
                sp.dma_start(selt[:, :], k.dram["c_sel7"]).then_inc(loaded.sem, 16)
                sp.wait_ge(loaded.sem, loaded.at(16))
        for pair in range(BATCH // PAIR):
            channels(k, pair, two, FT, LEFT, U, R, TMP, HV, KC, PAIR)
            deltas(k, two, U, DELTA, DU, TMP, REST, PARTS, HV, PAIR, RANK, GAP, NPART)
            scan(k, PAIR, HV, lambda b, hf: DELTA[:, hf, b, :], lambda b, hf: DU[:, hf, b, :],
                 lambda m, b, c: PARTS[0:NPART, m, b, c * BANK:(c + 1) * BANK],
                 lambda j: selt[:, bass.ds(j * P, P)], lambda hf, j: w["A7"][:, hf, bass.ds(j, 1)], k.ident,
                 lambda hf: w["D7"][:, hf, :], lambda b, hf, c: U[:, hf, b, c * BANK:(c + 1) * BANK],
                 lambda b, hf: R[:, hf, b, :], lambda b, hf: R[:, hf, b, :],
                 [k.arena[5][:, n * SEQ:(n + 1) * SEQ] for n in (2, 3)])
            project_back(k, [R[:, hf].rearrange("p b t -> p (b t)") for hf in range(HV)],
                         [w["w7_outT"][:, hf, :] for hf in range(HV)], range(pair * PAIR, (pair + 1) * PAIR), w["alpha"])


def channels(k, pair, two, FT, LEFT, U, R, TMP, HV, KC, PAIR):
    nc, w, bank = k.nc, k.w, k.bank
    left_up, right_up, left, right, conv = cs = [k.count("m7c_" + n) for n in ("left_up", "right_up", "left", "right", "conv")]
    with nc.Block() as block:
        @block.tensor
        def _(pe):
            for b in range(PAIR):
                for q in range(2 * HV):
                    n = b * HV + q % HV
                    if b:
                        done = left if q < HV else right
                        pe.wait_ge(done.sem, done.at((1 if q < HV else 0) + n - HV + 1))
                    for c in range(2):
                        at = (pair * PAIR + b) * SEQ + c * BANK
                        mm = pe.matmul(bank[2 * q + c], w["w7_inT"][:, q * P:(q + 1) * P], FT[:, at:at + BANK], start=True, stop=True)
                    mm.then_inc((left_up if q < HV else right_up).sem, 1)

        @block.vector
        def _(dve):
            dve.memset(LEFT[:, :, :, 0:KC - 1], 0.0).then_inc(left.sem, 1)
            for b in range(PAIR):
                for hf in range(HV):
                    n = b * HV + hf
                    dve.wait_ge(left_up.sem, left_up.at(n + 1))
                    dve.tensor_copy(LEFT[:, hf, b, KC - 1:], two(2 * hf)).then_inc(left.sem, 1)
                    dve.wait_ge(left.sem, left.at(n + 2))
                    acc, taps = TMP[:, hf, b, :], w["conv7_w"][:, hf, :]
                    dve.tensor_scalar(acc, LEFT[:, hf, b, 0:SEQ], taps[:, 0:1], None, ALU.mult).then_inc(conv.sem, 1)
                    for tap in range(1, KC):
                        dve.wait_ge(conv.sem, conv.at(KC * n + tap))
                        dve.scalar_tensor_tensor(out=acc, in0=LEFT[:, hf, b, tap:tap + SEQ], scalar=taps[:, tap:tap + 1],
                                                 in1=acc, op0=ALU.mult, op1=ALU.add).then_inc(conv.sem, 1)

        @block.scalar
        def _(act):
            for b in range(PAIR):
                for hf in range(HV):
                    act.wait_ge(right_up.sem, right_up.at(b * HV + hf + 1))
                    act.activation(R[:, hf, b, :], two(4 + 2 * hf), ACT.Silu).then_inc(right.sem, 1)
                for hf in range(HV):
                    act.wait_ge(conv.sem, conv.at(KC * (b * HV + hf + 1)))
                    act.activation(U[:, hf, b, :], TMP[:, hf, b, :], ACT.Silu, bias=w["conv7_b"][:, hf:hf + 1])
    for s in (left_up, right_up, right):
        s.passed(HV * PAIR)
    left.passed(HV * PAIR + 1)
    conv.passed(KC * HV * PAIR)


def deltas(k, two, U, DELTA, DU, TMP, REST, PARTS, HV, PAIR, RANK, GAP, NPART):
    nc, w, bank = k.nc, k.w, k.bank
    names = ("t_up", "dt", "d_up", "b_up", "c_up", "size", "decay", "log", "d_taken", "first", "rest", "mid", "parts", "delta")
    t_up, dt_in, d_up, b_up, c_up, size, decay, log, d_taken, first, rest, mid, done, delta_up = [k.count("m7d_" + n) for n in names]
    bc = (b_up, c_up)
    DT = REST[0:RANK, 2:2 + PAIR, :]
    with nc.Block() as block:
        @block.tensor
        def _(pe):
            def part(b, m):
                if b:
                    pe.wait_ge(rest.sem, rest.at(2 * (b - 1) + m + 1))
                for c in range(2):
                    for hf in range(HV):
                        mm = pe.matmul(bank[2 + 2 * m + c][0:NPART, :], w["bc7"][:, m, hf, :],
                                       U[:, hf, b, c * BANK:(c + 1) * BANK], start=hf == 0, stop=hf == HV - 1)
                mm.then_inc(bc[m].sem, 1)

            for b in range(PAIR):
                if b:
                    pe.wait_ge(d_taken.sem, d_taken.at(HV * (b - 1) + 1))
                    pe.wait_ge(size.sem, size.at(HV * (b - 1) + 1))
                for c in range(2):
                    for hf in range(HV):
                        mm = pe.matmul(bank[c][0:RANK, :], w["w7_dtin"][:, hf, :], U[:, hf, b, c * BANK:(c + 1) * BANK],
                                       start=hf == 0, stop=hf == HV - 1)
                mm.then_inc(t_up.sem, 1)
                part(b, 0)
                pe.wait_ge(dt_in.sem, dt_in.at(b + 1))
                for hf in range(HV):
                    if b and hf:
                        pe.wait_ge(d_taken.sem, d_taken.at(HV * b))
                        pe.wait_ge(size.sem, size.at(HV * b))
                    for c in range(2):
                        mm = pe.matmul(bank[6 * hf + c], w["w7_dtT"][:, hf * P:(hf + 1) * P], DT[:, b, c * BANK:(c + 1) * BANK],
                                       start=True, stop=True)
                    mm.then_inc(d_up.sem, 1)
                part(b, 1)

        @block.scalar
        def _(act):
            def first_part(b, m):
                act.wait_ge(bc[m].sem, bc[m].at(b + 1))
                act.activation(PARTS[0:NPART, m, b, :], two(2 + 2 * m)[0:NPART, :], ACT.Copy).then_inc(first.sem, 1)

            def second_part(b, m):
                act.wait_ge(rest.sem, rest.at(2 * b + m + 1))
                act.activation(PARTS[GAP:2 * GAP, m, b, :], REST[GAP:2 * GAP, m, :], ACT.Copy)
                act.activation(PARTS[2 * GAP:NPART, m, b, :], REST[2 * GAP:NPART, m, :], ACT.Copy).then_inc(mid.sem, 1)

            for b in range(PAIR):
                first_part(b, 0)
                for hf in range(HV):
                    act.wait_ge(d_up.sem, d_up.at(HV * b + hf + 1))
                    act.activation(TMP[:, hf, b, :], two(6 * hf), ACT.Abs, bias=w["b7_dt"][:, hf:hf + 1]).then_inc(size.sem, 1)
                for hf in range(HV):
                    act.wait_ge(size.sem, size.at(HV * b + hf + 1))
                    act.activation(TMP[:, hf, b, :], TMP[:, hf, b, :], ACT.Exp, scale=-1.0).then_inc(decay.sem, 1)
                second_part(b, 0)
                first_part(b, 1)
                for hf in range(HV):
                    act.wait_ge(decay.sem, decay.at(HV * b + hf + 1))
                    act.activation(TMP[:, hf, b, :], TMP[:, hf, b, :], ACT.Ln, bias=1.0).then_inc(log.sem, 1)
                second_part(b, 1)

        @block.vector
        def _(dve):
            def take_dt(b):
                dve.wait_ge(t_up.sem, t_up.at(b + 1))
                dve.tensor_copy(DT[:, b, :], two(0)[0:RANK, :]).then_inc(dt_in.sem, 1)

            def leave(b, m):
                n = 2 * b + m
                dve.wait_ge(first.sem, first.at(n + 1))
                if n >= 2:
                    dve.wait_ge(done.sem, done.at(n - 1))
                dve.tensor_tensor(REST[0:NPART, m, :], two(2 + 2 * m)[0:NPART, :], PARTS[0:NPART, m, b, :],
                                  ALU.subtract).then_inc(rest.sem, 1)

            def third_part(b, m):
                dve.wait_ge(mid.sem, mid.at(2 * b + m + 1))
                dve.tensor_tensor(PARTS[2 * GAP:NPART, m, b, :], REST[2 * GAP:NPART, m, :],
                                  PARTS[2 * GAP:NPART, m, b, :], ALU.subtract).then_inc(done.sem, 1)

            take_dt(0)
            for b in range(PAIR):
                leave(b, 0)
                for hf in range(HV):
                    n = HV * b + hf
                    dve.wait_ge(size.sem, size.at(n + 1))
                    dve.tensor_scalar(DELTA[:, hf, b, :], two(6 * hf), w["b7_dt"][:, hf:hf + 1], 0.0, ALU.add,
                                      ALU.max).then_inc(d_taken.sem, 1)
                third_part(b, 0)
                leave(b, 1)
                if b + 1 < PAIR:
                    take_dt(b + 1)
                for hf in range(HV):
                    n = HV * b + hf
                    dve.wait_ge(d_taken.sem, d_taken.at(n + 1))
                    dve.wait_ge(log.sem, log.at(n + 1))
                    dve.tensor_tensor(DELTA[:, hf, b, :], DELTA[:, hf, b, :], TMP[:, hf, b, :], ALU.add).then_inc(delta_up.sem, 1)
                third_part(b, 1)

        @block.gpsimd
        def _(pool):
            for b in range(PAIR):
                for hf in range(HV):
                    pool.wait_ge(delta_up.sem, delta_up.at(HV * b + hf + 1))
                    pool.tensor_tensor(DU[:, hf, b, :], DELTA[:, hf, b, :], U[:, hf, b, :], ALU.mult)
    for s in (t_up, dt_in, b_up, c_up):
        s.passed(PAIR)
    for s in (d_up, d_taken, delta_up, size, decay, log):
        s.passed(HV * PAIR)
    for s in (first, rest, mid, done):
        s.passed(2 * PAIR)



def turn_stream(k, into, stride, lead):
    nc, bank = k.nc, k.bank
    turned, taken = k.count("turned"), k.count("turned_taken")
    with nc.Block() as block:
        @block.tensor
        def _(pe):
            for b in range(BATCH):
                for j in range(TPB):
                    mm = pe.transpose(bank[2 * b + j // 4][:, P * (j % 4):P * (j % 4 + 1)], k.Zpad[:, k.zindex(b * TPB + j), :], k.ident)
                mm.then_inc(turned.sem, 1)

        def take(eng, copy, b):
            eng.wait_ge(turned.sem, turned.at(b + 1))
            copy(into[:, b * stride + lead:b * stride + lead + SEQ], k.psum[:, 2 * b * BANK:(2 * b + 2) * BANK])

        @block.vector
        def _(dve):
            for b in range(0, BATCH, 2):
                take(dve, dve.tensor_copy, b)

        @block.scalar
        def _(act):
            for b in range(1, BATCH, 2):
                take(act, act.copy, b)
    turned.passed(BATCH)



def band_attention(k):
    nc, w, bank = k.nc, k.w, k.bank
    WIN, KEYS = 64, 256
    layernorm(k)
    stride = SEQ + 2 * WIN
    ZT = k.big[:, TOK:TOK + BATCH * stride]
    names = ("qw", "q", "scores", "peak", "probs", "pt", "pts", "o", "inverse", "relu", "added", "cleared", "resid")
    qw, q_up, scores, peak, probs, pt, pts, o_up, inverse, relu, added, cleared, resid = [k.count("band_" + n) for n in names]
    credited = (q_up, pts, relu, added, pt, o_up, inverse)
    with ExitStack() as mem:
        def sb(name, shape, dt=F32):
            return mem.enter_context(nc.sbuf_tensor("band_" + name, shape, dt))

        mask = sb("mask", [P, TPB, KEYS], BF16)
        PR, PT, Q, RO = (k.arena[3][:, at:at + 2 * n].rearrange("p (s t) -> p s t", s=2)
                         for at, n in ((0, 3 * P), (6 * P, 3 * P), (12 * P, P), (14 * P, D)))
        low, total, inv = (sb(n, [P, 2]) for n in ("low", "total", "inv"))
        with nc.Block() as block:
            @block.sync
            def _(sp):
                sp.dma_start(mask[:, :, :], k.dram["c_band"].rearrange("p (j c) -> p j c", j=TPB)).then_inc(cleared.sem, 16)
                for s in credited:
                    sp.sem_inc(s.sem, 2)
                sp.wait_ge(cleared.sem, cleared.at(16))

            @block.gpsimd
            def _(pool):
                pool.memset(PR, 0.0)
                pool.memset(ZT, 0.0)
        for s in credited:
            s.passed(2)
        turn_stream(k, ZT, stride, WIN)

        def in_steps(eng, step):
            loops = (TILES - 3) // 2
            for i in range(2):
                step(i, i, 3, i)
            with eng.Fori(1, loops) as p:
                for s in range(2):
                    step(p * 2 + s, s, 3, 2)
            for i in range(2 * loops, TILES):
                step(i, i % 2, TILES - 1 - i, 2)

        with nc.Block() as block:
            @block.tensor
            def _(pe):
                def column(i):
                    return i * P + (i // TPB) * (2 * WIN)

                def query(i, s):
                    pe.wait_ge(q_up.sem, q_up.at(i - 1))
                    pe.matmul(bank[s][:, 0:P], w["W_band"], ZT[:, bass.ds(column(i) + WIN, P)], start=True,
                              stop=True).then_inc(qw.sem, 1)

                def score(i, s):
                    pe.wait_ge(q_up.sem, q_up.at(i + 1))
                    pe.matmul(bank[2 + s][:, 0:KEYS], Q[:, s, :], ZT[:, bass.ds(column(i), KEYS)], start=True, stop=False)
                    pe.matmul(bank[2 + s][:, 0:KEYS], k.identb, mask[:, i % TPB, :], start=False,
                              stop=True).then_inc(scores.sem, 1)

                def value(i, s):
                    pe.wait_ge(relu.sem, relu.at(i - 1))
                    pe.wait_ge(pts.sem, pts.at(i + 1))
                    for n in range(3):
                        mm = pe.matmul(bank[6 + s][:, 0:D], PT[:, s, n * P:(n + 1) * P], k.Zpad[:, k.zindex(i) - 1 + n, :],
                                       start=n == 0, stop=n == 2)
                    mm.then_inc(o_up.sem, 1)

                query(0, 0)
                query(1, 1)
                score(0, 0)
                query(2, 0)
                score(1, 1)

                def step(i, s, ahead, before):
                    pe.wait_ge(probs.sem, probs.at(i + 1))
                    pe.wait_ge(pts.sem, pts.at(i - 1))
                    for n in range(3):
                        mm = pe.transpose(bank[4 + s][:, n * P:(n + 1) * P], PR[:, s, n * P:(n + 1) * P], k.ident)
                    mm.then_inc(pt.sem, 1)
                    if ahead > 2:
                        query(i + 3, 1 - s)
                    if ahead > 1:
                        score(i + 2, s)
                    if before:
                        value(i - 1, 1 - s)
                in_steps(pe, step)
                value(TILES - 1, (TILES - 1) % 2)

            @block.scalar
            def _(act):
                def copy_q(i, s):
                    act.wait_ge(qw.sem, qw.at(i + 1))
                    act.copy(Q[:, s, :], bank[s][:, 0:P]).then_inc(q_up.sem, 1)

                def rectify(i, s):
                    act.wait_ge(o_up.sem, o_up.at(i + 1))
                    act.wait_ge(inverse.sem, inverse.at(i + 1))
                    act.wait_ge(added.sem, added.at(i - 1))
                    act.activation(RO[:, s, :], bank[6 + s][:, 0:D], ACT.Relu, scale=inv[:, s:s + 1]).then_inc(relu.sem, 1)

                copy_q(0, 0)
                copy_q(1, 1)

                def step(i, s, ahead, before):
                    act.wait_ge(pt.sem, pt.at(i - 1))
                    act.wait_ge(peak.sem, peak.at(i + 1))
                    act.wait_ge(inverse.sem, inverse.at(i - 1))
                    act.activation(PR[:, s, WIN:WIN + KEYS], bank[2 + s][:, 0:KEYS], ACT.Exp, bias=low[:, s:s + 1],
                                   accum_out=total[:, s:s + 1]).then_inc(probs.sem, 1)
                    if ahead > 1:
                        copy_q(i + 2, s)
                    if before > 1:
                        rectify(i - 2, s)
                in_steps(act, step)
                for i in (TILES - 2, TILES - 1):
                    rectify(i, i % 2)

            @block.vector
            def _(dve):
                def maximum(i, s):
                    dve.wait_ge(scores.sem, scores.at(i + 1))
                    dve.tensor_reduce(low[:, s:s + 1], bank[2 + s][:, 0:KEYS], AX_X, ALU.max, negate=True).then_inc(peak.sem, 1)

                def add(i, s):
                    dve.wait_ge(relu.sem, relu.at(i + 1))
                    dve.tensor_tensor(k.X[:, i, :], k.X[:, i, :], RO[:, s, :], ALU.add).then_inc(added.sem, 1)

                maximum(0, 0)

                def step(i, s, ahead, before):
                    if ahead:
                        maximum(i + 1, 1 - s)
                    dve.wait_ge(pt.sem, pt.at(i + 1))
                    dve.wait_ge(o_up.sem, o_up.at(i - 1))
                    dve.tensor_copy(PT[:, s, :], bank[4 + s][:, 0:3 * P]).then_inc(pts.sem, 1)
                    if before > 1:
                        add(i - 2, s)
                    else:
                        dve.wait_ge(resid.sem, resid.at(1))
                    dve.reciprocal(inv[:, s:s + 1], total[:, s:s + 1]).then_inc(inverse.sem, 1)
                in_steps(dve, step)
                for i in (TILES - 2, TILES - 1):
                    add(i, i % 2)

            @block.gpsimd
            def _(pool):
                for b in range(BATCH):
                    add = pool.tensor_tensor(k.xpart(b), k.xpart(b), k.zpart(b), ALU.add)
                add.then_inc(resid.sem, 1)



def causal_attention(k):
    nc, w, bank = k.nc, k.w, k.bank
    HEADS, HD, STRIP = 16, 8, 32
    GROUPS, IN, PARTS = 4, 4, 3
    ROUNDS, SLOTS = BATCH * GROUPS, 4
    ROWS = PARTS * HD
    PEAK = 96
    SCALE = float(1.0 / np.sqrt(HD))
    GROUP = IN * SEQ

    QK = k.big[:, 0:SLOTS * GROUP].bitcast(BF16).rearrange("p (s m t) -> p s m t", s=SLOTS, m=2)
    PT = k.big[:, SLOTS * GROUP:(SLOTS + 2) * GROUP].rearrange("p (s h t) -> p s h t", s=2, h=IN)
    FT = k.big[:, SLOTS * GROUP:(SLOTS + 1) * GROUP]
    REST = k.big[:, (SLOTS + 1) * GROUP:(SLOTS + 1) * GROUP + 2 * BANK].rearrange("p (s t) -> p s t", s=2)
    parts = [k.big[:, at:at + PARTS * SEQ].bitcast(BF16).rearrange("p (m a t) -> p m a t", m=2, a=PARTS)
             for at in ((SLOTS + 1) * GROUP + 2 * BANK, (SLOTS - 1) * GROUP)]
    V = k.arena6[:, 0:TOK].rearrange("p (r j c) -> p r j c", r=ROUNDS, j=TPB)
    zt = [k.Zpad[:, b * (TPB + 1) + 1:(b + 1) * (TPB + 1), :] for b in range(BATCH)]
    VS = zt[0].rearrange("p j (h e) -> p j h e", h=IN)
    OT, INV, ON = (z.rearrange("p j d -> p (j d)") for z in zt[1:])

    def clear(pool):
        for s in range(SLOTS - 1):
            pool.memset(k.big[:, s * GROUP:(s + 1) * GROUP], 0.0)

    layernorm(k, pool_first=clear)
    turn_stream(k, FT, SEQ, 0)
    kept = nc.dram_tensor("causal_parts", (2, BATCH, P, PARTS, SEQ), BF16).ap()

    names = ("qk_up", "first", "second", "left", "third", "v_up", "v_in", "cleared", "fed", "s1_up", "s1_free", "s2_up", "probs",
             "pv", "vs_in", "o_in", "sums_out", "inverse", "sums_in", "peak", "split", "zeroed")
    (qk_up, first, second, left, third, v_up, v_in, cleared, fed, s1_up, s1_free, s2_up, probs, pv, vs_in, o_in, sums_out,
     inverse, sums_in, peak, split, zeroed) = [k.count("causal_" + n) for n in names]
    written = [[k.count(f"causal_written{m}{b}") for b in range(BATCH)] for m in range(2)]
    loaded = [k.count(f"causal_loaded{s}") for s in range(SLOTS)]
    peaks_in = [k.count(f"causal_peaks_in{s}") for s in range(SLOTS)]
    with ExitStack() as mem:
        def sb(name, shape, dt=F32):
            return mem.enter_context(nc.sbuf_tensor("causal_" + name, shape, dt))

        mask = sb("mask", [P, 2, P], BF16)
        REST6 = k.arena6[:, TOK:]
        WP = REST6[:, 0:2 * P].rearrange("p (m t) -> p m t", m=2)
        WS = REST6[:, 2 * P:6 * P].rearrange("p (g d) -> p g d", g=GROUPS)
        sums = REST6[:, 6 * P:7 * P]
        part = sb("peak_parts", [P, IN, TPB, 2])
        top = sb("top", [P, IN, TPB])
        total, inv = (sb(n, [P, SEQ // STRIP]) for n in ("total", "inv"))
        low = sb("low", [IN * TPB, 2, P])
        lowb = sb("low_parts", [IN * TPB, PARTS, P], BF16)

        def load_round(sp, r, s):
            for m in range(2):
                of_round = kept[m].rearrange("b (g e h) a t -> (b g) e h a t", g=GROUPS, h=IN)
                of_round = of_round[r:r + 1] if isinstance(r, int) else of_round[bass.ds(r, 1)]
                of_round = of_round.rearrange("r e h a t -> (r e) h a t")
                for a in range(PARTS):
                    for c in range(PARTS):
                        rows = slice((a * PARTS + c) * HD, (a * PARTS + c + 1) * HD)
                        sp.dma_start(QK[rows, s, m, :].rearrange("e (h t) -> e h t", h=IN), of_round[:, :, a if m else c, :]).then_inc(loaded[s].sem, 16)

        CH = [(c, m) for c in range(TOK // BANK) for m in range(2)]
        with nc.Block() as block:
            @block.sync
            def _(sp):
                for m in range(2):
                    sp.dma_start(mask[:, m, :], k.dram["c_causal"] if m == 0 else k.dram["c_causal_turned"]).then_inc(cleared.sem, 16)
                sp.dma_start(sums, k.dram["c_sums"]).then_inc(cleared.sem, 16)
                sp.wait_ge(vs_in.sem, vs_in.at(1))
                for hh in range(IN):
                    sp.dma_start(WS[STRIP * hh:STRIP * hh + HD, :, :],
                                 k.dram["L1_attn_a_WO"].rearrange("(g h e) d -> h e g d", g=GROUPS, h=IN)[hh]).then_inc(cleared.sem, 16)
                for s in range(SLOTS - 1):
                    sp.dma_start(QK[PEAK:PEAK + PARTS, s, 1, :], k.dram["c_ones"]).then_inc(cleared.sem, 16)
                for i, (c, m) in enumerate(CH):
                    if c % 2:
                        b = c // 2
                        sp.wait_ge(first.sem, first.at(i + 1))
                        sp.wait_ge(second.sem, second.at(i + 1))
                        sp.wait_ge(third.sem, third.at(i + 1))
                        sp.dma_start(kept[m, b], parts[b % 2][:, m]).then_inc(written[m][b].sem, 16)
                        if m and b == 0:
                            for n in range(2):
                                sp.wait_ge(written[n][0].sem, written[n][0].at(16))
                            load_round(sp, 0, 0)
                for m in range(2):
                    for b in range(1, BATCH):
                        sp.wait_ge(written[m][b].sem, written[m][b].at(16))
                sp.wait_ge(cleared.sem, cleared.at(16 * (6 + SLOTS)))
                for s, v in ((s1_free, 2), (probs, 2), (pv, 2), (o_in, 1), (zeroed, 1)):
                    sp.sem_inc(s.sem, v)

            @block.gpsimd
            def _(pool):
                pool.memset(WS, 0.0).then_inc(vs_in.sem, 1)
                for m, n in enumerate("QK"):
                    cp = pool.tensor_copy(WP[:, m, :].rearrange("p (g e h) -> p g e h", g=GROUPS, e=HD),
                                          w["W" + n].rearrange("p (g h e) -> p g e h", g=GROUPS, h=IN))
                cp.then_inc(vs_in.sem, 1)
                pool.memset(VS, 0.0).then_inc(vs_in.sem, 1)
                pool.wait_ge(vs_in.sem, vs_in.at(3))
                pool.memset(VS[:, :, :, HD:HD + 1], 1.0)
                pool.memset(INV, 0.0)
                pool.memset(part[:, :, :, :], MASKED)
                for i, (c, m) in enumerate(CH):
                    b, t = c // 2, (c % 2) * BANK
                    pool.wait_ge(second.sem, second.at(i + 1))
                    pool.tensor_tensor(parts[b % 2][:, m, 2, t:t + BANK], REST[:, i % 2, :], parts[b % 2][:, m, 1, t:t + BANK], ALU.subtract).then_inc(third.sem, 1)

            @block.tensor
            def _(pe):
                pe.wait_ge(vs_in.sem, vs_in.at(2))
                for i, (c, m) in enumerate(CH):
                    if i >= 4:
                        pe.wait_ge(left.sem, left.at(i - 3))
                    pe.matmul(bank[i % 4], WP[:, m, :], FT[:, c * BANK:(c + 1) * BANK], start=True, stop=True).then_inc(qk_up.sem, 1)
                    if m:
                        if c >= 4:
                            pe.wait_ge(v_in.sem, v_in.at(c - 3))
                        for j in range(4):
                            mm = pe.matmul(bank[4 + c % 4][:, j * P:(j + 1) * P], FT[:, c * BANK + j * P:c * BANK + (j + 1) * P], w["WV"],
                                           start=True, stop=True)
                        mm.then_inc(v_up.sem, 1)

            @block.scalar
            def _(act):
                def part_two(i):
                    c, m = CH[i]
                    act.wait_ge(left.sem, left.at(i + 1))
                    act.copy(parts[c // 2 % 2][:, m, 1, (c % 2) * BANK:][:, 0:BANK], REST[:, i % 2, :]).then_inc(second.sem, 1)

                for i, (c, m) in enumerate(CH):
                    act.wait_ge(qk_up.sem, qk_up.at(i + 1))
                    if c >= 4 and c % 2 == 0:
                        act.wait_ge(written[m][c // 2 - 2].sem, written[m][c // 2 - 2].at(16))
                    act.copy(parts[c // 2 % 2][:, m, 0, (c % 2) * BANK:][:, 0:BANK], bank[i % 4]).then_inc(first.sem, 1)
                    if i:
                        part_two(i - 1)
                part_two(len(CH) - 1)

            @block.vector
            def _(dve):
                for i, (c, m) in enumerate(CH):
                    dve.wait_ge(first.sem, first.at(i + 1))
                    if i >= 2:
                        dve.wait_ge(third.sem, third.at(i - 1))
                    dve.tensor_tensor(REST[:, i % 2, :], bank[i % 4], parts[c // 2 % 2][:, m, 0, (c % 2) * BANK:][:, 0:BANK],
                                      ALU.subtract).then_inc(left.sem, 1)
                    if m:
                        dve.wait_ge(v_up.sem, v_up.at(c + 1))
                        dve.tensor_copy(V.rearrange("p (b g) j c -> p b j g c", b=BATCH)[:, c // 2, 4 * (c % 2):4 * (c % 2) + 4, :, :],
                                        bank[4 + c % 4].rearrange("p (j g c) -> p j g c", j=4, g=GROUPS)).then_inc(v_in.sem, 1)
        vs_in.passed(3)
        for s, v in ((s1_free, 2), (probs, 2), (pv, 2), (o_in, 1), (zeroed, 1)):
            s.passed(v)
        first_units = []
        for qt in range(TPB):
            for half, (_, n) in enumerate(halves((qt + 1) * P, BANK)):
                per = BANK // n
                first_units += [(qt, half, range(h, min(h + per, IN)), n) for h in range(0, IN, per)]
        second_units, after = [], {}
        for kt in range(TPB):
            n = SEQ - kt * P
            per = 1 if n > BANK else 2 if 2 * n > BANK else 4
            second_units += [(kt, range(h, h + per), n) for h in range(0, IN, per)]
            after[kt] = len(second_units)
        N1, N2 = len(first_units), len(second_units)
        ONES, OUT = [("sum", 0), ("sum", 1)], [("out", 0), ("out", 1)]
        scoring = [("score", i) for i in range(N1)]
        LEAD = 18
        SHORT, LONG = N1 + 1, N1 + 5
        soon = [("soon", i) for i in range(LEAD)]

        def ring_steps(before, more):
            steps = scoring[LEAD:] + [("turn", 0)] if more else []
            if more > 1:
                steps = steps + soon
            if before:
                steps = steps[0:SUMS_AT] + ONES + steps[SUMS_AT:OUT_AT] + OUT + steps[OUT_AT:]
            return steps

        def sums_step(r):
            return ring_start(r) + (SUMS_AT if not isinstance(r, int) or r + 1 < ROUNDS else 0)

        def ring_start(r):
            if isinstance(r, int) and r == ROUNDS - 1:
                return 2 * SHORT + LEAD + (r - 1) * LONG - LEAD
            return 2 * SHORT + LEAD + (r - 1) * LONG

        INVERSE_AT, SUMS_AT, OUT_AT = 10, 18, 26
        follow = {after[kt] + 1: kt for kt in range(TPB - 2)} | {0: TPB - 2, 1: TPB - 1}
        follow = {min(i, N2 - 1): kt for i, kt in follow.items()}
        items = []
        for i, (_, heads, size) in enumerate(second_units):
            items.append(("second", i, 0, size * len(heads) + P * len(heads)))
            if i in follow:
                kt = follow[i]
                items += [("values", kt, half, 4 * ((half + 1) * BANK - max(kt * P, half * BANK))) for half in range(2) if kt * P < (half + 1) * BANK]
        whole = sum(x[3] for x in items)
        start_of_end = sum(x[3] for x in items[0:8])

        def rounds(eng, body):
            body(0, 0, False, 2, 0, 0)
            with eng.Fori(0, BATCH - 1) as b:
                for j in range(1, GROUPS + 1):
                    body(b * GROUPS + j, j % SLOTS, True, 2, b, j - 1)
            for r in range((BATCH - 1) * GROUPS + 1, ROUNDS):
                body(r, r % SLOTS, True, min(2, ROUNDS - 1 - r), BATCH - 1, r - 1 - (BATCH - 1) * GROUPS)

        with nc.Block() as block:
            @block.sync
            def _(sp):
                def maxima(r, s):
                    sp.wait_ge(split.sem, split.at(4 * r + 4))
                    for a in range(PARTS):
                        sp.dma_start(QK[PEAK + a:PEAK + a + 1, s, 0, :].rearrange("a (p c) -> a p c", p=IN * TPB), lowb[:, a, :]).then_inc(peaks_in[s].sem, 16)

                def invert(r):
                    sp.wait_ge(o_in.sem, o_in.at(r + 1))
                    for hh in range(IN):
                        strip = slice(STRIP * hh, STRIP * (hh + 1))
                        row = STRIP * hh + HD
                        sp.dma_start(total[strip, :], OT[row:row + 1, :].rearrange("a (p c) -> a p c", p=STRIP)).then_inc(sums_out.sem, 16)
                    sp.wait_ge(inverse.sem, inverse.at(r + 1))
                    for hh in range(IN):
                        strip = slice(STRIP * hh, STRIP * (hh + 1))
                        row = STRIP * hh + HD
                        sp.dma_start(INV[row:row + 1, :].rearrange("a (p c) -> a p c", p=STRIP), inv[strip, :]).then_inc(sums_in.sem, 16)

                load_round(sp, 1, 1)
                maxima(0, 0)
                load_round(sp, 2, 2)

                def body(r, s, before, more, b, g):
                    if before:
                        invert(r - 1)
                    if more:
                        maxima(r + 1, (s + 1) % SLOTS)
                    if not before:
                        sp.wait_ge(fed.sem, fed.at(1))
                        sp.dma_start(QK[PEAK:PEAK + PARTS, 3, 1, :], k.dram["c_ones"]).then_inc(loaded[3].sem, 16)
                        load_round(sp, 3, 3)
                    if before and (not isinstance(r, int) or r + 3 < ROUNDS):
                        sp.wait_ge(s2_up.sem, s2_up.at(r * N2))
                        load_round(sp, r + 3, (s + 3) % SLOTS)
                rounds(sp, body)
                invert(ROUNDS - 1)

            @block.gpsimd
            def _(pool):
                def split_maxima(r, n, s, count):
                    pool.wait_ge(s1_free.sem, s1_free.at(n + 1))
                    if count is not None:
                        pool.wait_ge(*count)
                    pool.sem_inc(fed.sem, 1)
                    pool.tensor_copy(lowb[:, 0, :], low[:, 0, :]).then_inc(split.sem, 1)
                    pool.wait_ge(split.sem, split.at(4 * r + 1))
                    pool.tensor_tensor(low[:, 1, :], low[:, 0, :], lowb[:, 0, :], ALU.subtract).then_inc(split.sem, 1)
                    pool.wait_ge(split.sem, split.at(4 * r + 2))
                    pool.sem_inc(fed.sem, 1)
                    pool.tensor_copy(lowb[:, 1, :], low[:, 1, :]).then_inc(split.sem, 1)
                    pool.wait_ge(split.sem, split.at(4 * r + 3))
                    pool.tensor_tensor(lowb[:, 2, :], low[:, 1, :], lowb[:, 1, :], ALU.subtract).then_inc(split.sem, 1)

                def values(r):
                    pool.wait_ge(pv.sem, pv.at(r * TPB))
                    pool.wait_ge(split.sem, split.at(4 * r + 4))
                    pool.sem_inc(fed.sem, 1)
                    rr = slice(r, r + 1) if isinstance(r, int) else bass.ds(r, 1)
                    pool.tensor_copy(VS[:, :, :, 0:HD], V[:, rr, :, :].rearrange("p r j (h e) -> p (r j) h e", h=IN)).then_inc(vs_in.sem, 1)

                pool.memset(k.big[:, (SLOTS - 1) * GROUP:SLOTS * GROUP], 0.0).then_inc(fed.sem, 1)
                split_maxima(0, SHORT - 1, 0, None)

                def body(r, s, before, more, b, g):
                    steps = ring_steps(before, more)
                    start = ring_start(r) if before else SHORT + LEAD
                    values(r)
                    if before and (not isinstance(r, int) or r + 3 < ROUNDS):
                        pool.wait_ge(s2_up.sem, s2_up.at(r * N2))
                        pool.wait_ge(vs_in.sem, vs_in.at(r + 1))
                        pool.sem_inc(fed.sem, 1)
                        pool.memset(QK[PEAK:PEAK + PARTS, (s + 3) % SLOTS, 0, :], 0.0).then_inc(zeroed.sem, 1)
                        pool.wait_ge(zeroed.sem, zeroed.at(r))
                    else:
                        pool.wait_ge(vs_in.sem, vs_in.at(r + 1))
                    if more:
                        turn = b + 1 + (1 if s == 0 and before else 0)
                        split_maxima(r + 1, start + steps.index(("turn", 0)), s, (peaks_in[s].sem, peaks_in[s].at(turn * 16 * PARTS)))
                rounds(pool, body)

            @block.tensor
            def _(pe):
                ring = [0]

                def enter(n):
                    pe.wait_ge(s1_free.sem, s1_free.at(n - 1))
                    place = bank[ring[0]]
                    ring[0] = 1 - ring[0]
                    return place

                def ring_step(step, n, r, s, g):
                    kind, i = step
                    if kind in ("score", "soon"):
                        s = (s + 1 + (kind == "soon")) % SLOTS
                        qt, half, heads, size = first_units[i]
                        out = enter(n)
                        for at, hh in enumerate(heads):
                            col = hh * SEQ
                            o = out[:, at * size:(at + 1) * size]
                            diag = half == (qt * P) // BANK
                            mm = pe.matmul(o, QK[:, s, 0, col + qt * P:col + (qt + 1) * P], QK[:, s, 1, col + half * BANK:col + half * BANK + size],
                                           start=True, stop=True)
                            if diag:
                                mm = pe.matmul(o[:, size - P:size], k.identb, mask[:, 0, :], start=False, stop=True, skip_group_check=True)
                        mm.then_inc(s1_up.sem, 1)
                    elif kind == "turn":
                        pe.wait_ge(peak.sem, peak.at(r + 2))
                        out = enter(n)
                        pe.matmul(out[0:IN * TPB, 0:P], top[:, :, :].rearrange("p h j -> p (h j)"), k.ident, start=True, stop=True).then_inc(s1_up.sem, 1)
                    elif kind == "sum":
                        pe.wait_ge(sums_in.sem, sums_in.at(16 * IN * r))
                        out = enter(n)
                        pe.matmul(out, sums, INV[:, i * BANK:(i + 1) * BANK], start=True, stop=True).then_inc(s1_up.sem, 1)
                    else:
                        out = enter(n)
                        for j in range(4):
                            mm = pe.matmul(out[:, j * P:(j + 1) * P], ON[:, i * BANK + j * P:i * BANK + (j + 1) * P], WS[:, g, :], start=True, stop=True)
                        mm.then_inc(s1_up.sem, 1)

                def second(i, r, s):
                    kt, heads, size = second_units[i]
                    pe.wait_ge(probs.sem, probs.at(r * N2 + i - 1))
                    base = 2 + 2 * (i % 2)
                    for at, hh in enumerate(heads):
                        col = hh * SEQ
                        keys = QK[:, s, 1, col + kt * P:col + (kt + 1) * P]
                        if size > BANK:
                            places = [(base, kt * P, BANK), (base + 1, 0, BANK)]
                        else:
                            stride = 2 * BANK // len(heads) if size > P else P
                            lead = stride - size
                            places = [(base + at * stride // BANK, at * stride % BANK + lead, at * stride % BANK + lead + size)]
                        q = col + kt * P
                        for n, (bk, lo, hi) in enumerate(places):
                            mm = pe.matmul(bank[bk][:, lo:hi], keys, QK[:, s, 0, q:q + hi - lo], start=True, stop=True)
                            if n == 0:
                                mm = pe.matmul(bank[bk][:, lo:lo + P], k.identb, mask[:, 1, :], start=False, stop=True, skip_group_check=True)
                            q += hi - lo
                    mm.then_inc(s2_up.sem, 1)

                def values(kt, half, r):
                    lo, hi = max(kt * P, half * BANK), (half + 1) * BANK
                    pe.wait_ge(probs.sem, probs.at(r * N2 + after[kt]))
                    if kt == 0:
                        pe.wait_ge(vs_in.sem, vs_in.at(r + 1))
                        pe.wait_ge(o_in.sem, o_in.at(r))
                    for hh in range(IN):
                        mm = pe.matmul(bank[6 + half][STRIP * hh:STRIP * (hh + 1), lo - half * BANK:BANK], VS[:, kt, hh, :],
                                       PT[:, kt % 2, hh, lo:hi], start=kt == 0, stop=(kt + 1) * P == hi)
                    if half:
                        mm.then_inc(pv.sem, 1)

                def feed(r, s, fill):
                    pe.wait_ge(loaded[s].sem, loaded[s].at(16 * (fill * 2 * PARTS * PARTS + (s == 3))))
                    if not isinstance(r, int) or r >= SLOTS:
                        pe.wait_ge(zeroed.sem, zeroed.at(r - SLOTS + 1))

                feed(0, 0, 1)
                for n, step in enumerate(scoring + [("turn", 0)]):
                    ring_step(step, n, -1, SLOTS - 1, 0)
                feed(1, 1, 1)
                for n, step in enumerate(soon):
                    ring_step(step, SHORT + n, -1, SLOTS - 1, 0)

                def body(r, s, before, more, b, g):
                    steps = ring_steps(before, more)
                    start = ring_start(r) if before else SHORT + LEAD
                    fill = b + 1 + (1 if s == 0 and before else 0)
                    pe.wait_ge(peaks_in[s].sem, peaks_in[s].at(fill * 16 * PARTS))
                    done, spent = 0, 0
                    for kind, at, half, cost in items:
                        if kind == "second":
                            second(at, r, s)
                        elif at < TPB - 2:
                            values(at, half, r)
                        elif before:
                            values(at, half, r - 1)
                        spent += cost
                        goal = len(steps) * spent // whole if more else len(steps) * max(0, spent - start_of_end) // (whole - start_of_end)
                        while done < goal:
                            if steps[done] == soon[0]:
                                feed(r + 2, (s + 2) % SLOTS, b + 1 + (1 if s + 2 >= SLOTS or (s == 0 and before) else 0))
                            ring_step(steps[done], start + done, r, s, g)
                            done += 1
                rounds(pe, body)
                for kt in range(TPB - 2, TPB):
                    values(kt, 1, ROUNDS - 1)
                for i, step in enumerate(ONES + OUT):
                    ring_step(step, ring_start(ROUNDS - 1) + 4 + i, ROUNDS, 0, GROUPS - 1)

            @block.scalar
            def _(act):
                def outputs(r):
                    act.wait_ge(pv.sem, pv.at(TPB * (r + 1)))
                    if not isinstance(r, int) or r:
                        act.wait_ge(s1_free.sem, s1_free.at(sums_step(r) + 2))
                    act.copy(OT, k.psum[:, 6 * BANK:8 * BANK]).then_inc(o_in.sem, 1)

                def body(r, s, before, more, b, g):
                    for i, (kt, heads, size) in enumerate(second_units):
                        act.wait_ge(s2_up.sem, s2_up.at(r * N2 + i + 1))
                        if i == 0 or kt and after[kt - 1] == i:
                            act.wait_ge(pv.sem, pv.at(r * TPB + kt - 1))
                        base = (2 + 2 * (i % 2)) * BANK
                        if size > BANK:
                            place, into = k.psum[:, base + kt * P:base + 2 * BANK], PT[:, kt % 2, heads[0], kt * P:SEQ]
                        else:
                            stride = 2 * BANK // len(heads) if size > P else P
                            place = k.psum[:, base:base + len(heads) * stride].rearrange("p (h t) -> p h t", t=stride)[:, :, stride - size:]
                            into = PT[:, kt % 2, heads[0]:heads[0] + len(heads), kt * P:SEQ]
                        act.activation(into, place, ACT.Exp, scale=SCALE).then_inc(probs.sem, 1)
                        if i == 2 and before:
                            outputs(r - 1)
                rounds(act, body)
                outputs(ROUNDS - 1)

            @block.vector
            def _(dve):
                ring = [0]

                def ring_step(step, n, r, b, g):
                    kind, i = step
                    place = bank[ring[0]]
                    ring[0] = 1 - ring[0]
                    dve.wait_ge(s1_up.sem, s1_up.at(n + 1))
                    if kind in ("score", "soon"):
                        qt, half, heads, size = first_units[i]
                        dve.tensor_reduce(part[:, heads[0]:heads[0] + len(heads), qt, half:half + 1].rearrange("p h a -> p (h a)"),
                                          place[:, 0:len(heads) * size].rearrange("p (h t) -> p h t", t=size), AX_X, ALU.max).then_inc(s1_free.sem, 1)
                        if i == N1 - 1:
                            dve.wait_ge(s1_free.sem, s1_free.at(n + 1))
                            dve.tensor_tensor(top[:, :, :], part[:, :, :, 0], part[:, :, :, 1], ALU.max).then_inc(peak.sem, 1)
                    elif kind == "turn":
                        dve.tensor_scalar(low[:, 0, :], place[0:IN * TPB, 0:P], -1.0, None, ALU.mult).then_inc(s1_free.sem, 1)
                    elif kind == "sum":
                        half = slice(i * BANK, (i + 1) * BANK)
                        dve.tensor_tensor(ON[:, half], OT[:, half], place, ALU.mult).then_inc(s1_free.sem, 1)
                    else:
                        t = b * TPB + 4 * i
                        x = k.X[:, t:t + 4, :] if isinstance(t, int) else k.X[:, bass.ds(t, 4), :]
                        dve.tensor_tensor(x, x, place.rearrange("p (j d) -> p j d", d=D), ALU.add).then_inc(s1_free.sem, 1)

                def invert(r):
                    dve.wait_ge(sums_out.sem, sums_out.at(16 * IN * (r + 1)))
                    dve.reciprocal(inv[:, :], total[:, :]).then_inc(inverse.sem, 1)

                for n, step in enumerate(scoring + [("turn", 0)] + soon):
                    ring_step(step, n, -1, 0, 0)

                def body(r, s, before, more, b, g):
                    start = ring_start(r) if before else SHORT + LEAD
                    for n, step in enumerate(ring_steps(before, more)):
                        if before and n == (INVERSE_AT if more else 0):
                            invert(r - 1)
                        ring_step(step, start + n, r, b, g)
                rounds(dve, body)
                invert(ROUNDS - 1)
                for i, step in enumerate(ONES + OUT):
                    ring_step(step, ring_start(ROUNDS - 1) + 4 + i, ROUNDS, BATCH - 1, GROUPS - 1)



def local_transformer(k):
    nc = k.nc
    layernorm(k, sp_first=lambda sp: local_tables(k, sp))
    for depth in range(2):
        local_attention(k, depth)
        gated_units(k, depth)
    with nc.Block() as block:
        @block.vector
        def _(dve):
            for b in range(0, BATCH, 2):
                dve.tensor_tensor(k.xpart(b), k.xpart(b), k.zpart(b), ALU.add)

        @block.gpsimd
        def _(pool):
            for b in range(1, BATCH, 2):
                pool.tensor_tensor(k.xpart(b), k.xpart(b), k.zpart(b), ALU.add)


def local_tables(k, sp):
    d, loaded = k.dram, k.count("local_tables")
    HD = 64
    half = HD // 2
    base, mask, scales = local_places(k)
    sp.dma_start(base, d["c_rope"].rearrange("p (j a m d) -> p j a m d", j=TPB, a=2, m=2)).then_inc(loaded.sem, 16)
    sp.dma_start(mask, d["c_local"].rearrange("p (m c) -> p m c", m=2)).then_inc(loaded.sem, 16)
    for depth in range(2):
        for m, name in enumerate(("q_scale", "k_scale")):
            row = d["L1_ffn_" + name][depth]
            sp.dma_start(scales[depth][:, 0, m, :], row.partition_broadcast(P)).then_inc(loaded.sem, 16)
            sp.dma_start(scales[depth][:, 1, m, 0:half], row[half:HD].partition_broadcast(P)).then_inc(loaded.sem, 16)
            sp.dma_start(scales[depth][:, 1, m, half:HD], row[0:half].partition_broadcast(P)).then_inc(loaded.sem, 16)
    sp.wait_ge(loaded.sem, loaded.at(16 * 14))
    sp.wait_ge(k.layers_in.sem, 16 * 2 * LAYER_LOADS)


def local_places(k):
    base = k.arena[0][:, 2048:4096].rearrange("p (j a m d) -> p j a m d", j=TPB, a=2, m=2)
    mask = k.arena[3][:, 3584:4096].bitcast(BF16)[:, 0:2 * (64 + P)].rearrange("p (m c) -> p m c", m=2)
    return base, mask, [k.arena6[:, n:n + 256].rearrange("p (m a d) -> p m a d", m=2, a=2) for n in (512, 768)]


def local_attention(k, depth):
    nc, bank, psum = k.nc, k.bank, k.psum
    HEADS, HD, WIN = 8, 64, 64
    PAIRS, KEYS = HEADS // 2, WIN + P
    INNER = HEADS * HD
    A = k.arena
    w = k.layers[depth]
    names = ("zs", "ht_up", "ht", "qkv_up", "raw", "v_in", "sq", "ss", "ab", "rn", "rot", "tr_up", "qkt", "kt", "s_up", "peak", "probs",
             "pt_up", "pt_a", "pt_b", "pv_up", "o_in", "ot", "y_up", "added", "ready", "ready2", "held")
    (zs_in, ht_up, ht_in, qkv_up, raw_in, v_in, sq_in, ss_in, ab_in, rn_in, rot, tr_up, qkt, kt_in, s_up, peak, probs, pt_up, pt_a, pt_b,
     pv_up, o_in, ot_in, y_up, added, ready, ready2, held) = [k.count("local_" + n) for n in names]

    def cut(i, size, first, shape):
        n = int(np.prod(shape))
        flat = A[i][:, first:first + n]
        names = "abcd"[:len(shape)]
        return flat.rearrange(f"p ({' '.join(names)}) -> p {' '.join(names)}", **dict(zip(names, shape)))

    TABLE = cut(0, 0, 0, (TPB, 2, 2, HD))
    RAW = cut(1, 0, 0, (2, 2 * INNER))
    SQ = cut(1, 0, 2048, (2 * INNER,))
    HT = cut(1, 0, 3072, (2, P))
    ZS = cut(1, 0, 3328, (2, KEYS))
    COS = cut(2, 0, 0, (2, 2 * INNER))
    SIN = cut(2, 0, 2048, (2, 2 * INNER))
    QT = k.arena6[:, 1024:1024 + 4 * PAIRS * P].rearrange("p (s a c t) -> p s a c t", s=2, a=2, c=PAIRS)
    KT = cut(3, 0, 1024, (2, PAIRS, KEYS))
    OT = cut(3, 0, 3072, (PAIRS, P))
    BASE, MASK, scales = local_places(k)
    SC = scales[depth]
    PR = cut(4, 0, 0, (2, HEADS, 2 * P))
    PT = cut(5, 0, 0, (HEADS, 2, P))
    V = cut(5, 0, 2048, (4, INNER))
    small = k.arena6[:, 0:512].rearrange("p (s c) -> p s c", c=16)
    SS, RN, LOW, SUM, INV = (small[:, 2 * n:2 * n + 2, :] for n in range(5))
    SHIFT, CARRY = k.w["shift"], k.w["carry"]

    credited = (ht_in, v_in, qkt, kt_in, added, ot_in, pt_a, pt_b, ht_up, tr_up, rot, ab_in, s_up, pv_up, probs, pt_up, o_in, y_up,
                raw_in, ss_in, sq_in, zs_in, qkv_up, rn_in)
    CREDIT = RING = 4
    with nc.Block() as block:
        @block.sync
        def _(sp):
            for s in credited:
                sp.sem_inc(s.sem, CREDIT)

        @block.vector
        def _(dve):
            scales = SC.rearrange("p m a d -> p (m a) d")
            for j in range(TPB):
                dve.tensor_tensor(TABLE[:, j].rearrange("p m a d -> p (m a) d"), BASE[:, j].rearrange("p m a d -> p (m a) d"),
                                  scales, ALU.mult)
            if depth == 0:
                dve.memset(KT[:, 0, :, 0:WIN], 0.0)
                dve.memset(k.Zpad[:, 0:TILES + BATCH + 1:TPB + 1, :], 0.0)

        @block.gpsimd
        def _(pool):
            if depth == 0:
                pool.memset(PR[:, :, :, 0:WIN], 0.0)
                pool.memset(QT, 0.0)
                pool.memset(V[:, RING - 1, :], 0.0)
    for s in credited:
        s.passed(CREDIT)

    AHEAD = 4

    def group_of(g):
        return psum[:, (3 + 2 * g) * BANK:(5 + 2 * g) * BANK].rearrange("p (r c) -> p r c", c=2 * P)[:, :, 0:KEYS]

    def in_steps(eng, step, finish):
        loops = (TILES - RING - AHEAD) // RING
        for i in range(RING):
            step(i, i, AHEAD, i)
        with eng.Fori(1, 1 + loops) as p:
            for s in range(RING):
                step(p * RING + s, s, AHEAD, RING)
        for i in range(RING + RING * loops, TILES):
            step(i, i % RING, TILES - 1 - i, RING)
        finish(TILES - 1, (TILES - 1) % RING)

    with nc.Block() as block:
        @block.tensor
        def _(pe):
            def turn_in(i, s):
                pe.wait_ge(zs_in.sem, zs_in.at(i + 1))
                pe.wait_ge(ht_in.sem, ht_in.at(i))
                pe.wait_ge(ot_in.sem, ot_in.at(i - 3))
                pe.matmul(bank[7][0:64, 0:P], ZS[:, s, 64:128], k.ident, start=True, stop=True)
                pe.matmul(bank[7][64:P, 0:P], ZS[:, s, 128:192], SHIFT, start=True, stop=False)
                pe.matmul(bank[7][64:P, 0:P], ZS[:, s, 0:64], CARRY, start=False, stop=True).then_inc(ht_up.sem, 1)

            def project(i, s):
                pe.wait_ge(ht_in.sem, ht_in.at(i + 1))
                pe.wait_ge(qkt.sem, qkt.at(i - 1))
                pe.wait_ge(kt_in.sem, kt_in.at(i - 1))
                pe.wait_ge(added.sem, added.at(i - 3))
                for m in range(3):
                    mm = pe.matmul(bank[m], HT[:, s, :], w["wqkv"][:, m * INNER:(m + 1) * INNER], start=True, stop=True)
                mm.then_inc(qkv_up.sem, 1)

            def turn_qk(i, s):
                pe.wait_ge(rot.sem, rot.at(i + 1))
                for m in range(2):
                    for c in range(PAIRS):
                        mm = pe.transpose(bank[m][:, c * P:(c + 1) * P], COS[:, s, m * INNER + c * P:m * INNER + (c + 1) * P], k.ident)
                mm.then_inc(tr_up.sem, 1)

            def scores(i, s, g):
                pe.wait_ge(qkt.sem, qkt.at(i + 1))
                pe.wait_ge(kt_in.sem, kt_in.at(i + 1))
                pe.wait_ge((pt_a, pt_b)[g].sem, (pt_a, pt_b)[g].at(i))
                for c in range(PAIRS):
                    o = bank[3 + 2 * g + c // 2][:, 2 * P * (c % 2):2 * P * (c % 2) + KEYS]
                    pe.matmul(o, QT[:, s, g, c, :], KT[:, s, c, :], start=c % 2 == 0, stop=True, skip_group_check=True)
                for n in range(2):
                    o = bank[3 + 2 * g + n].rearrange("p (a c) -> p a c", a=2)[:, :, 0:KEYS]
                    rows = MASK[:, bass.ds((i % TPB + TPB - 1) // TPB, 1), :].broadcast_to([P, 2, KEYS])
                    mm = pe.matmul(o, k.identb, rows, start=False, stop=True, skip_group_check=True)
                mm.then_inc(s_up.sem, 1)

            def turn_probs(i, s, g):
                pe.wait_ge(o_in.sem, o_in.at(2 * i + g + 1))
                for c in range(PAIRS):
                    for n in range(2):
                        mm = pe.transpose(bank[3 + 2 * g + c // 2][:, P * (2 * (c % 2) + n):P * (2 * (c % 2) + n + 1)],
                                          PR[:, s, g * PAIRS + c, n * P:(n + 1) * P], k.ident)
                mm.then_inc(pt_up.sem, 1)

            def values(i, s, copied):
                pe.wait_ge(ht_in.sem, ht_in.at(copied))
                pe.wait_ge(pt_a.sem, pt_a.at(i + 1))
                pe.wait_ge(pt_b.sem, pt_b.at(i + 1))
                for c in range(PAIRS):
                    for n in range(2):
                        for a in range(2):
                            h = 2 * c + a
                            mm = pe.matmul(bank[7][64 * a:64 * a + 64, c * P:(c + 1) * P], V[:, (s + 3 + n) % RING, h * HD:(h + 1) * HD],
                                           PT[:, a * PAIRS + c, n, :], start=n == 0, stop=n == 1)
                mm.then_inc(pv_up.sem, 1)

            def output(i, copied):
                pe.wait_ge(v_in.sem, v_in.at(copied))
                pe.wait_ge(ot_in.sem, ot_in.at(i + 1))
                for c in range(PAIRS):
                    mm = pe.matmul(bank[2][:, 0:D], OT[:, c, :], w["wo"][:, c, :], start=c == 0, stop=c == PAIRS - 1)
                mm.then_inc(y_up.sem, 1)

            turn_in(0, 0)
            project(0, 0)
            turn_in(1, 1)
            for i in range(2):
                pe.wait_ge(raw_in.sem, raw_in.at(i + 1))
                pe.wait_ge(v_in.sem, v_in.at(i + 1))
                if i == 0:
                    project(1, 1)
                    turn_in(2, 0)
            turn_qk(0, 0)

            def step(i, s4, ahead, before):
                s = s4 % 2
                scores(i, s, 0)
                scores(i, s, 1)
                if before:
                    values(i - 1, s4 - 1, i + 3 if ahead > 1 else TILES)
                if ahead > 1:
                    if not before:
                        pe.wait_ge(v_in.sem, v_in.at(2))
                    project(i + 2, s)
                turn_probs(i, s, 0)
                if ahead > 2:
                    turn_in(i + 3, 1 - s)
                if ahead > 1:
                    pe.wait_ge(raw_in.sem, raw_in.at(i + 3))
                if ahead:
                    turn_qk(i + 1, 1 - s)
                if before:
                    output(i - 1, i + 3 if ahead > 1 else TILES)
                turn_probs(i, s, 1)

            def finish(i, s4):
                values(i, s4, TILES)
                pe.wait_ge(added.sem, added.at(i))
                output(i, TILES)
            in_steps(pe, step, finish)

        @block.scalar
        def _(act):
            def copy_h(i, s):
                act.wait_ge(ht_up.sem, ht_up.at(i + 1))
                act.wait_ge(qkv_up.sem, qkv_up.at(i - 1))
                act.copy(HT[:, s, :], bank[7][:, 0:P]).then_inc(ht_in.sem, 1)

            def take(i, s):
                act.wait_ge(qkv_up.sem, qkv_up.at(i + 1))
                act.wait_ge(ab_in.sem, ab_in.at(i - 1))
                act.copy(RAW[:, s, :], psum[:, 0:2 * BANK]).then_inc(raw_in.sem, 1)

            def take_v(i):
                act.wait_ge(pv_up.sem, pv_up.at(i - 2))
                act.sem_inc(held.sem, 1)
                act.copy(V[:, i % 4, :], bank[2]).then_inc(v_in.sem, 1)

            def square(i, s):
                act.wait_ge(raw_in.sem, raw_in.at(i + 1))
                act.wait_ge(ss_in.sem, ss_in.at(i))
                act.activation(SQ, RAW[:, s, :], ACT.Square).then_inc(sq_in.sem, 1)

            def copy_k(i, s):
                act.wait_ge(tr_up.sem, tr_up.at(i + 1))
                act.wait_ge(s_up.sem, s_up.at(2 * i))
                keys = bank[1].rearrange("p (c t) -> p c t", t=P)
                act.copy(KT[:, s, :, WIN:], keys)
                act.copy(KT[:, 1 - s, :, 0:WIN], keys[:, :, P - WIN:P]).then_inc(kt_in.sem, 1)

            def exponential(i, s, g):
                act.wait_ge(peak.sem, peak.at(2 * i + g + 1))
                act.wait_ge(pt_up.sem, pt_up.at(2 * (i - 1) + g - 1))
                for c in range(PAIRS):
                    r = g * PAIRS + c
                    e = act.activation(PR[:, s, r, WIN:], group_of(g)[:, c, :], ACT.Exp, bias=LOW[:, s, r:r + 1],
                                       accum_out=SUM[:, s, r:r + 1])
                e.then_inc(probs.sem, 1)

            copy_h(0, 0)
            for i in range(2):
                take(i, i)
                take_v(i)
                square(i, i)
                copy_h(i + 1, 1 - i)
            copy_k(0, 0)

            def step(i, s4, ahead, before):
                s = s4 % 2
                exponential(i, s, 0)
                exponential(i, s, 1)
                if ahead > 1:
                    take(i + 2, s)
                    take_v(i + 2)
                act.wait_ge(pt_up.sem, pt_up.at(2 * i + 1))
                act.wait_ge(pv_up.sem, pv_up.at(i))
                act.copy(PT[:, 0:4].rearrange("p r n t -> p (r n t)"), psum[:, 3 * BANK:5 * BANK]).then_inc(pt_a.sem, 1)
                if ahead > 2:
                    copy_h(i + 3, 1 - s)
                if ahead:
                    copy_k(i + 1, 1 - s)
                act.wait_ge(pt_up.sem, pt_up.at(2 * i + 2))
                act.copy(PT[:, 4:8].rearrange("p r n t -> p (r n t)"), psum[:, 5 * BANK:7 * BANK]).then_inc(pt_b.sem, 1)
                if ahead > 1:
                    square(i + 2, s)
            in_steps(act, step, lambda i, s: None)

        @block.vector
        def _(dve):
            def rotate(i, s, part):
                j = i % TPB
                raw = RAW[:, s, :].rearrange("p (m h d) -> p m h d", m=2, d=HD)
                cos = COS[:, s, :].rearrange("p (m h d) -> p m h d", m=2, d=HD)
                sin = SIN[:, s, :].rearrange("p (m h d) -> p m h d", m=2, d=HD)

                def table(a, lo, hi):
                    t = TABLE[:, bass.ds(j, 1), a, :, lo:hi].rearrange("p a m d -> p (a m) d")
                    return t.unsqueeze(2).broadcast_to([P, 2, HEADS, hi - lo])

                half = HD // 2
                if part == 0:
                    dve.wait_ge(raw_in.sem, raw_in.at(i + 1))
                    dve.wait_ge(tr_up.sem, tr_up.at(i - 1))
                    dve.tensor_tensor(cos, raw, table(0, 0, HD), ALU.mult)
                    return
                dve.tensor_tensor(sin[:, :, :, 0:half], raw[:, :, :, half:HD], table(1, 0, half), ALU.mult)
                dve.tensor_tensor(sin[:, :, :, half:HD], raw[:, :, :, 0:half], table(1, half, HD), ALU.mult).then_inc(ab_in.sem, 1)

            def squares(i, s):
                dve.wait_ge(sq_in.sem, sq_in.at(i + 1))
                dve.wait_ge(rn_in.sem, rn_in.at(2 * (i - 1)))
                dve.tensor_reduce(SS[:, s, :], SQ.rearrange("p (h d) -> p h d", d=HD), AX_X, ALU.add).then_inc(ss_in.sem, 1)

            def copy_q(i, s):
                dve.wait_ge(tr_up.sem, tr_up.at(i + 1))
                dve.wait_ge(s_up.sem, s_up.at(2 * i))
                for a in range(2):
                    half = slice(64 * a, 64 * a + 64)
                    q = dve.tensor_copy(QT[half, s, a].rearrange("p c t -> p (c t)"), bank[0][half, :])
                q.then_inc(qkt.sem, 1)

            def maximum(i, s, g):
                dve.wait_ge(s_up.sem, s_up.at(2 * i + g + 1))
                dve.tensor_reduce(LOW[:, s, g * PAIRS:(g + 1) * PAIRS], group_of(g), AX_X, ALU.max, negate=True).then_inc(peak.sem, 1)

            def normal(i, s, g):
                heads = slice(g * PAIRS, (g + 1) * PAIRS)
                dve.wait_ge(probs.sem, probs.at(2 * i + g + 1))
                dve.reciprocal(INV[:, s, heads], SUM[:, s, heads]).then_inc(ready.sem, 1)
                dve.wait_ge(ready.sem, ready.at(2 * i + g + 1))
                p = PR[:, s, heads, WIN:]
                dve.tensor_tensor(p, p, INV[:, s, heads].unsqueeze(2).broadcast_to([P, PAIRS, KEYS]), ALU.mult).then_inc(o_in.sem, 1)

            def copy_out(i):
                dve.wait_ge(pv_up.sem, pv_up.at(i + 1))
                dve.wait_ge(y_up.sem, y_up.at(i))
                dve.tensor_copy(OT.rearrange("p c t -> p (c t)"), bank[7]).then_inc(ot_in.sem, 1)

            def add(i):
                dve.wait_ge(y_up.sem, y_up.at(i + 1))
                z = k.Zpad[:, bass.ds(k.zindex(i), 1), :].rearrange("p a d -> p (a d)")
                dve.tensor_tensor(z, z, bank[2][:, 0:D], ALU.add).then_inc(added.sem, 1)

            for i in range(2):
                rotate(i, i, 0)
                rotate(i, i, 1)
                squares(i, i)
            copy_q(0, 0)

            def step(i, s4, ahead, before):
                s = s4 % 2
                maximum(i, s, 0)
                if before and ahead:
                    squares(i + 1, 1 - s)
                maximum(i, s, 1)
                if before > 1:
                    add(i - 2)
                normal(i, s, 0)
                if before:
                    copy_out(i - 1)
                normal(i, s, 1)
                if ahead > 1:
                    rotate(i + 2, s, 0)
                if ahead:
                    copy_q(i + 1, 1 - s)
                if ahead > 1:
                    rotate(i + 2, s, 1)

            def finish(i, s4):
                add(i - 1)
                copy_out(i)
                add(i)
            in_steps(dve, step, finish)

        @block.gpsimd
        def _(pool):
            def fetch(i, s):
                pool.wait_ge(ht_up.sem, ht_up.at(i - 1))
                pool.sem_inc(held.sem, 1)
                flat = k.Zpad.rearrange("p t d -> p (t d)")
                pool.tensor_copy(ZS[:, s, :], flat[:, bass.ds(k.zindex(i) * D - 64, KEYS)]).then_inc(zs_in.sem, 1)

            def norm(i, s):
                pool.wait_ge(ab_in.sem, ab_in.at(i + 1))
                pool.tensor_tensor(COS[:, s, :], COS[:, s, :], SIN[:, s, :], ALU.add).then_inc(ready2.sem, 1)
                pool.wait_ge(ss_in.sem, ss_in.at(i + 1))
                pool.tensor_tensor(RN[:, s, :], SS[:, s, :], k.minus_half[:, 0:2 * HEADS], ALU.pow).then_inc(rn_in.sem, 1)
                pool.wait_ge(rn_in.sem, rn_in.at(2 * i + 1))
                pool.sem_inc(held.sem, 1)
                pool.tensor_scalar(RN[:, s, :], RN[:, s, :], 1e12, 0.0, ALU.min, ALU.max).then_inc(rn_in.sem, 1)
                pool.wait_ge(ready2.sem, ready2.at(i + 1))
                pool.wait_ge(rn_in.sem, rn_in.at(2 * i + 2))
                heads = COS[:, s, :].rearrange("p (h d) -> p h d", d=HD)
                pool.tensor_tensor(heads, heads, RN[:, s, :].unsqueeze(2).broadcast_to([P, 2 * HEADS, HD]), ALU.mult).then_inc(
                    rot.sem, 1)

            for i in range(3):
                fetch(i, i % 2)
            norm(0, 0)
            fetch(3, 1)
            norm(1, 1)

            def step(i, s4, ahead, before):
                s = s4 % 2
                if ahead > 3:
                    fetch(i + 4, s)
                if ahead > 1:
                    norm(i + 2, s)
            in_steps(pool, step, lambda i, s: None)

    for s in (zs_in, ht_up, ht_in, qkv_up, raw_in, v_in, sq_in, ss_in, ab_in, rot, tr_up, qkt, kt_in, pt_a, pt_b, pv_up,
              ot_in, y_up, added, ready2):
        s.passed(TILES)
    for s in (peak, rn_in, s_up, probs, pt_up, o_in, ready):
        s.passed(2 * TILES)


LAYER_LOADS = 14


def load_layer(k, sp, depth, loaded):
    d, w, f = k.dram, k.layers[depth], "L1_ffn_"
    HID = d[f + "w2"].shape[1]
    whole = HID // P
    rest = HID - whole * P
    pairs = [
        (w["wqkv"], d[f + "wqkv"][depth]),
        (w["wo"], d[f + "wo"][depth].rearrange("(c p) d -> p c d", p=P)),
        (w["w1"], d[f + "w1"][depth].rearrange("p (m h) -> p m h", m=2)),
        (w["w2"][:, 0:whole, :], d[f + "w2"][depth][0:whole * P].rearrange("(c p) d -> p c d", p=P)),
        (w["w2"][0:rest, whole, :], d[f + "w2"][depth][whole * P:HID]),
        (w["w2"][rest:rest + 1, whole, :], d[f + "b2"][depth].rearrange("(a d) -> a d", a=1)),
        (w["ln"][:, 0:1], d[f + "ln_g"][depth].rearrange("(p a) -> p a", a=1)),
        (w["ln"][:, 1:2], d[f + "ln_b"][depth].rearrange("(p a) -> p a", a=1))]
    for m in range(2):
        for c, (a, r) in enumerate(halves(HID, P)):
            pairs.append((w["b1"][0:r, m, c:c + 1], d[f + "b1"][depth][m * HID + a:m * HID + a + r].rearrange("(p a) -> p a", a=1)))
    assert len(pairs) == LAYER_LOADS
    for into, source in pairs:
        sp.dma_start(into, source).then_inc(loaded.sem, 16)


def gated_units(k, depth):
    nc, bank, w = k.nc, k.bank, k.layers[depth]
    EPS = 1e-5
    UNIT = 4
    UNITS = TILES // UNIT
    HID = w["w1"].shape[2]
    CHUNKS = halves(HID, P)
    NC = len(CHUNKS)
    A = k.arena
    HN = A[0][:, 0:2 * BANK].rearrange("p (s j d) -> p s j d", s=2, d=D)
    HNT = A[0][:, 2 * BANK:4 * BANK].rearrange("p (s t) -> p s t", s=2)
    GL = A[1][:, 0:2 * BANK].rearrange("p (s t) -> p s t", s=2)
    PROD = A[2][:, 0:2 * NC * BANK].rearrange("p (s c t) -> p s c t", s=2, c=NC)
    small = k.arena6[:, 0:128]
    STATS = small[:, 0:24].rearrange("p (j c) -> p j c", j=UNIT)
    MV = small[:, 32:48].rearrange("p (s j c) -> p s j c", s=2, j=UNIT)
    RSTD = small[:, 48:56].rearrange("p (s j) -> p s j", s=2)
    VAR = small[:, 56:64].rearrange("p (s j) -> p s j", s=2)
    names = ("h_up", "stats", "moments", "rstd", "hn", "t_up", "hnt", "ag_up", "gelu", "prod", "y_up", "added", "held")
    h_up, stats, moments, rstd, hn, t_up, hnt, ag_up, gelu, prod, y_up, added, held = [k.count("units_" + n) for n in names]
    credited = (hn, hnt, prod, gelu, y_up, added, t_up, ag_up, h_up, rstd, moments, stats)
    CREDIT = 8
    for s in credited:
        s.passed(CREDIT)
    def in_steps(eng, step):
        loops = (UNITS - 2) // 2
        for u in range(2):
            step(u, u, 2, u > 0)
        with eng.Fori(1, loops) as p:
            for s in range(2):
                step(p * 2 + s, s, 2, True)
        for u in range(2 * loops, UNITS):
            step(u, u % 2, UNITS - 1 - u, True)

    with nc.Block() as block:
        @block.sync
        def _(sp):
            for s in credited:
                sp.sem_inc(s.sem, CREDIT)

        @block.tensor
        def _(pe):
            def shifted(u):
                pe.wait_ge(hn.sem, hn.at(u))
                z = k.zindex(u * UNIT)
                o = bank[0].rearrange("p (j d) -> p j d", d=D)
                pe.matmul(o[:, :, 0:64], k.ident, k.Zpad[:, bass.ds(z, UNIT), 0:64], start=True, stop=True, skip_group_check=True)
                pe.matmul(o[:, :, 64:P], k.w["shift"], k.Zpad[:, bass.ds(z, UNIT), 64:P], start=False, stop=False, skip_group_check=True)
                mm = pe.matmul(o[:, :, 64:P], k.w["carry"], k.Zpad[:, bass.ds(z - 1, UNIT), 64:P], start=False, stop=True,
                               skip_group_check=True)
                mm.then_inc(h_up.sem, 1)

            def turn(u, s):
                pe.wait_ge(hn.sem, hn.at(u + 1))
                pe.wait_ge(hnt.sem, hnt.at(u))
                for j in range(UNIT):
                    mm = pe.transpose(bank[1][:, j * P:(j + 1) * P], HN[:, s, j, :], k.ident)
                mm.then_inc(t_up.sem, 1)

            def back(u, s):
                pe.wait_ge(prod.sem, prod.at((u + 1) * NC))
                pe.wait_ge(added.sem, added.at(u))
                for j in range(UNIT):
                    for c, (a, r) in enumerate(CHUNKS):
                        r += c == NC - 1
                        mm = pe.matmul(bank[6][:, j * P:(j + 1) * P], PROD[0:r, s, c, j * P:(j + 1) * P], w["w2"][0:r, c, :],
                                       start=c == 0, stop=c == NC - 1)
                mm.then_inc(y_up.sem, 1)

            shifted(0)
            turn(0, 0)
            shifted(1)

            def step(u, s, ahead, before):
                pe.wait_ge(hnt.sem, hnt.at(u + 1))
                for c, (a, r) in enumerate(CHUNKS):
                    pe.wait_ge(prod.sem, prod.at(u * NC + c - 1))
                    for m in range(2):
                        mm = pe.matmul(bank[2 + 2 * ((s + c) % 2) + m][0:r, :], w["w1"][:, m, a:a + r], HNT[:, s, :], start=True, stop=True)
                    mm.then_inc(ag_up.sem, 1)
                    if c == 0 and before:
                        back(u - 1, 1 - s)
                    if c == 1 and ahead:
                        turn(u + 1, 1 - s)
                if ahead > 1:
                    shifted(u + 2)
            in_steps(pe, step)
            back(UNITS - 1, (UNITS - 1) % 2)

        @block.scalar
        def _(act):
            def affine(u, s):
                act.wait_ge(t_up.sem, t_up.at(u + 1))
                act.wait_ge(ag_up.sem, ag_up.at(NC * (u - 1)))
                act.activation(HNT[:, s, :], bank[1], ACT.Identity, scale=w["ln"][:, 0:1], bias=w["ln"][:, 1:2]).then_inc(hnt.sem, 1)

            affine(0, 0)

            def step(u, s, ahead, before):
                for c, (a, r) in enumerate(CHUNKS):
                    n = u * NC + c
                    act.wait_ge(ag_up.sem, ag_up.at(n + 1))
                    act.wait_ge(prod.sem, prod.at(n - 1))
                    act.activation(GL[0:r, (s + c) % 2, :], bank[3 + 2 * ((s + c) % 2)][0:r, :], ACT.Gelu,
                                   bias=w["b1"][0:r, 1, c:c + 1]).then_inc(gelu.sem, 1)
                    if c == 1 and ahead:
                        affine(u + 1, 1 - s)
            in_steps(act, step)

        @block.vector
        def _(dve):
            def moments_of(u, s):
                dve.wait_ge(h_up.sem, h_up.at(u + 1))
                for j in range(UNIT):
                    st = dve.bn_stats(STATS[:, j, :], bank[0][:, j * P:(j + 1) * P])
                st.then_inc(stats.sem, 1)
                dve.wait_ge(stats.sem, stats.at(u + 1))
                dve.wait_ge(rstd.sem, rstd.at(2 * u - 2))
                dve.sem_inc(held.sem, 1)
                for j in range(UNIT):
                    mv = dve.bn_aggr(MV[:, s, j, :], STATS[:, j, :])
                mv.then_inc(moments.sem, 1)

            def normalise(u, s):
                dve.wait_ge(rstd.sem, rstd.at(2 * u + 2))
                dve.wait_ge(t_up.sem, t_up.at(u - 1))
                for j in range(UNIT):
                    h = dve.tensor_scalar(HN[:, s, j, :], bank[0][:, j * P:(j + 1) * P], MV[:, s, j, 0:1], RSTD[:, s, j:j + 1],
                                          ALU.subtract, ALU.mult)
                h.then_inc(hn.sem, 1)

            def add(u):
                dve.wait_ge(y_up.sem, y_up.at(u + 1))
                z = k.Zpad[:, bass.ds(k.zindex(u * UNIT), UNIT), :]
                dve.tensor_tensor(z, z, bank[6].rearrange("p (j d) -> p j d", d=D), ALU.add).then_inc(added.sem, 1)

            moments_of(0, 0)
            dve.memset(PROD[:, :, NC - 1, :], 1.0)
            normalise(0, 0)
            moments_of(1, 1)

            def step(u, s, ahead, before):
                for c, (a, r) in enumerate(CHUNKS):
                    dve.wait_ge(gelu.sem, gelu.at(u * NC + c + 1))
                    dve.wait_ge(y_up.sem, y_up.at(u - 1))
                    dve.scalar_tensor_tensor(out=PROD[0:r, s, c, :], in0=bank[2 + 2 * ((s + c) % 2)][0:r, :],
                                             scalar=w["b1"][0:r, 0, c:c + 1], in1=GL[0:r, (s + c) % 2, :], op0=ALU.add,
                                             op1=ALU.mult).then_inc(prod.sem, 1)
                    if c == 0 and ahead:
                        normalise(u + 1, 1 - s)
                    if c == 1 and before:
                        add(u - 1)
                if ahead > 1:
                    moments_of(u + 2, s)
            in_steps(dve, step)
            add(UNITS - 1)

        @block.gpsimd
        def _(pool):
            with pool.Fori(0, UNITS // 2) as v:
                for s in range(2):
                    u = v * 2 + s
                    pool.wait_ge(moments.sem, moments.at(u + 1))
                    pool.sem_inc(held.sem, 1)
                    pool.tensor_scalar(VAR[:, s, :], MV[:, s, :, 1], 1.0, EPS, ALU.mult, ALU.add).then_inc(rstd.sem, 1)
                    pool.wait_ge(rstd.sem, rstd.at(2 * u + 1))
                    pool.tensor_tensor(RSTD[:, s, :], VAR[:, s, :], k.minus_half[:, 0:UNIT], ALU.pow).then_inc(rstd.sem, 1)

    for s in (h_up, stats, moments, hn, t_up, hnt, y_up, added):
        s.passed(UNITS)
    for s in (ag_up, gelu, prod):
        s.passed(UNITS * NC)
    rstd.passed(2 * UNITS)



def routed_ffn(k):
    nc, w, bank, psum = k.nc, k.w, k.bank, k.psum
    CAP, HEADS, HD, TOP = 64, 16, 8, 8
    T = BATCH * CAP // P
    PER = P // CAP
    N = BATCH * CAP
    EPS = 1e-6
    SCALE = float(1.0 / np.sqrt(HD))
    DFF = w["f_upT"].shape[2]
    CHUNKS = halves(DFF, P)
    GONE = -3.0e38
    A = k.arena
    layernorm(k)
    FT = A[0]
    HOTR = A[1][:, 0:T * SEQ].rearrange("p (t s) -> p t s", t=T)
    HOTT = A[1][:, T * SEQ:2 * T * SEQ].rearrange("p (t j r) -> p t j r", t=T, j=TPB)
    IOTA = A[2][:, 0:SEQ]
    SCORE = A[2][0:BATCH, SEQ:3 * SEQ].rearrange("p (s t) -> p s t", s=2)
    MASK = A[2][:, 3 * SEQ:3 * SEQ + BANK // 2].bitcast(BF16)
    QB = A[3].rearrange("p (b h q) -> p b h q", b=BATCH, h=HEADS)
    E = A[4][:, 0:BATCH * BANK].rearrange("p (b c t) -> p b c t", b=BATCH, c=TOP)
    PT = A[5][0:CAP, :].rearrange("p (b c r) -> p b c r", b=BATCH, c=HEADS // 2)
    at = [0]

    def place(*shape):
        n = int(np.prod(shape))
        names = "abcd"[:len(shape)]
        flat = k.arena6[:, at[0]:at[0] + n]
        at[0] += n
        return flat.rearrange(f"p ({' '.join(names)}) -> p {' '.join(names)}", **dict(zip(names, shape)))

    XS, XA, H, O, S2, H2, Y, SQ = (place(T, D) for _ in range(8))
    HT, QT, KT, OT, H2T = (place(N) for _ in range(5))
    V = place(BATCH, D)[0:CAP]
    SIL, PROD = place(len(CHUNKS), N), place(len(CHUNKS), N)
    HEADMASK = place(HEADS)
    IDX = place(T * CAP)[0:BATCH]
    IDXT = place(T)
    VALS = place(CAP)[0:BATCH]
    IDXU = place(CAP).bitcast(U32)[0:BATCH]
    SS, MS, RS = place(2, T), place(2, T), place(2, T)
    PEAK, SUM, INV = place(BATCH, TOP), place(BATCH, TOP), place(BATCH, TOP)
    names = ("loaded", "resid", "routed", "score", "rank", "idx", "idx_up", "idxT", "hotr", "hott_up", "hott", "picked", "xs", "ss",
             "rs", "h", "h_up", "ht", "qk_up", "qk", "v_up", "v", "qb", "s_up", "soft", "exp", "e", "pt_up", "pt", "pv", "o", "ot_up",
             "ot", "xa_up", "xa", "up", "sil", "prod", "down", "y", "spread", "added")
    c = {n: k.count("route_" + n) for n in names}

    def inc(ins, name):
        return ins.then_inc(c[name].sem, 16 if name == "loaded" else 1)

    def wait(eng, name, n):
        eng.wait_ge(c[name].sem, c[name].at(n))

    turn_stream(k, FT, SEQ, 0)
    with nc.Block() as block:
        @block.sync
        def _(sp):
            d = k.dram
            sp.dma_start(IOTA, d["c_iota"].partition_broadcast(P)).then_inc(c["loaded"].sem, 16)
            sp.dma_start(MASK, d["c_ranks"]).then_inc(c["loaded"].sem, 16)
            sp.dma_start(HEADMASK, d["c_heads"]).then_inc(c["loaded"].sem, 16)
            wait(sp, "loaded", 48)

        @block.gpsimd
        def _(pool):
            for b in range(BATCH):
                inc(pool.tensor_tensor(k.xpart(b), k.xpart(b), k.zpart(b), ALU.add), "resid")
            for n in range(2):
                wait(pool, "ss", T * (n + 1))
                inc(pool.tensor_scalar(MS[:, n, :], SS[:, n, :], 1.0 / D, EPS, ALU.mult, ALU.add), "rs")
                wait(pool, "rs", 2 * n + 1)
                inc(pool.tensor_tensor(RS[:, n, :], MS[:, n, :], k.minus_half[:, 0:T], ALU.pow), "rs")

        @block.tensor
        def _(pe):
            for h in range(2):
                for b in range(BATCH):
                    mm = pe.matmul(bank[h][0:BATCH, :], w["router4"][:, b, :], FT[:, b * SEQ + h * BANK:b * SEQ + (h + 1) * BANK],
                                   start=b == 0, stop=b == BATCH - 1)
            inc(mm, "routed")
            wait(pe, "idx", 2)
            inc(pe.matmul(bank[2][:, 0:BATCH], IDX, k.ident[0:BATCH, 0:BATCH], start=True, stop=True), "idx_up")
            for t in range(T):
                wait(pe, "hotr", t + 1)
                for j in range(TPB):
                    mm = pe.transpose(bank[4 + 2 * t + j // 4][:, (j % 4) * P:(j % 4 + 1) * P], HOTR[:, t, j * P:(j + 1) * P], k.ident)
                inc(mm, "hott_up")
            for t in range(T):
                wait(pe, "hott", t + 1)
                for i in range(PER):
                    for j in range(TPB):
                        mm = pe.matmul(bank[t][CAP * i:CAP * (i + 1), 0:D], HOTT[:, t, j, CAP * i:CAP * (i + 1)],
                                       k.Zpad[:, k.zindex((t * PER + i) * TPB + j), :], start=j == 0, stop=j == TPB - 1)
                inc(mm, "picked")
            for t in range(T):
                wait(pe, "h", t + 1)
                inc(pe.transpose(bank[2][:, t * P:(t + 1) * P], H[:, t, :], k.ident), "h_up")
            wait(pe, "ht", 1)
            for m in range(2):
                inc(pe.matmul(bank[3 + m][:, 0:N], w["qkvT"][:, m * D:(m + 1) * D], HT, start=True, stop=True), "qk_up")
            for b in range(BATCH):
                mm = pe.matmul(bank[5][0:CAP, b * D:(b + 1) * D], HT[:, b * CAP:(b + 1) * CAP], w["qkvT"][:, 2 * D:3 * D],
                               start=True, stop=True)
            inc(mm, "v_up")
            wait(pe, "qk", 2)
            wait(pe, "v", 1)
            wait(pe, "xs", T)
            for b in range(BATCH):
                wait(pe, "qb", b + 1)
                for n in range(HEADS // 2):
                    pe.matmul(bank[b][:, n * CAP:(n + 1) * CAP], QB[:, b, 2 * n:2 * n + 2, :].rearrange("p h q -> p (h q)"),
                              KT[:, b * CAP:(b + 1) * CAP], start=n == 0, stop=True, skip_group_check=True)
                inc(pe.matmul(bank[b], k.identb, MASK, start=False, stop=True, skip_group_check=True), "s_up")
            for b in range(BATCH):
                wait(pe, "e", b + 1)
                if b >= 2:
                    wait(pe, "pt", b - 1)
                for n in range(HEADS // 2):
                    mm = pe.transpose(bank[4 + 2 * (b % 2) + n // 4][0:CAP, (n % 4) * P:(n % 4 + 1) * P], E[:, b, n, :], k.ident)
                inc(mm, "pt_up")
            for b in range(BATCH):
                wait(pe, "pt", b + 1)
                for h in range(HEADS):
                    mm = pe.matmul(bank[b // PER][CAP * (b % PER):CAP * (b % PER + 1), h * HD:(h + 1) * HD],
                                   PT[:, b, h // 2, CAP * (h % 2):CAP * (h % 2 + 1)], V[:, b, h * HD:(h + 1) * HD], start=True, stop=True)
                inc(mm, "pv")
            for t in range(T):
                wait(pe, "o", t + 1)
                inc(pe.transpose(bank[2][:, t * P:(t + 1) * P], O[:, t, :], k.ident), "ot_up")
            wait(pe, "ot", 1)
            for t in range(T):
                inc(pe.matmul(bank[3][:, t * P:(t + 1) * P], OT[:, t * P:(t + 1) * P], w["f_outT"], start=True, stop=True), "xa_up")
            for t in range(T):
                wait(pe, "h", T + t + 1)
                inc(pe.transpose(bank[2][:, t * P:(t + 1) * P], H2[:, t, :], k.ident), "h_up")
            wait(pe, "ht", 2)
            for n, (a, r) in enumerate(CHUNKS):
                for m in range(2):
                    mm = pe.matmul(bank[4 + n][0:r, m * N:(m + 1) * N], w["f_upT"][:, m, a:a + r], H2T, start=True, stop=True)
                inc(mm, "up")
            for t in range(T):
                wait(pe, "prod", len(CHUNKS))
                for n, (a, r) in enumerate(CHUNKS):
                    mm = pe.matmul(bank[t][:, 0:D], PROD[0:r, n, t * P:(t + 1) * P], w["f_downT"][0:r, n, :], start=n == 0,
                                   stop=n == len(CHUNKS) - 1)
                inc(mm, "down")
            for b in range(BATCH):
                wait(pe, "y", b // PER + 1)
                wait(pe, "prod", len(CHUNKS))
                if b >= 3:
                    wait(pe, "added", b - 2)
                rows = slice(CAP * (b % PER), CAP * (b % PER + 1))
                for j in range(TPB):
                    mm = pe.matmul(bank[2 + 2 * (b % 3) + j // 4][:, (j % 4) * P:(j % 4 + 1) * P], HOTR[rows, b // PER, j * P:(j + 1) * P],
                                   Y[rows, b // PER, :], start=True, stop=True)
                inc(mm, "spread")

        @block.scalar
        def _(act):
            wait(act, "routed", 1)
            inc(act.copy(SCORE[:, 0, :], psum[0:BATCH, 0:SEQ]), "score")
            for t in range(T):
                wait(act, "hott_up", t + 1)
                inc(act.copy(HOTT[:, t].rearrange("p j r -> p (j r)"), psum[:, (4 + 2 * t) * BANK:(6 + 2 * t) * BANK]), "hott")
            for t in range(T):
                wait(act, "xs", t + 1)
                inc(act.activation(SQ[:, t, :], XS[:, t, :], ACT.Square, accum_out=SS[:, 0, t:t + 1]), "ss")
            wait(act, "h_up", T)
            inc(act.activation(HT, bank[2][:, 0:N], ACT.Copy, scale=w["f_g1"]), "ht")
            wait(act, "qk_up", 2)
            inc(act.copy(KT, bank[4][:, 0:N]), "qk")
            wait(act, "v_up", 1)
            inc(act.copy(V.rearrange("p b d -> p (b d)"), bank[5][0:CAP, :]), "v")
            for b in range(BATCH):
                wait(act, "soft", 2 * b + 2)
                e = E[:, b].rearrange("p c t -> p (c t)")
                inc(act.activation(e, e, ACT.Exp, scale=SCALE), "exp")
            for b in range(BATCH):
                wait(act, "pt_up", b + 1)
                first = 4 + 2 * (b % 2)
                inc(act.copy(PT[:, b].rearrange("p c r -> p (c r)"), psum[0:CAP, first * BANK:(first + 2) * BANK]), "pt")
            for t in range(T):
                wait(act, "xa", 2 * t + 2)
                inc(act.activation(SQ[:, t, :], S2[:, t, :], ACT.Square, accum_out=SS[:, 1, t:t + 1]), "ss")
            wait(act, "h_up", 2 * T)
            inc(act.activation(H2T, bank[2][:, 0:N], ACT.Copy, scale=w["f_g2"]), "ht")
            for n, (a, r) in enumerate(CHUNKS):
                wait(act, "up", n + 1)
                inc(act.activation(SIL[0:r, n, :], bank[4 + n][0:r, 0:N], ACT.Silu), "sil")

        @block.vector
        def _(dve):
            wait(dve, "score", 1)
            wait(dve, "loaded", 48)
            n = 0
            for r in range(CAP // TOP):
                cur, new = SCORE[:, r % 2, :], SCORE[:, (r + 1) % 2, :]
                part = slice(r * TOP, (r + 1) * TOP)
                if r:
                    wait(dve, "rank", 3 * r)
                inc(dve.max(VALS[:, part], cur), "rank")
                wait(dve, "rank", 3 * r + 1)
                inc(dve.max_index(IDXU[:, part], VALS[:, part], cur), "rank")
                inc(dve.match_replace(new, VALS[:, part], cur, GONE), "rank")
            wait(dve, "rank", 3 * CAP // TOP)
            for i in range(PER):
                inc(dve.tensor_copy(IDX[:, i * CAP:(i + 1) * CAP], IDXU), "idx")
            wait(dve, "idx_up", 1)
            for i in range(PER):
                rows = slice(i * CAP, (i + 1) * CAP)
                inc(dve.tensor_copy(IDXT[rows, :], bank[2][rows, i:BATCH:PER]), "idxT")
            wait(dve, "idxT", PER)
            for t in range(T):
                inc(dve.tensor_scalar(HOTR[:, t, :], IOTA, IDXT[:, t:t + 1], None, ALU.is_equal), "hotr")
            for t in range(T):
                wait(dve, "picked", t + 1)
                inc(dve.tensor_copy(XS[:, t, :], bank[t][:, 0:D]), "xs")
            wait(dve, "rs", 2)
            wait(dve, "xs", T)
            for t in range(T):
                inc(dve.tensor_scalar(H[:, t, :], XS[:, t, :], RS[:, 0, t:t + 1], None, ALU.mult), "h")
            wait(dve, "qk_up", 2)
            inc(dve.tensor_copy(QT, bank[3][:, 0:N]), "qk")
            wait(dve, "qk", 2)
            for b in range(BATCH):
                inc(dve.tensor_tensor(QB[:, b], QT[:, b * CAP:(b + 1) * CAP].unsqueeze(1).broadcast_to([P, HEADS, CAP]),
                                      HEADMASK.unsqueeze(2).broadcast_to([P, HEADS, CAP]), ALU.mult), "qb")
            for b in range(BATCH):
                s = bank[b].rearrange("p (c t) -> p c t", c=TOP)
                wait(dve, "s_up", b + 1)
                inc(dve.tensor_reduce(PEAK[:, b, :], s, AX_X, ALU.max), "soft")
                wait(dve, "soft", 2 * b + 1)
                inc(dve.tensor_tensor(E[:, b], s, PEAK[:, b, :].unsqueeze(2).broadcast_to([P, TOP, CAP]), ALU.subtract), "soft")
            for b in range(BATCH):
                wait(dve, "exp", b + 1)
                inc(dve.tensor_reduce(SUM[:, b, :], E[:, b], AX_X, ALU.add), "idx")
                wait(dve, "idx", 2 + 2 * b + 1)
                inc(dve.reciprocal(INV[:, b, :], SUM[:, b, :]), "idx")
                wait(dve, "idx", 2 + 2 * b + 2)
                inc(dve.tensor_tensor(E[:, b], E[:, b], INV[:, b, :].unsqueeze(2).broadcast_to([P, TOP, CAP]), ALU.mult), "e")
            for t in range(T):
                wait(dve, "pv", PER * (t + 1))
                inc(dve.tensor_copy(O[:, t, :], bank[t][:, 0:D]), "o")
            wait(dve, "ot_up", T)
            inc(dve.tensor_copy(OT, bank[2][:, 0:N]), "ot")
            wait(dve, "xa_up", T)
            for t in range(T):
                part = bank[3][:, t * P:(t + 1) * P]
                inc(dve.tensor_copy(XA[:, t, :], part), "xa")
                inc(dve.tensor_tensor(S2[:, t, :], XS[:, t, :], part, ALU.add), "xa")
            wait(dve, "rs", 4)
            wait(dve, "xa", 2 * T)
            for t in range(T):
                inc(dve.tensor_scalar(H2[:, t, :], S2[:, t, :], RS[:, 1, t:t + 1], None, ALU.mult), "h")
            for n, (a, r) in enumerate(CHUNKS):
                wait(dve, "sil", n + 1)
                inc(dve.tensor_tensor(PROD[0:r, n, :], SIL[0:r, n, :], bank[4 + n][0:r, N:2 * N], ALU.mult), "prod")
            for t in range(T):
                wait(dve, "down", t + 1)
                inc(dve.tensor_tensor(Y[:, t, :], XA[:, t, :], bank[t][:, 0:D], ALU.add), "y")
            wait(dve, "resid", BATCH)
            for b in range(BATCH):
                wait(dve, "spread", b + 1)
                first = 2 + 2 * (b % 3)
                inc(dve.tensor_tensor(k.xpart(b), k.xpart(b), psum[:, first * BANK:(first + 2) * BANK].rearrange(
                    "p (j d) -> p j d", d=D), ALU.add), "added")

    for n, total in (("loaded", 48), ("resid", BATCH), ("routed", 1), ("score", 1), ("rank", 3 * CAP // TOP), ("idx", 2 + 2 * BATCH),
                     ("idx_up", 1), ("idxT", PER), ("hotr", T), ("hott_up", T), ("hott", T), ("picked", T), ("xs", T), ("ss", 2 * T),
                     ("rs", 4), ("h", 2 * T), ("h_up", 2 * T), ("ht", 2), ("qk_up", 2), ("qk", 2), ("v_up", 1), ("v", 1),
                     ("qb", BATCH), ("s_up", BATCH), ("soft", 2 * BATCH), ("exp", BATCH), ("e", BATCH), ("pt_up", BATCH),
                     ("pt", BATCH), ("pv", BATCH), ("o", T), ("ot_up", T), ("ot", 1), ("xa_up", T), ("xa", 2 * T),
                     ("up", len(CHUNKS)), ("sil", len(CHUNKS)), ("prod", len(CHUNKS)), ("down", T), ("y", T), ("spread", BATCH),
                     ("added", BATCH)):
        c[n].passed(total)



def load(k):
    nc, d, w = k.nc, k.dram, k.w
    loads = []

    def keep(name, shape, *pairs, dt=F32):
        t = k.mem.enter_context(nc.sbuf_tensor("w_" + name, list(shape), dt))
        w[name] = t[tuple(slice(None) for _ in shape)]
        for into, source in pairs:
            loads.append((w[name] if into is None else t[into], source))
        return t

    def col(ap):
        return ap.rearrange("(p a) -> p a", a=1)

    def dup(name, ap):
        keep(name, (P, 1), ((slice(0, 64),), col(ap)), ((slice(64, 128),), col(ap)))

    x = k.dram["L0_attn_a_x"].rearrange("b s d -> (b s) d").rearrange("(t p) d -> p t d", p=P)
    for b in range(BATCH):
        loads.append((k.X[:, b * TPB:(b + 1) * TPB, :], x[:, b * TPB:(b + 1) * TPB, :]))
    keep("ident", (P, P), (None, d["c_ident"]))
    keep("identb", (P, P), (None, d["c_identb"]), dt=BF16)
    k.ident, k.identb = w["ident"], w["identb"]
    a = "L0_attn_a_"
    keep("W_up", (P, P), (None, d[a + "W_up"]))
    keep("up_left2", (P, P), ((slice(None), slice(0, 64)), d[a + "W_up"][:, 0:64]),
         ((slice(None), slice(64, 128)), d[a + "W_up"][:, 0:64]))
    keep("ln_gamma", (P, 1), (None, col(d[a + "ln_gamma"])))
    keep("ln_beta", (P, 1), (None, col(d[a + "ln_beta"])))
    dup("b_left2", d[a + "b_up"][0:64])
    keep("b_right", (64, 1), (None, col(d[a + "b_up"][64:128])))
    cw = d[a + "conv_w"].rearrange("d a c -> d (a c)")
    keep("conv_w2", (P, 3), ((slice(0, 64),), cw), ((slice(64, 128),), cw))
    dup("conv_b2", d[a + "conv_b"])
    dup("b_delta2", d[a + "b_delta"])
    keep("delta2", (64, P), ((slice(None), slice(0, 64)), d[a + "W_delta"]), ((slice(None), slice(64, 128)), d[a + "W_delta"]))
    keep("bc3", (64, 2, 96), *[((slice(None), m, slice(32 * r, 32 * r + 32)), d[a + n]) for m, n in enumerate(("W_B", "W_C"))
                               for r in range(3)])
    al = d[a + "A_log"].rearrange("d (n j) -> n d j", n=2)
    keep("A1", (P, 16), ((slice(0, 64),), al[0]), ((slice(64, 128),), al[1]))
    keep("D1col", (64, 1), (None, col(d[a + "D"])))
    keep("D1", (P, 64))
    keep("fold", (P, 64), (None, d["c_fold"]))
    keep("W_down", (64, P), (None, d[a + "W_down"]))
    keep("b_down_row", (P, P), (None, d[a + "b_down"].partition_broadcast(P)))
    keep("minus_half", (P, TILES))
    k.minus_half = w["minus_half"]
    LATER = len(loads)
    keep_later(k, keep, loads, col)

    FIRST = BATCH + 1
    assert loads[FIRST - 1][0] is w["ident"]
    loaded = k.count("loaded")
    with nc.Block() as block:
        @block.sync
        def _(sp):
            for into, source in loads[:FIRST]:
                sp.dma_start(into, source).then_inc(loaded.sem, 16)
            sp.wait_ge(loaded.sem, loaded.at(16 * FIRST))

        @block.vector
        def _(dve):
            dve.memset(w["minus_half"], -0.5)
            dve.memset(k.Zpad[:, 0:TILES + BATCH + 1:TPB + 1, :], 0.0)
    loaded.passed(16 * FIRST)

    def load_first(sp):
        for into, source in loads[FIRST:LATER]:
            sp.dma_start(into, source).then_inc(loaded.sem, 16)
        sp.wait_ge(loaded.sem, loaded.at(16 * (LATER - FIRST)))

    def load_later(sp, later):
        for into, source in loads[LATER:]:
            sp.dma_start(into, source).then_inc(later.sem, 16)
        if {6, 8} & set(STAGES):
            for depth in range(2):
                load_layer(k, sp, depth, k.layers_in)

    k.load_first, k.load_later, k.later_loads = load_first, load_later, 16 * (len(loads) - LATER)
    if 1 not in STAGES:
        later = k.count("later")
        with nc.Block() as block:
            @block.sync
            def _(sp):
                load_first(sp)
                load_later(sp, later)
                sp.wait_ge(later.sem, later.at(k.later_loads))
        later_weights(k)


def first_weights(k):
    nc, w = k.nc, k.w
    a_exp = k.count("a_exp")
    with nc.Block() as block:
        @block.scalar
        def _(act):
            act.activation(w["A1"], w["A1"], ACT.Exp).then_inc(a_exp.sem, 1)

        @block.vector
        def _(dve):
            dve.memset(w["D1"][64:P, :], 0.0)
            dve.tensor_scalar(w["D1"][0:64, :], k.ident[0:64, 0:64], w["D1col"], None, ALU.mult)
            dve.wait_ge(a_exp.sem, a_exp.at(1))
            dve.tensor_scalar(w["A1"], w["A1"], -1.0, None, ALU.mult)


def later_weights(k):
    nc, w = k.nc, k.w
    if 7 in STAGES:
        a_exp = k.count("a7_exp")
        with nc.Block() as block:
            @block.scalar
            def _(act):
                act.activation(w["A7"], w["A7"], ACT.Exp).then_inc(a_exp.sem, 1)

            @block.vector
            def _(dve):
                for hf in range(2):
                    dve.tensor_scalar(w["D7"][:, hf, :], k.ident, w["D7col"][:, hf:hf + 1], None, ALU.mult)
                dve.wait_ge(a_exp.sem, a_exp.at(1))
                dve.tensor_scalar(w["A7"], w["A7"], -1.0, None, ALU.mult)
    turn_weights(k)


def store(k):
    stored = k.count("stored")
    out = k.out.rearrange("b s d -> (b s) d").rearrange("(t p) d -> p t d", p=P)
    with k.nc.Block() as block:
        @block.sync
        def _(sp):
            for b in range(BATCH):
                part = slice(b * TPB, (b + 1) * TPB)
                sp.dma_start(out[:, part, :], k.X[:, part, :]).then_inc(stored.sem, 16)
            sp.wait_ge(stored.sem, 16 * BATCH)


def halves(n, size):
    return [(i, min(size, n - i)) for i in range(0, n, size)]


def keep_later(k, keep, loads, col):
    d, w = k.dram, k.w
    k.turn = turn = []
    natural = k.arena6
    at = [0]

    def turned(source, *pairs):
        r, c = source.shape
        place = natural[0:r, at[0]:at[0] + c]
        at[0] += c
        loads.append((place, source))
        turn.append((place, pairs or None))
        return len(turn) - 1

    def into(n, *pairs):
        turn[n] = (turn[n][0], pairs)

    full = slice(None)
    if {2, 4} & set(STAGES):
        f = "L0_ffn_"
        keep("qkvT", (P, 3 * D))
        for i, r in halves(3 * D, P):
            into(turned(d[f + "W_qkv"][i:i + r, :]), (w["qkvT"][:, i:i + r], full))
        keep("f_outT", (P, D))
        into(turned(d[f + "W_out"]), (w["f_outT"], full))
        DFF = d[f + "W1"].shape[0]
        keep("f_upT", (P, 2, DFF))
        for m, name in enumerate(("W1", "W2")):
            for i, r in halves(DFF, P):
                into(turned(d[f + name][i:i + r, :]), (w["f_upT"][:, m, i:i + r], full))
        keep("f_downT", (P, 3, D))
        for n, (i, r) in enumerate(halves(DFF, P)):
            into(turned(d[f + "W3"][:, i:i + r]), (w["f_downT"][0:r, n, :], full))
        keep("router", (P, 1), (None, col(d[f + "w_router"])))
        keep("router4", (P, BATCH, BATCH))
        keep("f_g1", (P, 1), (None, col(d[f + "g1"])))
        keep("f_g2", (P, 1), (None, col(d[f + "g2"])))
    if 3 in STAGES:
        keep("W_band", (P, P), (None, d["L0_attn_b_W"]))
    if 5 in STAGES:
        for n in "QKVO":
            keep("W" + n, (P, P), (None, d["L1_attn_a_W" + n]))
    if 7 in STAGES:
        f = "L1_attn_b_"
        keep("w7_inT", (P, 4 * P))
        for i, r in halves(4 * P, P):
            into(turned(d[f + "W_in"][i:i + r, :]), (w["w7_inT"][:, i:i + r], full))
        keep("w7_dtin", (P, 2, 64))
        keep("bc7", (P, 2, 2, 96))
        keep("w7_outT", (P, 2, P))
        for hf in range(2):
            into(turned(d[f + "W_x"][:, hf * P:(hf + 1) * P]), (w["w7_dtin"][:, hf, :], slice(0, 64)),
                 *[(w["bc7"][:, m, hf, 32 * r:32 * r + 16], slice(64 + 16 * m, 80 + 16 * m)) for m in range(2) for r in range(3)])
            into(turned(d[f + "W_out"][:, hf * P:(hf + 1) * P]), (w["w7_outT"][:, hf, :], full))
        keep("w7_dtT", (64, 2 * P))
        for i, r in halves(2 * P, P):
            into(turned(d[f + "W_dt"][i:i + r, :]), (w["w7_dtT"][:, i:i + r], full))

        def column2(ap):
            return [((full, slice(hf, hf + 1)), col(ap[hf * P:(hf + 1) * P])) for hf in range(2)]

        keep("ln7_g", (P, 1), (None, col(d[f + "ln_g"])))
        keep("ln7_b", (P, 1), (None, col(d[f + "ln_b"])))
        keep("conv7_w", (P, 2, 4), (None, d[f + "conv_w"].rearrange("(h p) a c -> p h (a c)", h=2)))
        keep("conv7_b", (P, 2), *column2(d[f + "conv_b"]))
        keep("b7_dt", (P, 2), *column2(d[f + "b_dt"]))
        keep("A7", (P, 2, 16), (None, d[f + "A_log"].rearrange("(h p) n -> p h n", h=2)))
        keep("D7col", (P, 2), *column2(d[f + "D_param"]))
        keep("D7", (P, 2, P))
        keep("alpha", (P, 1), (None, d[f + "alpha"].partition_broadcast(P)))
    if {6, 8} & set(STAGES):
        HID = d["L1_ffn_w2"].shape[1]
        k.layers = [{}, {}]
        k.layers_in = Count(k.mem.enter_context(k.nc.semaphore("layers_in")))
        for depth in range(2):
            for name, shape in (("wqkv", (P, 3 * 512)), ("wo", (P, 4, D)), ("w1", (P, 2, HID)), ("w2", (P, 3, D)), ("ln", (P, 2)),
                                ("b1", (P, 2, 3))):
                keep(f"layer{depth}_" + name, shape)
                k.layers[depth][name] = w[f"layer{depth}_" + name]
        keep("shift", (P, P), (None, d["c_shift"]))
        keep("carry", (P, P), (None, d["c_carry"]))


def turn_weights(k):
    nc, w = k.nc, k.w
    up, out, clear = k.count("turn_up"), k.count("turn_out"), k.count("turn_clear")
    if not k.turn:
        return
    with nc.Block() as block:
        @block.tensor
        def _(pe):
            for n, (place, _) in enumerate(k.turn):
                r, c = place.shape
                if n >= 8:
                    pe.wait_ge(out.sem, out.at(n - 7))
                pe.transpose(k.bank[n % 8][0:c, 0:r], place, k.ident[0:r, 0:r]).then_inc(up.sem, 1)

        @block.vector
        def _(dve):
            clears = 0
            if "bc7" in w:
                dve.memset(w["bc7"], 0.0).then_inc(clear.sem, 1)
                clears += 1
            if "router4" in w:
                dve.memset(w["router4"], 0.0).then_inc(clear.sem, 1)
                clears += 1
            if clears:
                dve.wait_ge(clear.sem, clear.at(clears))
            if "router4" in w:
                for b in range(BATCH):
                    dve.tensor_copy(w["router4"][:, b, b:b + 1], w["router"])
            for n, (place, pairs) in enumerate(k.turn):
                r, c = place.shape
                dve.wait_ge(up.sem, up.at(n + 1))
                for place2, cols in pairs:
                    cp = dve.tensor_copy(place2, k.bank[n % 8][0:c, 0:r][:, cols])
                cp.then_inc(out.sem, 1)


def more_constants(c, f32, bf16, eye):
    row = np.arange(96)
    state = np.where(row % 32 < 16, row % 32, -1)
    c["c_sel7"] = bf16(np.repeat(state[:, None] == np.arange(16)[None], P, axis=1))
    more_constants_attention(c, bf16)


def more_constants_attention(c, bf16):
    q, j, kk = np.arange(P)[:, None, None], np.arange(TPB)[None, :, None], np.arange(256)[None, None, :]
    key = j * P - 64 + kk
    ok = (np.abs(j * P + q - key) <= 64) & (key >= 0) & (key < SEQ)
    c["c_band"] = bf16(np.where(ok, 0.0, MASKED)).reshape(P, TPB * 256)
    i = np.arange(P)
    c["c_causal"] = bf16(np.where(i[:, None] >= i[None, :], 0.0, MASKED))
    c["c_causal_turned"] = bf16(np.where(i[:, None] <= i[None, :], 0.0, MASKED))
    c["c_ones"] = bf16(np.ones((3, 4 * SEQ)))
    c["c_sums"] = (i[:, None] == i[None, :] // 32 * 32 + 8).astype(np.float32)
    HD, WIN = 64, 64
    c["c_shift"] = np.eye(P, k=1, dtype=np.float32)
    carry = np.zeros((P, P), np.float32)
    carry[P - 1, 0] = 1
    c["c_carry"] = carry
    f32 = np.float32
    half = np.arange(0, HD, 2, dtype=f32)
    freq = (f32(1.0) / f32(10000.0) ** (half / f32(HD))).astype(f32)
    t = np.arange(SEQ, dtype=f32)
    angle = np.concatenate([t[:, None] * freq[None]] * 2, axis=1)
    base = ((half + f32(0.4 * HD)) / f32(1.4 * HD)).astype(f32)
    power = ((t - SEQ // 2) / f32(WIN // 2)).astype(f32)
    scale = np.concatenate([base[None] ** power[:, None]] * 2, axis=1).astype(f32)
    sign = np.where(np.arange(HD) < HD // 2, f32(-1), f32(1))
    cos, sin = np.cos(angle), np.sin(angle) * sign
    rope = np.stack([np.stack([cos * scale * f32(8), cos / scale]), np.stack([sin * scale * f32(8), sin / scale])])
    c["c_rope"] = rope.astype(f32).reshape(2, 2, TPB, P, HD).transpose(3, 2, 0, 1, 4).reshape(P, -1).copy()
    q, kk = np.arange(P)[:, None], np.arange(WIN + P)[None]
    back = q - (kk - WIN)
    ok = (back >= 0) & (back <= WIN)
    c["c_local"] = bf16(np.concatenate([np.where(ok & (kk >= WIN), 0.0, MASKED), np.where(ok, 0.0, MASKED)], axis=1))
    c["c_iota"] = np.arange(SEQ, dtype=f32)
    rank = np.arange(P)[:, None, None] % 64
    c["c_ranks"] = bf16(np.broadcast_to(np.where(rank >= np.arange(64)[None, None], 0.0, MASKED), (P, 8, 64)).reshape(P, 512))
    c["c_heads"] = (np.arange(P)[:, None] // 8 == np.arange(16)[None]).astype(f32)


def build(nc, dram, out):
    k = Core()
    k.nc, k.dram, k.out, k.w = nc, dram, out, {}
    counts, free = {}, []
    with ExitStack() as mem:
        k.mem = mem

        def count(name):
            if name not in counts:
                sem = free.pop() if free else mem.enter_context(nc.semaphore(name))
                counts[name] = Count(sem)
            return counts[name]

        def end_stage():
            used = [c.sem for c in counts.values()]
            with nc.Block() as block:
                @block.sync
                def _(sp):
                    for sem in used[0::3]:
                        sp.sem_clear(sem)

                @block.scalar
                def _(act):
                    for sem in used[1::3]:
                        act.sem_clear(sem)

                @block.gpsimd
                def _(pool):
                    for sem in used[2::3]:
                        pool.sem_clear(sem)
            free.extend(c.sem for c in counts.values())
            counts.clear()

        made = [0]

        def name(base):
            made[0] += 1
            return f"{base}_{made[0]}"

        k.count, k.name = count, name
        X = mem.enter_context(nc.sbuf_tensor("X", [P, TILES, D], F32))
        Zpad = mem.enter_context(nc.sbuf_tensor("Z", [P, TILES + BATCH + 1, D], F32))
        k.X, k.Zpad = X, Zpad[:, :, :]
        k.zindex = lambda i: i + i // TPB + 1
        k.zpart = lambda b: k.Zpad[:, b * (TPB + 1) + 1:(b + 1) * (TPB + 1), :]
        k.xpart = lambda b: k.X[:, b * TPB:(b + 1) * TPB, :]
        big = mem.enter_context(nc.sbuf_tensor("arena", [P, 6 * TOK + 16], F32))
        k.big = big
        k.arena = [big[:, (i * TOK + (16 if i > 2 else 0)):][:, 0:TOK] for i in range(6)]
        k.arena_wide = big[:, 2 * TOK:3 * TOK + 16]
        k.arena6 = mem.enter_context(nc.sbuf_tensor("arena6", [P, 6 * SEQ], F32))[:, :]
        k.ZZ = k.arena[0].rearrange("p (t d) -> p t d", d=D)
        psum = mem.enter_context(nc.psum_tensor("psum", [P, 8 * BANK], F32))
        k.psum = psum[:, :]
        k.bank = [psum[:, i * BANK:(i + 1) * BANK] for i in range(8)]
        load(k)
        stages = {1: mamba_small, 2: routed_ffn, 3: band_attention, 4: routed_ffn, 5: causal_attention,
                  6: local_transformer, 7: mamba_large, 8: local_transformer}
        for s in STAGES:
            stages[s](k)
            end_stage()
        store(k)


def upper_half(a):
    return (np.ascontiguousarray(a, dtype=np.float32).view(np.uint32) >> 16).astype(np.uint16)


def constants():
    f32, bf16 = np.float32, upper_half
    c = {}
    eye = np.eye(P, dtype=f32)
    c["c_ident"] = eye
    c["c_identb"] = bf16(eye)
    c["c_fold"] = np.concatenate([np.eye(64, dtype=f32)] * 2)
    row = np.arange(96) % 32
    lane = np.arange(16)[:, None] + 16 * (np.arange(P)[None, :] // 64)
    c["c_sel1"] = bf16((row[:, None, None] == lane[None]).reshape(96, 16 * P))
    more_constants(c, f32, bf16, eye)
    return c


def kernel(**inputs):
    import numpy as _np
    import concourse.bacc as _bacc
    from concourse import mybir as _mybir
    from concourse.bass_utils import run_bass_kernel_spmd as _run

    nc = _bacc.Bacc("TRN2", target_bir_lowering=False, num_devices=1)
    arrays, dram = {}, {}
    for source in (inputs, constants()):
        for name, value in source.items():
            a = _np.ascontiguousarray(value)
            arrays["in_" + name] = a
            dram[name] = nc.dram_tensor("in_" + name, a.shape, _mybir.dt.from_np(a.dtype), kind="ExternalInput").ap()
            if a.dtype == _np.uint16:
                dram[name] = dram[name].bitcast(_mybir.dt.bfloat16)
    out = nc.dram_tensor("out_x", (BATCH, SEQ, D), _mybir.dt.float32, kind="ExternalOutput").ap()
    build(nc, dram, out)
    r = _run(nc, [arrays], core_ids=[0])
    return r.results[0]["out_x"]
```
